# Optimizing a Trainium2 kernel written in Bass

```python
import numpy as np
import jax
import jax.numpy as jnp

def _softmax(x, axis=-1):
    return jax.nn.softmax(x, axis=axis)

def _gelu(x):
    return jax.nn.gelu(x, approximate=True)

def _silu(x):
    return jax.nn.silu(x)

def _sigmoid(x):
    return jax.nn.sigmoid(x)

def _layernorm(x, axis=-1, eps=1e-05):
    m = jnp.mean(x, axis=axis, keepdims=True)
    v = jnp.var(x, axis=axis, keepdims=True)
    return (x - m) / jnp.sqrt(v + eps)

def _scatter_add(tgt, idx, src, axis=0):
    return tgt.at[idx].add(src)

def _segment_sum(src, seg, n):
    return jax.ops.segment_sum(src, seg, n)
kernel_name = 'mk_seq_postln_d4_jaxref_r8_592770'

def setup_inputs(seed: int=0):
    np.random.seed(seed)
    _w = jnp.asarray

    def _L0_attn_setup():
        import jax, jax.numpy as jnp
        import numpy as np
        B, S, D, H = (4, 256, 128, 16)

        def _apply_rope(x):
            b, s, d = x.shape
            half = d // 2
            freq = jnp.exp(jnp.arange(0, d, 2, dtype=jnp.float32) * (-np.log(10000.0) / d))
            ang = jnp.arange(s, dtype=jnp.float32)[:, None] * freq[None, :]
            cos, sin = (jnp.cos(ang), jnp.sin(ang))
            x1, x2 = (x[..., :half], x[..., half:])
            return jnp.concatenate([x1 * cos - x2 * sin, x1 * sin + x2 * cos], axis=-1)
        key = jax.random.key(seed)
        ks = jax.random.split(key, 9)
        scale = 0.02
        x = jax.random.normal(ks[0], (B, S, D), dtype=jnp.float32)
        Wq = jax.random.normal(ks[1], (D, D), dtype=jnp.float32) * scale
        bq = jax.random.normal(ks[2], (D,), dtype=jnp.float32) * scale
        Wk = jax.random.normal(ks[3], (D, D), dtype=jnp.float32) * scale
        bk = jax.random.normal(ks[4], (D,), dtype=jnp.float32) * scale
        Wv = jax.random.normal(ks[5], (D, D), dtype=jnp.float32) * scale
        bv = jax.random.normal(ks[6], (D,), dtype=jnp.float32) * scale
        Wo = jax.random.normal(ks[7], (D, D), dtype=jnp.float32) * scale
        bo = jax.random.normal(ks[8], (D,), dtype=jnp.float32) * scale
        return {'x': x, 'Wq': Wq, 'bq': bq, 'Wk': Wk, 'bk': bk, 'Wv': Wv, 'bv': bv, 'Wo': Wo, 'bo': bo}
    _L0_attn_in = _L0_attn_setup()

    def _L0_ffn_setup():
        import jax, jax.numpy as jnp
        import numpy as np
        TOP_K = 2
        key = jax.random.key(seed)
        k1, k2, k3, k4 = jax.random.split(key, 4)
        B, T, D, F, E = (2, 128, 128, 256, 8)
        x = jax.random.normal(k1, (B, T, D), dtype=jnp.float32)
        Wg = jax.random.normal(k2, (D, E), dtype=jnp.float32) * 0.02
        W1 = jax.random.normal(k3, (E, D, F), dtype=jnp.float32) * 0.02
        W2 = jax.random.normal(k4, (E, F, D), dtype=jnp.float32) * 0.02
        return {'x': x, 'Wg': Wg, 'W1': W1, 'W2': W2}
    _L0_ffn_in = _L0_ffn_setup()

    def _L1_attn_setup():
        import jax, jax.numpy as jnp
        import numpy as np
        N_EMBD = 128
        EXPAND = 2
        D_INNER = N_EMBD * EXPAND
        D_STATE = 64
        N_HEADS = D_INNER // D_STATE
        HEAD_DIM = D_INNER // N_HEADS
        N_GROUPS = 1
        D_CONV = 4
        N_LAYERS = 48
        BATCH, SEQ = (1, 64)
        PROJ_SIZE = 2 * D_INNER + N_HEADS + 2 * N_GROUPS * D_STATE
        EPS = 1e-06

        def _mamba_fwd(x, norm_scale, w_in, conv_weight, conv_bias, A_log, dt_bias, w_out):
            b, T, _ = x.shape
            residual = x
            xn = x * jax.lax.rsqrt(jnp.mean(x * x, axis=-1, keepdims=True) + EPS) * norm_scale
            proj = xn @ w_in
            gate = proj[..., :D_INNER]
            ssm_in = proj[..., D_INNER:2 * D_INNER]
            dt_raw = proj[..., 2 * D_INNER:2 * D_INNER + N_HEADS]
            gs = N_GROUPS * D_STATE
            B = proj[..., 2 * D_INNER + N_HEADS:2 * D_INNER + N_HEADS + gs].reshape(b, T, N_GROUPS, D_STATE)
            C = proj[..., 2 * D_INNER + N_HEADS + gs:].reshape(b, T, N_GROUPS, D_STATE)
            xp = jnp.pad(ssm_in, ((0, 0), (D_CONV - 1, 0), (0, 0)))
            conv = conv_bias + sum((conv_weight[k] * xp[:, k:k + T, :] for k in range(D_CONV)))
            h = jax.nn.silu(conv)
            dt = jax.nn.softplus(dt_raw + dt_bias)
            A = -jnp.exp(A_log)
            A_bar = jnp.exp(A[None, None, :] * dt)
            hpg = N_HEADS // N_GROUPS
            xh = h.reshape(b, T, N_HEADS, HEAD_DIM)
            Bh = jnp.repeat(B, hpg, axis=2)
            Ch = jnp.repeat(C, hpg, axis=2)
            Bu = Bh[:, :, :, None, :] * (dt[..., None, None] * xh[..., None])

            def _binary_op(left, right):
                a_l, b_l = left
                a_r, b_r = right
                return (a_l * a_r, a_r * b_l + b_r)
            _, states = jax.lax.associative_scan(_binary_op, (A_bar[..., None, None], Bu), axis=1)
            y = jnp.einsum('bthpn,bthn->bthp', states, Ch).reshape(b, T, D_INNER)
            y = y * jax.nn.silu(gate)
            y = y @ w_out
            return residual + y
        key = jax.random.key(seed)
        ks = jax.random.split(key, 6)
        init_std = 0.02
        proj_std = 0.02 / np.sqrt(2 * N_LAYERS)
        return {'x': jax.random.normal(ks[0], (BATCH, SEQ, N_EMBD), jnp.float32), 'norm_scale': jnp.ones((N_EMBD,), jnp.float32), 'w_in': jax.random.normal(ks[1], (N_EMBD, PROJ_SIZE), jnp.float32) * init_std, 'conv_weight': jax.random.normal(ks[2], (D_CONV, D_INNER), jnp.float32) * 0.02, 'conv_bias': jnp.zeros((D_INNER,), jnp.float32), 'A_log': jnp.log(0.5 + jnp.arange(N_HEADS, dtype=jnp.float32) * 0.5 / N_HEADS), 'dt_bias': jax.random.normal(ks[3], (N_HEADS,), jnp.float32) * 0.1, 'w_out': jax.random.normal(ks[4], (D_INNER, N_EMBD), jnp.float32) * proj_std}
    _L1_attn_in = _L1_attn_setup()

    def _L1_ffn_setup():
        import jax, jax.numpy as jnp
        import numpy as np
        B, L, D = (4, 256, 128)
        H = 16
        E = 16
        NS = 16
        S = NS // E
        F = 512
        EPS = 1e-05

        def _layernorm(x, g, b):
            mu = jnp.mean(x, axis=-1, keepdims=True)
            var = jnp.mean(jnp.square(x - mu), axis=-1, keepdims=True)
            return (x - mu) * jax.lax.rsqrt(var + EPS) * g + b

        def _mha(q, k, v, Wq, bq, Wk, bk, Wv, bv, Wo, bo):
            Bq, Lq, Dm = q.shape
            dh = Dm // H
            qh = (q @ Wq + bq).reshape(Bq, Lq, H, dh)
            kh = (k @ Wk + bk).reshape(Bq, -1, H, dh)
            vh = (v @ Wv + bv).reshape(Bq, -1, H, dh)
            scores = jnp.einsum('bqhd,bkhd->bhqk', qh, kh) / jnp.asarray(np.sqrt(dh), q.dtype)
            attn = jax.nn.softmax(scores, axis=-1)
            out = jnp.einsum('bhqk,bkhd->bqhd', attn, vh).reshape(Bq, Lq, Dm)
            return out @ Wo + bo
        key = jax.random.key(seed)
        ks = jax.random.split(key, 32)
        s = 0.02
        d = {}
        d['x'] = jax.random.normal(ks[0], (B, L, D), jnp.float32)
        d['slot_query'] = jax.random.normal(ks[1], (1, NS, D), jnp.float32) * 0.01
        for i, nm in enumerate(['d_Wq', 'd_Wk', 'd_Wv', 'd_Wo']):
            d[nm] = jax.random.normal(ks[2 + i], (D, D), jnp.float32) * s
        for nm in ['d_bq', 'd_bk', 'd_bv', 'd_bo']:
            d[nm] = jnp.zeros((D,), jnp.float32)
        for i, nm in enumerate(['c_Wq', 'c_Wk', 'c_Wv', 'c_Wo']):
            d[nm] = jax.random.normal(ks[6 + i], (D, D), jnp.float32) * s
        for nm in ['c_bq', 'c_bk', 'c_bv', 'c_bo']:
            d[nm] = jnp.zeros((D,), jnp.float32)
        d['e_ln_g'] = jnp.ones((E, D), jnp.float32)
        d['e_ln_b'] = jnp.zeros((E, D), jnp.float32)
        d['e_W1'] = jax.random.normal(ks[10], (E, D, F), jnp.float32) * s
        d['e_b1'] = jnp.zeros((E, F), jnp.float32)
        d['e_Wg'] = jax.random.normal(ks[11], (E, D, F), jnp.float32) * s
        d['e_bg'] = jnp.zeros((E, F), jnp.float32)
        d['e_W2'] = jax.random.normal(ks[12], (E, F, D), jnp.float32) * s
        d['e_b2'] = jnp.zeros((E, D), jnp.float32)
        return d
    _L1_ffn_in = _L1_ffn_setup()

    def _L2_attn_setup():
        import jax, jax.numpy as jnp
        import numpy as np
        HEADS = 8
        K_SIZE = 64
        key = jax.random.key(seed)
        k1, k2, k3, k4 = jax.random.split(key, 4)
        B, C, D = (4, 256, 128)
        return {'x': jax.random.normal(k1, (B, C, D), dtype=jnp.float32), 'Mq': jax.random.normal(k2, (D, HEADS * K_SIZE), dtype=jnp.float32) * 0.02, 'Mk': jax.random.normal(k3, (D, HEADS * K_SIZE), dtype=jnp.float32) * 0.02, 'Mv': jax.random.normal(k4, (D, 128), dtype=jnp.float32) * 0.02}
    _L2_attn_in = _L2_attn_setup()

    def _L2_ffn_setup():
        import jax, jax.numpy as jnp
        import numpy as np
        ALPHA = 2.0
        TOP_K = 2
        key = jax.random.key(seed)
        ks = jax.random.split(key, 8)
        B, S, D, H, E = (2, 256, 128, 512, 8)
        Er = E - 1
        s_in = 1.0 / np.sqrt(D)
        s_hid = 1.0 / np.sqrt(H)
        return {'x': jax.random.normal(ks[0], (B, S, D), dtype=jnp.float32), 'router_w': jax.random.normal(ks[1], (D, E), dtype=jnp.float32) * s_in, 'up_w': jax.random.normal(ks[2], (Er, D, H), dtype=jnp.float32) * s_in, 'gate_w': jax.random.normal(ks[3], (Er, D, H), dtype=jnp.float32) * s_in, 'down_w': jax.random.normal(ks[4], (Er, H, D), dtype=jnp.float32) * s_hid * 0.1, 'shared_up_w': jax.random.normal(ks[5], (D, H), dtype=jnp.float32) * s_in, 'shared_gate_w': jax.random.normal(ks[6], (D, H), dtype=jnp.float32) * s_in, 'shared_down_w': jax.random.normal(ks[7], (H, D), dtype=jnp.float32) * s_hid * 0.1}
    _L2_ffn_in = _L2_ffn_setup()

    def _L3_attn_setup():
        import jax, jax.numpy as jnp
        import numpy as np
        DT_MIN, DT_MAX = (0.001, 0.1)
        STEP_RESCALE = 1.0

        def _s5_forward(u, Lambda_re, Lambda_im, B, C, D, log_step):
            Lambda = jnp.minimum(Lambda_re, -0.0001) + 1j * Lambda_im
            B_tilde = (B[..., 0] + 1j * B[..., 1]).astype(jnp.complex64)
            C_tilde = (C[..., 0] + 1j * C[..., 1]).astype(jnp.complex64)
            step = STEP_RESCALE * jnp.exp(log_step[:, 0])
            Lambda_bar = jnp.exp(Lambda * step)
            B_bar = ((Lambda_bar - 1.0) / Lambda)[:, None] * B_tilde
            Bu = jnp.einsum('blh,ph->blp', u.astype(jnp.complex64), B_bar)
            A = jnp.broadcast_to(Lambda_bar, Bu.shape)

            def combine(e_i, e_j):
                a_i, b_i = e_i
                a_j, b_j = e_j
                return (a_j * a_i, a_j * b_i + b_j)
            _, xs = jax.lax.associative_scan(combine, (A, Bu), axis=1)
            ys = jnp.einsum('blp,hp->blh', xs, C_tilde).real + D * u
            return ys
        key = jax.random.key(seed)
        ks = jax.random.split(key, 7)
        Bsz, L, H, P = (8, 512, 128, 64)
        u = jax.random.normal(ks[0], (Bsz, L, H), jnp.float32)
        Lambda_re = -0.5 * jnp.abs(jax.random.normal(ks[1], (P,), jnp.float32)) - 0.1
        Lambda_im = jnp.pi * jax.random.normal(ks[2], (P,), jnp.float32)
        Bp = jax.random.normal(ks[3], (P, H, 2), jnp.float32) / np.sqrt(H)
        Cp = jax.random.normal(ks[4], (H, P, 2), jnp.float32) / np.sqrt(P)
        D = jax.random.normal(ks[5], (H,), jnp.float32)
        log_step = jnp.log(jax.random.uniform(ks[6], (P, 1), jnp.float32) * (DT_MAX - DT_MIN) + DT_MIN)
        return {'u': u, 'Lambda_re': Lambda_re, 'Lambda_im': Lambda_im, 'B': Bp, 'C': Cp, 'D': D, 'log_step': log_step}
    _L3_attn_in = _L3_attn_setup()

    def _L3_ffn_setup():
        import jax, jax.numpy as jnp
        import numpy as np
        B, S, H = (4, 256, 128)
        E = 8
        GS = 2
        NG = E // GS
        F = int(H * 4 * (2.0 / 3.0))
        key = jax.random.key(seed)
        ks = jax.random.split(key, 7)
        sc_h = 1.0 / np.sqrt(H)
        sc_f = 1.0 / np.sqrt(F)
        return {'x': jax.random.normal(ks[0], (B, S, H), dtype=jnp.float32), 'Wr': jax.random.normal(ks[1], (H, E), dtype=jnp.float32) * sc_h, 'br': jnp.zeros((E,), dtype=jnp.float32), 'W_up': jax.random.normal(ks[2], (NG, H, F), dtype=jnp.float32) * sc_h, 'b_up': jax.random.normal(ks[3], (NG, F), dtype=jnp.float32) * 0.01, 'W_down': jax.random.normal(ks[4], (E, F, H), dtype=jnp.float32) * sc_f, 'b_down': jax.random.normal(ks[5], (E, H), dtype=jnp.float32) * 0.01}
    _L3_ffn_in = _L3_ffn_setup()
    _d = {'L0_attn_x': _L0_attn_in['x'], 'L0_attn_Wq': _L0_attn_in['Wq'], 'L0_attn_bq': _L0_attn_in['bq'], 'L0_attn_Wk': _L0_attn_in['Wk'], 'L0_attn_bk': _L0_attn_in['bk'], 'L0_attn_Wv': _L0_attn_in['Wv'], 'L0_attn_bv': _L0_attn_in['bv'], 'L0_attn_Wo': _L0_attn_in['Wo'], 'L0_attn_bo': _L0_attn_in['bo'], 'L0_ffn_Wg': _L0_ffn_in['Wg'], 'L0_ffn_W1': _L0_ffn_in['W1'], 'L0_ffn_W2': _L0_ffn_in['W2'], 'L1_attn_norm_scale': _L1_attn_in['norm_scale'], 'L1_attn_w_in': _L1_attn_in['w_in'], 'L1_attn_conv_weight': _L1_attn_in['conv_weight'], 'L1_attn_conv_bias': _L1_attn_in['conv_bias'], 'L1_attn_A_log': _L1_attn_in['A_log'], 'L1_attn_dt_bias': _L1_attn_in['dt_bias'], 'L1_attn_w_out': _L1_attn_in['w_out'], 'L1_ffn_slot_query': _L1_ffn_in['slot_query'], 'L1_ffn_d_Wq': _L1_ffn_in['d_Wq'], 'L1_ffn_d_Wk': _L1_ffn_in['d_Wk'], 'L1_ffn_d_Wv': _L1_ffn_in['d_Wv'], 'L1_ffn_d_Wo': _L1_ffn_in['d_Wo'], 'L1_ffn_d_bq': _L1_ffn_in['d_bq'], 'L1_ffn_d_bk': _L1_ffn_in['d_bk'], 'L1_ffn_d_bv': _L1_ffn_in['d_bv'], 'L1_ffn_d_bo': _L1_ffn_in['d_bo'], 'L1_ffn_c_Wq': _L1_ffn_in['c_Wq'], 'L1_ffn_c_Wk': _L1_ffn_in['c_Wk'], 'L1_ffn_c_Wv': _L1_ffn_in['c_Wv'], 'L1_ffn_c_Wo': _L1_ffn_in['c_Wo'], 'L1_ffn_c_bq': _L1_ffn_in['c_bq'], 'L1_ffn_c_bk': _L1_ffn_in['c_bk'], 'L1_ffn_c_bv': _L1_ffn_in['c_bv'], 'L1_ffn_c_bo': _L1_ffn_in['c_bo'], 'L1_ffn_e_ln_g': _L1_ffn_in['e_ln_g'], 'L1_ffn_e_ln_b': _L1_ffn_in['e_ln_b'], 'L1_ffn_e_W1': _L1_ffn_in['e_W1'], 'L1_ffn_e_b1': _L1_ffn_in['e_b1'], 'L1_ffn_e_Wg': _L1_ffn_in['e_Wg'], 'L1_ffn_e_bg': _L1_ffn_in['e_bg'], 'L1_ffn_e_W2': _L1_ffn_in['e_W2'], 'L1_ffn_e_b2': _L1_ffn_in['e_b2'], 'L2_attn_Mq': _L2_attn_in['Mq'], 'L2_attn_Mk': _L2_attn_in['Mk'], 'L2_attn_Mv': _L2_attn_in['Mv'], 'L2_ffn_router_w': _L2_ffn_in['router_w'], 'L2_ffn_up_w': _L2_ffn_in['up_w'], 'L2_ffn_gate_w': _L2_ffn_in['gate_w'], 'L2_ffn_down_w': _L2_ffn_in['down_w'], 'L2_ffn_shared_up_w': _L2_ffn_in['shared_up_w'], 'L2_ffn_shared_gate_w': _L2_ffn_in['shared_gate_w'], 'L2_ffn_shared_down_w': _L2_ffn_in['shared_down_w'], 'L3_attn_Lambda_re': _L3_attn_in['Lambda_re'], 'L3_attn_Lambda_im': _L3_attn_in['Lambda_im'], 'L3_attn_B': _L3_attn_in['B'], 'L3_attn_C': _L3_attn_in['C'], 'L3_attn_D': _L3_attn_in['D'], 'L3_attn_log_step': _L3_attn_in['log_step'], 'L3_ffn_Wr': _L3_ffn_in['Wr'], 'L3_ffn_br': _L3_ffn_in['br'], 'L3_ffn_W_up': _L3_ffn_in['W_up'], 'L3_ffn_b_up': _L3_ffn_in['b_up'], 'L3_ffn_W_down': _L3_ffn_in['W_down'], 'L3_ffn_b_down': _L3_ffn_in['b_down']}
    _x0 = _d['L0_attn_x']
    _d['L0_attn_x'] = jax.random.normal(jax.random.fold_in(jax.random.key(seed), 1), (4, 1024, 128), dtype=_x0.dtype)
    del _x0
    return _d

def reference(L0_attn_x, L0_attn_Wq, L0_attn_bq, L0_attn_Wk, L0_attn_bk, L0_attn_Wv, L0_attn_bv, L0_attn_Wo, L0_attn_bo, L0_ffn_Wg, L0_ffn_W1, L0_ffn_W2, L1_attn_norm_scale, L1_attn_w_in, L1_attn_conv_weight, L1_attn_conv_bias, L1_attn_A_log, L1_attn_dt_bias, L1_attn_w_out, L1_ffn_slot_query, L1_ffn_d_Wq, L1_ffn_d_Wk, L1_ffn_d_Wv, L1_ffn_d_Wo, L1_ffn_d_bq, L1_ffn_d_bk, L1_ffn_d_bv, L1_ffn_d_bo, L1_ffn_c_Wq, L1_ffn_c_Wk, L1_ffn_c_Wv, L1_ffn_c_Wo, L1_ffn_c_bq, L1_ffn_c_bk, L1_ffn_c_bv, L1_ffn_c_bo, L1_ffn_e_ln_g, L1_ffn_e_ln_b, L1_ffn_e_W1, L1_ffn_e_b1, L1_ffn_e_Wg, L1_ffn_e_bg, L1_ffn_e_W2, L1_ffn_e_b2, L2_attn_Mq, L2_attn_Mk, L2_attn_Mv, L2_ffn_router_w, L2_ffn_up_w, L2_ffn_gate_w, L2_ffn_down_w, L2_ffn_shared_up_w, L2_ffn_shared_gate_w, L2_ffn_shared_down_w, L3_attn_Lambda_re, L3_attn_Lambda_im, L3_attn_B, L3_attn_C, L3_attn_D, L3_attn_log_step, L3_ffn_Wr, L3_ffn_br, L3_ffn_W_up, L3_ffn_b_up, L3_ffn_W_down, L3_ffn_b_down):

    def _L0_attn_ref(x, Wq, bq, Wk, bk, Wv, bv, Wo, bo):
        import jax, jax.numpy as jnp
        import numpy as np
        B, S, D, H = (4, 256, 128, 16)

        def _apply_rope(x):
            b, s, d = x.shape
            half = d // 2
            freq = jnp.exp(jnp.arange(0, d, 2, dtype=jnp.float32) * (-np.log(10000.0) / d))
            ang = jnp.arange(s, dtype=jnp.float32)[:, None] * freq[None, :]
            cos, sin = (jnp.cos(ang), jnp.sin(ang))
            x1, x2 = (x[..., :half], x[..., half:])
            return jnp.concatenate([x1 * cos - x2 * sin, x1 * sin + x2 * cos], axis=-1)
        b, s, d = x.shape
        h = H
        hd = d // h
        rx = _apply_rope(x)

        def proj(W, bias):
            y = rx @ W.T + bias
            return y.reshape(b, s, h, hd).transpose(0, 2, 1, 3)
        q, k, v = (proj(Wq, bq), proj(Wk, bk), proj(Wv, bv))
        scores = jnp.einsum('bhqd,bhkd->bhqk', q, k) / np.sqrt(hd)
        attn = jax.nn.softmax(scores, axis=-1)
        attended = jnp.einsum('bhqk,bhkd->bhqd', attn, v)
        attended = attended.transpose(0, 2, 1, 3).reshape(b, s, d)
        return attended @ Wo.T + bo

    def _L0_ffn_ref(x, Wg, W1, W2):
        import jax, jax.numpy as jnp
        import numpy as np
        TOP_K = 2
        B, T, D = x.shape
        E = Wg.shape[-1]
        xt = x.reshape(B * T, D)
        logits = xt @ Wg
        probs = jax.nn.softmax(logits, axis=-1)
        topw, topi = jax.lax.top_k(probs, TOP_K)
        topw = topw / jnp.sum(topw, axis=-1, keepdims=True)
        combine = jnp.sum(jax.nn.one_hot(topi, E, dtype=xt.dtype) * topw[..., None], axis=1)
        h = jax.nn.relu(jnp.einsum('nd,edf->enf', xt, W1))
        y = jnp.einsum('enf,efd->end', h, W2)
        out = jnp.einsum('ne,end->nd', combine, y)
        return out.reshape(B, T, D)

    def _L1_attn_ref(x, norm_scale, w_in, conv_weight, conv_bias, A_log, dt_bias, w_out):
        import jax, jax.numpy as jnp
        import numpy as np
        N_EMBD = 128
        EXPAND = 2
        D_INNER = N_EMBD * EXPAND
        D_STATE = 64
        N_HEADS = D_INNER // D_STATE
        HEAD_DIM = D_INNER // N_HEADS
        N_GROUPS = 1
        D_CONV = 4
        N_LAYERS = 48
        BATCH, SEQ = (1, 64)
        PROJ_SIZE = 2 * D_INNER + N_HEADS + 2 * N_GROUPS * D_STATE
        EPS = 1e-06

        def _mamba_fwd(x, norm_scale, w_in, conv_weight, conv_bias, A_log, dt_bias, w_out):
            b, T, _ = x.shape
            residual = x
            xn = x * jax.lax.rsqrt(jnp.mean(x * x, axis=-1, keepdims=True) + EPS) * norm_scale
            proj = xn @ w_in
            gate = proj[..., :D_INNER]
            ssm_in = proj[..., D_INNER:2 * D_INNER]
            dt_raw = proj[..., 2 * D_INNER:2 * D_INNER + N_HEADS]
            gs = N_GROUPS * D_STATE
            B = proj[..., 2 * D_INNER + N_HEADS:2 * D_INNER + N_HEADS + gs].reshape(b, T, N_GROUPS, D_STATE)
            C = proj[..., 2 * D_INNER + N_HEADS + gs:].reshape(b, T, N_GROUPS, D_STATE)
            xp = jnp.pad(ssm_in, ((0, 0), (D_CONV - 1, 0), (0, 0)))
            conv = conv_bias + sum((conv_weight[k] * xp[:, k:k + T, :] for k in range(D_CONV)))
            h = jax.nn.silu(conv)
            dt = jax.nn.softplus(dt_raw + dt_bias)
            A = -jnp.exp(A_log)
            A_bar = jnp.exp(A[None, None, :] * dt)
            hpg = N_HEADS // N_GROUPS
            xh = h.reshape(b, T, N_HEADS, HEAD_DIM)
            Bh = jnp.repeat(B, hpg, axis=2)
            Ch = jnp.repeat(C, hpg, axis=2)
            Bu = Bh[:, :, :, None, :] * (dt[..., None, None] * xh[..., None])

            def _binary_op(left, right):
                a_l, b_l = left
                a_r, b_r = right
                return (a_l * a_r, a_r * b_l + b_r)
            _, states = jax.lax.associative_scan(_binary_op, (A_bar[..., None, None], Bu), axis=1)
            y = jnp.einsum('bthpn,bthn->bthp', states, Ch).reshape(b, T, D_INNER)
            y = y * jax.nn.silu(gate)
            y = y @ w_out
            return residual + y
        return _mamba_fwd(x, norm_scale, w_in, conv_weight, conv_bias, A_log, dt_bias, w_out)

    def _L1_ffn_ref(x, slot_query, d_Wq, d_Wk, d_Wv, d_Wo, d_bq, d_bk, d_bv, d_bo, c_Wq, c_Wk, c_Wv, c_Wo, c_bq, c_bk, c_bv, c_bo, e_ln_g, e_ln_b, e_W1, e_b1, e_Wg, e_bg, e_W2, e_b2):
        import jax, jax.numpy as jnp
        import numpy as np
        B, L, D = (4, 256, 128)
        H = 16
        E = 16
        NS = 16
        S = NS // E
        F = 512
        EPS = 1e-05

        def _layernorm(x, g, b):
            mu = jnp.mean(x, axis=-1, keepdims=True)
            var = jnp.mean(jnp.square(x - mu), axis=-1, keepdims=True)
            return (x - mu) * jax.lax.rsqrt(var + EPS) * g + b

        def _mha(q, k, v, Wq, bq, Wk, bk, Wv, bv, Wo, bo):
            Bq, Lq, Dm = q.shape
            dh = Dm // H
            qh = (q @ Wq + bq).reshape(Bq, Lq, H, dh)
            kh = (k @ Wk + bk).reshape(Bq, -1, H, dh)
            vh = (v @ Wv + bv).reshape(Bq, -1, H, dh)
            scores = jnp.einsum('bqhd,bkhd->bhqk', qh, kh) / jnp.asarray(np.sqrt(dh), q.dtype)
            attn = jax.nn.softmax(scores, axis=-1)
            out = jnp.einsum('bhqk,bkhd->bqhd', attn, vh).reshape(Bq, Lq, Dm)
            return out @ Wo + bo
        Bx = x.shape[0]
        q = jnp.broadcast_to(slot_query, (Bx, NS, D))
        o = q + _mha(q, x, x, d_Wq, d_bq, d_Wk, d_bk, d_Wv, d_bv, d_Wo, d_bo)
        os = o.reshape(Bx, E, S, D)
        h = _layernorm(os, e_ln_g[None, :, None, :], e_ln_b[None, :, None, :])
        u = jax.nn.silu(jnp.einsum('besd,edf->besf', h, e_W1) + e_b1[None, :, None, :])
        g = jax.nn.silu(jnp.einsum('besd,edf->besf', h, e_Wg) + e_bg[None, :, None, :])
        y = jnp.einsum('besf,efd->besd', u * g, e_W2) + e_b2[None, :, None, :]
        o = o + y.reshape(Bx, NS, D)
        out = _mha(x, o, o, c_Wq, c_bq, c_Wk, c_bk, c_Wv, c_bv, c_Wo, c_bo)
        return out

    def _L2_attn_ref(x, Mq, Mk, Mv):
        import jax, jax.numpy as jnp
        import numpy as np
        HEADS = 8
        K_SIZE = 64
        B, C, _ = x.shape
        H, K = (HEADS, K_SIZE)
        V = Mv.shape[1] // H
        q = (x @ Mq).reshape(B, H, C, K)
        k = (x @ Mk).reshape(B, H, C, K)
        v = (x @ Mv).reshape(B, H, C, V)
        scores = jnp.einsum('bhqk,bhck->bhqc', q, k).reshape(B * H, C, C)
        att = jax.nn.softmax(scores / jnp.sqrt(jnp.float32(K)), axis=1)
        att4 = att.reshape(B, C, H, C)
        out = jnp.einsum('bqhc,bhcd->bqhd', att4, v)
        return out.reshape(B, C, H * V)

    def _L2_ffn_ref(x, router_w, up_w, gate_w, down_w, shared_up_w, shared_gate_w, shared_down_w):
        import jax, jax.numpy as jnp
        import numpy as np
        ALPHA = 2.0
        TOP_K = 2
        logits = jnp.einsum('bsd,de->bse', x, router_w)
        probs = jax.nn.softmax(logits, axis=-1)
        topk_vals, topk_idx = jax.lax.top_k(probs, TOP_K)
        top1_val = topk_vals[..., 0]
        top1_idx = topk_idx[..., 0]
        hid = jnp.einsum('bsd,edh->ebsh', x, up_w) * jax.nn.silu(jnp.einsum('bsd,edh->ebsh', x, gate_w))
        Er = up_w.shape[0]
        mask = (top1_idx[None, :, :] == jnp.arange(Er)[:, None, None]).astype(x.dtype)
        routed = jnp.einsum('ebsh,ehd,ebs->bsd', hid, down_w, mask)
        shid = jnp.einsum('bsd,dh->bsh', x, shared_up_w) * jax.nn.silu(jnp.einsum('bsd,dh->bsh', x, shared_gate_w))
        shared = jnp.einsum('bsh,hd->bsd', shid, shared_down_w)
        return ALPHA * top1_val[..., None] * routed + shared

    def _L3_attn_ref(u, Lambda_re, Lambda_im, B, C, D, log_step):
        import jax, jax.numpy as jnp
        import numpy as np
        DT_MIN, DT_MAX = (0.001, 0.1)
        STEP_RESCALE = 1.0

        def _s5_forward(u, Lambda_re, Lambda_im, B, C, D, log_step):
            Lambda = jnp.minimum(Lambda_re, -0.0001) + 1j * Lambda_im
            B_tilde = (B[..., 0] + 1j * B[..., 1]).astype(jnp.complex64)
            C_tilde = (C[..., 0] + 1j * C[..., 1]).astype(jnp.complex64)
            step = STEP_RESCALE * jnp.exp(log_step[:, 0])
            Lambda_bar = jnp.exp(Lambda * step)
            B_bar = ((Lambda_bar - 1.0) / Lambda)[:, None] * B_tilde
            Bu = jnp.einsum('blh,ph->blp', u.astype(jnp.complex64), B_bar)
            A = jnp.broadcast_to(Lambda_bar, Bu.shape)

            def combine(e_i, e_j):
                a_i, b_i = e_i
                a_j, b_j = e_j
                return (a_j * a_i, a_j * b_i + b_j)
            _, xs = jax.lax.associative_scan(combine, (A, Bu), axis=1)
            ys = jnp.einsum('blp,hp->blh', xs, C_tilde).real + D * u
            return ys
        return _s5_forward(u, Lambda_re, Lambda_im, B, C, D, log_step)

    def _L3_ffn_ref(x, Wr, br, W_up, b_up, W_down, b_down):
        import jax, jax.numpy as jnp
        import numpy as np
        B, S, H = (4, 256, 128)
        E = 8
        GS = 2
        NG = E // GS
        F = int(H * 4 * (2.0 / 3.0))
        b, s, h = x.shape
        n_tok = b * s
        k = n_tok // E
        xf = x.reshape(n_tok, h)
        logits = xf @ Wr + br
        Sm = jax.nn.softmax(logits, axis=-1)
        G_t, idx_t = jax.lax.top_k(Sm.T, k)
        G = G_t.T
        idx = idx_t.T
        tokens = xf[idx]
        group = jnp.arange(E) // GS
        Wu = W_up[group]
        bu = b_up[group]
        mid = jax.nn.silu(jnp.einsum('keh,ehf->kef', tokens, Wu) + bu)
        out = jnp.einsum('kef,efh->keh', mid, W_down) + b_down
        y = jnp.zeros_like(xf).at[idx].add(G[..., None] * out)
        return y.reshape(b, s, h)
    x = L0_attn_x
    x = _layernorm(x + _L0_attn_ref(x, L0_attn_Wq, L0_attn_bq, L0_attn_Wk, L0_attn_bk, L0_attn_Wv, L0_attn_bv, L0_attn_Wo, L0_attn_bo), axis=-1)
    x = _layernorm(x + _L0_ffn_ref(x, L0_ffn_Wg, L0_ffn_W1, L0_ffn_W2), axis=-1)
    x = _layernorm(x + _L1_attn_ref(x, L1_attn_norm_scale, L1_attn_w_in, L1_attn_conv_weight, L1_attn_conv_bias, L1_attn_A_log, L1_attn_dt_bias, L1_attn_w_out), axis=-1)
    x = _layernorm(x + _L1_ffn_ref(x, L1_ffn_slot_query, L1_ffn_d_Wq, L1_ffn_d_Wk, L1_ffn_d_Wv, L1_ffn_d_Wo, L1_ffn_d_bq, L1_ffn_d_bk, L1_ffn_d_bv, L1_ffn_d_bo, L1_ffn_c_Wq, L1_ffn_c_Wk, L1_ffn_c_Wv, L1_ffn_c_Wo, L1_ffn_c_bq, L1_ffn_c_bk, L1_ffn_c_bv, L1_ffn_c_bo, L1_ffn_e_ln_g, L1_ffn_e_ln_b, L1_ffn_e_W1, L1_ffn_e_b1, L1_ffn_e_Wg, L1_ffn_e_bg, L1_ffn_e_W2, L1_ffn_e_b2), axis=-1)
    x = _layernorm(x + _L2_attn_ref(x, L2_attn_Mq, L2_attn_Mk, L2_attn_Mv), axis=-1)
    x = _layernorm(x + _L2_ffn_ref(x, L2_ffn_router_w, L2_ffn_up_w, L2_ffn_gate_w, L2_ffn_down_w, L2_ffn_shared_up_w, L2_ffn_shared_gate_w, L2_ffn_shared_down_w), axis=-1)
    x = _layernorm(x + _L3_attn_ref(x, L3_attn_Lambda_re, L3_attn_Lambda_im, L3_attn_B, L3_attn_C, L3_attn_D, L3_attn_log_step), axis=-1)
    x = _layernorm(x + _L3_ffn_ref(x, L3_ffn_Wr, L3_ffn_br, L3_ffn_W_up, L3_ffn_b_up, L3_ffn_W_down, L3_ffn_b_down), axis=-1)
    return x

_drawn_inputs = setup_inputs


def setup_inputs(seed=0):
    import zlib

    import numpy as np

    out = dict(_drawn_inputs(seed))
    spreads = {'L1_attn_norm_scale': (1.0, 0.6),
     'L1_attn_conv_bias': (0.0, 0.8),
     'L1_ffn_d_bq': (0.0, 0.8),
     'L1_ffn_d_bk': (0.0, 2.0),
     'L1_ffn_d_bv': (0.0, 0.8),
     'L1_ffn_d_bo': (0.0, 0.429),
     'L1_ffn_c_bq': (0.0, 0.8),
     'L1_ffn_c_bk': (0.0, 2.0),
     'L1_ffn_c_bv': (0.0, 0.454),
     'L1_ffn_c_bo': (0.0, 0.1),
     'L1_ffn_e_ln_g': (1.0, 0.6),
     'L1_ffn_e_ln_b': (0.0, 0.8),
     'L1_ffn_e_b1': (0.0, 0.8),
     'L1_ffn_e_bg': (0.0, 0.8),
     'L1_ffn_e_b2': (0.0, 0.8),
     'L3_ffn_br': (0.0, 0.1)}
    factors = {'L0_attn_Wq': 8.0,
     'L0_attn_bq': 8.0,
     'L0_attn_Wk': 8.0,
     'L0_attn_bk': 64.0,
     'L0_attn_Wv': 7.368,
     'L0_attn_bv': 3.494,
     'L0_attn_Wo': 3.968,
     'L1_attn_w_in': 8.0,
     'L1_attn_conv_weight': 8.0,
     'L1_attn_A_log': 8.0,
     'L1_attn_dt_bias': 8.0,
     'L1_attn_w_out': 8.0,
     'L1_ffn_slot_query': 8.0,
     'L1_ffn_d_Wq': 8.0,
     'L1_ffn_d_Wk': 8.0,
     'L1_ffn_d_Wv': 8.0,
     'L1_ffn_d_Wo': 8.0,
     'L1_ffn_c_Wq': 8.0,
     'L1_ffn_c_Wk': 8.0,
     'L1_ffn_c_Wv': 4.413,
     'L1_ffn_e_W1': 8.0,
     'L1_ffn_e_Wg': 8.0,
     'L1_ffn_e_W2': 8.0,
     'L2_attn_Mq': 8.0,
     'L2_attn_Mk': 8.0,
     'L2_attn_Mv': 2.788,
     'L3_ffn_b_up': 27.605,
     'L3_ffn_b_down': 8.0}
    for name, (base, spread) in spreads.items():
        noise = np.random.default_rng([zlib.crc32(name.encode()), seed]).standard_normal(out[name].shape)
        drawn = base * np.exp(spread * noise) if base else spread * noise
        out[name] = jnp.asarray(drawn.astype(out[name].dtype))
    for name, factor in factors.items():
        out[name] = (out[name] * factor).astype(out[name].dtype)
    return out
```

```python
import math
from contextlib import ExitStack

import numpy as np

import concourse.bass as bass
from concourse import mybir
from concourse.bass import ds

F32 = mybir.dt.float32
BF16 = mybir.dt.bfloat16
ACT = mybir.ActivationFunctionType
ALU = mybir.AluOpType
AX = mybir.AxisListType

P = 128
D = 128
B, S = 4, 1024
N = B * S
NT = N // P
GW = 512
NG = N // GW
TG = GW // P
RMS_EPS = 1e-6
EPS = 1e-5


class Core:

    def __init__(self, nc, stack, tag):
        self.nc, self.stack, self.tag = nc, stack, tag

    def sb(self, name, shape, dt=F32):
        return self.stack.enter_context(self.nc.sbuf_tensor(f"{self.tag}_{name}", shape, dt))

    def ps(self, name, shape, dt=F32):
        return self.stack.enter_context(self.nc.psum_tensor(f"{self.tag}_{name}", shape, dt))

    def sem(self, name):
        return self.nc.alloc_semaphore(name=f"{self.tag}_{name}")


class Chain:

    def __init__(self, engine, sem):
        self.engine, self.sem, self.count = engine, sem, 0

    def step(self, instruction):
        self.count += 1
        instruction.then_inc(self.sem, 1)
        self.engine.wait_ge(self.sem, self.count)


def constants(nc, keep):
    with ExitStack() as st:
        c = Core(nc, st, "const")
        zeroed, done = c.sem("zeroed"), c.sem("done")
        with nc.Block() as block:

            @block.gpsimd
            def _(pool):
                nc.gpsimd.memset(keep.ident[:], 0.0).then_inc(zeroed, 1)
                nc.gpsimd.memset(keep.ones[:], 1.0).then_inc(done, 1)
                nc.gpsimd.memset(keep.eps[:], EPS).then_inc(done, 1)
                nc.gpsimd.memset(keep.rms_eps[:], RMS_EPS).then_inc(done, 1)
                pool.wait_ge(zeroed, 1)
                nc.gpsimd.affine_select(out=keep.ident[:], in_=keep.ident[:], compare_op=ALU.not_equal, fill=1.0,
                                        base=0, pattern=[[-1, P]], channel_multiplier=1).then_inc(done, 1)
                pool.wait_ge(done, 3)
                nc.gpsimd.affine_select(out=keep.upto[:], in_=keep.ones[:, 0:P], compare_op=ALU.is_ge, fill=0.0,
                                        base=0, pattern=[[1, P]], channel_multiplier=-1).then_inc(done, 1)
                pool.wait_ge(done, 5)


def layernorm(nc, keep, tag, want_T=True, rms_T=None):
    x_tok, x_T = keep.x_tok, keep.x_T if rms_T is None else rms_T
    with ExitStack() as st:
        c = Core(nc, st, tag + "ln")
        stats = c.sb("stats", [P, NT * 6])
        mean, var = c.sb("mean", [P, NT]), c.sb("var", [P, NT])
        dm, std = c.sb("dm", [P, NT]), c.sb("std", [P, NT])
        rstd, shift = c.sb("rstd", [P, NT]), c.sb("shift", [P, NT])
        staged = c.sb("staged", [P, 2, GW])
        flipped = c.ps("flipped", [P, 2, GW])
        stats_done, chain_sem = c.sem("stats_done"), c.sem("chain")
        var_ready, std_ready, norm_ready = c.sem("var_ready"), c.sem("std_ready"), c.sem("norm_ready")
        tok_done = c.sem("tok_done")
        staged_ready, staged_free = c.sem("staged_ready"), c.sem("staged_free")
        flip_ready, flip_free = c.sem("flip_ready"), c.sem("flip_free")
        s3 = stats[:].rearrange("p (t k) -> p t k", k=6)

        with nc.Block() as block:

            @block.vector
            def _(dve):
                with dve.Fori(0, NT) as t:
                    nc.vector.bn_stats(stats[:, ds(t * 6, 6)], x_tok[:, ds(t * D, D)]).then_inc(stats_done, 1)
                dve.wait_ge(stats_done, NT)
                ch = Chain(dve, chain_sem)
                nc.vector.tensor_tensor(mean[:], s3[:, :, 1], s3[:, :, 4], ALU.add).then_inc(chain_sem, 1)
                ch.count += 1
                ch.step(nc.vector.tensor_tensor(dm[:], s3[:, :, 1], s3[:, :, 4], ALU.subtract))
                nc.vector.tensor_tensor(var[:], s3[:, :, 2], s3[:, :, 5], ALU.add).then_inc(chain_sem, 1)
                ch.count += 1
                ch.step(nc.vector.scalar_tensor_tensor(out=dm[:], in0=dm[:], scalar=0.25, in1=dm[:],
                                                       op0=ALU.mult, op1=ALU.mult))
                ch.step(nc.vector.scalar_tensor_tensor(out=var[:], in0=var[:], scalar=1.0 / D, in1=dm[:],
                                                       op0=ALU.mult, op1=ALU.add))
                if rms_T is None:
                    nc.vector.tensor_copy(dm[:], var[:]).then_inc(var_ready, 1)
                else:
                    ch.step(nc.vector.scalar_tensor_tensor(out=dm[:], in0=mean[:], scalar=0.25, in1=mean[:],
                                                           op0=ALU.mult, op1=ALU.mult))
                    nc.vector.tensor_tensor(dm[:], dm[:], var[:], ALU.add).then_inc(var_ready, 1)
                dve.wait_ge(std_ready, 1)
                ch.step(nc.vector.reciprocal(rstd[:], std[:]))
                nc.vector.scalar_tensor_tensor(out=shift[:], in0=mean[:], scalar=-0.5 if rms_T is None else 0.0, in1=rstd[:],
                                               op0=ALU.mult, op1=ALU.mult).then_inc(norm_ready, 1)
                dve.wait_ge(norm_ready, 1)
                with dve.Fori(0, NG // 2) as pair:
                    for k in range(2):
                        if rms_T is None:
                            dve.wait_ge(staged_free, pair * 2 + (k + 1))
                        if want_T:
                            dve.wait_ge(flip_ready, pair * 2 + (k + 1))
                        for j in range(TG):
                            t = (pair * 2 + k) * TG + j
                            ins = nc.vector.tensor_scalar(staged[:, k, j * D:(j + 1) * D], x_tok[:, ds(t * D, D)],
                                                          rstd[:, ds(t, 1)], shift[:, ds(t, 1)], ALU.mult, ALU.add)
                        ins.then_inc(staged_ready, 1)

            @block.scalar
            def _(act):
                act.wait_ge(var_ready, 1)
                nc.scalar.activation(std[:], dm[:], ACT.Sqrt, bias=(keep.eps if rms_T is None else keep.rms_eps)[:]).then_inc(std_ready, 1)
                with act.Fori(0, NG // 2) as pair:
                    for k in range(2):
                        act.wait_ge(staged_ready, pair * 2 + (k + 1))
                        if rms_T is None:
                            nc.scalar.copy(x_tok[:, ds((pair * 2 + k) * GW, GW)], staged[:, k]).then_inc(staged_free, 1)
                        if want_T:
                            act.wait_ge(flip_ready, pair * 2 + (k + 3))
                            nc.scalar.copy(x_T[:, ds((pair * 2 + k) * GW, GW)], flipped[:, k]).then_inc(flip_free, 1)

            @block.tensor
            def _(pe):
                if want_T:
                    pe.sem_inc(flip_free, 2)
                    pe.sem_inc(flip_ready, 2)
                    pe.sem_inc(staged_free, 2)
                    with pe.Fori(0, NG // 2) as pair:
                        for k in range(2):
                            pe.wait_ge(staged_ready, pair * 2 + (k + 1))
                            pe.wait_ge(flip_free, pair * 2 + (k + 1))
                            for j in range(TG):
                                ins = nc.tensor.transpose(flipped[:, k, j * D:(j + 1) * D],
                                                          staged[:, k, j * D:(j + 1) * D], keep.ident[:])
                            ins.then_inc(flip_ready, 1)
                else:
                    pe.sem_inc(staged_free, 2)


def router(nc, keep, tag, logits, w_dram, bias_dram, loads, rest=None):
    with ExitStack() as st:
        c = Core(nc, st, tag + "rt")
        w = c.sb("w", [P, 8])
        b = c.sb("b", [1, 8])
        staged = c.sb("staged", [P, 2, GW])
        acc = c.ps("acc", [P, 2, GW])
        loaded, staged_ready = c.sem("loaded"), c.sem("staged_ready")
        logit_ready, logit_done, w_loaded = c.sem("logit_ready"), c.sem("logit_done"), c.sem("w_loaded")
        chain_sem = c.sem("chain")
        with nc.Block() as block:

            @block.sync
            def _(sp):
                sp.dma_start(w[:], w_dram).then_inc(w_loaded, 16)
                if bias_dram is not None:
                    sp.dma_start(b[:], bias_dram).then_inc(w_loaded, 16)
                for dst, src in loads:
                    sp.dma_start(dst, src).then_inc(loaded, 16)
                sp.wait_ge(loaded, 16 * len(loads))

            @block.gpsimd
            def _(pool):
                with pool.Fori(0, NG // 2) as pair:
                    for k in range(2):
                        pool.wait_ge(logit_ready, pair * 2 + (k + 1))
                        nc.gpsimd.tensor_copy(staged[:, k], keep.x_T[:, ds((pair * 2 + k) * GW, GW)]).then_inc(staged_ready, 1)

            @block.tensor
            def _(pe):
                pe.sem_inc(logit_ready, 2)
                pe.sem_inc(logit_done, 2)
                pe.wait_ge(w_loaded, 16 if bias_dram is None else 32)
                with pe.Fori(0, NG // 2) as pair:
                    for k in range(2):
                        pe.wait_ge(staged_ready, pair * 2 + (k + 1))
                        pe.wait_ge(logit_done, pair * 2 + (k + 1))
                        for j in range(TG):
                            ins = nc.tensor.matmul(acc[:, k, j * 8:(j + 1) * 8], staged[:, k, j * P:(j + 1) * P], w[:],
                                                   start=True, stop=bias_dram is None)
                            if bias_dram is not None:
                                ins = nc.tensor.matmul(acc[:, k, j * 8:(j + 1) * 8], keep.ones[0:1, 0:P], b[:],
                                                       start=False, stop=True)
                        ins.then_inc(logit_ready, 1)

            @block.vector
            def _(dve):
                with dve.Fori(0, NG // 2) as pair:
                    for k in range(2):
                        dve.wait_ge(logit_ready, pair * 2 + (k + 3))
                        nc.vector.tensor_copy(logits[:, ds((pair * 2 + k) * TG * 8, TG * 8)],
                                              acc[:, k, 0:TG * 8]).then_inc(logit_done, 1)
                dve.wait_ge(logit_done, NG + 2)


def softmax8(nc, keep, tag, logits, probs):
    with ExitStack() as st:
        c = Core(nc, st, tag + "sm")
        top, total = c.sb("top", [P, NT]), c.sb("total", [P, NT])
        chain_sem, shifted, raised = c.sem("chain"), c.sem("shifted"), c.sem("raised")
        l3 = logits[:].rearrange("p (t e) -> p t e", e=8)
        p3 = probs[:].rearrange("p (t e) -> p t e", e=8)
        with nc.Block() as block:

            @block.vector
            def _(dve):
                ch = Chain(dve, chain_sem)
                ch.step(nc.vector.tensor_reduce(top[:], l3, AX.X, ALU.max))
                nc.vector.tensor_tensor(l3, l3, top[:].unsqueeze(2).to_broadcast([P, NT, 8]),
                                        ALU.subtract).then_inc(shifted, 1)
                dve.wait_ge(raised, 1)
                ch.step(nc.vector.tensor_reduce(total[:], p3, AX.X, ALU.add))
                ch.step(nc.vector.reciprocal(total[:], total[:]))
                ch.step(nc.vector.tensor_tensor(p3, p3, total[:].unsqueeze(2).to_broadcast([P, NT, 8]), ALU.mult))

            @block.scalar
            def _(act):
                act.wait_ge(shifted, 1)
                nc.scalar.activation(probs[:], logits[:], ACT.Exp).then_inc(raised, 1)


def pick_top(nc, keep, tag, probs, comb, k, scale_top=None):
    with ExitStack() as st:
        c = Core(nc, st, tag + "tk")
        rank = c.sb("rank", [P, NT * 8])
        left, hot, sc = c.sb("left", [P, NT * 8]), c.sb("hot", [P, NT * 8]), c.sb("sc", [P, NT * 8])
        top, best, total = c.sb("top", [P, NT]), c.sb("best", [P, NT]), c.sb("total", [P, NT])
        chain_sem, ranked = c.sem("chain"), c.sem("ranked")
        three = lambda a: a[:].rearrange("p (t e) -> p t e", e=8)
        wide = lambda a: a[:].unsqueeze(2).to_broadcast([P, NT, 8])
        with nc.Block() as block:

            @block.gpsimd
            def _(pool):
                nc.gpsimd.iota(three(rank), pattern=[[0, NT], [-1, 8]], base=8, channel_multiplier=0,
                               allow_small_or_imprecise_dtypes=True).then_inc(ranked, 1)

            @block.vector
            def _(dve):
                ch = Chain(dve, chain_sem)
                dve.wait_ge(ranked, 1)
                ch.step(nc.vector.tensor_copy(left[:], probs[:]))
                for n in range(k):
                    ch.step(nc.vector.tensor_reduce(top[:], three(left), AX.X, ALU.max))
                    ch.step(nc.vector.tensor_tensor(three(hot), three(left), wide(top), ALU.is_equal))
                    ch.step(nc.vector.tensor_tensor(hot[:], hot[:], rank[:], ALU.mult))
                    ch.step(nc.vector.tensor_reduce(best[:], three(hot), AX.X, ALU.max))
                    ch.step(nc.vector.tensor_tensor(three(hot), three(hot), wide(best), ALU.is_equal))
                    ch.step(nc.vector.scalar_tensor_tensor(out=left[:], in0=hot[:], scalar=-2.0, in1=left[:],
                                                           op0=ALU.mult, op1=ALU.add))
                    if k == 1:
                        ch.step(nc.vector.tensor_scalar(top[:], top[:], scale_top, None, ALU.mult))
                        ch.step(nc.vector.tensor_tensor(three(comb), three(hot), wide(top), ALU.mult))
                        ch.step(nc.vector.memset(three(comb)[:, :, 7:8], 1.0))
                    elif n == 0:
                        ch.step(nc.vector.tensor_tensor(three(comb), three(hot), wide(top), ALU.mult))
                        ch.step(nc.vector.tensor_copy(total[:], top[:]))
                    else:
                        ch.step(nc.vector.tensor_tensor(total[:], total[:], top[:], ALU.add))
                        ch.step(nc.vector.reciprocal(total[:], total[:]))
                        ch.step(nc.vector.tensor_tensor(three(sc), three(hot), wide(top), ALU.mult))
                        ch.step(nc.vector.tensor_tensor(comb[:], comb[:], sc[:], ALU.add))
                        ch.step(nc.vector.tensor_tensor(three(comb), three(comb), wide(total), ALU.mult))


def experts(nc, keep, tag, comb, units, rows, up, down, per_unit, func, gate=None, bias=None):
    nf = len(rows)
    upb = 2 if gate else 4
    ob = per_unit
    steps = units * nf
    with ExitStack() as st:
        c = Core(nc, st, tag + "ex")
        hid = c.sb("hid", [P, 2, nf, GW])
        silu = c.sb("silu", [P, 2, GW]) if gate else None
        raw = c.ps("raw", [P, 4, GW])
        res = c.ps("res", [P, 2, ob, GW])
        raw_ready = c.sem("raw_ready")
        silu_ready = c.sem("silu_ready")
        hid_ready = c.sem("hid_ready")
        res_ready = c.sem("res_ready")
        comb_done = c.sem("comb_done")
        ones_set, started = c.sem("ones_set"), c.sem("started")
        tiles_per_bank = GW // (per_unit * D)

        def result(k, j):
            b, o = divmod(j, tiles_per_bank)
            return res[:, k, b, o * per_unit * D:(o + 1) * per_unit * D]

        with nc.Block() as block:

            @block.tensor
            def _(pe):
                pe.sem_inc(hid_ready, upb)
                pe.sem_inc(res_ready, 2)
                pe.sem_inc(comb_done, 2)
                pe.wait_ge(ones_set, 1)

                def rise(g, u):
                    for f in range(nf):
                        i = u * nf + f
                        place = (i % upb) * (4 // upb)
                        x = keep.x_T[:, ds(g * GW, GW)]
                        pe.wait_ge(hid_ready, g * steps + (i + 1))
                        ins = nc.tensor.matmul(raw[0:rows[f], place], up(u, f), x, start=True, stop=True)
                        if gate:
                            ins = nc.tensor.matmul(raw[0:rows[f], place + 1], gate(u, f), x, start=True, stop=True)
                        ins.then_inc(raw_ready, 1)

                def fall(g, u):
                    pe.wait_ge(hid_ready, g * steps + (upb + (u + 1) * nf))
                    pe.wait_ge(comb_done, g * units + (u + 1))
                    for j in range(TG):
                        for f in range(nf):
                            w = down(u, f)
                            ins = nc.tensor.matmul(result(u % 2, j), hid[0:w.shape[0], u % 2, f, j * P:(j + 1) * P], w,
                                                   start=(f == 0), stop=(f == nf - 1))
                    ins.then_inc(res_ready, 1)

                with pe.Fori(0, NG) as g:
                    for u in range(units):
                        rise(g, u)
                        if u:
                            fall(g, u - 1)
                    fall(g, units - 1)

            @block.scalar
            def _(act):
                with act.Fori(0, NG) as g:
                    for u in range(units):
                        for f in range(nf):
                            i = u * nf + f
                            place = (i % upb) * (4 // upb)
                            act.wait_ge(raw_ready, g * steps + (i + 1))
                            if gate:
                                act.wait_ge(hid_ready, g * steps + (i + 1))
                                nc.scalar.activation(silu[0:rows[f], i % 2], raw[0:rows[f], place + 1],
                                                     func).then_inc(silu_ready, 1)
                            else:
                                if f == 0:
                                    act.wait_ge(res_ready, g * units + (u + 1))
                                kw = {"bias": bias(u, f)} if bias else {}
                                nc.scalar.activation(hid[0:rows[f], u % 2, f], raw[0:rows[f], place], func,
                                                     **kw).then_inc(hid_ready, 1)

            @block.vector
            def _(dve):
                nc.vector.memset(hid[:], 1.0).then_inc(ones_set, 1)

                def merge(g, u):
                    dve.wait_ge(res_ready, g * units + (u + 3))
                    for e in range(per_unit):
                        dve.wait_ge(merged, (g * units + u) * per_unit + (e + 1))
                        for j in range(TG):
                            t = g * TG + j
                            ins = nc.vector.scalar_tensor_tensor(
                                out=keep.x_tok[:, ds(t * D, D)], in0=result(u % 2, j)[:, e * D:(e + 1) * D],
                                scalar=comb[:, ds(t * 8 + (u * per_unit + e), 1)],
                                in1=keep.x_tok[:, ds(t * D, D)], op0=ALU.mult, op1=ALU.add)
                        ins.then_inc(merged, 1)
                    dve.wait_ge(merged, (g * units + u) * per_unit + (per_unit + 1))
                    dve.sem_inc(comb_done, 1)

                merged = started
                dve.sem_inc(merged, 1)
                with dve.Fori(0, NG) as g:
                    for u in range(units):
                        if gate:
                            for f in range(nf):
                                i = u * nf + f
                                dve.wait_ge(silu_ready, g * steps + (i + 1))
                                if f == 0:
                                    dve.wait_ge(res_ready, g * units + (u + 1))
                                nc.vector.tensor_tensor(hid[0:rows[f], u % 2, f], raw[0:rows[f], (i % 2) * 2],
                                                        silu[0:rows[f], i % 2], ALU.mult).then_inc(hid_ready, 1)
                        if u:
                            merge(g, u - 1)
                    merge(g, units - 1)


def flip_tokens(nc, keep, tag, src_tok, dst_T):
    with ExitStack() as st:
        c = Core(nc, st, tag + "fl")
        staged = c.sb("staged", [P, 2, GW])
        flipped = c.ps("flipped", [P, 2, GW])
        staged_ready, flip_ready, flip_done = c.sem("staged_ready"), c.sem("flip_ready"), c.sem("flip_done")
        with nc.Block() as block:

            @block.gpsimd
            def _(pool):
                with pool.Fori(0, NG // 2) as pair:
                    for k in range(2):
                        pool.wait_ge(flip_ready, pair * 2 + (k + 1))
                        nc.gpsimd.tensor_copy(staged[:, k], src_tok[:, ds((pair * 2 + k) * GW, GW)]).then_inc(staged_ready, 1)

            @block.tensor
            def _(pe):
                pe.sem_inc(flip_ready, 2)
                pe.sem_inc(flip_done, 2)
                with pe.Fori(0, NG // 2) as pair:
                    for k in range(2):
                        pe.wait_ge(staged_ready, pair * 2 + (k + 1))
                        pe.wait_ge(flip_done, pair * 2 + (k + 1))
                        for j in range(TG):
                            ins = nc.tensor.transpose(flipped[:, k, j * P:(j + 1) * P], staged[:, k, j * P:(j + 1) * P], keep.ident[:])
                        ins.then_inc(flip_ready, 1)

            @block.scalar
            def _(act):
                with act.Fori(0, NG // 2) as pair:
                    for k in range(2):
                        act.wait_ge(flip_ready, pair * 2 + (k + 3))
                        nc.scalar.copy(dst_T[:, ds((pair * 2 + k) * GW, GW)], flipped[:, k]).then_inc(flip_done, 1)


def layer0_attn(nc, keep, a):
    H, HD = 16, 8
    HEADS = B * H
    QT = S // P
    PARTS = [(0, 0), (0, 1), (0, 2), (1, 0), (1, 1), (1, 2), (2, 0), (2, 1)]
    ROWS = len(PARTS) * HD
    M1, M2 = 64, 96
    FULL = M2 + QT
    RING = 4
    V1 = 32
    QB = S // 4
    scratch = [nc.dram_tensor(f"l0_{n}_parts", (3, B * P, S), BF16, kind="Internal").ap() for n in ("query", "key")]
    with ExitStack() as st:
        c = Core(nc, st, "l0a")
        v_tok, at_tok = c.sb("v_tok", [P, N]), c.sb("at_tok", [P, N])

        with ExitStack() as st2:
            c2 = Core(nc, st2, "l0r")
            cos, sin = c2.sb("cos", [P, QT, D // 2]), c2.sb("sin", [P, QT, D // 2])
            prod = c2.sb("prod", [P, 2, N // 2])
            loaded, halves, joined = c2.sem("loaded"), c2.sem("halves"), c2.sem("joined")
            with nc.Block() as block:

                @block.sync
                def _(sp):
                    sp.dma_start(cos[:].rearrange("p t d -> p (t d)"), a["rope_cos"]).then_inc(loaded, 16)
                    sp.dma_start(sin[:].rearrange("p t d -> p (t d)"), a["rope_sin"]).then_inc(loaded, 16)

                x4 = keep.x_tok[:].rearrange("p (b t d) -> p b t d", b=B, d=D)
                r4 = at_tok[:].rearrange("p (b t d) -> p b t d", b=B, d=D)
                h = D // 2
                wide = lambda m: m[:].unsqueeze(1).to_broadcast([P, B, QT, h])
                p4 = lambda n: prod[:, n].rearrange("p (b t d) -> p b t d", b=B, d=h)

                @block.vector
                def _(dve):
                    dve.wait_ge(loaded, 32)
                    for n, (m1, m2, op, o) in enumerate(((cos, sin, ALU.subtract, 0), (sin, cos, ALU.add, h))):
                        nc.vector.tensor_tensor(r4[:, :, :, o:o + h], x4[:, :, :, 0:h], wide(m1), ALU.mult)
                        nc.vector.tensor_tensor(p4(n), x4[:, :, :, h:D], wide(m2), ALU.mult).then_inc(halves, 1)
                        dve.wait_ge(halves, n + 1)
                        nc.vector.tensor_tensor(r4[:, :, :, o:o + h], r4[:, :, :, o:o + h], p4(n), op).then_inc(joined, 1)
                    dve.wait_ge(joined, 2)

        rT = keep.x_T
        flip_tokens(nc, keep, "l0a", at_tok, rT)
        project_tokens(nc, keep, "l0v", rT, a["L0_attn_WvT"], v_tok, bias_dram=a["L0_attn_bv"])

        with ExitStack() as st2:
            c2 = Core(nc, st2, "l0p")
            w = c2.sb("w", [P, 2, P])
            bias = c2.sb("bias", [P, 2])
            full = c2.sb("full", [P, 2, GW])
            rest, rest2 = c2.sb("rest", [P, 2, GW]), c2.sb("rest2", [P, 2, GW])
            parts = c2.sb("parts", [P, 2, 3, GW], BF16)
            acc = c2.ps("acc", [P, 2, GW])
            loaded, acc_ready, full_done = c2.sem("loaded"), c2.sem("acc_ready"), c2.sem("full_done")
            cut, stored, chained = c2.sem("cut"), [c2.sem("stored0"), c2.sem("stored1")], c2.sem("chained")
            with nc.Block() as block:

                @block.sync
                def _(sp):
                    for m, n in enumerate(("q", "k")):
                        sp.dma_start(w[:, m], a[f"L0_attn_W{n}T"]).then_inc(loaded, 16)
                    sp.dma_start(bias[:], a["L0_attn_bqk_cols"]).then_inc(loaded, 16)
                    with sp.Fori(0, B) as b:
                        for half in range(2):
                            for m in range(2):
                                sp.wait_ge(cut, (b * 2 + half) * 6 + (3 * m + 3))
                                sp.dma_start(scratch[m][:, ds(b * P, P), half * GW:(half + 1) * GW].rearrange("i p s -> p i s"),
                                             parts[:, m]).then_inc(stored[m], 16)
                    for m in range(2):
                        sp.wait_ge(stored[m], 16 * NG + 16)

                @block.tensor
                def _(pe):
                    pe.sem_inc(full_done, 2)
                    pe.wait_ge(loaded, 48)
                    with pe.Fori(0, NG) as g:
                        for m in range(2):
                            pe.wait_ge(full_done, g * 2 + (m + 1))
                            nc.tensor.matmul(acc[:, m], w[:, m], rT[:, ds(g * GW, GW)], start=True, stop=True).then_inc(acc_ready, 1)

                @block.scalar
                def _(act):
                    with act.Fori(0, NG) as g:
                        for m in range(2):
                            act.wait_ge(acc_ready, g * 2 + (m + 1))
                            act.wait_ge(chained, g * 4 + (2 * m + 1))
                            nc.scalar.activation(full[:, m], acc[:, m], ACT.Identity, bias=bias[:, m:m + 1]).then_inc(full_done, 1)

                @block.vector
                def _(dve):
                    dve.sem_inc(chained, 4)
                    for m in range(2):
                        dve.sem_inc(stored[m], 16)
                    with dve.Fori(0, NG) as g:
                        for m in range(2):
                            dve.wait_ge(full_done, g * 2 + (m + 3))
                            dve.wait_ge(stored[m], g * 16 + 16)
                            nc.vector.tensor_copy(parts[:, m, 0], full[:, m]).then_inc(cut, 1)
                            dve.wait_ge(cut, g * 6 + (3 * m + 1))
                            nc.vector.tensor_tensor(rest[:, m], full[:, m], parts[:, m, 0], ALU.subtract).then_inc(chained, 1)
                            dve.wait_ge(chained, g * 4 + (2 * m + 5))
                            nc.vector.tensor_copy(parts[:, m, 1], rest[:, m]).then_inc(cut, 1)
                            dve.wait_ge(cut, g * 6 + (3 * m + 2))
                            nc.vector.tensor_tensor(rest2[:, m], rest[:, m], parts[:, m, 1], ALU.subtract).then_inc(chained, 1)
                            dve.wait_ge(chained, g * 4 + (2 * m + 6))
                            nc.vector.tensor_copy(parts[:, m, 2], rest2[:, m]).then_inc(cut, 1)

        with ExitStack() as st2:
            c2 = Core(nc, st2, "l0h")
            qs, ks = c2.sb("qs", [P, RING, S], BF16), c2.sb("ks", [P, RING, S], BF16)
            negmax = c2.sb("negmax", [P, 2, QT])
            first_part = c2.sb("first_part", [P, P], BF16)
            mcut = c2.sb("mcut", [P, P], BF16)
            diag = c2.sb("diag", [P, QT, P], BF16)
            vs = c2.sb("vs", [P, 2, QT, V1])
            TR = 4
            pT = c2.sb("pT", [P, TR, S])
            outT = c2.sb("outT", [P, QB])
            share = c2.sb("share", [P, QT])
            s1 = c2.ps("s1", [P, 2, S])
            s2 = c2.ps("s2", [P, 2, GW])
            mix = c2.ps("mix", [P, 2, GW])
            loaded = [c2.sem(f"loaded{r}") for r in range(RING)]
            s1_ready, max_done = c2.sem("s1_ready"), c2.sem("max_done")
            s2_ready, exp_done = c2.sem("s2_ready"), c2.sem("exp_done")
            pv_done, v_ready = c2.sem("pv_done"), c2.sem("v_ready")
            out_copied, flip_ready = c2.sem("out_copied"), c2.sem("flip_ready")
            m_cut, m_spread, prepared, hi_done = c2.sem("m_cut"), c2.sem("m_spread"), c2.sem("prepared"), c2.sem("hi_done")
            shared = c2.sem("shared")
            INV = 1.0 / math.sqrt(HD)
            v3 = v_tok[:].rearrange("p (t d) -> p t d", d=D)
            at3 = at_tok[:].rearrange("p (t d) -> p t d", d=D)
            LOADS = 6

            def over_heads(engine, head):
                for r in range(RING):
                    head(0, r, r == 0)
                with engine.Fori(1, HEADS // RING) as g:
                    for r in range(RING):
                        head(g, r, False)

            with nc.Block() as block:

                @block.sync
                def _(sp):
                    def load(n, r):
                        rows = ds(n % HEADS * HD, HD)
                        for i, j0, js in ((0, 0, 3), (1, 0, 3), (2, 0, 2)):
                            at = PARTS.index((i, j0)) * HD
                            sp.dma_start(ks[at:at + js * HD, r], scratch[1][0:js, rows]).then_inc(loaded[r], 16)
                            sp.dma_start(qs[at:at + js * HD, r],
                                         scratch[0][i:i + 1, rows].to_broadcast([js, HD, S])).then_inc(loaded[r], 16)

                    sp.wait_ge(prepared, 2)
                    for r in range(RING - 1):
                        load(r, r)

                    def head(g, r, first):
                        n = g * RING + r
                        if not first:
                            sp.wait_ge(s2_ready, n * (2 * QT))
                        load(n + (RING - 1), (r + RING - 1) % RING)

                    over_heads(sp, head)
                    for r in range(RING):
                        sp.wait_ge(loaded[r], 16 * LOADS * (HEADS // RING + (r < RING - 1)))

                @block.gpsimd
                def _(pool):
                    ch = Chain(pool, prepared)
                    ch.step(nc.gpsimd.memset(ks[ROWS:P], 1.0))
                    ch.step(nc.gpsimd.memset(qs[ROWS:P], 0.0))
                    ch.step(nc.gpsimd.memset(mcut[:], 0.0))
                    ch.step(nc.gpsimd.memset(vs[:], 0.0))
                    ch.step(nc.gpsimd.memset(vs[:, :, :, HD:HD + 1], 1.0))
                    ch.step(nc.gpsimd.memset(diag[:], 0.0))
                    for o in (M1, M2):
                        ch.step(nc.gpsimd.memset(diag[o:o + QT], 1.0))
                    for o in (M1, M2):
                        d = diag[o:o + QT]
                        ch.step(nc.gpsimd.affine_select(out=d, in_=d, compare_op=ALU.is_equal, fill=0.0, base=0,
                                                        pattern=[[-1, QT], [0, P]], channel_multiplier=1))

                    def values(n, q):
                        nc.gpsimd.tensor_copy(vs[:, q, :, 0:HD], v3[:, ds(n // H * QT, QT), ds(n % H * HD, HD)]).then_inc(v_ready, 1)

                    def spread(n, r):
                        pool.wait_ge(m_cut, (n + 1))
                        nc.gpsimd.tensor_tensor(qs[M1:FULL, r].rearrange("p (t q) -> p t q", q=P), diag[M1:FULL],
                                                mcut[M1:FULL].unsqueeze(1).to_broadcast([FULL - M1, QT, P]), ALU.mult).then_inc(m_spread, 1)
                        pool.wait_ge(m_spread, n + 1)

                    values(0, 0)
                    pool.wait_ge(v_ready, 1)
                    spread(0, 0)

                    def head(g, r, first):
                        n = g * RING + r
                        spread(n + 1, (r + 1) % RING)
                        pool.wait_ge(pv_done, n * QT + TR)
                        values((n + 1) % HEADS, (r + 1) % 2)
                        pool.wait_ge(v_ready, n + 2)

                    over_heads(pool, head)

                @block.tensor
                def _(pe):
                    pe.sem_inc(max_done, 2)
                    pe.sem_inc(exp_done, 2)
                    pe.sem_inc(pv_done, TR)

                    def first_product(n, r, t):
                        pe.wait_ge(max_done, n * QT + (t + 1))
                        for o in range(S // GW):
                            ins = nc.tensor.matmul(s1[:, t % 2, o * GW:(o + 1) * GW], qs[0:ROWS, r, t * P:(t + 1) * P],
                                                   ks[0:ROWS, r, o * GW:(o + 1) * GW], start=True, stop=True)
                        ins.then_inc(s1_ready, 1)

                    def second_product(n, r, t):
                        for o in range(S // GW):
                            pe.wait_ge(exp_done, (n * QT + t) * 2 + (o + 1))
                            nc.tensor.matmul(s2[:, o], ks[0:FULL, r, t * P:(t + 1) * P], qs[0:FULL, r, o * GW:(o + 1) * GW],
                                             start=True, stop=True).then_inc(s2_ready, 1)

                    def attend(n, q, t):
                        pe.wait_ge(exp_done, (n * QT + t) * 2 + 4)
                        if t == 0:
                            pe.wait_ge(v_ready, n + 1)
                            pe.wait_ge(m_cut, n + 1)
                        for k in range(4):
                            ins = nc.tensor.matmul(mix[k * V1:(k + 1) * V1, q, 0:QB], vs[:, q, t], pT[:, t % TR, k * QB:(k + 1) * QB],
                                                   start=(t == 0), stop=(t == QT - 1))
                        ins.then_inc(pv_done, 1)

                    def turn(n, q, result):
                        if result:
                            pe.wait_ge(out_copied, n)
                            for f in range(2):
                                nc.tensor.transpose(mix[:, q, (2 + f) * P:(3 + f) * P], outT[:, f * P:(f + 1) * P], keep.ident[:])
                        pe.wait_ge(max_done, (n + 2) * QT + 2)
                        nc.tensor.transpose(mix[0:QT, q, 0:P], negmax[:, q], keep.ident[:]).then_inc(flip_ready, 1)

                    for r in range(2):
                        pe.wait_ge(loaded[r], 16 * LOADS)
                        for t in range(QT):
                            first_product(r, r, t)
                        if r == 0:
                            turn(-1, 0, False)

                    def head(g, r, first):
                        n, q, r2 = g * RING + r, r % 2, (r + 2) % RING
                        pe.wait_ge(m_spread, n + 1)
                        pe.wait_ge(loaded[r2], (g + (1 if r < 2 else 2)) * (16 * LOADS))
                        for t in range(QT):
                            second_product(n, r, t)
                            first_product(n + 2, r2, t)
                            if t >= 2:
                                attend(n, q, t - 2)
                            elif not first:
                                attend(n - 1, 1 - q, QT - 2 + t)
                            if t == 2:
                                turn(n, 1 - q, not first)

                    over_heads(pe, head)
                    for t in range(QT - 2, QT):
                        attend(HEADS - 1, 1, t)
                    pe.wait_ge(out_copied, HEADS)
                    for f in range(2):
                        ins = nc.tensor.transpose(mix[:, 1, (2 + f) * P:(3 + f) * P], outT[:, f * P:(f + 1) * P], keep.ident[:])
                    ins.then_inc(flip_ready, 1)

                @block.scalar
                def _(act):
                    def copy_out(n, q):
                        act.wait_ge(pv_done, n * QT + (QT + TR))
                        nc.scalar.copy(outT[:], mix[:, q, 0:QB]).then_inc(out_copied, 1)

                    def head(g, r, first):
                        n = g * RING + r
                        for t in range(QT):
                            act.wait_ge(pv_done, n * QT + (t + 1))
                            for o in range(S // GW):
                                act.wait_ge(s2_ready, (n * QT + t) * 2 + (o + 1))
                                nc.scalar.activation(pT[:, t % TR, o * GW:(o + 1) * GW], s2[:, o], ACT.Exp, scale=INV).then_inc(exp_done, 1)
                            if t == 1 and not first:
                                copy_out(n - 1, (r + 1) % 2)

                    over_heads(act, head)
                    copy_out(HEADS - 1, 1)

                @block.vector
                def _(dve):
                    def maxima(n, q, t):
                        dve.wait_ge(s1_ready, n * QT + (t + 1))
                        nc.vector.tensor_reduce(negmax[:, q, t:t + 1], s1[:, t % 2], AX.X, ALU.max, negate=True).then_inc(max_done, 1)

                    def cut_maxima(n, q, count):
                        dve.wait_ge(flip_ready, count)
                        dve.wait_ge(m_spread, n)
                        src = mix[0:QT, q, 0:P]
                        nc.vector.tensor_copy(first_part[M2:M2 + QT], src).then_inc(hi_done, 1)
                        nc.vector.tensor_copy(mcut[M1:M1 + QT], src)
                        dve.wait_ge(hi_done, count)
                        nc.vector.tensor_tensor(mcut[M2:M2 + QT], src, first_part[M2:M2 + QT], ALU.subtract).then_inc(m_cut, 1)

                    def settle(n, q, count):
                        dve.wait_ge(flip_ready, count)
                        flat = mix[:, q, 2 * P:4 * P].rearrange("p (f k v) -> p f k v", f=2, v=V1)
                        nc.vector.reciprocal(share[:].rearrange("p (f k) -> p f k", f=2), flat[:, :, :, HD]).then_inc(shared, 1)
                        dve.wait_ge(shared, (n + 1))
                        dst = at3[:, ds(n // H * QT, QT), ds(n % H * HD, HD)].rearrange("p (k f) d -> p f k d", f=2)
                        nc.vector.tensor_tensor(dst, flat[:, :, :, 0:HD],
                                                share[:].rearrange("p (f k) -> p f k", f=2).unsqueeze(3).to_broadcast([P, 2, 4, HD]),
                                                ALU.mult)

                    for r in range(2):
                        for t in range(QT):
                            maxima(r, r, t)
                        if r == 0:
                            dve.wait_ge(prepared, 3)
                            cut_maxima(0, 0, 1)

                    def head(g, r, first):
                        n, q = g * RING + r, r % 2
                        for t in range(QT):
                            maxima(n + 2, q, t)
                            if t == 2:
                                cut_maxima(n + 1, 1 - q, n + 2)
                                if not first:
                                    settle(n - 1, 1 - q, n + 2)

                    over_heads(dve, head)
                    settle(HEADS - 1, 1, HEADS + 2)

        flip_tokens(nc, keep, "l0o", at_tok, rT)
        project_tokens(nc, keep, "l0o", rT, a["L0_attn_WoT"], keep.x_tok, bias_dram=a["L0_attn_bo"], add=True)


def layer0_ffn(nc, keep, a):
    E, F = 8, 256
    with ExitStack() as st:
        c = Core(nc, st, "l0f")
        w1, w2 = c.sb("w1", [P, E, F]), c.sb("w2", [P, E, 2, D])
        logits, probs, comb = c.sb("logits", [P, NT * 8]), c.sb("probs", [P, NT * 8]), c.sb("comb", [P, NT * 8])
        router(nc, keep, "l0f", logits, a["L0_ffn_Wg"], None,
               [(w1[:], a["L0_ffn_W1"].rearrange("e d f -> d e f")),
                (w2[:], a["L0_ffn_W2"].rearrange("e (k p) d -> p e k d", p=P))])
        softmax8(nc, keep, "l0f", logits, probs)
        pick_top(nc, keep, "l0f", probs, comb, 2)
        experts(nc, keep, "l0f", comb, E, [P, P], lambda u, f: w1[:, u, f * P:(f + 1) * P],
                lambda u, f: w2[:, u, f], 1, ACT.Relu)


def layer1_attn(nc, keep, a):
    DI, H, HD, DS, K = 256, 4, 64, 64, 4
    NC_ = S // P
    F2 = DI // P
    O_SSM, O_DT, O_B, O_C = DI, 2 * DI, 2 * DI + H, 2 * DI + H + DS
    PW = O_C + DS
    TM = H + DS
    PAD = K - 1
    with ExitStack() as st:
        c = Core(nc, st, "l1a")
        w_in, w_out = c.sb("w_in", [P, PW]), c.sb("w_out", [P, F2, D])
        scale = c.sb("scale", [P, 1])
        conv_w, conv_b = c.sb("conv_w", [P, F2, K]), c.sb("conv_b", [P, F2])
        a_log, dt_bias = c.sb("a_log", [P, H]), c.sb("dt_bias", [P, H])
        gate = c.sb("gate", [P, F2, N])
        tok = c.sb("tok", [P, NT, TM])
        bT, cT = c.sb("bT", [DS, N]), c.sb("cT", [DS, N])
        dt, adt = c.sb("dt", [P, NT, H]), c.sb("adt", [P, NT, H])
        hT = c.sb("hT", [P, F2, N])

        with ExitStack() as st2:
            c2 = Core(nc, st2, "l1p")
            ssm = c2.sb("ssm", [P, F2, B * (S + PAD)])
            s_b = S + PAD
            with ExitStack() as st3:
                c3 = Core(nc, st3, "l1q")
                xn = c3.sb("xn", [P, N])
                layernorm(nc, keep, "l1a", rms_T=xn)
                staged = c3.sb("staged", [P, 2, GW])
                acc = c3.ps("acc", [P, 5, GW])
                acc_t = c3.ps("acc_t", [P, 2, GW])
                loaded, scaled, staged_ready = c3.sem("loaded"), c3.sem("scaled"), c3.sem("staged_ready")
                acc_ready, acc_done = c3.sem("acc_ready"), c3.sem("acc_done")
                tok_ready, tok_done, padded = c3.sem("tok_ready"), c3.sem("tok_done"), c3.sem("padded")
                JOBS = [("gate", 0), ("gate", 1), ("ssm", 0), ("ssm", 1), ("bc", 0)]
                J = len(JOBS)
                with nc.Block() as block:

                    @block.sync
                    def _(sp):
                        for dst, src in [(w_in[:], a["L1_attn_w_in"]), (scale[:], a["L1_attn_norm_scale_col"]),
                                         (w_out[:], a["L1_attn_w_out"].rearrange("(k p) d -> p k d", p=P)),
                                         (conv_w[:].rearrange("p f k -> p (f k)"), a["L1_attn_conv_w_cols"]),
                                         (conv_b[:], a["L1_attn_conv_b_cols"]),
                                         (a_log[:], a["L1_attn_A_log"].rearrange("(o h) -> o h", o=1).broadcast_to([P, H])),
                                         (dt_bias[:], a["L1_attn_dt_bias"].rearrange("(o h) -> o h", o=1).broadcast_to([P, H]))]:
                            sp.dma_start(dst, src).then_inc(loaded, 16)
                        sp.wait_ge(loaded, 16 * 7)

                    @block.gpsimd
                    def _(pool):
                        nc.gpsimd.memset(ssm[:, :, :].rearrange("p f (b s) -> p (f b) s", b=B)[:, :, 0:PAD], 0.0).then_inc(padded, 1)
                        with pool.Fori(0, B) as b:
                            for k in range(2):
                                pool.wait_ge(tok_ready, b * 2 + (k + 1))
                                nc.gpsimd.tensor_copy(staged[:, k], xn[:, ds((b * 2 + k) * GW, GW)]).then_inc(staged_ready, 1)
                        pool.wait_ge(padded, 1)

                    @block.tensor
                    def _(pe):
                        pe.sem_inc(acc_done, 5)
                        pe.sem_inc(tok_ready, 2)
                        pe.sem_inc(tok_done, 2)
                        pe.wait_ge(scaled, 1)
                        cols = {"gate": 0, "ssm": O_SSM, "bc": O_B}
                        with pe.Fori(0, B) as b:
                            for k in range(2):
                                for i, (kind, f) in enumerate(JOBS):
                                    n = k * J + i
                                    pe.wait_ge(acc_done, b * (2 * J) + (n + 1))
                                    o = cols[kind] + f * P
                                    nc.tensor.matmul(acc[:, n % 5], w_in[:, o:o + P],
                                                     xn[:, ds((b * 2 + k) * GW, GW)], start=True, stop=True).then_inc(acc_ready, 1)
                                pe.wait_ge(staged_ready, b * 2 + (k + 1))
                                pe.wait_ge(tok_done, b * 2 + (k + 1))
                                for j in range(TG):
                                    ins = nc.tensor.matmul(acc_t[:, k, j * TM:(j + 1) * TM], staged[:, k, j * P:(j + 1) * P],
                                                           w_in[:, O_DT:O_DT + TM], start=True, stop=True)
                                ins.then_inc(tok_ready, 1)

                    @block.scalar
                    def _(act):
                        with act.Fori(0, B) as b:
                            for k in range(2):
                                for i, (kind, f) in enumerate(JOBS):
                                    n = k * J + i
                                    act.wait_ge(acc_ready, b * (2 * J) + (n + 1))
                                    here = ds((b * 2 + k) * GW, GW)
                                    src = acc[:, n % 5]
                                    if kind == "gate":
                                        ins = nc.scalar.activation(gate[:, f, here], src, ACT.Silu)
                                    elif kind == "ssm":
                                        ins = nc.scalar.copy(ssm[:, f, ds(b * s_b + (PAD + k * GW), GW)], src)
                                    else:
                                        nc.scalar.copy(bT[:, here], src[0:DS])
                                        ins = nc.scalar.copy(cT[:, here], src[DS:2 * DS])
                                    ins.then_inc(acc_done, 1)

                    @block.vector
                    def _(dve):
                        dve.wait_ge(loaded, 16 * 7)
                        nc.vector.tensor_scalar(w_in[:], w_in[:], scale[:], None, ALU.mult).then_inc(scaled, 1)
                        with dve.Fori(0, B) as b:
                            for k in range(2):
                                dve.wait_ge(tok_ready, b * 2 + (k + 3))
                                nc.vector.tensor_copy(tok[:].rearrange("p t m -> p (t m)")[:, ds((b * 2 + k) * TG * TM, TG * TM)],
                                                      acc_t[:, k, 0:TG * TM]).then_inc(tok_done, 1)

            with ExitStack() as st3:
                c3 = Core(nc, st3, "l1d")
                low, soft = c3.sb("low", [P, NT, H]), c3.sb("soft", [P, NT, H])
                conv = c3.sb("conv", [P, 2, S])
                chain_sem, low_ready, a_ready = c3.sem("chain"), c3.sem("low_ready"), c3.sem("a_ready")
                soft_ready, act_chain, conv_ready, h_ready = c3.sem("soft_ready"), c3.sem("act_chain"), c3.sem("conv_ready"), c3.sem("h_ready")
                with nc.Block() as block:

                    @block.vector
                    def _(dve):
                        ch = Chain(dve, chain_sem)
                        ch.step(nc.vector.tensor_tensor(dt[:], tok[:, :, 0:H], dt_bias[:].unsqueeze(1).to_broadcast([P, NT, H]), ALU.add))
                        nc.vector.scalar_tensor_tensor(out=low[:], in0=dt[:], scalar=-1.0, in1=dt[:],
                                                       op0=ALU.mult, op1=ALU.min).then_inc(low_ready, 1)
                        dve.wait_ge(soft_ready, 1)
                        ch.step(nc.vector.scalar_tensor_tensor(out=dt[:], in0=dt[:], scalar=0.0, in1=soft[:],
                                                               op0=ALU.max, op1=ALU.add))
                        dve.wait_ge(a_ready, 1)
                        ch.step(nc.vector.scalar_tensor_tensor(out=adt[:], in0=dt[:], scalar=-1.0,
                                                               in1=a_log[:].unsqueeze(1).to_broadcast([P, NT, H]),
                                                               op0=ALU.mult, op1=ALU.mult))
                        base = ch.count
                        with dve.Fori(0, B) as b:
                            for f in range(F2):
                                dve.wait_ge(h_ready, b * F2 + (f + 1))
                                for n, k in enumerate(reversed(range(K))):
                                    src = ssm[:, f, ds(b * s_b + k, S)]
                                    if n == 0:
                                        ins = nc.vector.tensor_scalar(conv[:, f], src, conv_w[:, f, k:k + 1], None, ALU.mult)
                                    else:
                                        dve.wait_ge(chain_sem, b * (F2 * (K - 1)) + (base + f * (K - 1) + n))
                                        ins = nc.vector.scalar_tensor_tensor(out=conv[:, f], in0=src, scalar=conv_w[:, f, k:k + 1],
                                                                             in1=conv[:, f], op0=ALU.mult, op1=ALU.add)
                                    ins.then_inc(conv_ready if n == K - 1 else chain_sem, 1)

                    @block.scalar
                    def _(act):
                        act.sem_inc(h_ready, 2)
                        act.wait_ge(low_ready, 1)
                        nc.scalar.activation(low[:], low[:], ACT.Exp).then_inc(act_chain, 1)
                        act.wait_ge(act_chain, 1)
                        nc.scalar.activation(soft[:], low[:], ACT.Ln, bias=keep.ones[:, 0:1]).then_inc(soft_ready, 1)
                        nc.scalar.activation(a_log[:], a_log[:], ACT.Exp).then_inc(a_ready, 1)
                        with act.Fori(0, B) as b:
                            for f in range(F2):
                                act.wait_ge(conv_ready, b * F2 + (f + 1))
                                nc.scalar.activation(hT[:, f, ds(b * S, S)], conv[:, f], ACT.Silu,
                                                     bias=conv_b[:, f:f + 1]).then_inc(h_ready, 1)

        with ExitStack() as st2:
            c2 = Core(nc, st2, "l1s")
            hs, bs, ts = c2.sb("hs", [P, 2, F2, P]), c2.sb("bs", [DS, 2, P]), c2.sb("ts", [P, 2, DS])
            acol = c2.sb("acol", [P, 2, H])
            gap, decay = c2.sb("gap", [P, 2, H, P]), c2.sb("decay", [P, 2, H, P])
            into = c2.sb("into", [DS, 2, H, P])
            wgap, wcol = c2.sb("wgap", [P, 2, H]), c2.sb("wcol", [P, 2, H])
            gm, mix = c2.sb("gm", [P, 2, P]), c2.sb("mix", [P, 2, H, P])
            hd, hw = c2.sb("hd", [P, 2, DI]), c2.sb("hw", [P, 2, DI])
            cs = c2.sb("cs", [DS, 2, H, P])
            state = c2.sb("state", [DS, B, DI])
            ys = c2.sb("ys", [P, 2, F2, P])
            run = c2.ps("run", [P, 2, H, P])
            mid = c2.ps("mid", [P, 2, GW])
            res = c2.ps("res", [P, 2, GW])
            fin = c2.ps("fin", [P, 2, GW])
            col = lambda q: mid[:, q, 0:H]
            htok = lambda q: mid[:, q, P:P + DI]
            gram = lambda q: mid[:, q, P + DI:P + DI + P]
            yT = lambda q, f: res[:, q, f * P:(f + 1) * P]
            delta = lambda q: res[0:DS, q, DI:2 * DI]
            staged, sums, gaps = c2.sem("staged"), c2.sem("sums"), c2.sem("gaps")
            raised, mixed, pool_mixed = c2.sem("raised"), c2.sem("mixed"), c2.sem("pool_mixed")
            y_ready, gated, out_ready, added = c2.sem("y_ready"), c2.sem("gated"), c2.sem("out_ready"), c2.sem("added")
            hd_sem, state_sem, zeroed = c2.sem("hd_sem"), c2.sem("state_sem"), c2.sem("zeroed")
            NS = 4
            with nc.Block() as block:

                @block.gpsimd
                def _(pool):
                    with pool.Fori(0, NC_) as ck:
                        for j in range(B):
                            q = j % 2
                            pool.wait_ge(y_ready, ck * B + (j + 1))
                            at = ck * P + j * S
                            nc.gpsimd.tensor_copy(acol[:, q], adt[:].rearrange("p t h -> p (t h)")[:, ds(ck * H + j * NC_ * H, H)]).then_inc(staged, 1)
                            nc.gpsimd.tensor_copy(hs[:, q], hT[:, :, ds(at, P)]).then_inc(staged, 1)
                            nc.gpsimd.tensor_copy(bs[:, q], bT[:, ds(at, P)]).then_inc(staged, 1)
                            nc.gpsimd.tensor_copy(ts[:, q], tok[:].rearrange("p t m -> p (t m)")[:, ds(ck * TM + (j * NC_ * TM + H), DS)]).then_inc(staged, 1)
                            pool.wait_ge(raised, (ck * B + j) * 3 + 3)
                            nc.gpsimd.tensor_tensor(cs[:, q], into[:, q], cT[:, ds(at, P)].unsqueeze(1).to_broadcast([DS, H, P]),
                                                    ALU.mult).then_inc(pool_mixed, 1)

                @block.tensor
                def _(pe):
                    pe.sem_inc(y_ready, 2)
                    pe.sem_inc(mixed, 2)
                    pe.sem_inc(added, 2)
                    pe.sem_inc(gated, 2)
                    pe.wait_ge(zeroed, 1)

                    def project(ck, j):
                        pe.wait_ge(gated, ck * B + (j + 3))
                        pe.wait_ge(added, ck * B + (j + 1))
                        for f in range(F2):
                            ins = nc.tensor.matmul(fin[:, j % 2, 0:D], ys[:, j % 2, f], w_out[:, f], start=(f == 0), stop=(f == F2 - 1))
                        ins.then_inc(out_ready, 1)

                    with pe.Fori(0, NC_) as ck:
                        for j in range(B):
                            q = j % 2
                            pe.wait_ge(staged, (ck * B + j) * NS + NS)
                            pe.wait_ge(mixed, ck * B + (j + 1))
                            for h in range(H):
                                nc.tensor.matmul(run[:, q, h], acol[:, q, h:h + 1].to_broadcast([P, P]), keep.upto[:], start=True, stop=True)
                            nc.tensor.matmul(col(q), keep.upto[:], acol[:, q], start=True, stop=True)
                            for f in range(F2):
                                nc.tensor.transpose(htok(q)[:, f * P:(f + 1) * P], hs[:, q, f], keep.ident[:])
                            nc.tensor.matmul(gram(q), bs[:, q], cT[:, ds(ck * P + j * S, P)], start=True, stop=True).then_inc(sums, 1)
                            if j:
                                project(ck, j - 1)
                            pe.wait_ge(mixed, ck * B + (j + 3))
                            pe.wait_ge(pool_mixed, ck * B + (j + 1))
                            pe.wait_ge(gated, ck * B + (j + 1))
                            for h in range(H):
                                f, o = divmod(h * HD, P)
                                out = yT(q, f)[o:o + HD]
                                nc.tensor.matmul(out, hd[:, q, h * HD:(h + 1) * HD], mix[:, q, h], start=True, stop=False)
                                nc.tensor.matmul(out, state[:, j, h * HD:(h + 1) * HD], cs[:, q, h], start=False, stop=True)
                            nc.tensor.matmul(delta(q), ts[:, q], hw[:, q], start=True, stop=True).then_inc(y_ready, 1)
                        project(ck, B - 1)

                @block.scalar
                def _(act):
                    with act.Fori(0, NC_) as ck:
                        for j in range(B):
                            q = j % 2
                            act.wait_ge(gaps, ck * B + (j + 1))
                            act.wait_ge(gated, ck * B + (j + 1))
                            act.wait_ge(y_ready, ck * B + (j + 1))
                            nc.scalar.activation(decay[:, q], gap[:, q], ACT.Exp).then_inc(raised, 1)
                            nc.scalar.activation(wcol[:, q], wgap[:, q], ACT.Exp).then_inc(raised, 1)
                            nc.scalar.activation(into[:, q], run[0:DS, q], ACT.Exp).then_inc(raised, 1)

                @block.vector
                def _(dve):
                    nc.vector.memset(state[:], 0.0).then_inc(zeroed, 1)

                    def finish(ck, j):
                        q = j % 2
                        dve.wait_ge(y_ready, ck * B + (j + 3))
                        last = into[:, q, :, P - 1:P].to_broadcast([DS, H, HD])
                        st_ = state[:, j].rearrange("n (h p) -> n h p", h=H)
                        nc.vector.tensor_tensor(st_, st_, last, ALU.mult).then_inc(state_sem, 1)
                        nc.vector.tensor_tensor(ys[:, q], res[:, q, 0:DI].rearrange("p (f t) -> p f t", f=F2),
                                                gate[:, :, ds(ck * P + j * S, P)], ALU.mult)
                        dve.wait_ge(state_sem, ck * B + (j + 1))
                        nc.vector.tensor_tensor(state[:, j], delta(q), state[:, j], ALU.add).then_inc(gated, 1)

                    def add(ck, j):
                        dve.wait_ge(out_ready, ck * B + (j + 1))
                        x = keep.x_tok[:, ds(ck * P + j * S, D)]
                        nc.vector.scalar_tensor_tensor(out=x, in0=x, scalar=2.0, in1=fin[:, j % 2, 0:D],
                                                       op0=ALU.mult, op1=ALU.add).then_inc(added, 1)

                    with dve.Fori(0, NC_) as ck:
                        for j in range(B):
                            q = j % 2
                            dve.wait_ge(sums, ck * B + (j + 1))
                            for h in range(H):
                                nc.vector.tensor_scalar(gap[:, q, h], run[:, q, h], col(q)[:, h:h + 1], 0.0, ALU.subtract, ALU.min)
                            nc.vector.tensor_copy(wcol[:, q], col(q)).then_inc(hd_sem, 1)
                            dve.wait_ge(hd_sem, (ck * B + j) * 2 + 1)
                            nc.vector.tensor_tensor(wgap[:, q], run[:, q, :, P - 1], wcol[:, q], ALU.subtract).then_inc(gaps, 1)
                            if j:
                                finish(ck, j - 1)
                            nc.vector.tensor_tensor(gm[:, q], gram(q), keep.upto[:], ALU.mult)
                            d = dt[:].rearrange("p t h -> p (t h)")[:, ds(ck * H + j * NC_ * H, H)]
                            nc.vector.tensor_tensor(hd[:, q].rearrange("p (h d) -> p h d", h=H), htok(q).rearrange("p (h d) -> p h d", h=H),
                                                    d.unsqueeze(2).to_broadcast([P, H, HD]), ALU.mult).then_inc(hd_sem, 1)
                            dve.wait_ge(raised, (ck * B + j) * 3 + 3)
                            dve.wait_ge(hd_sem, (ck * B + j) * 2 + 2)
                            nc.vector.tensor_tensor(hw[:, q].rearrange("p (h d) -> p h d", h=H), hd[:, q].rearrange("p (h d) -> p h d", h=H),
                                                    wcol[:, q].unsqueeze(2).to_broadcast([P, H, HD]), ALU.mult)
                            nc.vector.tensor_tensor(mix[:, q], decay[:, q], gm[:, q].unsqueeze(1).to_broadcast([P, H, P]),
                                                    ALU.mult).then_inc(mixed, 1)
                            if j:
                                add(ck, j - 1)
                        finish(ck, B - 1)
                        add(ck, B - 1)


def layer1_ffn(nc, keep, a):
    H, HD, SLOTS, F = 16, 8, 16, 512
    NF = F // P
    BS = B * SLOTS
    HQ = H * SLOTS
    INV = 1.0 / math.sqrt(HD)
    with ExitStack() as st:
        c = Core(nc, st, "l1f")
        w1, wg = c.sb("w1", [P, SLOTS, F]), c.sb("wg", [P, SLOTS, F])
        w2 = c.sb("w2", [P, SLOTS, NF, D])
        small = c.sb("small", [P, 8, D])
        cols = c.sb("cols", [P, 8])
        slot_T = c.sb("slot_T", [P, SLOTS])
        b1, bg = c.sb("b1", [P, SLOTS, NF]), c.sb("bg", [P, SLOTS, NF])
        ln_g, ln_b = c.sb("ln_g", [BS, D]), c.sb("ln_b", [BS, D])
        b2T = c.sb("b2T", [P, SLOTS])
        c_bo = c.sb("c_bo", [P, D])
        head_mask = c.sb("head_mask", [P, H])
        own = c.sb("own", [P, 2, D])
        fold = c.sb("fold", [P, SLOTS])
        qblk = c.sb("qblk", [P, H, SLOTS])
        attT = c.sb("attT", [P, BS])
        o_T, o2T = c.sb("o_T", [P, BS]), c.sb("o2T", [P, BS])
        kblk, vblk = c.sb("kblk", [P, B, H, SLOTS]), c.sb("vblk", [P, B, H, SLOTS])
        vw = c.sb("vw", [P, B, 2, D])
        big_loaded = c.sem("big_loaded")
        wide3 = lambda x, shape: x.to_broadcast(shape)

        with ExitStack() as st2:
            c2 = Core(nc, st2, "l1g")
            qT = c2.sb("qT", [P, SLOTS])
            acc = c2.ps("acc", [P, 512])
            loaded, masks, acc_ready, chain_sem = c2.sem("loaded"), c2.sem("masks"), c2.sem("acc_ready"), c2.sem("chain")
            SMALL = 8 + 2 + 2 + 1 + 1 + 2 * B
            with nc.Block() as block:

                @block.sync
                def _(sp):
                    for n, name in enumerate(("d_Wq", "d_Wk", "d_Wo", "c_Wq", "c_Wk", "c_Wv", "c_Wo")):
                        sp.dma_start(small[:, n], a["L1_ffn_" + name]).then_inc(loaded, 16)
                    for dst, src in ((cols[:], "L1_ffn_bias_cols"), (slot_T[:], "L1_ffn_slot_T"), (b1[:].rearrange("p e f -> p (e f)"), "L1_ffn_b1_cols"),
                                     (bg[:].rearrange("p e f -> p (e f)"), "L1_ffn_bg_cols"), (b2T[:], "L1_ffn_b2_T")):
                        sp.dma_start(dst, a[src]).then_inc(loaded, 16)
                    for b in range(B):
                        sp.dma_start(ln_g[b * SLOTS:(b + 1) * SLOTS], a["L1_ffn_e_ln_g"]).then_inc(loaded, 16)
                        sp.dma_start(ln_b[b * SLOTS:(b + 1) * SLOTS], a["L1_ffn_e_ln_b"]).then_inc(loaded, 16)
                    sp.dma_start(c_bo[:], a["L1_ffn_c_bo"].rearrange("(o d) -> o d", o=1).broadcast_to([P, D])).then_inc(loaded, 16)
                    sp.dma_start(w1[:], a["L1_ffn_e_W1"].rearrange("e d f -> d e f")).then_inc(big_loaded, 16)
                    sp.dma_start(wg[:], a["L1_ffn_e_Wg"].rearrange("e d f -> d e f")).then_inc(big_loaded, 16)
                    sp.dma_start(w2[:], a["L1_ffn_e_W2"].rearrange("e (k p) d -> p e k d", p=P)).then_inc(big_loaded, 16)
                    sp.wait_ge(loaded, 16 * (7 + 5 + 2 * B + 1))

                @block.gpsimd
                def _(pool):
                    ch = Chain(pool, masks)
                    sel = lambda ap, base, pattern, cm: ch.step(nc.gpsimd.affine_select(
                        out=ap, in_=ap, compare_op=ALU.is_ge, fill=0.0, base=base, pattern=pattern, channel_multiplier=cm))
                    ch.step(nc.gpsimd.memset(head_mask[:], 1.0))
                    sel(head_mask[:], 0, [[-HD, H]], 1)
                    sel(head_mask[:], HD - 1, [[HD, H]], -1)
                    ch.step(nc.gpsimd.memset(own[:], 1.0))
                    for f in range(2):
                        m = own[:, f].rearrange("p (h d) -> p h d", d=HD)
                        sel(m, P * f, [[-SLOTS, H], [0, HD]], 1)
                        sel(m, SLOTS - 1 - P * f, [[SLOTS, H], [0, HD]], -1)

                @block.tensor
                def _(pe):
                    pe.wait_ge(loaded, 16 * (7 + 5 + 2 * B + 1))
                    nc.tensor.matmul(acc[:, 0:SLOTS], small[:, 0], slot_T[:], start=True, stop=True).then_inc(acc_ready, 1)

                @block.vector
                def _(dve):
                    ch = Chain(dve, chain_sem)
                    ch.step(nc.vector.tensor_reduce(fold[:], keep.ident[:].rearrange("p (h q) -> p q h", q=SLOTS), AX.X, ALU.add))
                    dve.wait_ge(acc_ready, 1)
                    ch.step(nc.vector.tensor_scalar(qT[:], acc[:, 0:SLOTS], cols[:, 0:1], None, ALU.add))
                    dve.wait_ge(masks, 8)
                    ch.step(nc.vector.tensor_tensor(qblk[:], qT[:].unsqueeze(1).to_broadcast([P, H, SLOTS]),
                                                    head_mask[:].unsqueeze(2).to_broadcast([P, H, SLOTS]), ALU.mult))

        with ExitStack() as st2:
            c2 = Core(nc, st2, "l1h")
            kT = c2.sb("kT", [P, N])
            v_tok = c2.sb("v_tok", [P, N])
            project_tokens(nc, keep, "l1v", keep.x_T, a["L1_ffn_d_Wv"], v_tok, bias_dram=a["L1_ffn_d_bv"])
            with ExitStack() as st3:
                c3 = Core(nc, st3, "l1k")
                acc = c3.ps("acc", [P, 2, GW])
                acc_ready, acc_done = c3.sem("acc_ready"), c3.sem("acc_done")
                with nc.Block() as block:

                    @block.tensor
                    def _(pe):
                        pe.sem_inc(acc_done, 2)
                        with pe.Fori(0, NG // 2) as pair:
                            for k in range(2):
                                pe.wait_ge(acc_done, pair * 2 + (k + 1))
                                nc.tensor.matmul(acc[:, k], small[:, 1], keep.x_T[:, ds((pair * 2 + k) * GW, GW)], start=True, stop=True)\
                                    .then_inc(acc_ready, 1)

                    @block.scalar
                    def _(act):
                        with act.Fori(0, NG // 2) as pair:
                            for k in range(2):
                                act.wait_ge(acc_ready, pair * 2 + (k + 1))
                                nc.scalar.activation(kT[:, ds((pair * 2 + k) * GW, GW)], acc[:, k], ACT.Identity, bias=cols[:, 1:2]).then_inc(acc_done, 1)

            with ExitStack() as st3:
                c3 = Core(nc, st3, "l1m")
                prob = c3.sb("prob", [P, 2, S])
                probT = c3.sb("probT", [P, 2, S])
                negmax, total, share = c3.sb("negmax", [P, 2]), c3.sb("total", [P, 2]), c3.sb("share", [P, 2])
                res = c3.sb("res", [P, 2, D])
                sc = c3.ps("sc", [P, 2, S])
                out = c3.ps("out", [P, 2, GW])
                fin = c3.ps("fin", [P, 2, GW])
                sc_ready, max_done, p_ready = c3.sem("sc_ready"), c3.sem("max_done"), c3.sem("p_ready")
                t_ready, t_done, out_ready, share_done = c3.sem("t_ready"), c3.sem("t_done"), c3.sem("out_ready"), c3.sem("share_done")
                res_ready, fin_ready, fin_done, scaled = c3.sem("res_ready"), c3.sem("fin_ready"), c3.sem("fin_done"), c3.sem("scaled")
                v3 = v_tok[:].rearrange("p (t d) -> p t d", d=D)
                with nc.Block() as block:

                    @block.tensor
                    def _(pe):
                        pe.sem_inc(fin_done, 1)
                        with pe.Fori(0, B) as b:
                            for f in range(2):
                                pe.wait_ge(t_done, b * 2)
                                for o in range(2):
                                    ins = nc.tensor.matmul(sc[:, f, o * GW:(o + 1) * GW], qblk[:].rearrange("p h q -> p (h q)")[:, f * P:(f + 1) * P],
                                                           kT[:, ds(b * S + o * GW, GW)], start=True, stop=True)
                                ins.then_inc(sc_ready, 1)
                            for f in range(2):
                                pe.wait_ge(p_ready, b * 2 + (f + 1))
                                for t in range(S // P):
                                    ins = nc.tensor.transpose(sc[:, f, t * P:(t + 1) * P], prob[:, f, t * P:(t + 1) * P], keep.ident[:])
                                ins.then_inc(t_ready, 1)
                            for f in range(2):
                                pe.wait_ge(t_done, b * 2 + (f + 1))
                                pe.wait_ge(res_ready, b * 2)
                                for t in range(S // P):
                                    ins = nc.tensor.matmul(out[:, f, 0:D], probT[:, f, t * P:(t + 1) * P], v_tok[:, ds(b * S + t * P, D)],
                                                           start=(t == 0), stop=(t == S // P - 1))
                                ins.then_inc(out_ready, 1)
                            pe.wait_ge(res_ready, b * 2 + 2)
                            pe.wait_ge(fin_done, b + 1)
                            for f in range(2):
                                ins = nc.tensor.matmul(fin[:, 0, 0:SLOTS], res[:, f], fold[:], start=(f == 0), stop=(f == 1))
                            ins.then_inc(fin_ready, 1)

                    @block.scalar
                    def _(act):
                        with act.Fori(0, B) as b:
                            for f in range(2):
                                act.wait_ge(scaled, b * 2 + (f + 1))
                                act.wait_ge(t_ready, b * 2)
                                nc.scalar.activation(prob[:, f], sc[:, f], ACT.Exp, bias=share[:, f:f + 1], scale=INV,
                                                     accum_out=total[:, f:f + 1]).then_inc(p_ready, 1)
                            for f in range(2):
                                act.wait_ge(t_ready, b * 2 + (f + 1))
                                act.wait_ge(out_ready, b * 2)
                                nc.scalar.copy(probT[:, f], sc[:, f]).then_inc(t_done, 1)

                    @block.vector
                    def _(dve):
                        with dve.Fori(0, B) as b:
                            for f in range(2):
                                dve.wait_ge(sc_ready, b * 2 + (f + 1))
                                nc.vector.tensor_reduce(negmax[:, f:f + 1], sc[:, f], AX.X, ALU.max, negate=True).then_inc(max_done, 1)
                                dve.wait_ge(max_done, b * 2 + (f + 1))
                                nc.vector.tensor_scalar(share[:, f:f + 1], negmax[:, f:f + 1], INV, None, ALU.mult).then_inc(scaled, 1)
                            for f in range(2):
                                dve.wait_ge(out_ready, b * 2 + (f + 1))
                                nc.vector.reciprocal(negmax[:, f:f + 1], total[:, f:f + 1]).then_inc(share_done, 1)
                                dve.wait_ge(share_done, b * 2 + (f + 1))
                                dve.wait_ge(fin_ready, b)
                                nc.vector.scalar_tensor_tensor(out=res[:, f], in0=out[:, f, 0:D], scalar=negmax[:, f:f + 1], in1=own[:, f],
                                                               op0=ALU.mult, op1=ALU.mult).then_inc(res_ready, 1)
                            dve.wait_ge(fin_ready, b + 1)
                            nc.vector.tensor_copy(attT[:, ds(b * SLOTS, SLOTS)], fin[:, 0, 0:SLOTS]).then_inc(fin_done, 1)

        with ExitStack() as st2:
            c2 = Core(nc, st2, "l1e")
            o_tok, h_tok = c2.sb("o_tok", [BS, D]), c2.sb("h_tok", [BS, D])
            stat, mv = c2.sb("stat", [BS, 6]), c2.sb("mv", [BS, 2])
            std = c2.sb("std", [BS, 1])
            hT = c2.sb("hT", [P, BS])
            uu, gg = c2.sb("uu", [P, SLOTS, NF, B]), c2.sb("gg", [P, SLOTS, NF, B])
            kvT = c2.sb("kvT", [P, 2, BS])
            p0, p1, p2, p3 = (c2.ps(f"p{n}", [P, 512]) for n in range(4))
            dve_sem, pe_sem, act_sem = c2.sem("dve"), c2.sem("pe"), c2.sem("act")
            hidden = lambda x: x[:, 0:SLOTS * NF * B].rearrange("p (e f b) -> p e f b", e=SLOTS, f=NF)
            by_batch = lambda x: x.rearrange("p (b e) -> p b e", b=B)
            with nc.Block() as block:

                @block.tensor
                def _(pe):
                    nc.tensor.matmul(p0[:, 0:BS], small[:, 2], attT[:], start=True, stop=True).then_inc(pe_sem, 1)
                    pe.wait_ge(dve_sem, 2)
                    nc.tensor.transpose(p1[0:BS, 0:D], o_T[:], keep.ident[:]).then_inc(pe_sem, 1)
                    pe.wait_ge(dve_sem, 8)
                    nc.tensor.transpose(p2[:, 0:BS], h_tok[:], keep.ident[0:BS, 0:BS]).then_inc(pe_sem, 1)
                    pe.wait_ge(dve_sem, 9)
                    pe.wait_ge(big_loaded, 48)
                    for e in range(SLOTS):
                        x = by_batch(hT[:])[:, :, e]
                        for f in range(NF):
                            nc.tensor.matmul(hidden(p0)[:, e, f], w1[:, e, f * P:(f + 1) * P], x, start=True, stop=True)
                            ins = nc.tensor.matmul(hidden(p1)[:, e, f], wg[:, e, f * P:(f + 1) * P], x, start=True, stop=True)
                    ins.then_inc(pe_sem, 1)
                    pe.wait_ge(dve_sem, 12)
                    for e in range(SLOTS):
                        for f in range(NF):
                            ins = nc.tensor.matmul(by_batch(p2[:, 0:BS])[:, :, e], w2[:, e, f], uu[:, e, f], start=(f == 0), stop=(f == NF - 1))
                    ins.then_inc(pe_sem, 1)
                    pe.wait_ge(dve_sem, 14)
                    nc.tensor.matmul(p3[:, 0:BS], small[:, 4], o2T[:], start=True, stop=True)
                    nc.tensor.matmul(p3[:, BS:2 * BS], small[:, 5], o2T[:], start=True, stop=True).then_inc(pe_sem, 1)
                    pe.wait_ge(dve_sem, 16 + 2 * B)
                    for b in range(B):
                        for f in range(2):
                            ins = nc.tensor.matmul((p0, p1)[f][:, b * D:(b + 1) * D],
                                                   vblk[:, b].rearrange("p h k -> p (h k)")[:, f * P:(f + 1) * P], small[:, 6], start=True, stop=True)
                    ins.then_inc(pe_sem, 1)

                @block.scalar
                def _(act):
                    act.wait_ge(dve_sem, 4)
                    nc.scalar.activation(std[:], mv[:, 1:2], ACT.Sqrt, bias=keep.eps[0:BS]).then_inc(act_sem, 1)
                    act.wait_ge(dve_sem, 11)
                    nc.scalar.activation(uu[:], uu[:], ACT.Silu).then_inc(act_sem, 1)
                    nc.scalar.activation(gg[:], gg[:], ACT.Silu).then_inc(act_sem, 1)

                @block.vector
                def _(dve):
                    ch = Chain(dve, dve_sem)
                    dve.wait_ge(pe_sem, 1)
                    ch.step(nc.vector.tensor_scalar(o_T[:], p0[:, 0:BS], cols[:, 2:3], None, ALU.add))
                    ch.step(nc.vector.tensor_tensor(by_batch(o_T[:]), by_batch(o_T[:]), slot_T[:].unsqueeze(1).to_broadcast([P, B, SLOTS]), ALU.add))
                    dve.wait_ge(pe_sem, 2)
                    ch.step(nc.vector.bn_stats(stat[:], p1[0:BS, 0:D]))
                    ch.step(nc.vector.bn_aggr(mv[:], stat[:]))
                    dve.wait_ge(act_sem, 1)
                    ch.step(nc.vector.reciprocal(std[:], std[:]))
                    ch.step(nc.vector.tensor_scalar(h_tok[:], p1[0:BS, 0:D], mv[:, 0:1], std[:], ALU.subtract, ALU.mult))
                    ch.step(nc.vector.tensor_tensor(h_tok[:], h_tok[:], ln_g[:], ALU.mult))
                    ch.step(nc.vector.tensor_tensor(h_tok[:], h_tok[:], ln_b[:], ALU.add))
                    dve.wait_ge(pe_sem, 3)
                    ch.step(nc.vector.tensor_copy(hT[:], p2[:, 0:BS]))
                    dve.wait_ge(pe_sem, 4)
                    ch.step(nc.vector.tensor_tensor(uu[:], hidden(p0), b1[:].unsqueeze(3).to_broadcast([P, SLOTS, NF, B]), ALU.add))
                    ch.step(nc.vector.tensor_tensor(gg[:], hidden(p1), bg[:].unsqueeze(3).to_broadcast([P, SLOTS, NF, B]), ALU.add))
                    dve.wait_ge(act_sem, 3)
                    ch.step(nc.vector.tensor_tensor(uu[:], uu[:], gg[:], ALU.mult))
                    dve.wait_ge(pe_sem, 5)
                    ch.step(nc.vector.tensor_tensor(o2T[:], p2[:, 0:BS], o_T[:], ALU.add))
                    ch.step(nc.vector.tensor_tensor(by_batch(o2T[:]), by_batch(o2T[:]), b2T[:].unsqueeze(1).to_broadcast([P, B, SLOTS]), ALU.add))
                    dve.wait_ge(pe_sem, 6)
                    for m in range(2):
                        ch.step(nc.vector.tensor_scalar(kvT[:, m], p3[:, m * BS:(m + 1) * BS], cols[:, 4 + m:5 + m], None, ALU.add))
                    for b in range(B):
                        for m, dst in enumerate((kblk, vblk)):
                            ch.step(nc.vector.tensor_tensor(dst[:, b], kvT[:, m, b * SLOTS:(b + 1) * SLOTS].unsqueeze(1).to_broadcast([P, H, SLOTS]),
                                                            head_mask[:].unsqueeze(2).to_broadcast([P, H, SLOTS]), ALU.mult))
                    dve.wait_ge(pe_sem, 7)
                    for f in range(2):
                        ch.step(nc.vector.tensor_copy(vw[:, :, f], (p0, p1)[f][:].rearrange("p (b d) -> p b d", b=B)))

        with ExitStack() as st2:
            c2 = Core(nc, st2, "l1c")
            qT = c2.sb("qT", [P, 2, GW])
            z, e = c2.sb("z", [P, 2, GW]), c2.sb("e", [P, 2, GW])
            top, total = c2.sb("top", [P, 2, 2 * H]), c2.sb("total", [P, 2, 2 * H])
            pT = c2.sb("pT", [P, 2, GW])
            sums = c2.sb("sums", [P, 2, 2 * D])
            qp = c2.ps("qp", [P, GW])
            sc = c2.ps("sc", [P, 2, GW])
            tp = c2.ps("tp", [P, 2, GW])
            out = c2.ps("out", [P, 2, GW])
            q_ready, q_done = c2.sem("q_ready"), c2.sem("q_done")
            sc_ready, sc_done, top_done, raised = c2.sem("sc_ready"), c2.sem("sc_done"), c2.sem("top_done"), c2.sem("raised")
            normed, t_ready, t_done, out_ready = c2.sem("normed"), c2.sem("t_ready"), c2.sem("t_done"), c2.sem("out_ready")
            out_done, added, sum_done, p_used = c2.sem("out_done"), c2.sem("added"), c2.sem("sum_done"), c2.sem("p_used")
            k3 = kblk[:].rearrange("p b h k -> p (b h k)")
            vw3 = vw[:].rearrange("p b f d -> p (b f d)")
            heads = lambda x: x.rearrange("p (g k) -> p g k", k=SLOTS)
            wide = lambda x: x.unsqueeze(2).to_broadcast([P, 2 * H, SLOTS])
            with nc.Block() as block:

                @block.tensor
                def _(pe):
                    pe.sem_inc(sc_done, 2)
                    pe.sem_inc(t_done, 2)
                    pe.sem_inc(out_done, 2)

                    def finish(b, i):
                        k = i % 2
                        pe.wait_ge(t_done, b * 4 + (i + 3))
                        pe.wait_ge(out_done, b * 4 + (i + 1))
                        for t in range(2):
                            for f in range(2):
                                ins = nc.tensor.matmul(out[:, k, t * D:(t + 1) * D], pT[:, k, (t * 2 + f) * P:(t * 2 + f + 1) * P],
                                                       vw3[:, ds(b * (2 * D) + f * D, D)], start=(f == 0), stop=(f == 1))
                        ins.then_inc(out_ready, 1)

                    with pe.Fori(0, B) as b:
                        for i in range(4):
                            k = i % 2
                            if k == 0:
                                pe.wait_ge(q_done, b * 2 + i // 2)
                                nc.tensor.matmul(qp[:], small[:, 3], keep.x_T[:, ds((b * 2 + i // 2) * GW, GW)], start=True, stop=True).then_inc(q_ready, 1)
                                pe.wait_ge(q_done, b * 2 + (i // 2 + 1))
                            pe.wait_ge(sc_done, b * 4 + (i + 1))
                            for t in range(2):
                                ins = nc.tensor.matmul(sc[:, k, t * HQ:(t + 1) * HQ], qT[:, i // 2, (k * 2 + t) * P:(k * 2 + t + 1) * P],
                                                       k3[:, ds(b * HQ, HQ)], start=True, stop=True)
                            ins.then_inc(sc_ready, 1)
                            if i:
                                finish(b, i - 1)
                            pe.wait_ge(normed, b * 4 + (i + 1))
                            pe.wait_ge(t_done, b * 4 + (i + 1))
                            for t in range(4):
                                ins = nc.tensor.transpose(tp[:, k, t * P:(t + 1) * P], e[:, k, t * P:(t + 1) * P], keep.ident[:])
                            ins.then_inc(t_ready, 1)
                        finish(b, 3)

                @block.scalar
                def _(act):
                    with act.Fori(0, B) as b:
                        for i in range(4):
                            k = i % 2
                            if k == 0:
                                act.wait_ge(q_ready, b * 2 + (i // 2 + 1))
                                nc.scalar.activation(qT[:, i // 2], qp[:], ACT.Identity, bias=cols[:, 3:4]).then_inc(q_done, 1)
                            act.wait_ge(sc_done, b * 4 + (i + 3))
                            nc.scalar.activation(z[:, k], z[:, k], ACT.Exp, scale=INV).then_inc(raised, 1)
                            act.wait_ge(t_ready, b * 4 + (i + 1))
                            act.wait_ge(out_done, b * 4 + (i + 1))
                            nc.scalar.copy(pT[:, k], tp[:, k]).then_inc(t_done, 1)

                @block.vector
                def _(dve):
                    def add(b, i):
                        k = i % 2
                        dve.wait_ge(out_ready, b * 4 + (i + 1))
                        nc.vector.tensor_tensor(sums[:, k].rearrange("p (t d) -> p t d", d=D), out[:, k, 0:2 * D].rearrange("p (t d) -> p t d", d=D),
                                                c_bo[:].unsqueeze(1).to_broadcast([P, 2, D]), ALU.add).then_inc(out_done, 1)
                        dve.wait_ge(out_done, b * 4 + (i + 3))
                        x = keep.x_tok[:, ds(b * S + i * (2 * D), 2 * D)]
                        nc.vector.tensor_tensor(x, x, sums[:, k], ALU.add).then_inc(added, 1)

                    with dve.Fori(0, B) as b:
                        for i in range(4):
                            k = i % 2
                            n = b * 4 + i
                            dve.wait_ge(sc_ready, n + 1)
                            nc.vector.tensor_reduce(top[:, k], heads(sc[:, k]), AX.X, ALU.max).then_inc(top_done, 1)
                            dve.wait_ge(top_done, n + 1)
                            nc.vector.tensor_tensor(heads(z[:, k]), heads(sc[:, k]), wide(top[:, k]), ALU.subtract).then_inc(sc_done, 1)
                            if i:
                                add(b, i - 1)
                            dve.wait_ge(raised, n + 1)
                            nc.vector.tensor_reduce(total[:, k], heads(z[:, k]), AX.X, ALU.add).then_inc(sum_done, 1)
                            dve.wait_ge(sum_done, n * 2 + 1)
                            nc.vector.reciprocal(total[:, k], total[:, k]).then_inc(sum_done, 1)
                            dve.wait_ge(sum_done, n * 2 + 2)
                            nc.vector.tensor_tensor(heads(e[:, k]), heads(z[:, k]), wide(total[:, k]), ALU.mult).then_inc(normed, 1)
                        add(b, 3)


def project_tokens(nc, keep, tag, src_T, w_dram, out, scaled=(), loads=(), bias_dram=None, add=False):
    with ExitStack() as st:
        c = Core(nc, st, tag + "pt")
        w = c.sb("w", [P, D])
        bias = c.sb("bias", [P, D]) if bias_dram is not None else None
        staged = c.sb("staged", [P, 2, GW])
        acc = c.ps("acc", [P, 2, GW])
        sums = c.sb("sums", [P, 2, GW])
        biased = c.sem("biased")
        loaded, w_loaded, staged_ready = c.sem("loaded"), c.sem("w_loaded"), c.sem("staged_ready")
        acc_ready, acc_done, scale_done = c.sem("acc_ready"), c.sem("acc_done"), c.sem("scale_done")
        with nc.Block() as block:

            @block.sync
            def _(sp):
                sp.dma_start(w[:], w_dram).then_inc(w_loaded, 16)
                if bias_dram is not None:
                    sp.dma_start(bias[:], bias_dram.rearrange("(o d) -> o d", o=1).broadcast_to([P, D])).then_inc(w_loaded, 16)
                for dst, src in loads:
                    sp.dma_start(dst, src).then_inc(loaded, 16)
                if loads:
                    sp.wait_ge(loaded, 16 * len(loads))

            @block.gpsimd
            def _(pool):
                with pool.Fori(0, NG // 2) as pair:
                    for k in range(2):
                        pool.wait_ge(acc_ready, pair * 2 + (k + 1))
                        nc.gpsimd.tensor_copy(staged[:, k], src_T[:, ds((pair * 2 + k) * GW, GW)]).then_inc(staged_ready, 1)

            @block.tensor
            def _(pe):
                pe.sem_inc(acc_ready, 2)
                pe.sem_inc(acc_done, 2)
                pe.wait_ge(w_loaded, 16 if bias_dram is None else 32)
                with pe.Fori(0, NG // 2) as pair:
                    for k in range(2):
                        pe.wait_ge(staged_ready, pair * 2 + (k + 1))
                        pe.wait_ge(acc_done, pair * 2 + (k + 1))
                        for j in range(TG):
                            ins = nc.tensor.matmul(acc[:, k, j * D:(j + 1) * D], staged[:, k, j * P:(j + 1) * P], w[:],
                                                   start=True, stop=True)
                        ins.then_inc(acc_ready, 1)

            @block.vector
            def _(dve):
                with dve.Fori(0, NG // 2) as pair:
                    for k in range(2):
                        dve.wait_ge(acc_ready, pair * 2 + (k + 3))
                        dst = out[:, ds((pair * 2 + k) * GW, GW)]
                        if bias is None:
                            nc.vector.tensor_copy(dst, acc[:, k]).then_inc(acc_done, 1)
                            continue
                        wide = lambda x: x.rearrange("p (t d) -> p t d", d=D)
                        to = sums[:, k] if add else dst
                        nc.vector.tensor_tensor(wide(to), wide(acc[:, k]), bias[:].unsqueeze(1).to_broadcast([P, TG, D]),
                                                ALU.add).then_inc(acc_done, 1)
                        if add:
                            dve.wait_ge(acc_done, pair * 2 + (k + 3))
                            nc.vector.tensor_tensor(dst, dst, sums[:, k], ALU.add).then_inc(biased, 1)
                            dve.wait_ge(biased, pair * 2 + (k + 1))
                if loads:
                    dve.wait_ge(loaded, 16 * len(loads))
                for tile, factor in scaled:
                    nc.vector.tensor_scalar(tile, tile, factor, None, ALU.mult).then_inc(scale_done, 1)


def layer2_attn(nc, keep, a):
    SL, KS, VD = 8, 64, 16
    VP = 32
    HEADS = B * S // P
    Q = SL * P
    with ExitStack() as st:
        c = Core(nc, st, "l2a")
        mq, mk = c.sb("mq", [P, SL * KS]), c.sb("mk", [P, SL * KS])
        xv = c.sb("xv", [P, NT * D])
        project_tokens(nc, keep, "l2a", keep.x_T, a["L2_attn_Mv"], xv, scaled=[(mq[:], 1.0 / math.sqrt(KS))],
                       loads=[(mq[:], a["L2_attn_Mq"]), (mk[:], a["L2_attn_Mk"])])
        kT, qT = c.sb("kT", [KS, 2, Q]), c.sb("qT", [KS, 2, Q])
        RING = 4
        pT = c.sb("pT", [P, RING, Q])
        vs = c.sb("vs", [P, RING, SL, VP])
        negmax, total, share = c.sb("negmax", [P, 2]), c.sb("total", [P, RING]), c.sb("share", [P, RING])
        outT = c.sb("outT", [P, 2, 2 * P])
        xv3 = xv[:].rearrange("p (t d) -> p t d", d=D)
        sc = c.ps("sc", [P, 2, Q])
        pj = c.ps("pj", [P, 2, GW])
        out = c.ps("out", [P, 2, GW])
        qk_ready, max_done, p_ready = c.sem("qk_ready"), c.sem("max_done"), c.sem("p_ready")
        share_done, v_ready, pv_done = c.sem("share_done"), c.sem("v_ready"), c.sem("pv_done")
        pj_ready, pj_done, out_done = c.sem("pj_ready"), c.sem("pj_done"), c.sem("out_done")
        outT_ready, fin_ready, padded = c.sem("outT_ready"), c.sem("fin_ready"), c.sem("padded")

        def over_heads(engine, part):
            part(0, 0, True, False)
            part(1, 1, False, False)
            with engine.Fori(1, HEADS // 2 - 1) as pair:
                for q in range(2):
                    part(pair * 2 + q, q, False, False)
            part(HEADS - 2, 0, False, False)
            part(HEADS - 1, 1, False, True)

        with nc.Block() as block:

            @block.gpsimd
            def _(pool):
                nc.gpsimd.memset(vs[:].rearrange("p r j v -> p (r j) v")[:, :, VD:VP], 0.0).then_inc(padded, 1)
                pool.wait_ge(padded, 1)

            @block.tensor
            def _(pe):
                pe.sem_inc(p_ready, 2)
                pe.sem_inc(pv_done, RING)
                pe.sem_inc(out_done, 2)
                pe.wait_ge(padded, 1)

                def project(n):
                    pe.wait_ge(pj_done, n * 4)
                    for m, w in enumerate((mk, mq)):
                        for jj in range(SL // 2):
                            ins = nc.tensor.matmul(pj[:, m, jj * P:(jj + 1) * P], w[:, jj * P:(jj + 1) * P],
                                                   keep.x_T[:, ds(n * P, P)], start=True, stop=True)
                    ins.then_inc(pj_ready, 1)

                def values(n, q, kt):
                    pe.wait_ge(v_ready, n * SL + (kt + 1))
                    if kt == 0:
                        pe.wait_ge(out_done, n + 1)
                    for j in range(SL):
                        g, half = j % 4, j // 4
                        ins = nc.tensor.matmul(out[g * VP:(g + 1) * VP, q, half * P:(half + 1) * P], vs[:, kt % RING, j],
                                               pT[:, kt % RING, j * P:(j + 1) * P], start=(kt == 0 and half == 0),
                                               stop=(kt == SL - 1), skip_group_check=True)
                    ins.then_inc(pv_done, 1)

                def turn(n, q):
                    pe.wait_ge(outT_ready, n + 1)
                    for half in range(2):
                        ins = nc.tensor.transpose(out[:, q, (2 + half) * P:(3 + half) * P], outT[:, q, half * P:(half + 1) * P],
                                                  keep.ident[:])
                    ins.then_inc(fin_ready, 1)

                def head(n, q, first, last):
                    pe.wait_ge(pj_done, n * 4 + 4)
                    for kt in range(SL):
                        pe.wait_ge(p_ready, n * SL + (kt + 1))
                        for o in range(Q // GW):
                            ins = nc.tensor.matmul(sc[:, kt % 2, o * GW:(o + 1) * GW], kT[:, q, kt * P:(kt + 1) * P],
                                                   qT[:, q, o * GW:(o + 1) * GW], start=True, stop=True)
                        ins.then_inc(qk_ready, 1)
                        if kt >= 2:
                            values(n, q, kt - 2)
                        elif not first:
                            values(n - 1, 1 - q, SL - 2 + kt)
                        if kt == 2 and not last:
                            project(n + 1)
                        if kt == 3 and not first:
                            turn(n - 1, 1 - q)

                project(0)
                over_heads(pe, head)
                values(HEADS - 1, 1, SL - 2)
                values(HEADS - 1, 1, SL - 1)
                turn(HEADS - 1, 1)

            @block.scalar
            def _(act):
                def evacuate(n, q):
                    act.wait_ge(pj_ready, n + 1)
                    for m, dst in enumerate((kT, qT)):
                        d4 = dst[:, q].rearrange("k (j two r) -> k j two r", two=2, r=P)
                        for par in range(2):
                            nc.scalar.copy(d4[:, :, par], pj[par * KS:(par + 1) * KS, m].rearrange("k (j r) -> k j r", r=P))\
                                .then_inc(pj_done, 1)

                def result(n, q):
                    act.wait_ge(pv_done, n * SL + (SL + RING))
                    nc.scalar.copy(outT[:, q], out[:, q, 0:2 * P]).then_inc(outT_ready, 1)

                def head(n, q, first, last):
                    for kt in range(SL):
                        i = n * SL + kt
                        act.wait_ge(max_done, i + 1)
                        act.wait_ge(pv_done, i + 1)
                        nc.scalar.activation(pT[:, kt % RING], sc[:, kt % 2], ACT.Exp, bias=negmax[:, kt % 2:kt % 2 + 1],
                                             accum_out=total[:, kt % RING:kt % RING + 1]).then_inc(p_ready, 1)
                        if kt == 2 and not first:
                            result(n - 1, 1 - q)
                        if kt == 4 and not last:
                            evacuate(n + 1, 1 - q)

                evacuate(0, 0)
                over_heads(act, head)
                result(HEADS - 1, 1)

            @block.vector
            def _(dve):
                def head(n, q, first, last):
                    for kt in range(SL):
                        dve.wait_ge(qk_ready, n * SL + (kt + 1))
                        nc.vector.tensor_reduce(negmax[:, kt % 2:kt % 2 + 1], sc[:, kt % 2], AX.X, ALU.max,
                                                negate=True).then_inc(max_done, 1)
                        if kt:
                            apply(n, kt - 1)
                        elif not first:
                            apply(n - 1, SL - 1)
                        if kt == 4 and not first:
                            take(n - 1, 1 - q)

                def apply(n, kt):
                    r = kt % RING
                    dve.wait_ge(p_ready, n * SL + (kt + 3))
                    nc.vector.reciprocal(share[:, r:r + 1], total[:, r:r + 1]).then_inc(share_done, 1)
                    dve.wait_ge(share_done, n * SL + (kt + 1))
                    v = xv3[:, ds(n // SL * SL, SL), kt * VD:(kt + 1) * VD]
                    nc.vector.tensor_scalar(vs[:, r, :, 0:VD], v, share[:, r:r + 1], None, ALU.mult).then_inc(v_ready, 1)

                def take(n, q):
                    dve.wait_ge(fin_ready, n + 1)
                    x = keep.x_tok[:, ds(n * D, D)].rearrange("p (j d) -> p j d", d=VD)
                    res = out[:, q, 2 * P:4 * P].rearrange("p (j d) -> p j d", d=VP)[:, :, 0:VD]
                    nc.vector.tensor_tensor(x, res, x, ALU.add).then_inc(out_done, 1)

                over_heads(dve, head)
                apply(HEADS - 1, SL - 1)
                take(HEADS - 1, 1)


def layer2_ffn(nc, keep, a):
    E, F = 8, 512
    nf = F // P
    with ExitStack() as st:
        c = Core(nc, st, "l2f")
        up, gate = c.sb("up", [P, E, F]), c.sb("gate", [P, E, F])
        down = c.sb("down", [P, E, nf, D])
        logits, probs, comb = c.sb("logits", [P, NT * 8]), c.sb("probs", [P, NT * 8]), c.sb("comb", [P, NT * 8])
        router(nc, keep, "l2f", logits, a["L2_ffn_router_w"], None,
               [(up[:, 0:E - 1], a["L2_ffn_up_w"].rearrange("e d f -> d e f")),
                (up[:, E - 1], a["L2_ffn_shared_up_w"]),
                (gate[:, 0:E - 1], a["L2_ffn_gate_w"].rearrange("e d f -> d e f")),
                (gate[:, E - 1], a["L2_ffn_shared_gate_w"]),
                (down[:, 0:E - 1], a["L2_ffn_down_w"].rearrange("e (k p) d -> p e k d", p=P)),
                (down[:, E - 1], a["L2_ffn_shared_down_w"].rearrange("(k p) d -> p k d", p=P))])
        softmax8(nc, keep, "l2f", logits, probs)
        pick_top(nc, keep, "l2f", probs, comb, 1, scale_top=2.0)
        experts(nc, keep, "l2f", comb, E, [P] * nf, lambda u, f: up[:, u, f * P:(f + 1) * P],
                lambda u, f: down[:, u, f], 1, ACT.Silu, gate=lambda u, f: gate[:, u, f * P:(f + 1) * P])


def layer3_attn(nc, keep, a):
    H2 = P // 2
    LV = int(math.log2(S))
    two_pi = 2 * math.pi
    C1 = float(np.float32(6.28125))
    C2 = float(np.float32(1.93500518798828125e-3))
    C3 = two_pi - C1 - C2
    MAGIC = 1.5 * 2 ** 23
    with ExitStack() as st:
        c = Core(nc, st, "l3a")
        par = c.sb("par", [P, 3])
        b_ri = c.sb("b_ri", [P, 2, D])
        c_ri = c.sb("c_ri", [P, 2, D])
        dvec = c.sb("dvec", [P, D])
        cosT, sinT = c.sb("cosT", [P, S]), c.sb("sinT", [P, S])
        w12 = c.sb("w12", [P, 2, D])
        v12 = c.sb("v12", [P, 2, D])
        mag = c.sb("mag", [P, 1])
        with ExitStack() as st2:
            c2 = Core(nc, st2, "l3b")
            col = {}
            for name in ("step x y t q em1 g2 re im den gr gi al1 be1 al2 be2 u1 u2 sgn").split():
                col[name] = c2.sb("v_" + name, [P, 1])
            pw, ang, kk = c2.sb("pw", [P, LV]), c2.sb("ang", [P, LV]), c2.sb("kk", [P, LV])
            half, habs = c2.sb("half", [P, LV]), c2.sb("habs", [P, LV])
            sh, chh = c2.sb("sh", [P, LV]), c2.sb("chh", [P, LV])
            cs_, sn_ = c2.sb("cs_", [P, LV]), c2.sb("sn_", [P, LV])
            tmp = c2.sb("tmp", [P, S // 2])
            wrow = c2.sb("wrow", [P, 2, D])
            half_pi = c2.sb("half_pi", [P, 1])
            wT = c2.ps("wT", [P, 2, 512])
            loaded, chain_sem, to_act, from_act = c2.sem("loaded"), c2.sem("chain"), c2.sem("to_act"), c2.sem("from_act")
            rows_ready, turned = c2.sem("rows_ready"), c2.sem("turned")
            v = {k: t[:] for k, t in col.items()}
            with nc.Block() as block:

                @block.sync
                def _(sp):
                    for dst, src in [(par[:], a["L3_attn_par"]), (b_ri[:], a["L3_attn_B_ri"]), (c_ri[:], a["L3_attn_C_ri"]),
                                     (dvec[:], a["L3_attn_D"].rearrange("(o d) -> o d", o=1).broadcast_to([P, D]))]:
                        sp.dma_start(dst, src).then_inc(loaded, 16)
                    sp.wait_ge(loaded, 64)

                @block.scalar
                def _(act):
                    act.wait_ge(loaded, 64)
                    nc.scalar.activation(v["step"], par[:, 2:3], ACT.Exp).then_inc(from_act, 1)
                    act.wait_ge(to_act, 1)
                    nc.scalar.activation(v["t"], v["x"], ACT.Tanh, scale=0.5).then_inc(from_act, 1)
                    act.wait_ge(to_act, 2)
                    nc.scalar.activation(sh[:], half[:], ACT.Sin).then_inc(from_act, 1)
                    nc.scalar.activation(chh[:], habs[:], ACT.Sin).then_inc(from_act, 1)

                @block.tensor
                def _(pe):
                    pe.wait_ge(rows_ready, 1)
                    nc.tensor.transpose(wT[:, 0, 0:D], wrow[:, 0], keep.ident[:])
                    nc.tensor.transpose(wT[:, 1, 0:D], wrow[:, 1], keep.ident[:]).then_inc(turned, 1)

                @block.vector
                def _(dve):
                    ch = Chain(dve, chain_sem)
                    tt = lambda o, x, y_, op: ch.step(nc.vector.tensor_tensor(o, x, y_, op))
                    t1 = lambda o, x, s1, op, s2=None, op1=ALU.bypass: ch.step(nc.vector.tensor_scalar(o, x, s1, s2, op, op1))
                    M, A_, S_ = ALU.mult, ALU.add, ALU.subtract
                    for k in range(LV):
                        ch.step(nc.vector.memset(pw[:, k:k + 1], float(2 ** k)))
                    ch.step(nc.vector.memset(v["sgn"][0:H2], 1.0))
                    ch.step(nc.vector.memset(v["sgn"][H2:P], -1.0))
                    dve.wait_ge(from_act, 1)
                    t1(v["q"], par[:, 0:1], -1e-4, ALU.min)
                    tt(v["y"], par[:, 1:2], v["step"], M)
                    nc.vector.tensor_tensor(v["x"], v["q"], v["step"], M).then_inc(to_act, 1)
                    t1(ang[:], pw[:], v["y"], M)
                    t1(kk[:], ang[:], 1.0 / two_pi, M, MAGIC, A_)
                    t1(kk[:], kk[:], MAGIC, S_)
                    for part in (C1, C2, C3):
                        ch.step(nc.vector.scalar_tensor_tensor(out=ang[:], in0=kk[:], scalar=-part, in1=ang[:], op0=M, op1=A_))
                    t1(half[:], ang[:], 0.5, M, math.pi / 2, ALU.min)
                    t1(half[:], half[:], -math.pi / 2, ALU.max)
                    ch.step(nc.vector.scalar_tensor_tensor(out=habs[:], in0=half[:], scalar=-1.0, in1=half[:], op0=M, op1=ALU.min))
                    nc.vector.tensor_scalar(habs[:], habs[:], math.pi / 2, None, A_).then_inc(to_act, 1)
                    dve.wait_ge(from_act, 2)
                    t1(v["em1"], v["t"], -1.0, M, 1.0, A_)
                    ch.step(nc.vector.reciprocal(v["em1"], v["em1"]))
                    tt(v["em1"], v["em1"], v["t"], M)
                    t1(v["em1"], v["em1"], 2.0, M)
                    t1(mag[:], v["em1"], 1.0, A_)
                    dve.wait_ge(from_act, 4)
                    tt(kk[:], sh[:], sh[:], M)
                    t1(cs_[:], kk[:], -2.0, M, 1.0, A_)
                    ch.step(nc.vector.scalar_tensor_tensor(out=sn_[:], in0=sh[:], scalar=2.0, in1=chh[:], op0=M, op1=M))
                    tt(v["re"], v["em1"], cs_[:, 0:1], M)
                    ch.step(nc.vector.scalar_tensor_tensor(out=v["re"], in0=kk[:, 0:1], scalar=-2.0, in1=v["re"], op0=M, op1=A_))
                    tt(v["im"], mag[:], sn_[:, 0:1], M)
                    lre, lim = v["q"], par[:, 1:2]
                    tt(v["den"], lre, lre, M)
                    ch.step(nc.vector.scalar_tensor_tensor(out=v["den"], in0=lim, scalar=lim, in1=v["den"], op0=M, op1=A_))
                    ch.step(nc.vector.reciprocal(v["den"], v["den"]))
                    tt(v["u1"], v["im"], lim, M)
                    ch.step(nc.vector.scalar_tensor_tensor(out=v["gr"], in0=v["re"], scalar=lre, in1=v["u1"], op0=M, op1=A_))
                    tt(v["gr"], v["gr"], v["den"], M)
                    tt(v["u2"], v["re"], lim, M)
                    ch.step(nc.vector.scalar_tensor_tensor(out=v["gi"], in0=v["im"], scalar=lre, in1=v["u2"], op0=M, op1=S_))
                    tt(v["gi"], v["gi"], v["den"], M)
                    lo, hi = slice(0, H2), slice(H2, P)
                    for dst, half_, src, sign in (("al1", lo, "gr", 1.0), ("be1", lo, "gi", -1.0), ("al1", hi, "gi", 1.0), ("be1", hi, "gr", 1.0),
                                                  ("al2", lo, "gi", 1.0), ("be2", lo, "gr", 1.0), ("al2", hi, "gr", -1.0), ("be2", hi, "gi", 1.0)):
                        t1(v[dst][half_], v[src][half_], sign, M)
                    for n, (al, be) in enumerate((("al1", "be1"), ("al2", "be2"))):
                        t1(wrow[:, n], b_ri[:, 0], v[al], M)
                        ins = nc.vector.scalar_tensor_tensor(out=wrow[:, n], in0=b_ri[:, 1], scalar=v[be], in1=wrow[:, n], op0=M, op1=A_)
                        ch.step(ins)
                    dve.sem_inc(rows_ready, 1)
                    t1(v12[:, 0], c_ri[:, 0], v["sgn"], M)
                    t1(v12[:, 1], c_ri[:, 1], -1.0, M)
                    t1(dvec[:], dvec[:], 1.0, A_)
                    ch.step(nc.vector.memset(cosT[:, 0:1], 1.0))
                    ch.step(nc.vector.memset(sinT[:, 0:1], 0.0))
                    for k in range(LV):
                        w = 2 ** k
                        ck_, sk_ = cs_[:, k:k + 1], sn_[:, k:k + 1]
                        t1(tmp[:, 0:w], sinT[:, 0:w], sk_, M)
                        ch.step(nc.vector.scalar_tensor_tensor(out=cosT[:, w:2 * w], in0=cosT[:, 0:w], scalar=ck_, in1=tmp[:, 0:w], op0=M, op1=S_))
                        t1(tmp[:, 0:w], cosT[:, 0:w], sk_, M)
                        ch.step(nc.vector.scalar_tensor_tensor(out=sinT[:, w:2 * w], in0=sinT[:, 0:w], scalar=ck_, in1=tmp[:, 0:w], op0=M, op1=A_))
                    dve.wait_ge(turned, 1)
                    ch.step(nc.vector.tensor_copy(w12[:], wT[:, :, 0:D]))

        with ExitStack() as st2:
            c2 = Core(nc, st2, "l3c")
            uc, us = c2.sb("uc", [P, 2, GW]), c2.sb("us", [P, 2, GW])
            z, z1, z2 = c2.sb("z", [P, 2, GW]), c2.sb("z1", [P, 2, GW]), c2.sb("z2", [P, 2, GW])
            u = c2.ps("u", [P, 2, 2, GW])
            y = c2.ps("y", [P, 2, GW])
            u_ready, u_turned, summed = c2.sem("u_ready"), c2.sem("u_turned"), c2.sem("summed")
            scanned, back, y_ready, added, skipped = (c2.sem("scanned"), c2.sem("back"), c2.sem("y_ready"), c2.sem("added"), c2.sem("skipped"))
            K2 = range(2)
            with nc.Block() as block:

                @block.tensor
                def _(pe):
                    pe.sem_inc(u_turned, 2)
                    pe.sem_inc(added, 2)
                    pe.sem_inc(y_ready, 2)
                    with pe.Fori(0, B) as b:
                        for k in K2:
                            pe.wait_ge(u_turned, b * 2 + (k + 1))
                            x = keep.x_T[:, ds((b * 2 + k) * GW, GW)]
                            nc.tensor.matmul(u[:, k, 0], w12[:, 0], x, start=True, stop=True)
                            nc.tensor.matmul(u[:, k, 1], w12[:, 1], x, start=True, stop=True).then_inc(u_ready, 1)
                        for k in K2:
                            pe.wait_ge(back, (b * 2 + k) * 2 + 2)
                            pe.wait_ge(added, b * 2 + (k + 1))
                            for j in range(TG):
                                o = slice(j * P, (j + 1) * P)
                                nc.tensor.matmul(y[:, k, o], z1[:, k, o], v12[:, 0], start=True, stop=False)
                                ins = nc.tensor.matmul(y[:, k, o], z2[:, k, o], v12[:, 1], start=False, stop=True)
                            ins.then_inc(y_ready, 1)

                @block.gpsimd
                def _(pool):
                    with pool.Fori(0, B) as b:
                        for k in K2:
                            pool.wait_ge(u_turned, b * 2 + (k + 3))
                            nc.gpsimd.tensor_tensor(uc[:, k], uc[:, k], us[:, k], ALU.add).then_inc(summed, 1)
                        for k in K2:
                            x3 = keep.x_tok[:, ds((b * 2 + k) * GW, GW)].rearrange("p (t d) -> p t d", d=D)
                            nc.gpsimd.tensor_tensor(x3, x3, dvec[:].unsqueeze(1).to_broadcast([P, TG, D]), ALU.mult).then_inc(skipped, 1)
                        for k in K2:
                            o = slice(k * GW, (k + 1) * GW)
                            pool.wait_ge(scanned, b * 2 + (k + 1))
                            pool.wait_ge(y_ready, b * 2 + (k + 1))
                            nc.gpsimd.tensor_tensor(z1[:, k], z[:, k], cosT[:, o], ALU.mult).then_inc(back, 1)
                            nc.gpsimd.tensor_tensor(z2[:, k], z[:, k], sinT[:, o], ALU.mult).then_inc(back, 1)

                @block.vector
                def _(dve):
                    with dve.Fori(0, B) as b:
                        for k in K2:
                            o = slice(k * GW, (k + 1) * GW)
                            dve.wait_ge(u_ready, b * 2 + (k + 1))
                            nc.vector.tensor_tensor(uc[:, k], u[:, k, 0], cosT[:, o], ALU.mult)
                            nc.vector.tensor_tensor(us[:, k], u[:, k, 1], sinT[:, o], ALU.mult).then_inc(u_turned, 1)
                        for k in K2:
                            dve.wait_ge(summed, b * 2 + (k + 1))
                            if k:
                                dve.wait_ge(scanned, b * 2 + k)
                            nc.vector.tensor_tensor_scan(z[:, k], mag[:].to_broadcast([P, GW]), uc[:, k],
                                                         z[:, 0, GW - 1:GW] if k else 0.0, ALU.mult, ALU.add).then_inc(scanned, 1)
                        for k in K2:
                            x = keep.x_tok[:, ds((b * 2 + k) * GW, GW)]
                            dve.wait_ge(y_ready, b * 2 + (k + 3))
                            dve.wait_ge(skipped, b * 2 + (k + 1))
                            nc.vector.tensor_tensor(x, y[:, k], x, ALU.add).then_inc(added, 1)


def top_tokens(nc, keep, tag, probs, comb, count):
    Q = 16
    W = N // Q
    TP = NT // Q
    BITS = 30
    with ExitStack() as st:
        c = Core(nc, st, tag + "tt")
        val = c.sb("val", [P, W])
        ge, eq, before = c.sb("ge", [P, W]), c.sb("eq", [P, W]), c.sb("before", [P, W])
        cnt, carry = c.sb("cnt", [P, 2]), c.sb("carry", [P, 2])
        cut, trial = c.sb("cut", [P, 1], mybir.dt.int32), c.sb("trial", [P, 1], mybir.dt.int32)
        keepbit, room = c.sb("keepbit", [P, 1], mybir.dt.int32), c.sb("room", [P, 1])
        flag = c.sb("flag", [P, 1])
        same, prior = c.sb("same", [P, P]), c.sb("prior", [P, P])
        tmp = c.sb("tmp", [P, P])
        zeros = c.sb("zeros", [P, W])
        spread = c.sb("spread", [P, 8, NT])
        turned = c.ps("turned", [P, 8, 512])
        sums = turned[:, 6]
        chain_sem, pool_sem, masks = c.sem("chain"), c.sem("pool_sem"), c.sem("masks")
        flips, counted, moved = c.sem("flips"), c.sem("counted"), c.sem("moved")
        asked, cast = c.sem("asked"), c.sem("cast")
        with nc.Block() as block:

            @block.gpsimd
            def _(pool):
                ch = Chain(pool, pool_sem)
                ch.step(nc.gpsimd.memset(same[:], 1.0))
                s3 = same[:].rearrange("p (e q) -> p e q", q=Q)
                ch.step(nc.gpsimd.affine_select(out=s3, in_=s3, compare_op=ALU.is_ge, fill=0.0, base=0,
                                                pattern=[[-Q, 8], [0, Q]], channel_multiplier=1))
                ch.step(nc.gpsimd.affine_select(out=s3, in_=s3, compare_op=ALU.is_ge, fill=0.0, base=Q - 1,
                                                pattern=[[Q, 8], [0, Q]], channel_multiplier=-1))
                ch.step(nc.gpsimd.affine_select(out=prior[:], in_=same[:], compare_op=ALU.is_gt, fill=0.0, base=0,
                                                pattern=[[1, P]], channel_multiplier=-1))
                nc.gpsimd.memset(zeros[:], 0.0).then_inc(masks, 1)
                pool.wait_ge(masks, 1)

            p3 = probs[:].rearrange("p (t e) -> p t e", e=8)
            @block.vector
            def _(dve):
                ch = Chain(dve, chain_sem)
                s4 = spread[:].rearrange("p e (q r) -> p r e q", r=TP)
                for r in range(TP):
                    ch.step(nc.vector.tensor_copy(spread[:].rearrange("p (r a) t -> p r (a t)", r=TP)[:, r].rearrange(
                        "p (e q) -> p e q", q=Q), p3.rearrange("p (q r) e -> p r e q", r=TP)[:, r]))
                nc.vector.memset(cut[:], 0).then_inc(asked, 1)
                dve.wait_ge(flips, 1)
                for r in range(TP):
                    ins = nc.vector.tensor_copy(val[:, r * P:(r + 1) * P], turned[:, r, 0:P])
                ch.step(ins)
                dve.wait_ge(masks, 1)
                n = [0]

                def count_from(bits, op, out_tile):
                    ch.step(nc.vector.tensor_scalar(out_tile[:], val[:], bits.bitcast(F32), None, op, ALU.add,
                                                    accum_out=cnt[:, 0:1]))
                    n[0] += 1
                    dve.sem_inc(asked, 1)
                    dve.wait_ge(counted, n[0])

                for bit in reversed(range(BITS)):
                    ch.step(nc.vector.tensor_scalar(trial[:], cut[:], 1 << bit, None, ALU.bitwise_or))
                    count_from(trial[:], ALU.is_ge, ge)
                    ch.step(nc.vector.tensor_scalar(flag[:], sums[:, 0:1], float(count), None, ALU.is_ge))
                    ch.step(nc.vector.tensor_copy(keepbit[:], flag[:]))
                    ch.step(nc.vector.tensor_scalar(keepbit[:], keepbit[:], bit, None, ALU.logical_shift_left))
                    ch.step(nc.vector.tensor_tensor(cut[:], cut[:], keepbit[:], ALU.bitwise_or))
                count_from(cut[:], ALU.is_gt, ge)
                ch.step(nc.vector.tensor_scalar(room[:], sums[:, 0:1], -1.0, float(count), ALU.mult, ALU.add))
                ch.step(nc.vector.tensor_scalar(eq[:], val[:], cut[:].bitcast(F32), None, ALU.is_equal, ALU.add,
                                                accum_out=cnt[:, 0:1]))
                n[0] += 1
                dve.sem_inc(asked, 1)
                dve.wait_ge(counted, n[0])
                ch.step(nc.vector.tensor_copy(carry[:, 0:1], sums[:, 1:2]))
                ch.step(nc.vector.tensor_tensor_scan(before[:], eq[:], zeros[:], carry[:, 0:1], ALU.add, ALU.add))
                ch.step(nc.vector.tensor_scalar(before[:], before[:], room[:], None, ALU.is_le))
                ch.step(nc.vector.tensor_tensor(eq[:], eq[:], before[:], ALU.mult))
                ch.step(nc.vector.tensor_tensor(ge[:], ge[:], eq[:], ALU.add))
                nc.vector.tensor_tensor(val[:], val[:], ge[:], ALU.mult).then_inc(moved, 1)
                dve.wait_ge(flips, 2)
                for r in range(TP):
                    ch.step(nc.vector.tensor_copy(
                        comb[:].rearrange("p (q r e) -> p r e q", r=TP, e=8)[:, r],
                        turned[:, 2 + r, 0:P].rearrange("p (e q) -> p e q", q=Q)))

            @block.tensor
            def _(pe):
                pe.wait_ge(asked, 1)
                pe.wait_ge(chain_sem, TP)
                for r in range(TP):
                    ins = nc.tensor.transpose(turned[:, r, 0:P], spread[:].rearrange("p (r a) t -> p r (a t)", r=TP)[:, r],
                                              keep.ident[:])
                ins.then_inc(flips, 1)
                pe.wait_ge(masks, 1)
                for i in range(BITS + 2):
                    pe.wait_ge(asked, i + 2)
                    nc.tensor.matmul(sums[:, 0:1], same[:], cnt[:, 0:1], start=True, stop=True)
                    nc.tensor.matmul(sums[:, 1:2], prior[:], cnt[:, 0:1], start=True, stop=True).then_inc(counted, 1)
                pe.wait_ge(moved, 1)
                for r in range(TP):
                    ins = nc.tensor.transpose(turned[:, 2 + r, 0:P], val[:, r * P:(r + 1) * P], keep.ident[:])
                ins.then_inc(flips, 1)


def layer3_ffn(nc, keep, a):
    E, F, pairs = 8, 341, 4
    rows = [P, P, F - 2 * P]
    with ExitStack() as st:
        c = Core(nc, st, "l3f")
        up = c.sb("up", [P, pairs, F])
        b_up = c.sb("b_up", [P, pairs, 3])
        down = c.sb("down", [P, pairs, 3, 2, D])
        logits, probs, comb = c.sb("logits", [P, NT * 8]), c.sb("probs", [P, NT * 8]), c.sb("comb", [P, NT * 8])
        wd = a["L3_ffn_W_down"]
        loads = [(up[:], a["L3_ffn_W_up"].rearrange("g h f -> h g f")),
                 (b_up[:].rearrange("p g k -> p (g k)"), a["L3_ffn_b_up_cols"])]
        for f, r in enumerate(rows):
            for g in range(pairs):
                loads.append((down[0:r, g, f], wd[2 * g:2 * g + 2, f * P:f * P + r, :].rearrange("e p h -> p e h")))
        for g in range(pairs):
            loads.append((down[rows[2]:rows[2] + 1, g, 2],
                          a["L3_ffn_b_down"][2 * g:2 * g + 2].rearrange("(o e) h -> o e h", o=1)))
        router(nc, keep, "l3f", logits, a["L3_ffn_Wr"], a["L3_ffn_br"].rearrange("(o e) -> o e", o=1), loads)
        softmax8(nc, keep, "l3f", logits, probs)
        top_tokens(nc, keep, "l3f", probs, comb, N // E)
        heights = [P, P, rows[2] + 1]
        experts(nc, keep, "l3f", comb, pairs, rows, lambda u, f: up[:, u, f * P:f * P + rows[f]],
                lambda u, f: down[0:heights[f], u, f], 2, ACT.Silu, bias=lambda u, f: b_up[0:rows[f], u, f:f + 1])


def laid_out(inputs):
    out = {k: np.ascontiguousarray(v) for k, v in inputs.items()}
    b_up = out.pop("L3_ffn_b_up")
    cols = np.zeros((b_up.shape[0], 3 * P), b_up.dtype)
    cols[:, :b_up.shape[1]] = b_up
    out["L3_ffn_b_up_cols"] = np.ascontiguousarray(cols.reshape(-1, P).T)
    out["L1_attn_norm_scale_col"] = out.pop("L1_attn_norm_scale").reshape(P, 1)
    conv_w = out.pop("L1_attn_conv_weight")
    out["L1_attn_conv_w_cols"] = np.ascontiguousarray(conv_w.reshape(-1, 2, P).transpose(2, 1, 0).reshape(P, -1))
    out["L1_attn_conv_b_cols"] = np.ascontiguousarray(out.pop("L1_attn_conv_bias").reshape(2, P).T)
    par = np.stack([out.pop("L3_attn_Lambda_re"), out.pop("L3_attn_Lambda_im"), out.pop("L3_attn_log_step")[:, 0]], 1)
    out["L3_attn_par"] = np.concatenate([par, par])
    b_ri = out.pop("L3_attn_B").transpose(0, 2, 1)
    out["L3_attn_B_ri"] = np.concatenate([b_ri, b_ri])
    c_ri = out.pop("L3_attn_C").transpose(1, 2, 0)
    out["L3_attn_C_ri"] = np.concatenate([c_ri, c_ri[:, ::-1]])
    for n in ("q", "k", "v", "o"):
        out[f"L0_attn_W{n}T"] = np.ascontiguousarray(out.pop(f"L0_attn_W{n}").T)
    out["L0_attn_bqk_cols"] = np.ascontiguousarray(np.stack([out.pop("L0_attn_bq"), out.pop("L0_attn_bk")], 1))
    freq = np.exp(np.arange(0, D, 2, dtype=np.float32) * np.float32(-np.log(10000.0) / D))
    angle = np.arange(S, dtype=np.float32)[:, None] * freq[None, :]
    for name, f in (("rope_cos", np.cos), ("rope_sin", np.sin)):
        table = f(angle).astype(np.float32).reshape(S // P, P, D // 2)
        out[name] = np.ascontiguousarray(table.transpose(1, 0, 2).reshape(P, -1))
    cols = [out.pop("L1_ffn_" + n) for n in ("d_bq", "d_bk", "d_bo", "c_bq", "c_bk", "c_bv")]
    out["L1_ffn_bias_cols"] = np.ascontiguousarray(np.stack(cols + [np.zeros_like(cols[0])] * 2, 1))
    out["L1_ffn_slot_T"] = np.ascontiguousarray(out.pop("L1_ffn_slot_query")[0].T)
    for n in ("b1", "bg"):
        b = out.pop("L1_ffn_e_" + n)
        out[f"L1_ffn_{n}_cols"] = np.ascontiguousarray(b.reshape(b.shape[0], -1, P).transpose(2, 0, 1).reshape(P, -1))
    out["L1_ffn_b2_T"] = np.ascontiguousarray(out.pop("L1_ffn_e_b2").T)
    return out


class Keep:

    def __init__(self, nc, stack):
        sb = lambda name, shape: stack.enter_context(nc.sbuf_tensor(name, shape, F32))
        self.x_tok = sb("x_tok", [P, N])
        self.x_T = sb("x_T", [P, N])
        self.ident = sb("ident", [P, P])
        self.upto = sb("upto", [P, P])
        self.ones = sb("ones", [P, GW])
        self.eps, self.rms_eps = sb("eps", [P, 1]), sb("rms_eps", [P, 1])


def sequence_kernel(nc, a, out):
    with ExitStack() as st:
        keep = Keep(nc, st)
        moved = st.enter_context(nc.semaphore("moved"))
        tiles = lambda x: x.rearrange("(t p) d -> p t d", p=P)
        x3 = keep.x_tok[:].rearrange("p (t d) -> p t d", d=D)
        with nc.Block() as block:

            @block.sync
            def _(sp):
                sp.dma_start(x3, tiles(a["L0_attn_x"])).then_inc(moved, 16)
                sp.wait_ge(moved, 16)

        constants(nc, keep)
        layers = (layer0_attn, layer0_ffn, layer1_attn, layer1_ffn, layer2_attn, layer2_ffn, layer3_attn, layer3_ffn)
        for n, layer in enumerate(layers):
            with nc.cleanup_on_exit():
                layer(nc, keep, a)
                layernorm(nc, keep, f"n{n}", want_T=n < len(layers) - 1)
        with nc.Block() as block:

            @block.sync
            def _(sp):
                sp.dma_start(tiles(out), x3).then_inc(moved, 16)
                sp.wait_ge(moved, 32)


def kernel(**inputs):
    import concourse.bacc as bacc
    from concourse.bass_utils import run_bass_kernel_spmd

    arrays = laid_out({k: np.asarray(v) for k, v in inputs.items()})
    arrays["L0_attn_x"] = arrays["L0_attn_x"].reshape(N, D)
    nc = bacc.Bacc("TRN2", target_bir_lowering=False, num_devices=1)
    a = {k: nc.dram_tensor(f"in_{k}", v.shape, mybir.dt.from_np(v.dtype), kind="ExternalInput").ap() for k, v in arrays.items()}
    out = nc.dram_tensor("out", (N, D), F32, kind="ExternalOutput").ap()
    sequence_kernel(nc, a, out)
    result = run_bass_kernel_spmd(nc, [{f"in_{k}": v for k, v in arrays.items()}], core_ids=[0])
    return result.results[0]["out"].reshape(B, S, D)
```

```python
import math
from contextlib import ExitStack

import numpy as np

import concourse.bass as bass
from concourse import mybir
from concourse.bass import ds

F32 = mybir.dt.float32
BF16 = mybir.dt.bfloat16
ACT = mybir.ActivationFunctionType
ALU = mybir.AluOpType
AX = mybir.AxisListType

P = 128
D = 128
B, S = 4, 1024
N = B * S
NT = N // P
GW = 512
NG = N // GW
TG = GW // P
RMS_EPS = 1e-6
EPS = 1e-5


class Core:

    def __init__(self, nc, stack, tag):
        self.nc, self.stack, self.tag = nc, stack, tag

    def sb(self, name, shape, dt=F32):
        return self.stack.enter_context(self.nc.sbuf_tensor(f"{self.tag}_{name}", shape, dt))

    def ps(self, name, shape, dt=F32):
        return self.stack.enter_context(self.nc.psum_tensor(f"{self.tag}_{name}", shape, dt))

    def sem(self, name):
        return self.nc.alloc_semaphore(name=f"{self.tag}_{name}")


class Chain:

    def __init__(self, engine, sem):
        self.engine, self.sem, self.count = engine, sem, 0

    def step(self, instruction):
        self.count += 1
        instruction.then_inc(self.sem, 1)
        self.engine.wait_ge(self.sem, self.count)


def constants(nc, keep):
    with ExitStack() as st:
        c = Core(nc, st, "const")
        zeroed, done = c.sem("zeroed"), c.sem("done")
        with nc.Block() as block:

            @block.gpsimd
            def _(pool):
                nc.gpsimd.memset(keep.ident[:], 0.0).then_inc(zeroed, 1)
                nc.gpsimd.memset(keep.ones[:], 1.0).then_inc(done, 1)
                nc.gpsimd.memset(keep.eps[:], EPS).then_inc(done, 1)
                nc.gpsimd.memset(keep.rms_eps[:], RMS_EPS).then_inc(done, 1)
                pool.wait_ge(zeroed, 1)
                nc.gpsimd.affine_select(out=keep.ident[:], in_=keep.ident[:], compare_op=ALU.not_equal, fill=1.0,
                                        base=0, pattern=[[-1, P]], channel_multiplier=1).then_inc(done, 1)
                pool.wait_ge(done, 3)
                nc.gpsimd.affine_select(out=keep.upto[:], in_=keep.ones[:, 0:P], compare_op=ALU.is_ge, fill=0.0,
                                        base=0, pattern=[[1, P]], channel_multiplier=-1).then_inc(done, 1)
                pool.wait_ge(done, 5)


def layernorm(nc, keep, tag, want_T=True, rms_T=None):
    x_tok, x_T = keep.x_tok, keep.x_T if rms_T is None else rms_T
    with ExitStack() as st:
        c = Core(nc, st, tag + "ln")
        stats = c.sb("stats", [P, NT * 6])
        mean, var = c.sb("mean", [P, NT]), c.sb("var", [P, NT])
        dm, std = c.sb("dm", [P, NT]), c.sb("std", [P, NT])
        rstd, shift = c.sb("rstd", [P, NT]), c.sb("shift", [P, NT])
        RING = 4
        staged = c.sb("staged", [P, RING, GW])
        flipped = c.ps("flipped", [P, RING, GW])
        stats_done, chain_sem = c.sem("stats_done"), c.sem("chain")
        var_ready, std_ready, norm_ready = c.sem("var_ready"), c.sem("std_ready"), c.sem("norm_ready")
        by_dve, by_act, copied = c.sem("by_dve"), c.sem("by_act"), c.sem("copied")
        flip_ready, flip_free = c.sem("flip_ready"), c.sem("flip_free")
        s3 = stats[:].rearrange("p (t k) -> p t k", k=6)

        def free_place(engine, i, k):
            if rms_T is None:
                engine.wait_ge(copied, i * RING + (k + 1))
            if want_T:
                engine.wait_ge(flip_ready, i * RING + (k + 1))

        with nc.Block() as block:

            @block.vector
            def _(dve):
                with dve.Fori(0, NT // 8) as t8:
                    for t in range(8):
                        ins = nc.vector.bn_stats(stats[:, ds(t8 * 48 + t * 6, 6)], x_tok[:, ds(t8 * (8 * D) + t * D, D)])
                    ins.then_inc(stats_done, 1)
                dve.wait_ge(stats_done, NT // 8)
                ch = Chain(dve, chain_sem)
                nc.vector.tensor_tensor(mean[:], s3[:, :, 1], s3[:, :, 4], ALU.add).then_inc(chain_sem, 1)
                ch.count += 1
                ch.step(nc.vector.tensor_tensor(dm[:], s3[:, :, 1], s3[:, :, 4], ALU.subtract))
                nc.vector.tensor_tensor(var[:], s3[:, :, 2], s3[:, :, 5], ALU.add).then_inc(chain_sem, 1)
                ch.count += 1
                ch.step(nc.vector.scalar_tensor_tensor(out=dm[:], in0=dm[:], scalar=0.25, in1=dm[:],
                                                       op0=ALU.mult, op1=ALU.mult))
                ch.step(nc.vector.scalar_tensor_tensor(out=var[:], in0=var[:], scalar=1.0 / D, in1=dm[:],
                                                       op0=ALU.mult, op1=ALU.add))
                if rms_T is None:
                    nc.vector.tensor_copy(dm[:], var[:]).then_inc(var_ready, 1)
                else:
                    ch.step(nc.vector.scalar_tensor_tensor(out=dm[:], in0=mean[:], scalar=0.25, in1=mean[:],
                                                           op0=ALU.mult, op1=ALU.mult))
                    nc.vector.tensor_tensor(dm[:], dm[:], var[:], ALU.add).then_inc(var_ready, 1)
                dve.wait_ge(std_ready, 1)
                ch.step(nc.vector.reciprocal(rstd[:], std[:]))
                nc.vector.scalar_tensor_tensor(out=shift[:], in0=mean[:], scalar=-0.5 if rms_T is None else 0.0, in1=rstd[:],
                                               op0=ALU.mult, op1=ALU.mult).then_inc(norm_ready, 1)
                dve.wait_ge(norm_ready, 1)
                with dve.Fori(0, NG // RING) as i:
                    for k in (0, 2):
                        free_place(dve, i, k)
                        for j in range(TG):
                            t = (i * RING + k) * TG + j
                            ins = nc.vector.tensor_scalar(staged[:, k, j * D:(j + 1) * D], x_tok[:, ds(t * D, D)],
                                                          rstd[:, ds(t, 1)], shift[:, ds(t, 1)], ALU.mult, ALU.add)
                        ins.then_inc(by_dve, 1)
                    if rms_T is None:
                        for k in range(RING):
                            dve.wait_ge((by_dve, by_act)[k % 2], i * 2 + (k // 2 + 1))
                            nc.vector.tensor_copy(x_tok[:, ds((i * RING + k) * GW, GW)], staged[:, k]).then_inc(copied, 1)

            @block.scalar
            def _(act):
                act.wait_ge(var_ready, 1)
                nc.scalar.activation(std[:], dm[:], ACT.Sqrt, bias=(keep.eps if rms_T is None else keep.rms_eps)[:]).then_inc(std_ready, 1)
                act.wait_ge(norm_ready, 1)

                def norm(i, k):
                    free_place(act, i, k)
                    for j in range(TG):
                        t = (i * RING + k) * TG + j
                        ins = nc.scalar.activation(staged[:, k, j * D:(j + 1) * D], x_tok[:, ds(t * D, D)], ACT.Identity,
                                                   bias=shift[:, ds(t, 1)], scale=rstd[:, ds(t, 1)])
                    ins.then_inc(by_act, 1)

                def take(i, k):
                    act.wait_ge(flip_ready, i * RING + (k + 1 + RING))
                    nc.scalar.copy(x_T[:, ds((i * RING + k) * GW, GW)], flipped[:, k]).then_inc(flip_free, 1)

                with act.Fori(0, NG // RING) as i:
                    norm(i, 1)
                    if want_T:
                        take(i, 0)
                    norm(i, 3)
                    if want_T:
                        for k in range(1, RING):
                            take(i, k)

            @block.tensor
            def _(pe):
                pe.sem_inc(copied, RING)
                if want_T:
                    pe.sem_inc(flip_free, RING)
                    pe.sem_inc(flip_ready, RING)
                    with pe.Fori(0, NG // RING) as i:
                        for k in range(RING):
                            pe.wait_ge((by_dve, by_act)[k % 2], i * 2 + (k // 2 + 1))
                            pe.wait_ge(flip_free, i * RING + (k + 1))
                            for j in range(TG):
                                ins = nc.tensor.transpose(flipped[:, k, j * D:(j + 1) * D],
                                                          staged[:, k, j * D:(j + 1) * D], keep.ident[:])
                            ins.then_inc(flip_ready, 1)


def router(nc, keep, tag, logits, w_dram, bias_dram, loads, weights_in):
    CT, E = 32, 8
    HALVES = NG // 4
    with ExitStack() as st:
        c = Core(nc, st, tag + "rt")
        w, b = c.sb("w", [P, CT]), c.sb("b", [1, CT])
        byexp = c.sb("byexp", [P, HALVES, GW])
        acc = c.ps("acc", [P, HALVES, GW])
        flipped = c.ps("flipped", [P, HALVES, GW])
        padded, w_loaded, acc_ready, copied = c.sem("padded"), c.sem("w_loaded"), c.sem("acc_ready"), c.sem("copied")
        flip_ready, logit_done = c.sem("flip_ready"), c.sem("logit_done")
        with nc.Block() as block:

            @block.sync
            def _(sp):
                sp.wait_ge(padded, 2)
                sp.dma_start(w[:, 0:E], w_dram).then_inc(w_loaded, 16)
                if bias_dram is not None:
                    sp.dma_start(b[:, 0:E], bias_dram).then_inc(w_loaded, 16)
                for dst, src in loads:
                    sp.dma_start(dst, src).then_inc(weights_in, 16)

            @block.tensor
            def _(pe):
                pe.wait_ge(w_loaded, 16 if bias_dram is None else 32)
                for s in range(HALVES):
                    for q in range(4):
                        g = s * 4 + q
                        out = acc[q * CT:(q + 1) * CT, s]
                        ins = nc.tensor.matmul(out, w[:], keep.x_T[:, g * GW:(g + 1) * GW], start=True, stop=bias_dram is None)
                        if bias_dram is not None:
                            ins = nc.tensor.matmul(out, b[:], keep.ones[0:1], start=False, stop=True)
                    ins.then_inc(acc_ready, 1)
                for s in range(HALVES):
                    pe.wait_ge(copied, s + 1)
                    for j in range(TG):
                        ins = nc.tensor.transpose(flipped[:, s, j * P:(j + 1) * P], byexp[:, s, j * P:(j + 1) * P], keep.ident[:])
                    ins.then_inc(flip_ready, 1)

            @block.vector
            def _(dve):
                nc.vector.memset(w[:], 0.0).then_inc(padded, 1)
                nc.vector.memset(b[:], 0.0).then_inc(padded, 1)
                for s in range(HALVES):
                    dve.wait_ge(acc_ready, s + 1)
                    nc.vector.tensor_copy(byexp[:, s], acc[:, s]).then_inc(copied, 1)
                for s in range(HALVES):
                    dve.wait_ge(flip_ready, s + 1)
                    dst = logits[:].rearrange("p (s q j e) -> p s j q e", s=HALVES, q=4, e=E)[:, s]
                    src = flipped[:, s].rearrange("p (j q e) -> p j q e", j=TG, e=CT)[:, :, :, 0:E]
                    nc.vector.tensor_copy(dst, src).then_inc(logit_done, 1)
                dve.wait_ge(logit_done, HALVES)


def softmax8(nc, keep, tag, logits, probs):
    with ExitStack() as st:
        c = Core(nc, st, tag + "sm")
        top, total = c.sb("top", [P, NT]), c.sb("total", [P, NT])
        chain_sem, shifted, raised = c.sem("chain"), c.sem("shifted"), c.sem("raised")
        l3 = logits[:].rearrange("p (t e) -> p t e", e=8)
        p3 = probs[:].rearrange("p (t e) -> p t e", e=8)
        with nc.Block() as block:

            @block.vector
            def _(dve):
                ch = Chain(dve, chain_sem)
                ch.step(nc.vector.tensor_reduce(top[:], l3, AX.X, ALU.max))
                nc.vector.tensor_tensor(l3, l3, top[:].unsqueeze(2).to_broadcast([P, NT, 8]),
                                        ALU.subtract).then_inc(shifted, 1)
                dve.wait_ge(raised, 1)
                ch.step(nc.vector.tensor_reduce(total[:], p3, AX.X, ALU.add))
                ch.step(nc.vector.reciprocal(total[:], total[:]))
                ch.step(nc.vector.tensor_tensor(p3, p3, total[:].unsqueeze(2).to_broadcast([P, NT, 8]), ALU.mult))

            @block.scalar
            def _(act):
                act.wait_ge(shifted, 1)
                nc.scalar.activation(probs[:], logits[:], ACT.Exp).then_inc(raised, 1)


def pick_top(nc, keep, tag, probs, comb, k, scale_top=None):
    with ExitStack() as st:
        c = Core(nc, st, tag + "tk")
        rank = c.sb("rank", [P, NT * 8])
        left, hot, sc = c.sb("left", [P, NT * 8]), c.sb("hot", [P, NT * 8]), c.sb("sc", [P, NT * 8])
        top, best, total = c.sb("top", [P, NT]), c.sb("best", [P, NT]), c.sb("total", [P, NT])
        chain_sem, ranked = c.sem("chain"), c.sem("ranked")
        three = lambda a: a[:].rearrange("p (t e) -> p t e", e=8)
        wide = lambda a: a[:].unsqueeze(2).to_broadcast([P, NT, 8])
        with nc.Block() as block:

            @block.gpsimd
            def _(pool):
                nc.gpsimd.iota(three(rank), pattern=[[0, NT], [-1, 8]], base=8, channel_multiplier=0,
                               allow_small_or_imprecise_dtypes=True).then_inc(ranked, 1)

            @block.vector
            def _(dve):
                ch = Chain(dve, chain_sem)
                dve.wait_ge(ranked, 1)
                ch.step(nc.vector.tensor_copy(left[:], probs[:]))
                for n in range(k):
                    ch.step(nc.vector.tensor_reduce(top[:], three(left), AX.X, ALU.max))
                    ch.step(nc.vector.tensor_tensor(three(hot), three(left), wide(top), ALU.is_equal))
                    ch.step(nc.vector.tensor_tensor(hot[:], hot[:], rank[:], ALU.mult))
                    ch.step(nc.vector.tensor_reduce(best[:], three(hot), AX.X, ALU.max))
                    ch.step(nc.vector.tensor_tensor(three(hot), three(hot), wide(best), ALU.is_equal))
                    ch.step(nc.vector.scalar_tensor_tensor(out=left[:], in0=hot[:], scalar=-2.0, in1=left[:],
                                                           op0=ALU.mult, op1=ALU.add))
                    if k == 1:
                        ch.step(nc.vector.tensor_scalar(top[:], top[:], scale_top, None, ALU.mult))
                        ch.step(nc.vector.tensor_tensor(three(comb), three(hot), wide(top), ALU.mult))
                        ch.step(nc.vector.memset(three(comb)[:, :, 7:8], 1.0))
                    elif n == 0:
                        ch.step(nc.vector.tensor_tensor(three(comb), three(hot), wide(top), ALU.mult))
                        ch.step(nc.vector.tensor_copy(total[:], top[:]))
                    else:
                        ch.step(nc.vector.tensor_tensor(total[:], total[:], top[:], ALU.add))
                        ch.step(nc.vector.reciprocal(total[:], total[:]))
                        ch.step(nc.vector.tensor_tensor(three(sc), three(hot), wide(top), ALU.mult))
                        ch.step(nc.vector.tensor_tensor(comb[:], comb[:], sc[:], ALU.add))
                        ch.step(nc.vector.tensor_tensor(three(comb), three(comb), wide(total), ALU.mult))


def experts(nc, keep, tag, comb, weights_in, loads, units, rows, up, down, per_unit, func, gate=None, bias=None):
    nf = len(rows)
    upb = 2 if gate else 4
    ob = per_unit
    steps = units * nf
    with ExitStack() as st:
        c = Core(nc, st, tag + "ex")
        hid = c.sb("hid", [P, 2, nf, GW])
        silu = c.sb("silu", [P, 2, GW]) if gate else None
        raw = c.ps("raw", [P, 4, GW])
        res = c.ps("res", [P, 2, ob, GW])
        raw_ready = c.sem("raw_ready")
        silu_ready = c.sem("silu_ready")
        hid_ready = c.sem("hid_ready")
        res_ready = c.sem("res_ready")
        comb_done = c.sem("comb_done")
        ones_set, started = c.sem("ones_set"), c.sem("started")
        tiles_per_bank = GW // (per_unit * D)

        def result(k, j):
            b, o = divmod(j, tiles_per_bank)
            return res[:, k, b, o * per_unit * D:(o + 1) * per_unit * D]

        with nc.Block() as block:

            @block.tensor
            def _(pe):
                pe.sem_inc(hid_ready, upb)
                pe.sem_inc(res_ready, 2)
                pe.sem_inc(comb_done, 2)
                pe.wait_ge(ones_set, 1)
                pe.wait_ge(weights_in, 16 * loads)

                def rise(g, u):
                    for f in range(nf):
                        i = u * nf + f
                        place = (i % upb) * (4 // upb)
                        x = keep.x_T[:, ds(g * GW, GW)]
                        pe.wait_ge(hid_ready, g * steps + (i + 1))
                        ins = nc.tensor.matmul(raw[0:rows[f], place], up(u, f), x, start=True, stop=True)
                        if gate:
                            ins = nc.tensor.matmul(raw[0:rows[f], place + 1], gate(u, f), x, start=True, stop=True)
                        ins.then_inc(raw_ready, 1)

                def fall(g, u):
                    pe.wait_ge(hid_ready, g * steps + (upb + (u + 1) * nf))
                    pe.wait_ge(comb_done, g * units + (u + 1))
                    for j in range(TG):
                        for f in range(nf):
                            w = down(u, f)
                            ins = nc.tensor.matmul(result(u % 2, j), hid[0:w.shape[0], u % 2, f, j * P:(j + 1) * P], w,
                                                   start=(f == 0), stop=(f == nf - 1))
                    ins.then_inc(res_ready, 1)

                with pe.Fori(0, NG) as g:
                    for u in range(units):
                        rise(g, u)
                        if u:
                            fall(g, u - 1)
                    fall(g, units - 1)

            @block.scalar
            def _(act):
                act.wait_ge(weights_in, 16 * loads)
                with act.Fori(0, NG) as g:
                    for u in range(units):
                        for f in range(nf):
                            i = u * nf + f
                            place = (i % upb) * (4 // upb)
                            act.wait_ge(raw_ready, g * steps + (i + 1))
                            if gate:
                                act.wait_ge(hid_ready, g * steps + (i + 1))
                                nc.scalar.activation(silu[0:rows[f], i % 2], raw[0:rows[f], place + 1],
                                                     func).then_inc(silu_ready, 1)
                            else:
                                if f == 0:
                                    act.wait_ge(res_ready, g * units + (u + 1))
                                kw = {"bias": bias(u, f)} if bias else {}
                                nc.scalar.activation(hid[0:rows[f], u % 2, f], raw[0:rows[f], place], func,
                                                     **kw).then_inc(hid_ready, 1)

            @block.vector
            def _(dve):
                nc.vector.memset(hid[:], 1.0).then_inc(ones_set, 1)

                def merge(g, u):
                    dve.wait_ge(res_ready, g * units + (u + 3))
                    for e in range(per_unit):
                        dve.wait_ge(merged, (g * units + u) * per_unit + (e + 1))
                        for j in range(TG):
                            t = g * TG + j
                            ins = nc.vector.scalar_tensor_tensor(
                                out=keep.x_tok[:, ds(t * D, D)], in0=result(u % 2, j)[:, e * D:(e + 1) * D],
                                scalar=comb[:, ds(t * 8 + (u * per_unit + e), 1)],
                                in1=keep.x_tok[:, ds(t * D, D)], op0=ALU.mult, op1=ALU.add)
                        ins.then_inc(merged, 1)
                    dve.wait_ge(merged, (g * units + u) * per_unit + (per_unit + 1))
                    dve.sem_inc(comb_done, 1)

                merged = started
                dve.sem_inc(merged, 1)
                with dve.Fori(0, NG) as g:
                    for u in range(units):
                        if gate:
                            for f in range(nf):
                                i = u * nf + f
                                dve.wait_ge(silu_ready, g * steps + (i + 1))
                                if f == 0:
                                    dve.wait_ge(res_ready, g * units + (u + 1))
                                nc.vector.tensor_tensor(hid[0:rows[f], u % 2, f], raw[0:rows[f], (i % 2) * 2],
                                                        silu[0:rows[f], i % 2], ALU.mult).then_inc(hid_ready, 1)
                        if u:
                            merge(g, u - 1)
                    merge(g, units - 1)


def flip_tokens(nc, keep, tag, src_tok, dst_T):
    with ExitStack() as st:
        c = Core(nc, st, tag + "fl")
        staged = c.sb("staged", [P, 2, GW])
        flipped = c.ps("flipped", [P, 2, GW])
        staged_ready, flip_ready, flip_done = c.sem("staged_ready"), c.sem("flip_ready"), c.sem("flip_done")
        with nc.Block() as block:

            @block.vector
            def _(dve):
                with dve.Fori(0, NG // 2) as pair:
                    for k in range(2):
                        dve.wait_ge(flip_ready, pair * 2 + (k + 1))
                        nc.vector.tensor_copy(staged[:, k], src_tok[:, ds((pair * 2 + k) * GW, GW)]).then_inc(staged_ready, 1)

            @block.tensor
            def _(pe):
                pe.sem_inc(flip_ready, 2)
                pe.sem_inc(flip_done, 2)
                with pe.Fori(0, NG // 2) as pair:
                    for k in range(2):
                        pe.wait_ge(staged_ready, pair * 2 + (k + 1))
                        pe.wait_ge(flip_done, pair * 2 + (k + 1))
                        for j in range(TG):
                            ins = nc.tensor.transpose(flipped[:, k, j * P:(j + 1) * P], staged[:, k, j * P:(j + 1) * P], keep.ident[:])
                        ins.then_inc(flip_ready, 1)

            @block.scalar
            def _(act):
                with act.Fori(0, NG // 2) as pair:
                    for k in range(2):
                        act.wait_ge(flip_ready, pair * 2 + (k + 3))
                        nc.scalar.copy(dst_T[:, ds((pair * 2 + k) * GW, GW)], flipped[:, k]).then_inc(flip_done, 1)


def layer0_attn(nc, keep, a):
    H, HD = 16, 8
    HEADS = B * H
    QT = S // P
    PARTS = [(0, 0), (0, 1), (0, 2), (1, 0), (1, 1), (1, 2), (2, 0), (2, 1)]
    ROWS = len(PARTS) * HD
    M1, M2 = 64, 96
    FULL = M2 + QT
    RING = 4
    V1 = 32
    QB = S // 4
    scratch = [nc.dram_tensor(f"l0_{n}_parts", (3, B * P, S), BF16, kind="Internal").ap() for n in ("query", "key")]
    with ExitStack() as st:
        c = Core(nc, st, "l0a")
        v_tok, at_tok = c.sb("v_tok", [P, N]), c.sb("at_tok", [P, N])

        with ExitStack() as st2:
            c2 = Core(nc, st2, "l0r")
            cos, sin = c2.sb("cos", [P, QT, D // 2]), c2.sb("sin", [P, QT, D // 2])
            prod = c2.sb("prod", [P, 2, N // 2])
            loaded, halves, joined = c2.sem("loaded"), c2.sem("halves"), c2.sem("joined")
            with nc.Block() as block:

                @block.sync
                def _(sp):
                    sp.dma_start(cos[:].rearrange("p t d -> p (t d)"), a["rope_cos"]).then_inc(loaded, 16)
                    sp.dma_start(sin[:].rearrange("p t d -> p (t d)"), a["rope_sin"]).then_inc(loaded, 16)

                x4 = keep.x_tok[:].rearrange("p (b t d) -> p b t d", b=B, d=D)
                r4 = at_tok[:].rearrange("p (b t d) -> p b t d", b=B, d=D)
                h = D // 2
                wide = lambda m: m[:].unsqueeze(1).to_broadcast([P, B, QT, h])
                p4 = lambda n: prod[:, n].rearrange("p (b t d) -> p b t d", b=B, d=h)

                @block.vector
                def _(dve):
                    dve.wait_ge(loaded, 32)
                    for n, (m1, m2, op, o) in enumerate(((cos, sin, ALU.subtract, 0), (sin, cos, ALU.add, h))):
                        nc.vector.tensor_tensor(r4[:, :, :, o:o + h], x4[:, :, :, 0:h], wide(m1), ALU.mult)
                        nc.vector.tensor_tensor(p4(n), x4[:, :, :, h:D], wide(m2), ALU.mult).then_inc(halves, 1)
                        dve.wait_ge(halves, n + 1)
                        nc.vector.tensor_tensor(r4[:, :, :, o:o + h], r4[:, :, :, o:o + h], p4(n), op).then_inc(joined, 1)
                    dve.wait_ge(joined, 2)

        rT = keep.x_T
        flip_tokens(nc, keep, "l0a", at_tok, rT)
        project_tokens(nc, keep, "l0v", rT, a["L0_attn_WvT"], v_tok, bias_dram=a["L0_attn_bv"])

        with ExitStack() as st2:
            c2 = Core(nc, st2, "l0p")
            w = c2.sb("w", [P, 2, P])
            bias = c2.sb("bias", [P, 2])
            full = c2.sb("full", [P, 2, GW])
            rest, rest2 = c2.sb("rest", [P, 2, GW]), c2.sb("rest2", [P, 2, GW])
            parts = c2.sb("parts", [P, 2, 3, GW], BF16)
            acc = c2.ps("acc", [P, 2, GW])
            loaded, acc_ready, full_done = c2.sem("loaded"), c2.sem("acc_ready"), c2.sem("full_done")
            cut, stored, chained = c2.sem("cut"), [c2.sem("stored0"), c2.sem("stored1")], c2.sem("chained")
            with nc.Block() as block:

                @block.sync
                def _(sp):
                    for m, n in enumerate(("q", "k")):
                        sp.dma_start(w[:, m], a[f"L0_attn_W{n}T"]).then_inc(loaded, 16)
                    sp.dma_start(bias[:], a["L0_attn_bqk_cols"]).then_inc(loaded, 16)
                    with sp.Fori(0, B) as b:
                        for half in range(2):
                            for m in range(2):
                                sp.wait_ge(cut, (b * 2 + half) * 6 + (3 * m + 3))
                                sp.dma_start(scratch[m][:, ds(b * P, P), half * GW:(half + 1) * GW].rearrange("i p s -> p i s"),
                                             parts[:, m]).then_inc(stored[m], 16)
                    for m in range(2):
                        sp.wait_ge(stored[m], 16 * NG + 16)

                @block.tensor
                def _(pe):
                    pe.sem_inc(full_done, 2)
                    pe.wait_ge(loaded, 48)
                    with pe.Fori(0, NG) as g:
                        for m in range(2):
                            pe.wait_ge(full_done, g * 2 + (m + 1))
                            nc.tensor.matmul(acc[:, m], w[:, m], rT[:, ds(g * GW, GW)], start=True, stop=True).then_inc(acc_ready, 1)

                @block.scalar
                def _(act):
                    with act.Fori(0, NG) as g:
                        for m in range(2):
                            act.wait_ge(acc_ready, g * 2 + (m + 1))
                            act.wait_ge(chained, g * 4 + (2 * m + 1))
                            nc.scalar.activation(full[:, m], acc[:, m], ACT.Identity, bias=bias[:, m:m + 1]).then_inc(full_done, 1)

                @block.vector
                def _(dve):
                    dve.sem_inc(chained, 4)
                    for m in range(2):
                        dve.sem_inc(stored[m], 16)
                    with dve.Fori(0, NG) as g:
                        for m in range(2):
                            dve.wait_ge(full_done, g * 2 + (m + 3))
                            dve.wait_ge(stored[m], g * 16 + 16)
                            nc.vector.tensor_copy(parts[:, m, 0], full[:, m]).then_inc(cut, 1)
                            dve.wait_ge(cut, g * 6 + (3 * m + 1))
                            nc.vector.tensor_tensor(rest[:, m], full[:, m], parts[:, m, 0], ALU.subtract).then_inc(chained, 1)
                            dve.wait_ge(chained, g * 4 + (2 * m + 5))
                            nc.vector.tensor_copy(parts[:, m, 1], rest[:, m]).then_inc(cut, 1)
                            dve.wait_ge(cut, g * 6 + (3 * m + 2))
                            nc.vector.tensor_tensor(rest2[:, m], rest[:, m], parts[:, m, 1], ALU.subtract).then_inc(chained, 1)
                            dve.wait_ge(chained, g * 4 + (2 * m + 6))
                            nc.vector.tensor_copy(parts[:, m, 2], rest2[:, m]).then_inc(cut, 1)

        with ExitStack() as st2:
            c2 = Core(nc, st2, "l0h")
            qs, ks = c2.sb("qs", [P, RING, S], BF16), c2.sb("ks", [P, RING, S], BF16)
            negmax = c2.sb("negmax", [P, 2, QT])
            first_part = c2.sb("first_part", [P, P], BF16)
            mcut = c2.sb("mcut", [P, P], BF16)
            diag = c2.sb("diag", [P, QT, P], BF16)
            vs = c2.sb("vs", [P, 2, QT, V1])
            TR = 4
            pT = c2.sb("pT", [P, TR, S])
            outT = c2.sb("outT", [P, QB])
            share = c2.sb("share", [P, QT])
            s1 = c2.ps("s1", [P, 2, S])
            s2 = c2.ps("s2", [P, 2, GW])
            mix = c2.ps("mix", [P, 2, GW])
            loaded = [c2.sem(f"loaded{r}") for r in range(RING)]
            s1_ready, max_done = c2.sem("s1_ready"), c2.sem("max_done")
            s2_ready, exp_done = c2.sem("s2_ready"), c2.sem("exp_done")
            pv_done, v_ready = c2.sem("pv_done"), c2.sem("v_ready")
            out_copied, flip_ready = c2.sem("out_copied"), c2.sem("flip_ready")
            m_cut, m_spread, prepared, hi_done = c2.sem("m_cut"), c2.sem("m_spread"), c2.sem("prepared"), c2.sem("hi_done")
            shared = c2.sem("shared")
            INV = 1.0 / math.sqrt(HD)
            v3 = v_tok[:].rearrange("p (t d) -> p t d", d=D)
            at3 = at_tok[:].rearrange("p (t d) -> p t d", d=D)
            LOADS = 6

            def over_heads(engine, head):
                for r in range(RING):
                    head(0, r, r == 0)
                with engine.Fori(1, HEADS // RING) as g:
                    for r in range(RING):
                        head(g, r, False)

            with nc.Block() as block:

                @block.sync
                def _(sp):
                    def load(n, r):
                        rows = ds(n % HEADS * HD, HD)
                        for i, j0, js in ((0, 0, 3), (1, 0, 3), (2, 0, 2)):
                            at = PARTS.index((i, j0)) * HD
                            sp.dma_start(ks[at:at + js * HD, r], scratch[1][0:js, rows]).then_inc(loaded[r], 16)
                            sp.dma_start(qs[at:at + js * HD, r],
                                         scratch[0][i:i + 1, rows].to_broadcast([js, HD, S])).then_inc(loaded[r], 16)

                    sp.wait_ge(prepared, 2)
                    for r in range(RING - 1):
                        load(r, r)

                    def head(g, r, first):
                        n = g * RING + r
                        if not first:
                            sp.wait_ge(s2_ready, n * (2 * QT))
                        load(n + (RING - 1), (r + RING - 1) % RING)

                    over_heads(sp, head)
                    for r in range(RING):
                        sp.wait_ge(loaded[r], 16 * LOADS * (HEADS // RING + (r < RING - 1)))

                @block.gpsimd
                def _(pool):
                    ch = Chain(pool, prepared)
                    ch.step(nc.gpsimd.memset(ks[ROWS:P], 1.0))
                    ch.step(nc.gpsimd.memset(qs[ROWS:P], 0.0))
                    ch.step(nc.gpsimd.memset(mcut[:], 0.0))
                    ch.step(nc.gpsimd.memset(vs[:], 0.0))
                    ch.step(nc.gpsimd.memset(vs[:, :, :, HD:HD + 1], 1.0))
                    ch.step(nc.gpsimd.memset(diag[:], 0.0))
                    for o in (M1, M2):
                        ch.step(nc.gpsimd.memset(diag[o:o + QT], 1.0))
                    for o in (M1, M2):
                        d = diag[o:o + QT]
                        ch.step(nc.gpsimd.affine_select(out=d, in_=d, compare_op=ALU.is_equal, fill=0.0, base=0,
                                                        pattern=[[-1, QT], [0, P]], channel_multiplier=1))

                    def values(n, q):
                        nc.gpsimd.tensor_copy(vs[:, q, :, 0:HD], v3[:, ds(n // H * QT, QT), ds(n % H * HD, HD)]).then_inc(v_ready, 1)

                    def spread(n, r):
                        pool.wait_ge(m_cut, (n + 1))
                        nc.gpsimd.tensor_tensor(qs[M1:FULL, r].rearrange("p (t q) -> p t q", q=P), diag[M1:FULL],
                                                mcut[M1:FULL].unsqueeze(1).to_broadcast([FULL - M1, QT, P]), ALU.mult).then_inc(m_spread, 1)
                        pool.wait_ge(m_spread, n + 1)

                    values(0, 0)
                    pool.wait_ge(v_ready, 1)
                    spread(0, 0)

                    def head(g, r, first):
                        n = g * RING + r
                        spread(n + 1, (r + 1) % RING)
                        pool.wait_ge(pv_done, n * QT + TR)
                        values((n + 1) % HEADS, (r + 1) % 2)
                        pool.wait_ge(v_ready, n + 2)

                    over_heads(pool, head)

                @block.tensor
                def _(pe):
                    pe.sem_inc(max_done, 2)
                    pe.sem_inc(exp_done, 2)
                    pe.sem_inc(pv_done, TR)

                    def first_product(n, r, t):
                        pe.wait_ge(max_done, n * QT + (t + 1))
                        for o in range(S // GW):
                            ins = nc.tensor.matmul(s1[:, t % 2, o * GW:(o + 1) * GW], qs[0:ROWS, r, t * P:(t + 1) * P],
                                                   ks[0:ROWS, r, o * GW:(o + 1) * GW], start=True, stop=True)
                        ins.then_inc(s1_ready, 1)

                    def second_product(n, r, t):
                        for o in range(S // GW):
                            pe.wait_ge(exp_done, (n * QT + t) * 2 + (o + 1))
                            nc.tensor.matmul(s2[:, o], ks[0:FULL, r, t * P:(t + 1) * P], qs[0:FULL, r, o * GW:(o + 1) * GW],
                                             start=True, stop=True).then_inc(s2_ready, 1)

                    def attend(n, q, t):
                        pe.wait_ge(exp_done, (n * QT + t) * 2 + 4)
                        if t == 0:
                            pe.wait_ge(v_ready, n + 1)
                            pe.wait_ge(m_cut, n + 1)
                        for k in range(4):
                            ins = nc.tensor.matmul(mix[k * V1:(k + 1) * V1, q, 0:QB], vs[:, q, t], pT[:, t % TR, k * QB:(k + 1) * QB],
                                                   start=(t == 0), stop=(t == QT - 1))
                        ins.then_inc(pv_done, 1)

                    def turn(n, q, result):
                        if result:
                            pe.wait_ge(out_copied, n)
                            for f in range(2):
                                nc.tensor.transpose(mix[:, q, (2 + f) * P:(3 + f) * P], outT[:, f * P:(f + 1) * P], keep.ident[:])
                        pe.wait_ge(max_done, (n + 2) * QT + 2)
                        nc.tensor.transpose(mix[0:QT, q, 0:P], negmax[:, q], keep.ident[:]).then_inc(flip_ready, 1)

                    for r in range(2):
                        pe.wait_ge(loaded[r], 16 * LOADS)
                        for t in range(QT):
                            first_product(r, r, t)
                        if r == 0:
                            turn(-1, 0, False)

                    def head(g, r, first):
                        n, q, r2 = g * RING + r, r % 2, (r + 2) % RING
                        pe.wait_ge(m_spread, n + 1)
                        pe.wait_ge(loaded[r2], (g + (1 if r < 2 else 2)) * (16 * LOADS))
                        for t in range(QT):
                            second_product(n, r, t)
                            first_product(n + 2, r2, t)
                            if t >= 2:
                                attend(n, q, t - 2)
                            elif not first:
                                attend(n - 1, 1 - q, QT - 2 + t)
                            if t == 2:
                                turn(n, 1 - q, not first)

                    over_heads(pe, head)
                    for t in range(QT - 2, QT):
                        attend(HEADS - 1, 1, t)
                    pe.wait_ge(out_copied, HEADS)
                    for f in range(2):
                        ins = nc.tensor.transpose(mix[:, 1, (2 + f) * P:(3 + f) * P], outT[:, f * P:(f + 1) * P], keep.ident[:])
                    ins.then_inc(flip_ready, 1)

                @block.scalar
                def _(act):
                    def copy_out(n, q):
                        act.wait_ge(pv_done, n * QT + (QT + TR))
                        nc.scalar.copy(outT[:], mix[:, q, 0:QB]).then_inc(out_copied, 1)

                    def head(g, r, first):
                        n = g * RING + r
                        for t in range(QT):
                            act.wait_ge(pv_done, n * QT + (t + 1))
                            for o in range(S // GW):
                                act.wait_ge(s2_ready, (n * QT + t) * 2 + (o + 1))
                                nc.scalar.activation(pT[:, t % TR, o * GW:(o + 1) * GW], s2[:, o], ACT.Exp, scale=INV).then_inc(exp_done, 1)
                            if t == 1 and not first:
                                copy_out(n - 1, (r + 1) % 2)

                    over_heads(act, head)
                    copy_out(HEADS - 1, 1)

                @block.vector
                def _(dve):
                    def maxima(n, q, t):
                        dve.wait_ge(s1_ready, n * QT + (t + 1))
                        nc.vector.tensor_reduce(negmax[:, q, t:t + 1], s1[:, t % 2], AX.X, ALU.max, negate=True).then_inc(max_done, 1)

                    def cut_maxima(n, q, count):
                        dve.wait_ge(flip_ready, count)
                        dve.wait_ge(m_spread, n)
                        src = mix[0:QT, q, 0:P]
                        nc.vector.tensor_copy(first_part[M2:M2 + QT], src).then_inc(hi_done, 1)
                        nc.vector.tensor_copy(mcut[M1:M1 + QT], src)
                        dve.wait_ge(hi_done, count)
                        nc.vector.tensor_tensor(mcut[M2:M2 + QT], src, first_part[M2:M2 + QT], ALU.subtract).then_inc(m_cut, 1)

                    def settle(n, q, count):
                        dve.wait_ge(flip_ready, count)
                        flat = mix[:, q, 2 * P:4 * P].rearrange("p (f k v) -> p f k v", f=2, v=V1)
                        nc.vector.reciprocal(share[:].rearrange("p (f k) -> p f k", f=2), flat[:, :, :, HD]).then_inc(shared, 1)
                        dve.wait_ge(shared, (n + 1))
                        dst = at3[:, ds(n // H * QT, QT), ds(n % H * HD, HD)].rearrange("p (k f) d -> p f k d", f=2)
                        nc.vector.tensor_tensor(dst, flat[:, :, :, 0:HD],
                                                share[:].rearrange("p (f k) -> p f k", f=2).unsqueeze(3).to_broadcast([P, 2, 4, HD]),
                                                ALU.mult)

                    for r in range(2):
                        for t in range(QT):
                            maxima(r, r, t)
                        if r == 0:
                            dve.wait_ge(prepared, 3)
                            cut_maxima(0, 0, 1)

                    def head(g, r, first):
                        n, q = g * RING + r, r % 2
                        for t in range(QT):
                            maxima(n + 2, q, t)
                            if t == 2:
                                cut_maxima(n + 1, 1 - q, n + 2)
                                if not first:
                                    settle(n - 1, 1 - q, n + 2)

                    over_heads(dve, head)
                    settle(HEADS - 1, 1, HEADS + 2)

        flip_tokens(nc, keep, "l0o", at_tok, rT)
        project_tokens(nc, keep, "l0o", rT, a["L0_attn_WoT"], keep.x_tok, bias_dram=a["L0_attn_bo"], add=True)


def layer0_ffn(nc, keep, a):
    E, F = 8, 256
    with ExitStack() as st:
        c = Core(nc, st, "l0f")
        w1, w2 = c.sb("w1", [P, E, F]), c.sb("w2", [P, E, 2, D])
        logits, probs, comb = c.sb("logits", [P, NT * 8]), c.sb("probs", [P, NT * 8]), c.sb("comb", [P, NT * 8])
        weights_in = c.sem("weights_in")
        router(nc, keep, "l0f", logits, a["L0_ffn_Wg"], None,
               [(w1[:], a["L0_ffn_W1"].rearrange("e d f -> d e f")),
                (w2[:], a["L0_ffn_W2"].rearrange("e (k p) d -> p e k d", p=P))], weights_in)
        softmax8(nc, keep, "l0f", logits, probs)
        pick_top(nc, keep, "l0f", probs, comb, 2)
        experts(nc, keep, "l0f", comb, weights_in, 2, E, [P, P], lambda u, f: w1[:, u, f * P:(f + 1) * P],
                lambda u, f: w2[:, u, f], 1, ACT.Relu)


def layer1_attn(nc, keep, a):
    DI, H, HD, DS, K = 256, 4, 64, 64, 4
    NC_ = S // P
    F2 = DI // P
    O_SSM, O_DT, O_B, O_C = DI, 2 * DI, 2 * DI + H, 2 * DI + H + DS
    PW = O_C + DS
    TM = H + DS
    PAD = K - 1
    with ExitStack() as st:
        c = Core(nc, st, "l1a")
        w_in, w_out = c.sb("w_in", [P, PW]), c.sb("w_out", [P, F2, D])
        scale = c.sb("scale", [P, 1])
        conv_w, conv_b = c.sb("conv_w", [P, F2, K]), c.sb("conv_b", [P, F2])
        a_log, dt_bias = c.sb("a_log", [P, H]), c.sb("dt_bias", [P, H])
        gate = c.sb("gate", [P, F2, N])
        tok = c.sb("tok", [P, NT, TM])
        bT, cT = c.sb("bT", [DS, N]), c.sb("cT", [DS, N])
        dt, adt = c.sb("dt", [P, NT, H]), c.sb("adt", [P, NT, H])
        hT = c.sb("hT", [P, F2, N])

        with ExitStack() as st2:
            c2 = Core(nc, st2, "l1p")
            ssm = c2.sb("ssm", [P, F2, B * (S + PAD)])
            s_b = S + PAD
            with ExitStack() as st3:
                c3 = Core(nc, st3, "l1q")
                xn = c3.sb("xn", [P, N])
                layernorm(nc, keep, "l1a", rms_T=xn)
                staged = c3.sb("staged", [P, 2, GW])
                acc = c3.ps("acc", [P, 5, GW])
                acc_t = c3.ps("acc_t", [P, 2, GW])
                loaded, scaled, staged_ready = c3.sem("loaded"), c3.sem("scaled"), c3.sem("staged_ready")
                acc_ready, acc_done = c3.sem("acc_ready"), c3.sem("acc_done")
                tok_ready, tok_done, padded = c3.sem("tok_ready"), c3.sem("tok_done"), c3.sem("padded")
                JOBS = [("gate", 0), ("gate", 1), ("ssm", 0), ("ssm", 1), ("bc", 0)]
                J = len(JOBS)
                with nc.Block() as block:

                    @block.sync
                    def _(sp):
                        for dst, src in [(w_in[:], a["L1_attn_w_in"]), (scale[:], a["L1_attn_norm_scale_col"]),
                                         (w_out[:], a["L1_attn_w_out"].rearrange("(k p) d -> p k d", p=P)),
                                         (conv_w[:].rearrange("p f k -> p (f k)"), a["L1_attn_conv_w_cols"]),
                                         (conv_b[:], a["L1_attn_conv_b_cols"]),
                                         (a_log[:], a["L1_attn_A_log"].rearrange("(o h) -> o h", o=1).broadcast_to([P, H])),
                                         (dt_bias[:], a["L1_attn_dt_bias"].rearrange("(o h) -> o h", o=1).broadcast_to([P, H]))]:
                            sp.dma_start(dst, src).then_inc(loaded, 16)
                        sp.wait_ge(loaded, 16 * 7)

                    @block.gpsimd
                    def _(pool):
                        nc.gpsimd.memset(ssm[:, :, :].rearrange("p f (b s) -> p (f b) s", b=B)[:, :, 0:PAD], 0.0).then_inc(padded, 1)
                        pool.wait_ge(padded, 1)

                    @block.tensor
                    def _(pe):
                        pe.sem_inc(acc_done, 5)
                        pe.sem_inc(tok_ready, 2)
                        pe.sem_inc(tok_done, 2)
                        pe.wait_ge(scaled, 1)
                        cols = {"gate": 0, "ssm": O_SSM, "bc": O_B}
                        with pe.Fori(0, B) as b:
                            for k in range(2):
                                for i, (kind, f) in enumerate(JOBS):
                                    n = k * J + i
                                    pe.wait_ge(acc_done, b * (2 * J) + (n + 1))
                                    o = cols[kind] + f * P
                                    nc.tensor.matmul(acc[:, n % 5], w_in[:, o:o + P],
                                                     xn[:, ds((b * 2 + k) * GW, GW)], start=True, stop=True).then_inc(acc_ready, 1)
                                pe.wait_ge(staged_ready, b * 2 + (k + 1))
                                pe.wait_ge(tok_done, b * 2 + (k + 1))
                                for j in range(TG):
                                    ins = nc.tensor.matmul(acc_t[:, k, j * TM:(j + 1) * TM], staged[:, k, j * P:(j + 1) * P],
                                                           w_in[:, O_DT:O_DT + TM], start=True, stop=True)
                                ins.then_inc(tok_ready, 1)

                    @block.scalar
                    def _(act):
                        with act.Fori(0, B) as b:
                            for k in range(2):
                                for i, (kind, f) in enumerate(JOBS):
                                    n = k * J + i
                                    act.wait_ge(acc_ready, b * (2 * J) + (n + 1))
                                    here = ds((b * 2 + k) * GW, GW)
                                    src = acc[:, n % 5]
                                    if kind == "gate":
                                        ins = nc.scalar.activation(gate[:, f, here], src, ACT.Silu)
                                    elif kind == "ssm":
                                        ins = nc.scalar.copy(ssm[:, f, ds(b * s_b + (PAD + k * GW), GW)], src)
                                    else:
                                        nc.scalar.copy(bT[:, here], src[0:DS])
                                        ins = nc.scalar.copy(cT[:, here], src[DS:2 * DS])
                                    ins.then_inc(acc_done, 1)

                    @block.vector
                    def _(dve):
                        dve.wait_ge(loaded, 16 * 7)
                        nc.vector.tensor_scalar(w_in[:], w_in[:], scale[:], None, ALU.mult).then_inc(scaled, 1)
                        with dve.Fori(0, B) as b:
                            for k in range(2):
                                nc.vector.tensor_copy(staged[:, k], xn[:, ds((b * 2 + k) * GW, GW)]).then_inc(staged_ready, 1)
                                dve.wait_ge(tok_ready, b * 2 + (k + 3))
                                nc.vector.tensor_copy(tok[:].rearrange("p t m -> p (t m)")[:, ds((b * 2 + k) * TG * TM, TG * TM)],
                                                      acc_t[:, k, 0:TG * TM]).then_inc(tok_done, 1)

            with ExitStack() as st3:
                c3 = Core(nc, st3, "l1d")
                low, soft = c3.sb("low", [P, NT, H]), c3.sb("soft", [P, NT, H])
                conv = c3.sb("conv", [P, 2, S])
                chain_sem, low_ready, a_ready = c3.sem("chain"), c3.sem("low_ready"), c3.sem("a_ready")
                soft_ready, act_chain, conv_ready, h_ready = c3.sem("soft_ready"), c3.sem("act_chain"), c3.sem("conv_ready"), c3.sem("h_ready")
                with nc.Block() as block:

                    @block.vector
                    def _(dve):
                        ch = Chain(dve, chain_sem)
                        ch.step(nc.vector.tensor_tensor(dt[:], tok[:, :, 0:H], dt_bias[:].unsqueeze(1).to_broadcast([P, NT, H]), ALU.add))
                        nc.vector.scalar_tensor_tensor(out=low[:], in0=dt[:], scalar=-1.0, in1=dt[:],
                                                       op0=ALU.mult, op1=ALU.min).then_inc(low_ready, 1)
                        dve.wait_ge(soft_ready, 1)
                        ch.step(nc.vector.scalar_tensor_tensor(out=dt[:], in0=dt[:], scalar=0.0, in1=soft[:],
                                                               op0=ALU.max, op1=ALU.add))
                        dve.wait_ge(a_ready, 1)
                        ch.step(nc.vector.scalar_tensor_tensor(out=adt[:], in0=dt[:], scalar=-1.0,
                                                               in1=a_log[:].unsqueeze(1).to_broadcast([P, NT, H]),
                                                               op0=ALU.mult, op1=ALU.mult))
                        base = ch.count
                        with dve.Fori(0, B) as b:
                            for f in range(F2):
                                dve.wait_ge(h_ready, b * F2 + (f + 1))
                                for n, k in enumerate(reversed(range(K))):
                                    src = ssm[:, f, ds(b * s_b + k, S)]
                                    if n == 0:
                                        ins = nc.vector.tensor_scalar(conv[:, f], src, conv_w[:, f, k:k + 1], None, ALU.mult)
                                    else:
                                        dve.wait_ge(chain_sem, b * (F2 * (K - 1)) + (base + f * (K - 1) + n))
                                        ins = nc.vector.scalar_tensor_tensor(out=conv[:, f], in0=src, scalar=conv_w[:, f, k:k + 1],
                                                                             in1=conv[:, f], op0=ALU.mult, op1=ALU.add)
                                    ins.then_inc(conv_ready if n == K - 1 else chain_sem, 1)

                    @block.scalar
                    def _(act):
                        act.sem_inc(h_ready, 2)
                        act.wait_ge(low_ready, 1)
                        nc.scalar.activation(low[:], low[:], ACT.Exp).then_inc(act_chain, 1)
                        act.wait_ge(act_chain, 1)
                        nc.scalar.activation(soft[:], low[:], ACT.Ln, bias=keep.ones[:, 0:1]).then_inc(soft_ready, 1)
                        nc.scalar.activation(a_log[:], a_log[:], ACT.Exp).then_inc(a_ready, 1)
                        with act.Fori(0, B) as b:
                            for f in range(F2):
                                act.wait_ge(conv_ready, b * F2 + (f + 1))
                                nc.scalar.activation(hT[:, f, ds(b * S, S)], conv[:, f], ACT.Silu,
                                                     bias=conv_b[:, f:f + 1]).then_inc(h_ready, 1)

        with ExitStack() as st2:
            c2 = Core(nc, st2, "l1s")
            hs, bs, ts = c2.sb("hs", [P, B, F2, P]), c2.sb("bs", [DS, B, P]), c2.sb("ts", [P, B, DS])
            acol = c2.sb("acol", [P, B, H])
            gap, decay = c2.sb("gap", [P, 2, H, P]), c2.sb("decay", [P, 2, H, P])
            into = c2.sb("into", [DS, 2, H, P])
            wgap, wcol = c2.sb("wgap", [P, 2, H]), c2.sb("wcol", [P, 2, H])
            gm, mix = c2.sb("gm", [P, 2, P]), c2.sb("mix", [P, 2, H, P])
            hd, hw = c2.sb("hd", [P, 2, DI]), c2.sb("hw", [P, 2, DI])
            cs = c2.sb("cs", [DS, 2, H, P])
            state = c2.sb("state", [DS, B, DI])
            ys = c2.sb("ys", [P, 2, F2, P])
            run = c2.ps("run", [P, 2, H, P])
            mid = c2.ps("mid", [P, 2, GW])
            res = c2.ps("res", [P, 2, GW])
            fin = c2.ps("fin", [P, 2, GW])
            col = lambda q: mid[:, q, 0:H]
            htok = lambda q: mid[:, q, P:P + DI]
            gram = lambda q: mid[:, q, P + DI:P + DI + P]
            yT = lambda q, f: res[:, q, f * P:(f + 1) * P]
            delta = lambda q: res[0:DS, q, DI:2 * DI]
            staged, sums, gaps = c2.sem("staged"), c2.sem("sums"), c2.sem("gaps")
            raised, mixed, pool_mixed = c2.sem("raised"), c2.sem("mixed"), c2.sem("pool_mixed")
            y_ready, gated, out_ready, added = c2.sem("y_ready"), c2.sem("gated"), c2.sem("out_ready"), c2.sem("added")
            hd_sem, state_sem, zeroed = c2.sem("hd_sem"), c2.sem("state_sem"), c2.sem("zeroed")
            NS = 4

            def over_chunks(engine, part):
                part(0, True, False)
                with engine.Fori(1, NC_ - 1) as ck:
                    part(ck, False, False)
                part(NC_ - 1, False, True)

            def back(ck, j, steps):
                return (ck, j - steps) if j >= steps else (ck - 1, j - steps + B)

            with nc.Block() as block:

                @block.gpsimd
                def _(pool):
                    def stage(ck, j):
                        pool.wait_ge(y_ready, ck * B + (j + 1))
                        at = ck * P + j * S
                        nc.gpsimd.tensor_copy(acol[:, j], adt[:].rearrange("p t h -> p (t h)")[:, ds(ck * H + j * NC_ * H, H)]).then_inc(staged, 1)
                        nc.gpsimd.tensor_copy(hs[:, j], hT[:, :, ds(at, P)]).then_inc(staged, 1)
                        nc.gpsimd.tensor_copy(bs[:, j], bT[:, ds(at, P)]).then_inc(staged, 1)
                        nc.gpsimd.tensor_copy(ts[:, j], tok[:].rearrange("p t m -> p (t m)")[:, ds(ck * TM + (j * NC_ * TM + H), DS)]).then_inc(staged, 1)

                    def chunk(ck, first, last):
                        for j in range(B):
                            if not (last and j == B - 1):
                                stage(ck if j < B - 1 else ck + 1, (j + 1) % B)
                            pool.wait_ge(raised, (ck * B + j) * 3 + 3)
                            pool.wait_ge(y_ready, ck * B + (j + 3))
                            nc.gpsimd.tensor_tensor(cs[:, j % 2], into[:, j % 2],
                                                    cT[:, ds(ck * P + j * S, P)].unsqueeze(1).to_broadcast([DS, H, P]),
                                                    ALU.mult).then_inc(pool_mixed, 1)

                    stage(0, 0)
                    over_chunks(pool, chunk)

                @block.tensor
                def _(pe):
                    pe.sem_inc(y_ready, B)
                    pe.sem_inc(mixed, 2)
                    pe.sem_inc(added, 2)
                    pe.sem_inc(gated, 2)
                    pe.wait_ge(zeroed, 1)

                    def project(ck, j):
                        pe.wait_ge(gated, ck * B + (j + 3))
                        pe.wait_ge(added, ck * B + (j + 1))
                        for f in range(F2):
                            ins = nc.tensor.matmul(fin[:, j % 2, 0:D], ys[:, j % 2, f], w_out[:, f], start=(f == 0), stop=(f == F2 - 1))
                        ins.then_inc(out_ready, 1)

                    def prepare(ck, j):
                        q = j % 2
                        pe.wait_ge(staged, (ck * B + j) * NS + NS)
                        pe.wait_ge(mixed, ck * B + (j + 1))
                        for h in range(H):
                            nc.tensor.matmul(run[:, q, h], acol[:, j, h:h + 1].to_broadcast([P, P]), keep.upto[:], start=True, stop=True)
                        nc.tensor.matmul(col(q), keep.upto[:], acol[:, j], start=True, stop=True)
                        for f in range(F2):
                            nc.tensor.transpose(htok(q)[:, f * P:(f + 1) * P], hs[:, j, f], keep.ident[:])
                        nc.tensor.matmul(gram(q), bs[:, j], cT[:, ds(ck * P + j * S, P)], start=True, stop=True).then_inc(sums, 1)

                    def chunk(ck, first, last):
                        for j in range(B):
                            q = j % 2
                            if not (last and j == B - 1):
                                prepare(ck if j < B - 1 else ck + 1, (j + 1) % B)
                            pe.wait_ge(mixed, ck * B + (j + 3))
                            pe.wait_ge(pool_mixed, ck * B + (j + 1))
                            pe.wait_ge(gated, ck * B + (j + 1))
                            for h in range(H):
                                f, o = divmod(h * HD, P)
                                out = yT(q, f)[o:o + HD]
                                nc.tensor.matmul(out, hd[:, q, h * HD:(h + 1) * HD], mix[:, q, h], start=True, stop=False)
                                nc.tensor.matmul(out, state[:, j, h * HD:(h + 1) * HD], cs[:, q, h], start=False, stop=True)
                            nc.tensor.matmul(delta(q), ts[:, j], hw[:, q], start=True, stop=True).then_inc(y_ready, 1)
                            if not (first and j == 0):
                                project(*back(ck, j, 1))

                    prepare(0, 0)
                    over_chunks(pe, chunk)
                    project(NC_ - 1, B - 1)

                @block.scalar
                def _(act):
                    def chunk(ck, first, last):
                        for j in range(B):
                            q = j % 2
                            act.wait_ge(gaps, ck * B + (j + 1))
                            act.wait_ge(gated, ck * B + (j + 1))
                            act.wait_ge(y_ready, ck * B + (j + 3))
                            nc.scalar.activation(decay[:, q], gap[:, q], ACT.Exp).then_inc(raised, 1)
                            nc.scalar.activation(wcol[:, q], wgap[:, q], ACT.Exp).then_inc(raised, 1)
                            nc.scalar.activation(into[:, q], run[0:DS, q], ACT.Exp).then_inc(raised, 1)

                    over_chunks(act, chunk)

                @block.vector
                def _(dve):
                    nc.vector.memset(state[:], 0.0).then_inc(zeroed, 1)

                    def finish(ck, j):
                        q = j % 2
                        dve.wait_ge(y_ready, ck * B + (j + 1 + B))
                        last = into[:, q, :, P - 1:P].to_broadcast([DS, H, HD])
                        st_ = state[:, j].rearrange("n (h p) -> n h p", h=H)
                        nc.vector.tensor_tensor(st_, st_, last, ALU.mult).then_inc(state_sem, 1)
                        nc.vector.tensor_tensor(ys[:, q], res[:, q, 0:DI].rearrange("p (f t) -> p f t", f=F2),
                                                gate[:, :, ds(ck * P + j * S, P)], ALU.mult)
                        dve.wait_ge(state_sem, ck * B + (j + 1))
                        nc.vector.tensor_tensor(state[:, j], delta(q), state[:, j], ALU.add).then_inc(gated, 1)

                    def add(ck, j):
                        dve.wait_ge(out_ready, ck * B + (j + 1))
                        x = keep.x_tok[:, ds(ck * P + j * S, D)]
                        nc.vector.scalar_tensor_tensor(out=x, in0=x, scalar=2.0, in1=fin[:, j % 2, 0:D],
                                                       op0=ALU.mult, op1=ALU.add).then_inc(added, 1)

                    def chunk(ck, first, last):
                        for j in range(B):
                            q = j % 2
                            dve.wait_ge(sums, ck * B + (j + 1))
                            for h in range(H):
                                nc.vector.tensor_scalar(gap[:, q, h], run[:, q, h], col(q)[:, h:h + 1], 0.0, ALU.subtract, ALU.min)
                            nc.vector.tensor_copy(wcol[:, q], col(q)).then_inc(hd_sem, 1)
                            dve.wait_ge(hd_sem, (ck * B + j) * 2 + 1)
                            nc.vector.tensor_tensor(wgap[:, q], run[:, q, :, P - 1], wcol[:, q], ALU.subtract).then_inc(gaps, 1)
                            if not (first and j < 2):
                                finish(*back(ck, j, 2))
                            nc.vector.tensor_tensor(gm[:, q], gram(q), keep.upto[:], ALU.mult)
                            d = dt[:].rearrange("p t h -> p (t h)")[:, ds(ck * H + j * NC_ * H, H)]
                            nc.vector.tensor_tensor(hd[:, q].rearrange("p (h d) -> p h d", h=H), htok(q).rearrange("p (h d) -> p h d", h=H),
                                                    d.unsqueeze(2).to_broadcast([P, H, HD]), ALU.mult).then_inc(hd_sem, 1)
                            dve.wait_ge(raised, (ck * B + j) * 3 + 3)
                            dve.wait_ge(hd_sem, (ck * B + j) * 2 + 2)
                            nc.vector.tensor_tensor(hw[:, q].rearrange("p (h d) -> p h d", h=H), hd[:, q].rearrange("p (h d) -> p h d", h=H),
                                                    wcol[:, q].unsqueeze(2).to_broadcast([P, H, HD]), ALU.mult)
                            nc.vector.tensor_tensor(mix[:, q], decay[:, q], gm[:, q].unsqueeze(1).to_broadcast([P, H, P]),
                                                    ALU.mult).then_inc(mixed, 1)
                            if not (first and j < 3):
                                add(*back(ck, j, 3))

                    over_chunks(dve, chunk)
                    for j in range(B - 2, B):
                        finish(NC_ - 1, j)
                    for j in range(B - 3, B):
                        add(NC_ - 1, j)


def layer1_ffn(nc, keep, a):
    H, HD, SLOTS, F = 16, 8, 16, 512
    NF = F // P
    CT = 32
    ROUNDS = SLOTS * CT // P
    BS = B * SLOTS
    HQ = H * SLOTS
    INV = 1.0 / math.sqrt(HD)
    with ExitStack() as st:
        c = Core(nc, st, "l1f")
        w1, wg = c.sb("w1", [P, SLOTS, F]), c.sb("wg", [P, SLOTS, F])
        w2 = c.sb("w2", [P, SLOTS, NF, D])
        small = c.sb("small", [P, 8, D])
        cols = c.sb("cols", [P, 8])
        slot_T = c.sb("slot_T", [P, SLOTS])
        ln_g, ln_b = c.sb("ln_g", [BS, D]), c.sb("ln_b", [BS, D])
        b2T = c.sb("b2T", [P, SLOTS])
        c_bo = c.sb("c_bo", [P, D])
        head_mask = c.sb("head_mask", [P, H])
        own = c.sb("own", [P, 2, D])
        fold = c.sb("fold", [P, SLOTS])
        qblk = c.sb("qblk", [P, H, SLOTS])
        attT = c.sb("attT", [P, BS])
        o_T, o2T = c.sb("o_T", [P, BS]), c.sb("o2T", [P, BS])
        kblk, vblk = c.sb("kblk", [P, B, H, SLOTS]), c.sb("vblk", [P, B, H, SLOTS])
        vw = c.sb("vw", [P, B, 2, D])
        big_loaded = c.sem("big_loaded")
        wide3 = lambda x, shape: x.to_broadcast(shape)

        with ExitStack() as st2:
            c2 = Core(nc, st2, "l1g")
            qT = c2.sb("qT", [P, SLOTS])
            acc = c2.ps("acc", [P, 512])
            loaded, masks, acc_ready, chain_sem = c2.sem("loaded"), c2.sem("masks"), c2.sem("acc_ready"), c2.sem("chain")
            with nc.Block() as block:

                @block.sync
                def _(sp):
                    for n, name in enumerate(("d_Wq", "d_Wk", "d_Wo", "c_Wq", "c_Wk", "c_Wv", "c_Wo")):
                        sp.dma_start(small[:, n], a["L1_ffn_" + name]).then_inc(loaded, 16)
                    for dst, src in ((cols[:], "L1_ffn_bias_cols"), (slot_T[:], "L1_ffn_slot_T"), (b2T[:], "L1_ffn_b2_T")):
                        sp.dma_start(dst, a[src]).then_inc(loaded, 16)
                    for b in range(B):
                        sp.dma_start(ln_g[b * SLOTS:(b + 1) * SLOTS], a["L1_ffn_e_ln_g"]).then_inc(loaded, 16)
                        sp.dma_start(ln_b[b * SLOTS:(b + 1) * SLOTS], a["L1_ffn_e_ln_b"]).then_inc(loaded, 16)
                    sp.dma_start(c_bo[:], a["L1_ffn_c_bo"].rearrange("(o d) -> o d", o=1).broadcast_to([P, D])).then_inc(loaded, 16)
                    sp.wait_ge(loaded, 16 * (7 + 3 + 2 * B + 1))

                @block.gpsimd
                def _(pool):
                    ch = Chain(pool, masks)
                    sel = lambda ap, base, pattern, cm: ch.step(nc.gpsimd.affine_select(
                        out=ap, in_=ap, compare_op=ALU.is_ge, fill=0.0, base=base, pattern=pattern, channel_multiplier=cm))
                    ch.step(nc.gpsimd.memset(head_mask[:], 1.0))
                    sel(head_mask[:], 0, [[-HD, H]], 1)
                    sel(head_mask[:], HD - 1, [[HD, H]], -1)
                    ch.step(nc.gpsimd.memset(own[:], 1.0))
                    for f in range(2):
                        m = own[:, f].rearrange("p (h d) -> p h d", d=HD)
                        sel(m, P * f, [[-SLOTS, H], [0, HD]], 1)
                        sel(m, SLOTS - 1 - P * f, [[SLOTS, H], [0, HD]], -1)

                @block.tensor
                def _(pe):
                    pe.wait_ge(loaded, 16 * (7 + 3 + 2 * B + 1))
                    nc.tensor.matmul(acc[:, 0:SLOTS], small[:, 0], slot_T[:], start=True, stop=True).then_inc(acc_ready, 1)

                @block.vector
                def _(dve):
                    ch = Chain(dve, chain_sem)
                    ch.step(nc.vector.tensor_reduce(fold[:], keep.ident[:].rearrange("p (h q) -> p q h", q=SLOTS), AX.X, ALU.add))
                    dve.wait_ge(acc_ready, 1)
                    ch.step(nc.vector.tensor_scalar(qT[:], acc[:, 0:SLOTS], cols[:, 0:1], None, ALU.add))
                    dve.wait_ge(masks, 8)
                    ch.step(nc.vector.tensor_tensor(qblk[:], qT[:].unsqueeze(1).to_broadcast([P, H, SLOTS]),
                                                    head_mask[:].unsqueeze(2).to_broadcast([P, H, SLOTS]), ALU.mult))

        with ExitStack() as st2:
            c2 = Core(nc, st2, "l1h")
            kT = c2.sb("kT", [P, N])
            v_tok = c2.sb("v_tok", [P, N])
            project_tokens(nc, keep, "l1v", keep.x_T, a["L1_ffn_d_Wv"], v_tok, bias_dram=a["L1_ffn_d_bv"],
                           later=[(w1[:], a["L1_ffn_e_W1"].rearrange("e d f -> d e f")),
                                  (wg[:], a["L1_ffn_e_Wg"].rearrange("e d f -> d e f")),
                                  (w2[:], a["L1_ffn_e_W2"].rearrange("e (k p) d -> p e k d", p=P))], later_in=big_loaded)
            with ExitStack() as st3:
                c3 = Core(nc, st3, "l1k")
                acc = c3.ps("acc", [P, 2, GW])
                acc_ready, acc_done = c3.sem("acc_ready"), c3.sem("acc_done")
                with nc.Block() as block:

                    @block.tensor
                    def _(pe):
                        pe.sem_inc(acc_done, 2)
                        with pe.Fori(0, NG // 2) as pair:
                            for k in range(2):
                                pe.wait_ge(acc_done, pair * 2 + (k + 1))
                                nc.tensor.matmul(acc[:, k], small[:, 1], keep.x_T[:, ds((pair * 2 + k) * GW, GW)], start=True, stop=True)\
                                    .then_inc(acc_ready, 1)

                    @block.scalar
                    def _(act):
                        with act.Fori(0, NG // 2) as pair:
                            for k in range(2):
                                act.wait_ge(acc_ready, pair * 2 + (k + 1))
                                nc.scalar.activation(kT[:, ds((pair * 2 + k) * GW, GW)], acc[:, k], ACT.Identity, bias=cols[:, 1:2]).then_inc(acc_done, 1)

            with ExitStack() as st3:
                c3 = Core(nc, st3, "l1m")
                prob = c3.sb("prob", [P, 2, S])
                probT = c3.sb("probT", [P, 2, S])
                negmax, total, share = c3.sb("negmax", [P, 2]), c3.sb("total", [P, 2]), c3.sb("share", [P, 2])
                res = c3.sb("res", [P, 2, D])
                sc = c3.ps("sc", [P, 2, S])
                out = c3.ps("out", [P, 2, GW])
                fin = c3.ps("fin", [P, 2, GW])
                sc_ready, max_done, p_ready = c3.sem("sc_ready"), c3.sem("max_done"), c3.sem("p_ready")
                t_ready, t_done, out_ready, share_done = c3.sem("t_ready"), c3.sem("t_done"), c3.sem("out_ready"), c3.sem("share_done")
                res_ready, fin_ready, fin_done, scaled = c3.sem("res_ready"), c3.sem("fin_ready"), c3.sem("fin_done"), c3.sem("scaled")
                v3 = v_tok[:].rearrange("p (t d) -> p t d", d=D)
                with nc.Block() as block:

                    @block.tensor
                    def _(pe):
                        pe.sem_inc(fin_done, 1)
                        with pe.Fori(0, B) as b:
                            for f in range(2):
                                pe.wait_ge(t_done, b * 2)
                                for o in range(2):
                                    ins = nc.tensor.matmul(sc[:, f, o * GW:(o + 1) * GW], qblk[:].rearrange("p h q -> p (h q)")[:, f * P:(f + 1) * P],
                                                           kT[:, ds(b * S + o * GW, GW)], start=True, stop=True)
                                ins.then_inc(sc_ready, 1)
                            for f in range(2):
                                pe.wait_ge(p_ready, b * 2 + (f + 1))
                                for t in range(S // P):
                                    ins = nc.tensor.transpose(sc[:, f, t * P:(t + 1) * P], prob[:, f, t * P:(t + 1) * P], keep.ident[:])
                                ins.then_inc(t_ready, 1)
                            for f in range(2):
                                pe.wait_ge(t_done, b * 2 + (f + 1))
                                pe.wait_ge(res_ready, b * 2)
                                for t in range(S // P):
                                    ins = nc.tensor.matmul(out[:, f, 0:D], probT[:, f, t * P:(t + 1) * P], v_tok[:, ds(b * S + t * P, D)],
                                                           start=(t == 0), stop=(t == S // P - 1))
                                ins.then_inc(out_ready, 1)
                            pe.wait_ge(res_ready, b * 2 + 2)
                            pe.wait_ge(fin_done, b + 1)
                            for f in range(2):
                                ins = nc.tensor.matmul(fin[:, 0, 0:SLOTS], res[:, f], fold[:], start=(f == 0), stop=(f == 1))
                            ins.then_inc(fin_ready, 1)

                    @block.scalar
                    def _(act):
                        with act.Fori(0, B) as b:
                            for f in range(2):
                                act.wait_ge(scaled, b * 2 + (f + 1))
                                act.wait_ge(t_ready, b * 2)
                                nc.scalar.activation(prob[:, f], sc[:, f], ACT.Exp, bias=share[:, f:f + 1], scale=INV,
                                                     accum_out=total[:, f:f + 1]).then_inc(p_ready, 1)
                            for f in range(2):
                                act.wait_ge(t_ready, b * 2 + (f + 1))
                                act.wait_ge(out_ready, b * 2)
                                nc.scalar.copy(probT[:, f], sc[:, f]).then_inc(t_done, 1)

                    @block.vector
                    def _(dve):
                        with dve.Fori(0, B) as b:
                            for f in range(2):
                                dve.wait_ge(sc_ready, b * 2 + (f + 1))
                                nc.vector.tensor_reduce(negmax[:, f:f + 1], sc[:, f], AX.X, ALU.max, negate=True).then_inc(max_done, 1)
                                dve.wait_ge(max_done, b * 2 + (f + 1))
                                nc.vector.tensor_scalar(share[:, f:f + 1], negmax[:, f:f + 1], INV, None, ALU.mult).then_inc(scaled, 1)
                            for f in range(2):
                                dve.wait_ge(out_ready, b * 2 + (f + 1))
                                nc.vector.reciprocal(negmax[:, f:f + 1], total[:, f:f + 1]).then_inc(share_done, 1)
                                dve.wait_ge(share_done, b * 2 + (f + 1))
                                dve.wait_ge(fin_ready, b)
                                nc.vector.scalar_tensor_tensor(out=res[:, f], in0=out[:, f, 0:D], scalar=negmax[:, f:f + 1], in1=own[:, f],
                                                               op0=ALU.mult, op1=ALU.mult).then_inc(res_ready, 1)
                            dve.wait_ge(fin_ready, b + 1)
                            nc.vector.tensor_copy(attT[:, ds(b * SLOTS, SLOTS)], fin[:, 0, 0:SLOTS]).then_inc(fin_done, 1)

        with ExitStack() as st2:
            c2 = Core(nc, st2, "l1e")
            o_tok, h_tok = c2.sb("o_tok", [BS, D]), c2.sb("h_tok", [BS, D])
            stat, mv = c2.sb("stat", [BS, 6]), c2.sb("mv", [BS, 2])
            std = c2.sb("std", [BS, 1])
            hT = c2.sb("hT", [P, SLOTS, CT])
            b1, bg = c2.sb("b1", [P, ROUNDS, F]), c2.sb("bg", [P, ROUNDS, F])
            uu, gg = c2.sb("uu", [P, ROUNDS, F]), c2.sb("gg", [P, ROUNDS, F])
            loaded = c2.sem("loaded")
            hidT = c2.sb("hidT", [P, ROUNDS, NF, P])
            fell = c2.sb("fell", [P, ROUNDS, D])
            kvT = c2.sb("kvT", [P, 2, BS])
            bank = c2.ps("bank", [P, 2 * ROUNDS, GW])
            dve_sem, pe_sem, act_sem, padded = c2.sem("dve"), c2.sem("pe"), c2.sem("act"), c2.sem("padded")
            raw_ready, biased, lit, joined = c2.sem("raw_ready"), c2.sem("biased"), c2.sem("lit"), c2.sem("joined")
            turned, copied, down_ready, down_copied = c2.sem("turned"), c2.sem("copied"), c2.sem("down_ready"), c2.sem("down_copied")
            by_batch = lambda x: x.rearrange("p (b e) -> p b e", b=B)
            with nc.Block() as block:

                @block.sync
                def _(sp):
                    sp.dma_start(b1[:].rearrange("p r f -> p (r f)"), a["L1_ffn_b1_rows"]).then_inc(loaded, 16)
                    sp.dma_start(bg[:].rearrange("p r f -> p (r f)"), a["L1_ffn_bg_rows"]).then_inc(loaded, 16)

                @block.gpsimd
                def _(pool):
                    nc.gpsimd.memset(hT[:], 0.0).then_inc(padded, 1)

                @block.tensor
                def _(pe):
                    def down(r):
                        pe.wait_ge(copied, r + 1)
                        for q in range(4):
                            for f in range(NF):
                                ins = nc.tensor.matmul(bank[q * CT:(q + 1) * CT, ROUNDS + r, 0:D], hidT[:, r, f, q * CT:(q + 1) * CT],
                                                       w2[:, r * 4 + q, f], start=(f == 0), stop=(f == NF - 1))
                        ins.then_inc(down_ready, 1)

                    nc.tensor.matmul(bank[:, 0, 0:BS], small[:, 2], attT[:], start=True, stop=True).then_inc(pe_sem, 1)
                    pe.wait_ge(dve_sem, 2)
                    nc.tensor.transpose(bank[0:BS, 1, 0:D], o_T[:], keep.ident[:]).then_inc(pe_sem, 1)
                    pe.wait_ge(dve_sem, 8)
                    nc.tensor.transpose(bank[:, 2, 0:BS], h_tok[:], keep.ident[0:BS, 0:BS]).then_inc(pe_sem, 1)
                    pe.wait_ge(dve_sem, 9)
                    pe.wait_ge(big_loaded, 48)
                    for r in range(ROUNDS):
                        for place, w in ((r, w1), (ROUNDS + r, wg)):
                            for q in range(4):
                                e = r * 4 + q
                                ins = nc.tensor.matmul(bank[q * CT:(q + 1) * CT, place], hT[:, e], w[:, e], start=True, stop=True)
                        ins.then_inc(raw_ready, 1)
                    for r in range(ROUNDS):
                        pe.wait_ge(joined, r + 1)
                        for f in range(NF):
                            ins = nc.tensor.transpose(bank[:, r, f * P:(f + 1) * P], uu[:, r, f * P:(f + 1) * P], keep.ident[:])
                        ins.then_inc(turned, 1)
                        if r:
                            down(r - 1)
                    down(ROUNDS - 1)
                    for r in range(ROUNDS):
                        pe.wait_ge(down_copied, r + 1)
                        ins = nc.tensor.transpose(bank[:, 0, r * P:(r + 1) * P], fell[:, r], keep.ident[:])
                    ins.then_inc(pe_sem, 1)
                    pe.wait_ge(dve_sem, 11)
                    nc.tensor.matmul(bank[:, 1, 0:BS], small[:, 4], o2T[:], start=True, stop=True)
                    nc.tensor.matmul(bank[:, 1, BS:2 * BS], small[:, 5], o2T[:], start=True, stop=True).then_inc(pe_sem, 1)
                    pe.wait_ge(dve_sem, 13 + 2 * B)
                    for b in range(B):
                        for f in range(2):
                            ins = nc.tensor.matmul(bank[:, 2 + f, b * D:(b + 1) * D],
                                                   vblk[:, b].rearrange("p h k -> p (h k)")[:, f * P:(f + 1) * P], small[:, 6], start=True, stop=True)
                    ins.then_inc(pe_sem, 1)

                @block.scalar
                def _(act):
                    act.wait_ge(dve_sem, 4)
                    nc.scalar.activation(std[:], mv[:, 1:2], ACT.Sqrt, bias=keep.eps[0:BS]).then_inc(act_sem, 1)
                    for r in range(ROUNDS):
                        act.wait_ge(biased, r + 1)
                        nc.scalar.activation(uu[:, r], uu[:, r], ACT.Silu)
                        nc.scalar.activation(gg[:, r], gg[:, r], ACT.Silu).then_inc(lit, 1)
                    for r in range(ROUNDS):
                        act.wait_ge(turned, r + 1)
                        nc.scalar.copy(hidT[:, r].rearrange("p f c -> p (f c)"), bank[:, r]).then_inc(copied, 1)

                @block.vector
                def _(dve):
                    ch = Chain(dve, dve_sem)
                    dve.wait_ge(pe_sem, 1)
                    ch.step(nc.vector.tensor_scalar(o_T[:], bank[:, 0, 0:BS], cols[:, 2:3], None, ALU.add))
                    ch.step(nc.vector.tensor_tensor(by_batch(o_T[:]), by_batch(o_T[:]), slot_T[:].unsqueeze(1).to_broadcast([P, B, SLOTS]), ALU.add))
                    dve.wait_ge(pe_sem, 2)
                    ch.step(nc.vector.bn_stats(stat[:], bank[0:BS, 1, 0:D]))
                    ch.step(nc.vector.bn_aggr(mv[:], stat[:]))
                    dve.wait_ge(act_sem, 1)
                    ch.step(nc.vector.reciprocal(std[:], std[:]))
                    ch.step(nc.vector.tensor_scalar(h_tok[:], bank[0:BS, 1, 0:D], mv[:, 0:1], std[:], ALU.subtract, ALU.mult))
                    ch.step(nc.vector.tensor_tensor(h_tok[:], h_tok[:], ln_g[:], ALU.mult))
                    ch.step(nc.vector.tensor_tensor(h_tok[:], h_tok[:], ln_b[:], ALU.add))
                    dve.wait_ge(pe_sem, 3)
                    dve.wait_ge(padded, 1)
                    ch.step(nc.vector.tensor_copy(hT[:, :, 0:B].rearrange("p e b -> p b e"), by_batch(bank[:, 2, 0:BS])))

                    def join(r):
                        dve.wait_ge(lit, r + 1)
                        nc.vector.tensor_tensor(uu[:, r], uu[:, r], gg[:, r], ALU.mult).then_inc(joined, 1)

                    dve.wait_ge(loaded, 32)
                    for r in range(ROUNDS):
                        dve.wait_ge(raw_ready, r + 1)
                        nc.vector.tensor_tensor(uu[:, r], bank[:, r], b1[:, r], ALU.add)
                        nc.vector.tensor_tensor(gg[:, r], bank[:, ROUNDS + r], bg[:, r], ALU.add).then_inc(biased, 1)
                        if r:
                            join(r - 1)
                    join(ROUNDS - 1)
                    for r in range(ROUNDS):
                        dve.wait_ge(down_ready, r + 1)
                        nc.vector.tensor_copy(fell[:, r], bank[:, ROUNDS + r, 0:D]).then_inc(down_copied, 1)
                    dve.wait_ge(pe_sem, 4)
                    e_out = bank[:, 0].rearrange("p (r q z) -> p z r q", r=ROUNDS, z=CT)[:, 0:B]
                    four = lambda x: x.rearrange("p (b r q) -> p b r q", b=B, q=4)
                    ch.step(nc.vector.tensor_tensor(four(o2T[:]), e_out, four(o_T[:]), ALU.add))
                    ch.step(nc.vector.tensor_tensor(by_batch(o2T[:]), by_batch(o2T[:]), b2T[:].unsqueeze(1).to_broadcast([P, B, SLOTS]), ALU.add))
                    dve.wait_ge(pe_sem, 5)
                    for m in range(2):
                        ch.step(nc.vector.tensor_scalar(kvT[:, m], bank[:, 1, m * BS:(m + 1) * BS], cols[:, 4 + m:5 + m], None, ALU.add))
                    for b in range(B):
                        for m, dst in enumerate((kblk, vblk)):
                            ch.step(nc.vector.tensor_tensor(dst[:, b], kvT[:, m, b * SLOTS:(b + 1) * SLOTS].unsqueeze(1).to_broadcast([P, H, SLOTS]),
                                                            head_mask[:].unsqueeze(2).to_broadcast([P, H, SLOTS]), ALU.mult))
                    dve.wait_ge(pe_sem, 6)
                    for f in range(2):
                        ch.step(nc.vector.tensor_copy(vw[:, :, f], bank[:, 2 + f].rearrange("p (b d) -> p b d", b=B)))

        with ExitStack() as st2:
            c2 = Core(nc, st2, "l1c")
            PB = S // (2 * P)
            qT = c2.sb("qT", [P, 2, GW])
            z, e = c2.sb("z", [P, 2, GW]), c2.sb("e", [P, 2, GW])
            top, total = c2.sb("top", [P, 2, 2 * H]), c2.sb("total", [P, 2, 2 * H])
            pT = c2.sb("pT", [P, 2, GW])
            sums = c2.sb("sums", [P, 2, 2 * D])
            qp = c2.ps("qp", [P, GW])
            sc = c2.ps("sc", [P, 2, GW])
            tp = c2.ps("tp", [P, 2, GW])
            out = c2.ps("out", [P, 2, GW])
            q_ready, q_done = c2.sem("q_ready"), c2.sem("q_done")
            sc_ready, sc_done, top_done, raised = c2.sem("sc_ready"), c2.sem("sc_done"), c2.sem("top_done"), c2.sem("raised")
            normed, t_ready, t_done, out_ready = c2.sem("normed"), c2.sem("t_ready"), c2.sem("t_done"), c2.sem("out_ready")
            out_done, added, sum_done = c2.sem("out_done"), c2.sem("added"), c2.sem("sum_done")
            k3 = kblk[:].rearrange("p b h k -> p (b h k)")
            vw3 = vw[:].rearrange("p b f d -> p (b f d)")
            heads = lambda x: x.rearrange("p (g k) -> p g k", k=SLOTS)
            wide = lambda x: x.unsqueeze(2).to_broadcast([P, 2 * H, SLOTS])

            def over_batches(engine, part):
                part(0, True, False)
                with engine.Fori(1, B - 1) as b:
                    part(b, False, False)
                part(B - 1, False, True)

            def shifted(b, i, steps):
                return b + (i + steps) // PB, (i + steps) % PB

            with nc.Block() as block:

                @block.tensor
                def _(pe):
                    pe.sem_inc(sc_done, 2)
                    pe.sem_inc(t_done, 2)
                    pe.sem_inc(t_ready, 2)
                    pe.sem_inc(out_done, 2)
                    pe.sem_inc(out_ready, 2)

                    def queries(b, half):
                        pe.wait_ge(q_done, b * 2 + half)
                        nc.tensor.matmul(qp[:], small[:, 3], keep.x_T[:, ds((b * 2 + half) * GW, GW)], start=True, stop=True).then_inc(q_ready, 1)

                    def scores(b, i):
                        k = i % 2
                        pe.wait_ge(q_done, b * 2 + (i // 2 + 1))
                        pe.wait_ge(sc_done, b * PB + (i + 1))
                        for t in range(2):
                            ins = nc.tensor.matmul(sc[:, k, t * HQ:(t + 1) * HQ], qT[:, i // 2, (k * 2 + t) * P:(k * 2 + t + 1) * P],
                                                   k3[:, ds(b * HQ, HQ)], start=True, stop=True)
                        ins.then_inc(sc_ready, 1)

                    def turn(b, i):
                        k = i % 2
                        pe.wait_ge(normed, b * PB + (i + 1))
                        pe.wait_ge(t_done, b * PB + (i + 1))
                        for t in range(4):
                            ins = nc.tensor.transpose(tp[:, k, t * P:(t + 1) * P], e[:, k, t * P:(t + 1) * P], keep.ident[:])
                        ins.then_inc(t_ready, 1)

                    def finish(b, i):
                        k = i % 2
                        pe.wait_ge(t_done, b * PB + (i + 3))
                        pe.wait_ge(out_done, b * PB + (i + 1))
                        for t in range(2):
                            for f in range(2):
                                ins = nc.tensor.matmul(out[:, k, t * D:(t + 1) * D], pT[:, k, (t * 2 + f) * P:(t * 2 + f + 1) * P],
                                                       vw3[:, ds(b * (2 * D) + f * D, D)], start=(f == 0), stop=(f == 1))
                        ins.then_inc(out_ready, 1)

                    def batch(b, first, last):
                        for i in range(PB):
                            k = i % 2
                            if not (last and i == PB - 1):
                                scores(*shifted(b, i, 1))
                            if k == 0 and not (last and i == 2):
                                queries(b + i // 2, 1 - i // 2)
                            if not (first and i == 0):
                                turn(*shifted(b, i, -1))
                            if not (first and i < 2):
                                finish(*shifted(b, i, -2))

                    queries(0, 0)
                    scores(0, 0)
                    over_batches(pe, batch)
                    turn(B - 1, PB - 1)
                    finish(B - 1, PB - 2)
                    finish(B - 1, PB - 1)

                @block.scalar
                def _(act):
                    def queries(b, half):
                        act.wait_ge(q_ready, b * 2 + (half + 1))
                        nc.scalar.activation(qT[:, half], qp[:], ACT.Identity, bias=cols[:, 3:4]).then_inc(q_done, 1)

                    def take(b, i):
                        act.wait_ge(t_ready, b * PB + (i + 3))
                        act.wait_ge(out_ready, b * PB + (i + 1))
                        nc.scalar.copy(pT[:, i % 2], tp[:, i % 2]).then_inc(t_done, 1)

                    def raise_(b, i):
                        act.wait_ge(sc_done, b * PB + (i + 3))
                        nc.scalar.activation(z[:, i % 2], z[:, i % 2], ACT.Exp, scale=INV).then_inc(raised, 1)

                    def batch(b, first, last):
                        for i in range(PB):
                            k = i % 2
                            if not (last and i == PB - 1):
                                raise_(*shifted(b, i, 1))
                            if k == 0 and not (last and i == 2):
                                queries(b + i // 2, 1 - i // 2)
                            if not (first and i == 0):
                                take(*shifted(b, i, -1))

                    queries(0, 0)
                    raise_(0, 0)
                    over_batches(act, batch)
                    take(B - 1, PB - 1)

                @block.vector
                def _(dve):
                    def shift(b, i):
                        k, n = i % 2, b * PB + i
                        dve.wait_ge(sc_ready, n + 1)
                        nc.vector.tensor_reduce(top[:, k], heads(sc[:, k]), AX.X, ALU.max).then_inc(top_done, 1)
                        dve.wait_ge(top_done, n + 1)
                        nc.vector.tensor_tensor(heads(z[:, k]), heads(sc[:, k]), wide(top[:, k]), ALU.subtract).then_inc(sc_done, 1)

                    def add(b, i):
                        k, n = i % 2, b * PB + i
                        dve.wait_ge(out_ready, n + 3)
                        nc.vector.tensor_tensor(sums[:, k].rearrange("p (t d) -> p t d", d=D), out[:, k, 0:2 * D].rearrange("p (t d) -> p t d", d=D),
                                                c_bo[:].unsqueeze(1).to_broadcast([P, 2, D]), ALU.add).then_inc(out_done, 1)
                        dve.wait_ge(out_done, n + 3)
                        x = keep.x_tok[:, ds(b * S + i * (2 * D), 2 * D)]
                        nc.vector.tensor_tensor(x, x, sums[:, k], ALU.add).then_inc(added, 1)

                    def batch(b, first, last):
                        for i in range(PB):
                            k, n = i % 2, b * PB + i
                            if not (last and i == PB - 1):
                                shift(*shifted(b, i, 1))
                            if not (first and i < 3):
                                add(*shifted(b, i, -3))
                            dve.wait_ge(raised, n + 1)
                            nc.vector.tensor_reduce(total[:, k], heads(z[:, k]), AX.X, ALU.add).then_inc(sum_done, 1)
                            dve.wait_ge(sum_done, n * 2 + 1)
                            nc.vector.reciprocal(total[:, k], total[:, k]).then_inc(sum_done, 1)
                            dve.wait_ge(sum_done, n * 2 + 2)
                            dve.wait_ge(t_ready, n + 1)
                            nc.vector.tensor_tensor(heads(e[:, k]), heads(z[:, k]), wide(total[:, k]), ALU.mult).then_inc(normed, 1)

                    shift(0, 0)
                    over_batches(dve, batch)
                    for i in range(PB - 3, PB):
                        add(B - 1, i)


def project_tokens(nc, keep, tag, src_T, w_dram, out, scaled=(), loads=(), bias_dram=None, add=False, later=(), later_in=None):
    with ExitStack() as st:
        c = Core(nc, st, tag + "pt")
        w = c.sb("w", [P, D])
        bias = c.sb("bias", [P, D]) if bias_dram is not None else None
        staged = c.sb("staged", [P, 2, GW])
        acc = c.ps("acc", [P, 2, GW])
        sums = c.sb("sums", [P, 2, GW]) if add else None
        biased = c.sem("biased")
        loaded, w_loaded, staged_ready = c.sem("loaded"), c.sem("w_loaded"), c.sem("staged_ready")
        acc_ready, acc_done, scale_done = c.sem("acc_ready"), c.sem("acc_done"), c.sem("scale_done")
        with nc.Block() as block:

            @block.sync
            def _(sp):
                sp.dma_start(w[:], w_dram).then_inc(w_loaded, 16)
                if bias_dram is not None:
                    sp.dma_start(bias[:], bias_dram.rearrange("(o d) -> o d", o=1).broadcast_to([P, D])).then_inc(w_loaded, 16)
                for dst, src in loads:
                    sp.dma_start(dst, src).then_inc(loaded, 16)
                for dst, src in later:
                    sp.dma_start(dst, src).then_inc(later_in, 16)
                if loads:
                    sp.wait_ge(loaded, 16 * len(loads))

            @block.scalar
            def _(act):
                with act.Fori(0, NG // 2) as pair:
                    for k in range(2):
                        act.wait_ge(acc_ready, pair * 2 + (k + 1))
                        nc.scalar.copy(staged[:, k], src_T[:, ds((pair * 2 + k) * GW, GW)]).then_inc(staged_ready, 1)

            @block.tensor
            def _(pe):
                pe.sem_inc(acc_ready, 2)
                pe.sem_inc(acc_done, 2)
                pe.wait_ge(w_loaded, 16 if bias_dram is None else 32)
                with pe.Fori(0, NG // 2) as pair:
                    for k in range(2):
                        pe.wait_ge(staged_ready, pair * 2 + (k + 1))
                        pe.wait_ge(acc_done, pair * 2 + (k + 1))
                        for j in range(TG):
                            ins = nc.tensor.matmul(acc[:, k, j * D:(j + 1) * D], staged[:, k, j * P:(j + 1) * P], w[:],
                                                   start=True, stop=True)
                        ins.then_inc(acc_ready, 1)

            @block.vector
            def _(dve):
                with dve.Fori(0, NG // 2) as pair:
                    for k in range(2):
                        dve.wait_ge(acc_ready, pair * 2 + (k + 3))
                        dst = out[:, ds((pair * 2 + k) * GW, GW)]
                        if bias is None:
                            nc.vector.tensor_copy(dst, acc[:, k]).then_inc(acc_done, 1)
                            continue
                        wide = lambda x: x.rearrange("p (t d) -> p t d", d=D)
                        to = sums[:, k] if add else dst
                        nc.vector.tensor_tensor(wide(to), wide(acc[:, k]), bias[:].unsqueeze(1).to_broadcast([P, TG, D]),
                                                ALU.add).then_inc(acc_done, 1)
                        if add:
                            dve.wait_ge(acc_done, pair * 2 + (k + 3))
                            nc.vector.tensor_tensor(dst, dst, sums[:, k], ALU.add).then_inc(biased, 1)
                            dve.wait_ge(biased, pair * 2 + (k + 1))
                if loads:
                    dve.wait_ge(loaded, 16 * len(loads))
                for tile, factor in scaled:
                    nc.vector.tensor_scalar(tile, tile, factor, None, ALU.mult).then_inc(scale_done, 1)


def layer2_attn(nc, keep, a):
    SL, KS, VD = 8, 64, 16
    VP = 32
    HEADS = B * S // P
    Q = SL * P
    with ExitStack() as st:
        c = Core(nc, st, "l2a")
        mq, mk = c.sb("mq", [P, SL * KS]), c.sb("mk", [P, SL * KS])
        xv = c.sb("xv", [P, NT * D])
        project_tokens(nc, keep, "l2a", keep.x_T, a["L2_attn_Mv"], xv, scaled=[(mq[:], 1.0 / math.sqrt(KS))],
                       loads=[(mq[:], a["L2_attn_Mq"]), (mk[:], a["L2_attn_Mk"])])
        kT, qT = c.sb("kT", [KS, 2, Q]), c.sb("qT", [KS, 2, Q])
        RING = 4
        pT = c.sb("pT", [P, RING, Q])
        vs = c.sb("vs", [P, RING, SL, VP])
        negmax, total, share = c.sb("negmax", [P, 2]), c.sb("total", [P, RING]), c.sb("share", [P, RING])
        outT = c.sb("outT", [P, 2, 2 * P])
        xv3 = xv[:].rearrange("p (t d) -> p t d", d=D)
        sc = c.ps("sc", [P, 2, Q])
        pj = c.ps("pj", [P, 2, GW])
        out = c.ps("out", [P, 2, GW])
        qk_ready, max_done, p_ready = c.sem("qk_ready"), c.sem("max_done"), c.sem("p_ready")
        share_done, v_ready, pv_done = c.sem("share_done"), c.sem("v_ready"), c.sem("pv_done")
        pj_ready, pj_done, out_done = c.sem("pj_ready"), c.sem("pj_done"), c.sem("out_done")
        outT_ready, fin_ready, padded = c.sem("outT_ready"), c.sem("fin_ready"), c.sem("padded")

        def over_heads(engine, part):
            part(0, 0, True, False)
            part(1, 1, False, False)
            with engine.Fori(1, HEADS // 2 - 1) as pair:
                for q in range(2):
                    part(pair * 2 + q, q, False, False)
            part(HEADS - 2, 0, False, False)
            part(HEADS - 1, 1, False, True)

        with nc.Block() as block:

            @block.gpsimd
            def _(pool):
                nc.gpsimd.memset(vs[:].rearrange("p r j v -> p (r j) v")[:, :, VD:VP], 0.0).then_inc(padded, 1)
                pool.wait_ge(padded, 1)

            @block.tensor
            def _(pe):
                pe.sem_inc(p_ready, 2)
                pe.sem_inc(pv_done, RING)
                pe.sem_inc(out_done, 2)
                pe.wait_ge(padded, 1)

                def project(n):
                    pe.wait_ge(pj_done, n * 4)
                    for m, w in enumerate((mk, mq)):
                        for jj in range(SL // 2):
                            ins = nc.tensor.matmul(pj[:, m, jj * P:(jj + 1) * P], w[:, jj * P:(jj + 1) * P],
                                                   keep.x_T[:, ds(n * P, P)], start=True, stop=True)
                    ins.then_inc(pj_ready, 1)

                def values(n, q, kt):
                    pe.wait_ge(v_ready, n * SL + (kt + 1))
                    if kt == 0:
                        pe.wait_ge(out_done, n + 1)
                    for j in range(SL):
                        g, half = j % 4, j // 4
                        ins = nc.tensor.matmul(out[g * VP:(g + 1) * VP, q, half * P:(half + 1) * P], vs[:, kt % RING, j],
                                               pT[:, kt % RING, j * P:(j + 1) * P], start=(kt == 0 and half == 0),
                                               stop=(kt == SL - 1), skip_group_check=True)
                    ins.then_inc(pv_done, 1)

                def turn(n, q):
                    pe.wait_ge(outT_ready, n + 1)
                    for half in range(2):
                        ins = nc.tensor.transpose(out[:, q, (2 + half) * P:(3 + half) * P], outT[:, q, half * P:(half + 1) * P],
                                                  keep.ident[:])
                    ins.then_inc(fin_ready, 1)

                def head(n, q, first, last):
                    pe.wait_ge(pj_done, n * 4 + 4)
                    for kt in range(SL):
                        pe.wait_ge(p_ready, n * SL + (kt + 1))
                        for o in range(Q // GW):
                            ins = nc.tensor.matmul(sc[:, kt % 2, o * GW:(o + 1) * GW], kT[:, q, kt * P:(kt + 1) * P],
                                                   qT[:, q, o * GW:(o + 1) * GW], start=True, stop=True)
                        ins.then_inc(qk_ready, 1)
                        if kt >= 2:
                            values(n, q, kt - 2)
                        elif not first:
                            values(n - 1, 1 - q, SL - 2 + kt)
                        if kt == 2 and not last:
                            project(n + 1)
                        if kt == 3 and not first:
                            turn(n - 1, 1 - q)

                project(0)
                over_heads(pe, head)
                values(HEADS - 1, 1, SL - 2)
                values(HEADS - 1, 1, SL - 1)
                turn(HEADS - 1, 1)

            @block.scalar
            def _(act):
                def evacuate(n, q):
                    act.wait_ge(pj_ready, n + 1)
                    for m, dst in enumerate((kT, qT)):
                        d4 = dst[:, q].rearrange("k (j two r) -> k j two r", two=2, r=P)
                        for par in range(2):
                            nc.scalar.copy(d4[:, :, par], pj[par * KS:(par + 1) * KS, m].rearrange("k (j r) -> k j r", r=P))\
                                .then_inc(pj_done, 1)

                def result(n, q):
                    act.wait_ge(pv_done, n * SL + (SL + RING))
                    nc.scalar.copy(outT[:, q], out[:, q, 0:2 * P]).then_inc(outT_ready, 1)

                def head(n, q, first, last):
                    for kt in range(SL):
                        i = n * SL + kt
                        act.wait_ge(max_done, i + 1)
                        act.wait_ge(pv_done, i + 1)
                        nc.scalar.activation(pT[:, kt % RING], sc[:, kt % 2], ACT.Exp, bias=negmax[:, kt % 2:kt % 2 + 1],
                                             accum_out=total[:, kt % RING:kt % RING + 1]).then_inc(p_ready, 1)
                        if kt == 2 and not first:
                            result(n - 1, 1 - q)
                        if kt == 4 and not last:
                            evacuate(n + 1, 1 - q)

                evacuate(0, 0)
                over_heads(act, head)
                result(HEADS - 1, 1)

            @block.vector
            def _(dve):
                def head(n, q, first, last):
                    for kt in range(SL):
                        dve.wait_ge(qk_ready, n * SL + (kt + 1))
                        nc.vector.tensor_reduce(negmax[:, kt % 2:kt % 2 + 1], sc[:, kt % 2], AX.X, ALU.max,
                                                negate=True).then_inc(max_done, 1)
                        if kt:
                            apply(n, kt - 1)
                        elif not first:
                            apply(n - 1, SL - 1)
                        if kt == 4 and not first:
                            take(n - 1, 1 - q)

                def apply(n, kt):
                    r = kt % RING
                    dve.wait_ge(p_ready, n * SL + (kt + 3))
                    nc.vector.reciprocal(share[:, r:r + 1], total[:, r:r + 1]).then_inc(share_done, 1)
                    dve.wait_ge(share_done, n * SL + (kt + 1))
                    v = xv3[:, ds(n // SL * SL, SL), kt * VD:(kt + 1) * VD]
                    nc.vector.tensor_scalar(vs[:, r, :, 0:VD], v, share[:, r:r + 1], None, ALU.mult).then_inc(v_ready, 1)

                def take(n, q):
                    dve.wait_ge(fin_ready, n + 1)
                    x = keep.x_tok[:, ds(n * D, D)].rearrange("p (j d) -> p j d", d=VD)
                    res = out[:, q, 2 * P:4 * P].rearrange("p (j d) -> p j d", d=VP)[:, :, 0:VD]
                    nc.vector.tensor_tensor(x, res, x, ALU.add).then_inc(out_done, 1)

                over_heads(dve, head)
                apply(HEADS - 1, SL - 1)
                take(HEADS - 1, 1)


def layer2_ffn(nc, keep, a):
    E, F = 8, 512
    nf = F // P
    with ExitStack() as st:
        c = Core(nc, st, "l2f")
        up, gate = c.sb("up", [P, E, F]), c.sb("gate", [P, E, F])
        down = c.sb("down", [P, E, nf, D])
        logits, probs, comb = c.sb("logits", [P, NT * 8]), c.sb("probs", [P, NT * 8]), c.sb("comb", [P, NT * 8])
        weights_in = c.sem("weights_in")
        router(nc, keep, "l2f", logits, a["L2_ffn_router_w"], None,
               [(up[:, 0:E - 1], a["L2_ffn_up_w"].rearrange("e d f -> d e f")),
                (up[:, E - 1], a["L2_ffn_shared_up_w"]),
                (gate[:, 0:E - 1], a["L2_ffn_gate_w"].rearrange("e d f -> d e f")),
                (gate[:, E - 1], a["L2_ffn_shared_gate_w"]),
                (down[:, 0:E - 1], a["L2_ffn_down_w"].rearrange("e (k p) d -> p e k d", p=P)),
                (down[:, E - 1], a["L2_ffn_shared_down_w"].rearrange("(k p) d -> p k d", p=P))], weights_in)
        softmax8(nc, keep, "l2f", logits, probs)
        pick_top(nc, keep, "l2f", probs, comb, 1, scale_top=2.0)
        experts(nc, keep, "l2f", comb, weights_in, 6, E, [P] * nf, lambda u, f: up[:, u, f * P:(f + 1) * P],
                lambda u, f: down[:, u, f], 1, ACT.Silu, gate=lambda u, f: gate[:, u, f * P:(f + 1) * P])


def layer3_attn(nc, keep, a):
    H2 = P // 2
    LV = int(math.log2(S))
    two_pi = 2 * math.pi
    C1 = float(np.float32(6.28125))
    C2 = float(np.float32(1.93500518798828125e-3))
    C3 = two_pi - C1 - C2
    MAGIC = 1.5 * 2 ** 23
    with ExitStack() as st:
        c = Core(nc, st, "l3a")
        par = c.sb("par", [P, 3])
        b_ri = c.sb("b_ri", [P, 2, D])
        c_ri = c.sb("c_ri", [P, 2, D])
        dvec = c.sb("dvec", [P, D])
        cosT, sinT = c.sb("cosT", [P, S]), c.sb("sinT", [P, S])
        w12 = c.sb("w12", [P, 2, D])
        v12 = c.sb("v12", [P, 2, D])
        mag = c.sb("mag", [P, 1])
        with ExitStack() as st2:
            c2 = Core(nc, st2, "l3b")
            col = {}
            for name in ("step x y t q em1 g2 re im den gr gi al1 be1 al2 be2 u1 u2 sgn").split():
                col[name] = c2.sb("v_" + name, [P, 1])
            pw, ang, kk = c2.sb("pw", [P, LV]), c2.sb("ang", [P, LV]), c2.sb("kk", [P, LV])
            half, habs = c2.sb("half", [P, LV]), c2.sb("habs", [P, LV])
            sh, chh = c2.sb("sh", [P, LV]), c2.sb("chh", [P, LV])
            cs_, sn_ = c2.sb("cs_", [P, LV]), c2.sb("sn_", [P, LV])
            tmp = c2.sb("tmp", [P, S // 2])
            wrow = c2.sb("wrow", [P, 2, D])
            half_pi = c2.sb("half_pi", [P, 1])
            wT = c2.ps("wT", [P, 2, 512])
            loaded, chain_sem, to_act, from_act = c2.sem("loaded"), c2.sem("chain"), c2.sem("to_act"), c2.sem("from_act")
            rows_ready, turned = c2.sem("rows_ready"), c2.sem("turned")
            v = {k: t[:] for k, t in col.items()}
            with nc.Block() as block:

                @block.sync
                def _(sp):
                    for dst, src in [(par[:], a["L3_attn_par"]), (b_ri[:], a["L3_attn_B_ri"]), (c_ri[:], a["L3_attn_C_ri"]),
                                     (dvec[:], a["L3_attn_D"].rearrange("(o d) -> o d", o=1).broadcast_to([P, D]))]:
                        sp.dma_start(dst, src).then_inc(loaded, 16)
                    sp.wait_ge(loaded, 64)

                @block.scalar
                def _(act):
                    act.wait_ge(loaded, 64)
                    nc.scalar.activation(v["step"], par[:, 2:3], ACT.Exp).then_inc(from_act, 1)
                    act.wait_ge(to_act, 1)
                    nc.scalar.activation(v["t"], v["x"], ACT.Tanh, scale=0.5).then_inc(from_act, 1)
                    act.wait_ge(to_act, 2)
                    nc.scalar.activation(sh[:], half[:], ACT.Sin).then_inc(from_act, 1)
                    nc.scalar.activation(chh[:], habs[:], ACT.Sin).then_inc(from_act, 1)

                @block.tensor
                def _(pe):
                    pe.wait_ge(rows_ready, 1)
                    nc.tensor.transpose(wT[:, 0, 0:D], wrow[:, 0], keep.ident[:])
                    nc.tensor.transpose(wT[:, 1, 0:D], wrow[:, 1], keep.ident[:]).then_inc(turned, 1)

                @block.vector
                def _(dve):
                    ch = Chain(dve, chain_sem)
                    tt = lambda o, x, y_, op: ch.step(nc.vector.tensor_tensor(o, x, y_, op))
                    t1 = lambda o, x, s1, op, s2=None, op1=ALU.bypass: ch.step(nc.vector.tensor_scalar(o, x, s1, s2, op, op1))
                    M, A_, S_ = ALU.mult, ALU.add, ALU.subtract
                    for k in range(LV):
                        ch.step(nc.vector.memset(pw[:, k:k + 1], float(2 ** k)))
                    ch.step(nc.vector.memset(v["sgn"][0:H2], 1.0))
                    ch.step(nc.vector.memset(v["sgn"][H2:P], -1.0))
                    dve.wait_ge(from_act, 1)
                    t1(v["q"], par[:, 0:1], -1e-4, ALU.min)
                    tt(v["y"], par[:, 1:2], v["step"], M)
                    nc.vector.tensor_tensor(v["x"], v["q"], v["step"], M).then_inc(to_act, 1)
                    t1(ang[:], pw[:], v["y"], M)
                    t1(kk[:], ang[:], 1.0 / two_pi, M, MAGIC, A_)
                    t1(kk[:], kk[:], MAGIC, S_)
                    for part in (C1, C2, C3):
                        ch.step(nc.vector.scalar_tensor_tensor(out=ang[:], in0=kk[:], scalar=-part, in1=ang[:], op0=M, op1=A_))
                    t1(half[:], ang[:], 0.5, M, math.pi / 2, ALU.min)
                    t1(half[:], half[:], -math.pi / 2, ALU.max)
                    ch.step(nc.vector.scalar_tensor_tensor(out=habs[:], in0=half[:], scalar=-1.0, in1=half[:], op0=M, op1=ALU.min))
                    nc.vector.tensor_scalar(habs[:], habs[:], math.pi / 2, None, A_).then_inc(to_act, 1)
                    dve.wait_ge(from_act, 2)
                    t1(v["em1"], v["t"], -1.0, M, 1.0, A_)
                    ch.step(nc.vector.reciprocal(v["em1"], v["em1"]))
                    tt(v["em1"], v["em1"], v["t"], M)
                    t1(v["em1"], v["em1"], 2.0, M)
                    t1(mag[:], v["em1"], 1.0, A_)
                    dve.wait_ge(from_act, 4)
                    tt(kk[:], sh[:], sh[:], M)
                    t1(cs_[:], kk[:], -2.0, M, 1.0, A_)
                    ch.step(nc.vector.scalar_tensor_tensor(out=sn_[:], in0=sh[:], scalar=2.0, in1=chh[:], op0=M, op1=M))
                    tt(v["re"], v["em1"], cs_[:, 0:1], M)
                    ch.step(nc.vector.scalar_tensor_tensor(out=v["re"], in0=kk[:, 0:1], scalar=-2.0, in1=v["re"], op0=M, op1=A_))
                    tt(v["im"], mag[:], sn_[:, 0:1], M)
                    lre, lim = v["q"], par[:, 1:2]
                    tt(v["den"], lre, lre, M)
                    ch.step(nc.vector.scalar_tensor_tensor(out=v["den"], in0=lim, scalar=lim, in1=v["den"], op0=M, op1=A_))
                    ch.step(nc.vector.reciprocal(v["den"], v["den"]))
                    tt(v["u1"], v["im"], lim, M)
                    ch.step(nc.vector.scalar_tensor_tensor(out=v["gr"], in0=v["re"], scalar=lre, in1=v["u1"], op0=M, op1=A_))
                    tt(v["gr"], v["gr"], v["den"], M)
                    tt(v["u2"], v["re"], lim, M)
                    ch.step(nc.vector.scalar_tensor_tensor(out=v["gi"], in0=v["im"], scalar=lre, in1=v["u2"], op0=M, op1=S_))
                    tt(v["gi"], v["gi"], v["den"], M)
                    lo, hi = slice(0, H2), slice(H2, P)
                    for dst, half_, src, sign in (("al1", lo, "gr", 1.0), ("be1", lo, "gi", -1.0), ("al1", hi, "gi", 1.0), ("be1", hi, "gr", 1.0),
                                                  ("al2", lo, "gi", 1.0), ("be2", lo, "gr", 1.0), ("al2", hi, "gr", -1.0), ("be2", hi, "gi", 1.0)):
                        t1(v[dst][half_], v[src][half_], sign, M)
                    for n, (al, be) in enumerate((("al1", "be1"), ("al2", "be2"))):
                        t1(wrow[:, n], b_ri[:, 0], v[al], M)
                        ins = nc.vector.scalar_tensor_tensor(out=wrow[:, n], in0=b_ri[:, 1], scalar=v[be], in1=wrow[:, n], op0=M, op1=A_)
                        ch.step(ins)
                    dve.sem_inc(rows_ready, 1)
                    t1(v12[:, 0], c_ri[:, 0], v["sgn"], M)
                    t1(v12[:, 1], c_ri[:, 1], -1.0, M)
                    t1(dvec[:], dvec[:], 1.0, A_)
                    ch.step(nc.vector.memset(cosT[:, 0:1], 1.0))
                    ch.step(nc.vector.memset(sinT[:, 0:1], 0.0))
                    for k in range(LV):
                        w = 2 ** k
                        ck_, sk_ = cs_[:, k:k + 1], sn_[:, k:k + 1]
                        t1(tmp[:, 0:w], sinT[:, 0:w], sk_, M)
                        ch.step(nc.vector.scalar_tensor_tensor(out=cosT[:, w:2 * w], in0=cosT[:, 0:w], scalar=ck_, in1=tmp[:, 0:w], op0=M, op1=S_))
                        t1(tmp[:, 0:w], cosT[:, 0:w], sk_, M)
                        ch.step(nc.vector.scalar_tensor_tensor(out=sinT[:, w:2 * w], in0=sinT[:, 0:w], scalar=ck_, in1=tmp[:, 0:w], op0=M, op1=A_))
                    dve.wait_ge(turned, 1)
                    ch.step(nc.vector.tensor_copy(w12[:], wT[:, :, 0:D]))

        with ExitStack() as st2:
            c2 = Core(nc, st2, "l3c")
            uc, us = c2.sb("uc", [P, 2, GW]), c2.sb("us", [P, 2, GW])
            z, z1, z2 = c2.sb("z", [P, 2, GW]), c2.sb("z1", [P, 2, GW]), c2.sb("z2", [P, 2, GW])
            u = c2.ps("u", [P, 2, 2, GW])
            y = c2.ps("y", [P, 2, GW])
            u_ready, u_turned, summed = c2.sem("u_ready"), c2.sem("u_turned"), c2.sem("summed")
            scanned, back, y_ready, added, skipped = (c2.sem("scanned"), c2.sem("back"), c2.sem("y_ready"), c2.sem("added"), c2.sem("skipped"))
            K2 = range(2)
            with nc.Block() as block:

                @block.tensor
                def _(pe):
                    pe.sem_inc(u_turned, 2)
                    pe.sem_inc(added, 2)
                    pe.sem_inc(y_ready, 2)
                    with pe.Fori(0, B) as b:
                        for k in K2:
                            pe.wait_ge(u_turned, b * 2 + (k + 1))
                            x = keep.x_T[:, ds((b * 2 + k) * GW, GW)]
                            nc.tensor.matmul(u[:, k, 0], w12[:, 0], x, start=True, stop=True)
                            nc.tensor.matmul(u[:, k, 1], w12[:, 1], x, start=True, stop=True).then_inc(u_ready, 1)
                        for k in K2:
                            pe.wait_ge(back, (b * 2 + k) * 2 + 2)
                            pe.wait_ge(added, b * 2 + (k + 1))
                            for j in range(TG):
                                o = slice(j * P, (j + 1) * P)
                                nc.tensor.matmul(y[:, k, o], z1[:, k, o], v12[:, 0], start=True, stop=False)
                                ins = nc.tensor.matmul(y[:, k, o], z2[:, k, o], v12[:, 1], start=False, stop=True)
                            ins.then_inc(y_ready, 1)

                @block.gpsimd
                def _(pool):
                    with pool.Fori(0, B) as b:
                        for k in K2:
                            pool.wait_ge(u_turned, b * 2 + (k + 3))
                            nc.gpsimd.tensor_tensor(uc[:, k], uc[:, k], us[:, k], ALU.add).then_inc(summed, 1)
                        for k in K2:
                            x3 = keep.x_tok[:, ds((b * 2 + k) * GW, GW)].rearrange("p (t d) -> p t d", d=D)
                            nc.gpsimd.tensor_tensor(x3, x3, dvec[:].unsqueeze(1).to_broadcast([P, TG, D]), ALU.mult).then_inc(skipped, 1)
                        for k in K2:
                            o = slice(k * GW, (k + 1) * GW)
                            pool.wait_ge(scanned, b * 2 + (k + 1))
                            pool.wait_ge(y_ready, b * 2 + (k + 1))
                            nc.gpsimd.tensor_tensor(z1[:, k], z[:, k], cosT[:, o], ALU.mult).then_inc(back, 1)
                            nc.gpsimd.tensor_tensor(z2[:, k], z[:, k], sinT[:, o], ALU.mult).then_inc(back, 1)

                @block.vector
                def _(dve):
                    with dve.Fori(0, B) as b:
                        for k in K2:
                            o = slice(k * GW, (k + 1) * GW)
                            dve.wait_ge(u_ready, b * 2 + (k + 1))
                            nc.vector.tensor_tensor(uc[:, k], u[:, k, 0], cosT[:, o], ALU.mult)
                            nc.vector.tensor_tensor(us[:, k], u[:, k, 1], sinT[:, o], ALU.mult).then_inc(u_turned, 1)
                        for k in K2:
                            dve.wait_ge(summed, b * 2 + (k + 1))
                            if k:
                                dve.wait_ge(scanned, b * 2 + k)
                            nc.vector.tensor_tensor_scan(z[:, k], mag[:].to_broadcast([P, GW]), uc[:, k],
                                                         z[:, 0, GW - 1:GW] if k else 0.0, ALU.mult, ALU.add).then_inc(scanned, 1)
                        for k in K2:
                            x = keep.x_tok[:, ds((b * 2 + k) * GW, GW)]
                            dve.wait_ge(y_ready, b * 2 + (k + 3))
                            dve.wait_ge(skipped, b * 2 + (k + 1))
                            nc.vector.tensor_tensor(x, y[:, k], x, ALU.add).then_inc(added, 1)


def top_tokens(nc, keep, tag, probs, comb, count):
    Q = 16
    W = N // Q
    TP = NT // Q
    BITS = 30
    with ExitStack() as st:
        c = Core(nc, st, tag + "tt")
        val = c.sb("val", [P, W])
        ge, eq, before = c.sb("ge", [P, W]), c.sb("eq", [P, W]), c.sb("before", [P, W])
        cnt, carry = c.sb("cnt", [P, 2]), c.sb("carry", [P, 2])
        cut, trial = c.sb("cut", [P, 1], mybir.dt.int32), c.sb("trial", [P, 1], mybir.dt.int32)
        keepbit, room = c.sb("keepbit", [P, 1], mybir.dt.int32), c.sb("room", [P, 1])
        flag = c.sb("flag", [P, 1])
        same, prior = c.sb("same", [P, P]), c.sb("prior", [P, P])
        tmp = c.sb("tmp", [P, P])
        zeros = c.sb("zeros", [P, W])
        spread = c.sb("spread", [P, 8, NT])
        turned = c.ps("turned", [P, 8, 512])
        sums = turned[:, 6]
        chain_sem, pool_sem, masks = c.sem("chain"), c.sem("pool_sem"), c.sem("masks")
        flips, counted, moved = c.sem("flips"), c.sem("counted"), c.sem("moved")
        asked, cast = c.sem("asked"), c.sem("cast")
        with nc.Block() as block:

            @block.gpsimd
            def _(pool):
                ch = Chain(pool, pool_sem)
                ch.step(nc.gpsimd.memset(same[:], 1.0))
                s3 = same[:].rearrange("p (e q) -> p e q", q=Q)
                ch.step(nc.gpsimd.affine_select(out=s3, in_=s3, compare_op=ALU.is_ge, fill=0.0, base=0,
                                                pattern=[[-Q, 8], [0, Q]], channel_multiplier=1))
                ch.step(nc.gpsimd.affine_select(out=s3, in_=s3, compare_op=ALU.is_ge, fill=0.0, base=Q - 1,
                                                pattern=[[Q, 8], [0, Q]], channel_multiplier=-1))
                ch.step(nc.gpsimd.affine_select(out=prior[:], in_=same[:], compare_op=ALU.is_gt, fill=0.0, base=0,
                                                pattern=[[1, P]], channel_multiplier=-1))
                nc.gpsimd.memset(zeros[:], 0.0).then_inc(masks, 1)
                pool.wait_ge(masks, 1)

            p3 = probs[:].rearrange("p (t e) -> p t e", e=8)
            @block.vector
            def _(dve):
                ch = Chain(dve, chain_sem)
                s4 = spread[:].rearrange("p e (q r) -> p r e q", r=TP)
                for r in range(TP):
                    ch.step(nc.vector.tensor_copy(spread[:].rearrange("p (r a) t -> p r (a t)", r=TP)[:, r].rearrange(
                        "p (e q) -> p e q", q=Q), p3.rearrange("p (q r) e -> p r e q", r=TP)[:, r]))
                nc.vector.memset(cut[:], 0).then_inc(asked, 1)
                dve.wait_ge(flips, 1)
                for r in range(TP):
                    ins = nc.vector.tensor_copy(val[:, r * P:(r + 1) * P], turned[:, r, 0:P])
                ch.step(ins)
                dve.wait_ge(masks, 1)
                n = [0]

                def count_from(bits, op, out_tile):
                    ch.step(nc.vector.tensor_scalar(out_tile[:], val[:], bits.bitcast(F32), None, op, ALU.add,
                                                    accum_out=cnt[:, 0:1]))
                    n[0] += 1
                    dve.sem_inc(asked, 1)
                    dve.wait_ge(counted, n[0])

                for bit in reversed(range(BITS)):
                    ch.step(nc.vector.tensor_scalar(trial[:], cut[:], 1 << bit, None, ALU.bitwise_or))
                    count_from(trial[:], ALU.is_ge, ge)
                    ch.step(nc.vector.tensor_scalar(flag[:], sums[:, 0:1], float(count), None, ALU.is_ge))
                    ch.step(nc.vector.tensor_copy(keepbit[:], flag[:]))
                    ch.step(nc.vector.tensor_scalar(keepbit[:], keepbit[:], bit, None, ALU.logical_shift_left))
                    ch.step(nc.vector.tensor_tensor(cut[:], cut[:], keepbit[:], ALU.bitwise_or))
                count_from(cut[:], ALU.is_gt, ge)
                ch.step(nc.vector.tensor_scalar(room[:], sums[:, 0:1], -1.0, float(count), ALU.mult, ALU.add))
                ch.step(nc.vector.tensor_scalar(eq[:], val[:], cut[:].bitcast(F32), None, ALU.is_equal, ALU.add,
                                                accum_out=cnt[:, 0:1]))
                n[0] += 1
                dve.sem_inc(asked, 1)
                dve.wait_ge(counted, n[0])
                ch.step(nc.vector.tensor_copy(carry[:, 0:1], sums[:, 1:2]))
                ch.step(nc.vector.tensor_tensor_scan(before[:], eq[:], zeros[:], carry[:, 0:1], ALU.add, ALU.add))
                ch.step(nc.vector.tensor_scalar(before[:], before[:], room[:], None, ALU.is_le))
                ch.step(nc.vector.tensor_tensor(eq[:], eq[:], before[:], ALU.mult))
                ch.step(nc.vector.tensor_tensor(ge[:], ge[:], eq[:], ALU.add))
                nc.vector.tensor_tensor(val[:], val[:], ge[:], ALU.mult).then_inc(moved, 1)
                dve.wait_ge(flips, 2)
                for r in range(TP):
                    ch.step(nc.vector.tensor_copy(
                        comb[:].rearrange("p (q r e) -> p r e q", r=TP, e=8)[:, r],
                        turned[:, 2 + r, 0:P].rearrange("p (e q) -> p e q", q=Q)))

            @block.tensor
            def _(pe):
                pe.wait_ge(asked, 1)
                pe.wait_ge(chain_sem, TP)
                for r in range(TP):
                    ins = nc.tensor.transpose(turned[:, r, 0:P], spread[:].rearrange("p (r a) t -> p r (a t)", r=TP)[:, r],
                                              keep.ident[:])
                ins.then_inc(flips, 1)
                pe.wait_ge(masks, 1)
                for i in range(BITS + 2):
                    pe.wait_ge(asked, i + 2)
                    nc.tensor.matmul(sums[:, 0:1], same[:], cnt[:, 0:1], start=True, stop=True)
                    nc.tensor.matmul(sums[:, 1:2], prior[:], cnt[:, 0:1], start=True, stop=True).then_inc(counted, 1)
                pe.wait_ge(moved, 1)
                for r in range(TP):
                    ins = nc.tensor.transpose(turned[:, 2 + r, 0:P], val[:, r * P:(r + 1) * P], keep.ident[:])
                ins.then_inc(flips, 1)


def layer3_ffn(nc, keep, a):
    E, F, pairs = 8, 341, 4
    rows = [P, P, F - 2 * P]
    with ExitStack() as st:
        c = Core(nc, st, "l3f")
        up = c.sb("up", [P, pairs, F])
        b_up = c.sb("b_up", [P, pairs, 3])
        down = c.sb("down", [P, pairs, 3, 2, D])
        logits, probs, comb = c.sb("logits", [P, NT * 8]), c.sb("probs", [P, NT * 8]), c.sb("comb", [P, NT * 8])
        wd = a["L3_ffn_W_down"]
        loads = [(up[:], a["L3_ffn_W_up"].rearrange("g h f -> h g f")),
                 (b_up[:].rearrange("p g k -> p (g k)"), a["L3_ffn_b_up_cols"])]
        for f, r in enumerate(rows):
            for g in range(pairs):
                loads.append((down[0:r, g, f], wd[2 * g:2 * g + 2, f * P:f * P + r, :].rearrange("e p h -> p e h")))
        for g in range(pairs):
            loads.append((down[rows[2]:rows[2] + 1, g, 2],
                          a["L3_ffn_b_down"][2 * g:2 * g + 2].rearrange("(o e) h -> o e h", o=1)))
        weights_in = c.sem("weights_in")
        router(nc, keep, "l3f", logits, a["L3_ffn_Wr"], a["L3_ffn_br"].rearrange("(o e) -> o e", o=1), loads, weights_in)
        softmax8(nc, keep, "l3f", logits, probs)
        top_tokens(nc, keep, "l3f", probs, comb, N // E)
        heights = [P, P, rows[2] + 1]
        experts(nc, keep, "l3f", comb, weights_in, len(loads), pairs, rows, lambda u, f: up[:, u, f * P:f * P + rows[f]],
                lambda u, f: down[0:heights[f], u, f], 2, ACT.Silu, bias=lambda u, f: b_up[0:rows[f], u, f:f + 1])


def laid_out(inputs):
    out = {k: np.ascontiguousarray(v) for k, v in inputs.items()}
    b_up = out.pop("L3_ffn_b_up")
    cols = np.zeros((b_up.shape[0], 3 * P), b_up.dtype)
    cols[:, :b_up.shape[1]] = b_up
    out["L3_ffn_b_up_cols"] = np.ascontiguousarray(cols.reshape(-1, P).T)
    out["L1_attn_norm_scale_col"] = out.pop("L1_attn_norm_scale").reshape(P, 1)
    conv_w = out.pop("L1_attn_conv_weight")
    out["L1_attn_conv_w_cols"] = np.ascontiguousarray(conv_w.reshape(-1, 2, P).transpose(2, 1, 0).reshape(P, -1))
    out["L1_attn_conv_b_cols"] = np.ascontiguousarray(out.pop("L1_attn_conv_bias").reshape(2, P).T)
    par = np.stack([out.pop("L3_attn_Lambda_re"), out.pop("L3_attn_Lambda_im"), out.pop("L3_attn_log_step")[:, 0]], 1)
    out["L3_attn_par"] = np.concatenate([par, par])
    b_ri = out.pop("L3_attn_B").transpose(0, 2, 1)
    out["L3_attn_B_ri"] = np.concatenate([b_ri, b_ri])
    c_ri = out.pop("L3_attn_C").transpose(1, 2, 0)
    out["L3_attn_C_ri"] = np.concatenate([c_ri, c_ri[:, ::-1]])
    for n in ("q", "k", "v", "o"):
        out[f"L0_attn_W{n}T"] = np.ascontiguousarray(out.pop(f"L0_attn_W{n}").T)
    out["L0_attn_bqk_cols"] = np.ascontiguousarray(np.stack([out.pop("L0_attn_bq"), out.pop("L0_attn_bk")], 1))
    freq = np.exp(np.arange(0, D, 2, dtype=np.float32) * np.float32(-np.log(10000.0) / D))
    angle = np.arange(S, dtype=np.float32)[:, None] * freq[None, :]
    for name, f in (("rope_cos", np.cos), ("rope_sin", np.sin)):
        table = f(angle).astype(np.float32).reshape(S // P, P, D // 2)
        out[name] = np.ascontiguousarray(table.transpose(1, 0, 2).reshape(P, -1))
    cols = [out.pop("L1_ffn_" + n) for n in ("d_bq", "d_bk", "d_bo", "c_bq", "c_bk", "c_bv")]
    out["L1_ffn_bias_cols"] = np.ascontiguousarray(np.stack(cols + [np.zeros_like(cols[0])] * 2, 1))
    out["L1_ffn_slot_T"] = np.ascontiguousarray(out.pop("L1_ffn_slot_query")[0].T)
    for n in ("b1", "bg"):
        b = out.pop("L1_ffn_e_" + n)
        rows = np.zeros((4, P // 4, b.shape[0] // 4, b.shape[1]), b.dtype)
        rows[:, :B] = b.reshape(-1, 4, b.shape[1]).transpose(1, 0, 2)[:, None]
        out[f"L1_ffn_{n}_rows"] = rows.reshape(P, -1)
    out["L1_ffn_b2_T"] = np.ascontiguousarray(out.pop("L1_ffn_e_b2").T)
    return out


class Keep:

    def __init__(self, nc, stack):
        sb = lambda name, shape: stack.enter_context(nc.sbuf_tensor(name, shape, F32))
        self.x_tok = sb("x_tok", [P, N])
        self.x_T = sb("x_T", [P, N])
        self.ident = sb("ident", [P, P])
        self.upto = sb("upto", [P, P])
        self.ones = sb("ones", [P, GW])
        self.eps, self.rms_eps = sb("eps", [P, 1]), sb("rms_eps", [P, 1])


def sequence_kernel(nc, a, out):
    with ExitStack() as st:
        keep = Keep(nc, st)
        moved = st.enter_context(nc.semaphore("moved"))
        tiles = lambda x: x.rearrange("(t p) d -> p t d", p=P)
        x3 = keep.x_tok[:].rearrange("p (t d) -> p t d", d=D)
        with nc.Block() as block:

            @block.sync
            def _(sp):
                sp.dma_start(x3, tiles(a["L0_attn_x"])).then_inc(moved, 16)
                sp.wait_ge(moved, 16)

        constants(nc, keep)
        layers = (layer0_attn, layer0_ffn, layer1_attn, layer1_ffn, layer2_attn, layer2_ffn, layer3_attn, layer3_ffn)
        for n, layer in enumerate(layers):
            with nc.cleanup_on_exit():
                layer(nc, keep, a)
                layernorm(nc, keep, f"n{n}", want_T=n < len(layers) - 1)
        with nc.Block() as block:

            @block.sync
            def _(sp):
                sp.dma_start(tiles(out), x3).then_inc(moved, 16)
                sp.wait_ge(moved, 32)


def kernel(**inputs):
    import concourse.bacc as bacc
    from concourse.bass_utils import run_bass_kernel_spmd

    arrays = laid_out({k: np.asarray(v) for k, v in inputs.items()})
    arrays["L0_attn_x"] = arrays["L0_attn_x"].reshape(N, D)
    nc = bacc.Bacc("TRN2", target_bir_lowering=False, num_devices=1)
    a = {k: nc.dram_tensor(f"in_{k}", v.shape, mybir.dt.from_np(v.dtype), kind="ExternalInput").ap() for k, v in arrays.items()}
    out = nc.dram_tensor("out", (N, D), F32, kind="ExternalOutput").ap()
    sequence_kernel(nc, a, out)
    result = run_bass_kernel_spmd(nc, [{f"in_{k}": v for k, v in arrays.items()}], core_ids=[0])
    return result.results[0]["out"].reshape(B, S, D)
```

```python
import math
from contextlib import ExitStack

import numpy as np

import concourse.bass as bass
from concourse import mybir
from concourse.bass import ds

F32 = mybir.dt.float32
BF16 = mybir.dt.bfloat16
ACT = mybir.ActivationFunctionType
ALU = mybir.AluOpType
AX = mybir.AxisListType

P = 128
D = 128
B, S = 4, 1024
N = B * S
NT = N // P
GW = 512
NG = N // GW
TG = GW // P
RMS_EPS = 1e-6
EPS = 1e-5


class Core:

    def __init__(self, nc, stack, tag):
        self.nc, self.stack, self.tag = nc, stack, tag

    def sb(self, name, shape, dt=F32):
        return self.stack.enter_context(self.nc.sbuf_tensor(f"{self.tag}_{name}", shape, dt))

    def ps(self, name, shape, dt=F32):
        return self.stack.enter_context(self.nc.psum_tensor(f"{self.tag}_{name}", shape, dt))

    def sem(self, name):
        return self.nc.alloc_semaphore(name=f"{self.tag}_{name}")


class Chain:

    def __init__(self, engine, sem):
        self.engine, self.sem, self.count = engine, sem, 0

    def step(self, instruction):
        self.count += 1
        instruction.then_inc(self.sem, 1)
        self.engine.wait_ge(self.sem, self.count)


def bring_table(nc, keep, spare, func):
    nc.scalar.activation(spare[:], keep.ones[0:1, 0:1], func)


def constants(nc, keep):
    with ExitStack() as st:
        c = Core(nc, st, "const")
        zeroed, done = c.sem("zeroed"), c.sem("done")
        with nc.Block() as block:

            @block.gpsimd
            def _(pool):
                nc.gpsimd.memset(keep.ident[:], 0.0).then_inc(zeroed, 1)
                nc.gpsimd.memset(keep.ones[:], 1.0).then_inc(done, 1)
                nc.gpsimd.memset(keep.eps[:], EPS).then_inc(done, 1)
                nc.gpsimd.memset(keep.rms_eps[:], RMS_EPS).then_inc(done, 1)
                pool.wait_ge(zeroed, 1)
                nc.gpsimd.affine_select(out=keep.ident[:], in_=keep.ident[:], compare_op=ALU.not_equal, fill=1.0,
                                        base=0, pattern=[[-1, P]], channel_multiplier=1).then_inc(done, 1)
                pool.wait_ge(done, 3)
                nc.gpsimd.affine_select(out=keep.upto[:], in_=keep.ones[:, 0:P], compare_op=ALU.is_ge, fill=0.0,
                                        base=0, pattern=[[1, P]], channel_multiplier=-1).then_inc(done, 1)
                pool.wait_ge(done, 5)


def layernorm(nc, keep, tag, want_T=True, rms_T=None, scratch=None):
    x_tok, x_T = keep.x_tok, keep.x_T if rms_T is None else rms_T
    with ExitStack() as st:
        c = Core(nc, st, tag + "ln")
        stats = c.sb("stats", [P, NT * 6])
        mean, var = c.sb("mean", [P, NT]), c.sb("var", [P, NT])
        dm, std = c.sb("dm", [P, NT]), c.sb("std", [P, NT])
        rstd, shift = c.sb("rstd", [P, NT]), c.sb("shift", [P, NT])
        normed = x_tok if rms_T is None else scratch
        flipped = c.ps("flipped", [P, NG, GW])
        BY_ACT = range(3, NG, 4)
        stats_done, chain_sem = c.sem("stats_done"), c.sem("chain")
        var_ready, std_ready, norm_ready = c.sem("var_ready"), c.sem("std_ready"), c.sem("norm_ready")
        by_dve, by_act = c.sem("by_dve"), c.sem("by_act")
        flip_ready, flip_taken = c.sem("flip_ready"), c.sem("flip_taken")
        s3 = stats[:].rearrange("p (t k) -> p t k", k=6)

        with nc.Block() as block:

            @block.vector
            def _(dve):
                for t in range(NT):
                    ins = nc.vector.bn_stats(stats[:, t * 6:(t + 1) * 6], x_tok[:, t * D:(t + 1) * D])
                ins.then_inc(stats_done, 1)
                dve.wait_ge(stats_done, 1)
                ch = Chain(dve, chain_sem)
                nc.vector.tensor_tensor(mean[:], s3[:, :, 1], s3[:, :, 4], ALU.add).then_inc(chain_sem, 1)
                ch.count += 1
                ch.step(nc.vector.tensor_tensor(dm[:], s3[:, :, 1], s3[:, :, 4], ALU.subtract))
                nc.vector.tensor_tensor(var[:], s3[:, :, 2], s3[:, :, 5], ALU.add).then_inc(chain_sem, 1)
                ch.count += 1
                ch.step(nc.vector.scalar_tensor_tensor(out=dm[:], in0=dm[:], scalar=0.25, in1=dm[:],
                                                       op0=ALU.mult, op1=ALU.mult))
                ch.step(nc.vector.scalar_tensor_tensor(out=var[:], in0=var[:], scalar=1.0 / D, in1=dm[:],
                                                       op0=ALU.mult, op1=ALU.add))
                if rms_T is None:
                    nc.vector.tensor_copy(dm[:], var[:]).then_inc(var_ready, 1)
                else:
                    ch.step(nc.vector.scalar_tensor_tensor(out=dm[:], in0=mean[:], scalar=0.25, in1=mean[:],
                                                           op0=ALU.mult, op1=ALU.mult))
                    nc.vector.tensor_tensor(dm[:], dm[:], var[:], ALU.add).then_inc(var_ready, 1)
                dve.wait_ge(std_ready, 1)
                ch.step(nc.vector.reciprocal(rstd[:], std[:]))
                nc.vector.scalar_tensor_tensor(out=shift[:], in0=mean[:], scalar=-0.5 if rms_T is None else 0.0, in1=rstd[:],
                                               op0=ALU.mult, op1=ALU.mult).then_inc(norm_ready, 1)
                dve.wait_ge(norm_ready, 1)
                for g in range(NG):
                    if g not in BY_ACT:
                        for t in range(g * TG, (g + 1) * TG):
                            ins = nc.vector.tensor_scalar(normed[:, t * D:(t + 1) * D], x_tok[:, t * D:(t + 1) * D],
                                                          rstd[:, t:t + 1], shift[:, t:t + 1], ALU.mult, ALU.add)
                        ins.then_inc(by_dve, 1)

            @block.scalar
            def _(act):
                act.wait_ge(var_ready, 1)
                nc.scalar.activation(std[:], dm[:], ACT.Sqrt, bias=(keep.eps if rms_T is None else keep.rms_eps)[:]).then_inc(std_ready, 1)
                act.wait_ge(norm_ready, 1)

                def take(g):
                    act.wait_ge(flip_ready, g + 1)
                    nc.scalar.copy(x_T[:, g * GW:(g + 1) * GW], flipped[:, g]).then_inc(flip_taken, 1)

                for n, g in enumerate(BY_ACT):
                    for t in range(g * TG, (g + 1) * TG):
                        ins = nc.scalar.activation(normed[:, t * D:(t + 1) * D], x_tok[:, t * D:(t + 1) * D], ACT.Identity,
                                                   bias=shift[:, t:t + 1], scale=rstd[:, t:t + 1])
                    ins.then_inc(by_act, 1)
                    if want_T and n == 0:
                        take(0)
                        take(1)
                if want_T:
                    for g in range(2, NG):
                        take(g)

            @block.tensor
            def _(pe):
                if want_T:
                    for g in range(NG):
                        acts = sum(k <= g for k in BY_ACT)
                        if g in BY_ACT:
                            pe.wait_ge(by_act, acts)
                        else:
                            pe.wait_ge(by_dve, g + 1 - acts)
                        for j in range(TG):
                            ins = nc.tensor.transpose(flipped[:, g, j * D:(j + 1) * D],
                                                      normed[:, (g * TG + j) * D:(g * TG + j + 1) * D], keep.ident[:])
                        ins.then_inc(flip_ready, 1)


def router(nc, keep, tag, logits, w_dram, bias_dram, loads, weights_in):
    CT, E = 32, 8
    HALVES = NG // 4
    with ExitStack() as st:
        c = Core(nc, st, tag + "rt")
        w, b = c.sb("w", [P, CT]), c.sb("b", [1, CT])
        byexp = c.sb("byexp", [P, HALVES, GW])
        acc = c.ps("acc", [P, HALVES, GW])
        flipped = c.ps("flipped", [P, HALVES, GW])
        padded, w_loaded, acc_ready, copied = c.sem("padded"), c.sem("w_loaded"), c.sem("acc_ready"), c.sem("copied")
        flip_ready, logit_done = c.sem("flip_ready"), c.sem("logit_done")
        with nc.Block() as block:

            @block.sync
            def _(sp):
                sp.wait_ge(padded, 2)
                sp.dma_start(w[:, 0:E], w_dram).then_inc(w_loaded, 16)
                if bias_dram is not None:
                    sp.dma_start(b[:, 0:E], bias_dram).then_inc(w_loaded, 16)
                for dst, src, *own in loads:
                    sp.dma_start(dst, src).then_inc(own[0] if own else weights_in, 16)

            @block.tensor
            def _(pe):
                pe.wait_ge(w_loaded, 16 if bias_dram is None else 32)
                for s in range(HALVES):
                    for q in range(4):
                        g = s * 4 + q
                        out = acc[q * CT:(q + 1) * CT, s]
                        ins = nc.tensor.matmul(out, w[:], keep.x_T[:, g * GW:(g + 1) * GW], start=True, stop=bias_dram is None)
                        if bias_dram is not None:
                            ins = nc.tensor.matmul(out, b[:], keep.ones[0:1], start=False, stop=True)
                    ins.then_inc(acc_ready, 1)
                for s in range(HALVES):
                    pe.wait_ge(copied, s + 1)
                    for j in range(TG):
                        ins = nc.tensor.transpose(flipped[:, s, j * P:(j + 1) * P], byexp[:, s, j * P:(j + 1) * P], keep.ident[:])
                    ins.then_inc(flip_ready, 1)

            @block.vector
            def _(dve):
                nc.vector.memset(w[:], 0.0).then_inc(padded, 1)
                nc.vector.memset(b[:], 0.0).then_inc(padded, 1)
                for s in range(HALVES):
                    dve.wait_ge(acc_ready, s + 1)
                    nc.vector.tensor_copy(byexp[:, s], acc[:, s]).then_inc(copied, 1)
                for s in range(HALVES):
                    dve.wait_ge(flip_ready, s + 1)
                    dst = logits[:].rearrange("p (s q j e) -> p s j q e", s=HALVES, q=4, e=E)[:, s]
                    src = flipped[:, s].rearrange("p (j q e) -> p j q e", j=TG, e=CT)[:, :, :, 0:E]
                    nc.vector.tensor_copy(dst, src).then_inc(logit_done, 1)
                dve.wait_ge(logit_done, HALVES)


def softmax8(nc, keep, tag, logits, probs):
    with ExitStack() as st:
        c = Core(nc, st, tag + "sm")
        top, total = c.sb("top", [P, NT]), c.sb("total", [P, NT])
        chain_sem, shifted, raised = c.sem("chain"), c.sem("shifted"), c.sem("raised")
        l3 = logits[:].rearrange("p (t e) -> p t e", e=8)
        p3 = probs[:].rearrange("p (t e) -> p t e", e=8)
        with nc.Block() as block:

            @block.vector
            def _(dve):
                ch = Chain(dve, chain_sem)
                ch.step(nc.vector.tensor_reduce(top[:], l3, AX.X, ALU.max))
                nc.vector.tensor_tensor(l3, l3, top[:].unsqueeze(2).to_broadcast([P, NT, 8]),
                                        ALU.subtract).then_inc(shifted, 1)
                dve.wait_ge(raised, 1)
                ch.step(nc.vector.tensor_reduce(total[:], p3, AX.X, ALU.add))
                ch.step(nc.vector.reciprocal(total[:], total[:]))
                ch.step(nc.vector.tensor_tensor(p3, p3, total[:].unsqueeze(2).to_broadcast([P, NT, 8]), ALU.mult))

            @block.scalar
            def _(act):
                act.wait_ge(shifted, 1)
                nc.scalar.activation(probs[:], logits[:], ACT.Exp).then_inc(raised, 1)


def pick_top(nc, keep, tag, probs, comb, k, scale_top=None):
    with ExitStack() as st:
        c = Core(nc, st, tag + "tk")
        rank = c.sb("rank", [P, NT * 8])
        left, hot, sc = c.sb("left", [P, NT * 8]), c.sb("hot", [P, NT * 8]), c.sb("sc", [P, NT * 8])
        top, best, total = c.sb("top", [P, NT]), c.sb("best", [P, NT]), c.sb("total", [P, NT])
        chain_sem, ranked = c.sem("chain"), c.sem("ranked")
        three = lambda a: a[:].rearrange("p (t e) -> p t e", e=8)
        wide = lambda a: a[:].unsqueeze(2).to_broadcast([P, NT, 8])
        with nc.Block() as block:

            @block.gpsimd
            def _(pool):
                nc.gpsimd.iota(three(rank), pattern=[[0, NT], [-1, 8]], base=8, channel_multiplier=0,
                               allow_small_or_imprecise_dtypes=True).then_inc(ranked, 1)

            @block.vector
            def _(dve):
                ch = Chain(dve, chain_sem)
                dve.wait_ge(ranked, 1)
                ch.step(nc.vector.tensor_copy(left[:], probs[:]))
                for n in range(k):
                    ch.step(nc.vector.tensor_reduce(top[:], three(left), AX.X, ALU.max))
                    ch.step(nc.vector.tensor_tensor(three(hot), three(left), wide(top), ALU.is_equal))
                    ch.step(nc.vector.tensor_tensor(hot[:], hot[:], rank[:], ALU.mult))
                    ch.step(nc.vector.tensor_reduce(best[:], three(hot), AX.X, ALU.max))
                    ch.step(nc.vector.tensor_tensor(three(hot), three(hot), wide(best), ALU.is_equal))
                    ch.step(nc.vector.scalar_tensor_tensor(out=left[:], in0=hot[:], scalar=-2.0, in1=left[:],
                                                           op0=ALU.mult, op1=ALU.add))
                    if k == 1:
                        ch.step(nc.vector.tensor_scalar(top[:], top[:], scale_top, None, ALU.mult))
                        ch.step(nc.vector.tensor_tensor(three(comb), three(hot), wide(top), ALU.mult))
                        ch.step(nc.vector.memset(three(comb)[:, :, 7:8], 1.0))
                    elif n == 0:
                        ch.step(nc.vector.tensor_tensor(three(comb), three(hot), wide(top), ALU.mult))
                        ch.step(nc.vector.tensor_copy(total[:], top[:]))
                    else:
                        ch.step(nc.vector.tensor_tensor(total[:], total[:], top[:], ALU.add))
                        ch.step(nc.vector.reciprocal(total[:], total[:]))
                        ch.step(nc.vector.tensor_tensor(three(sc), three(hot), wide(top), ALU.mult))
                        ch.step(nc.vector.tensor_tensor(comb[:], comb[:], sc[:], ALU.add))
                        ch.step(nc.vector.tensor_tensor(three(comb), three(comb), wide(total), ALU.mult))


def experts(nc, keep, tag, comb, weights_in, loads, units, rows, up, down, per_unit, func, gate=None, bias=None,
            first_column=0, beside=None, ahead=None, groups=NG, first_group=0):
    nf = len(rows)
    upb = 2 if gate else 4
    ob = per_unit
    steps = units * nf
    ones_row = rows[-1] < P
    with ExitStack() as st:
        c = Core(nc, st, tag + "ex")
        hid = c.sb("hid", [P, 2, nf, GW])
        spare = c.sb("spare", [1, 1])
        silu = c.sb("silu", [P, 2, GW]) if gate else None
        raw = c.ps("raw", [P, 4, GW])
        res = c.ps("res", [P, 2, ob, GW])
        raw_ready = c.sem("raw_ready")
        silu_ready = c.sem("silu_ready")
        hid_ready = c.sem("hid_ready")
        res_ready = c.sem("res_ready")
        comb_done = c.sem("comb_done")
        ones_set, started = c.sem("ones_set"), c.sem("started")
        tiles_per_bank = GW // (per_unit * D)

        def result(k, j):
            b, o = divmod(j, tiles_per_bank)
            return res[:, k, b, o * per_unit * D:(o + 1) * per_unit * D]

        with nc.Block() as block:

            @block.tensor
            def _(pe):
                pe.sem_inc(hid_ready, upb)
                pe.sem_inc(res_ready, 2)
                pe.sem_inc(comb_done, 2)
                if ones_row:
                    pe.wait_ge(ones_set, 1)
                pe.wait_ge(weights_in, 16 * loads)

                def rise(g, u):
                    for f in range(nf):
                        i = u * nf + f
                        place = (i % upb) * (4 // upb)
                        x = keep.x_T[:, ds(g * GW + first_group * GW, GW)]
                        pe.wait_ge(hid_ready, g * steps + (i + 1))
                        ins = nc.tensor.matmul(raw[0:rows[f], place], up(u, f), x, start=True, stop=True)
                        if gate:
                            ins = nc.tensor.matmul(raw[0:rows[f], place + 1], gate(u, f), x, start=True, stop=True)
                        ins.then_inc(raw_ready, 1)

                def fall(g, u):
                    pe.wait_ge(hid_ready, g * steps + (upb + (u + 1) * nf))
                    pe.wait_ge(comb_done, g * units + (u + 1))
                    for j in range(TG):
                        for f in range(nf):
                            w = down(u, f)
                            ins = nc.tensor.matmul(result(u % 2, j), hid[0:w.shape[0], u % 2, f, j * P:(j + 1) * P], w,
                                                   start=(f == 0), stop=(f == nf - 1))
                    ins.then_inc(res_ready, 1)

                with pe.Fori(0, groups) as g:
                    for u in range(units):
                        rise(g, u)
                        if u:
                            fall(g, u - 1)
                    fall(g, units - 1)

            @block.scalar
            def _(act):
                bring_table(nc, keep, spare, func)
                act.wait_ge(weights_in, 16 * loads)
                with act.Fori(0, groups) as g:
                    for u in range(units):
                        for f in range(nf):
                            i = u * nf + f
                            place = (i % upb) * (4 // upb)
                            act.wait_ge(raw_ready, g * steps + (i + 1))
                            if gate:
                                act.wait_ge(hid_ready, g * steps + (i + 1))
                                nc.scalar.activation(silu[0:rows[f], i % 2], raw[0:rows[f], place + 1],
                                                     func).then_inc(silu_ready, 1)
                            else:
                                if f == 0:
                                    act.wait_ge(res_ready, g * units + (u + 1))
                                kw = {"bias": bias(u, f)} if bias else {}
                                nc.scalar.activation(hid[0:rows[f], u % 2, f], raw[0:rows[f], place], func,
                                                     **kw).then_inc(hid_ready, 1)

            if beside:
                @block.gpsimd
                def _(pool):
                    beside(pool)

            @block.vector
            def _(dve):
                if ones_row:
                    nc.vector.memset(hid[:, :, nf - 1], 1.0).then_inc(ones_set, 1)
                if ahead:
                    ahead(dve)

                def merge(g, u):
                    dve.wait_ge(res_ready, g * units + (u + 3))
                    for e in range(per_unit):
                        dve.wait_ge(merged, (g * units + u) * per_unit + (e + 1))
                        for j in range(TG):
                            t = g * TG + (first_group * TG + j)
                            ins = nc.vector.scalar_tensor_tensor(
                                out=keep.x_tok[:, ds(t * D, D)], in0=result(u % 2, j)[:, e * D:(e + 1) * D],
                                scalar=comb[:, ds(t * 8 + (first_column + u * per_unit + e), 1)],
                                in1=keep.x_tok[:, ds(t * D, D)], op0=ALU.mult, op1=ALU.add)
                        ins.then_inc(merged, 1)
                    dve.wait_ge(merged, (g * units + u) * per_unit + (per_unit + 1))
                    dve.sem_inc(comb_done, 1)

                merged = started
                dve.sem_inc(merged, 1)
                with dve.Fori(0, groups) as g:
                    for u in range(units):
                        if gate:
                            for f in range(nf):
                                i = u * nf + f
                                dve.wait_ge(silu_ready, g * steps + (i + 1))
                                if f == 0:
                                    dve.wait_ge(res_ready, g * units + (u + 1))
                                nc.vector.tensor_tensor(hid[0:rows[f], u % 2, f], raw[0:rows[f], (i % 2) * 2],
                                                        silu[0:rows[f], i % 2], ALU.mult).then_inc(hid_ready, 1)
                        if u:
                            merge(g, u - 1)
                    merge(g, units - 1)


def flip_tokens(nc, keep, tag, src_tok, dst_T):
    with ExitStack() as st:
        c = Core(nc, st, tag + "fl")
        flipped = c.ps("flipped", [P, NG, GW])
        flip_ready, flip_taken = c.sem("flip_ready"), c.sem("flip_taken")
        with nc.Block() as block:

            @block.tensor
            def _(pe):
                for g in range(NG):
                    for j in range(TG):
                        ins = nc.tensor.transpose(flipped[:, g, j * P:(j + 1) * P],
                                                  src_tok[:, (g * TG + j) * D:(g * TG + j + 1) * D], keep.ident[:])
                    ins.then_inc(flip_ready, 1)

            @block.scalar
            def _(act):
                for g in range(NG):
                    act.wait_ge(flip_ready, g + 1)
                    nc.scalar.copy(dst_T[:, g * GW:(g + 1) * GW], flipped[:, g]).then_inc(flip_taken, 1)


def layer0_attn(nc, keep, a):
    H, HD = 16, 8
    HEADS = B * H
    QT = S // P
    PARTS = [(0, 0), (0, 1), (0, 2), (1, 0), (1, 1), (1, 2), (2, 0), (2, 1)]
    ROWS = len(PARTS) * HD
    M1, M2 = 64, 96
    FULL = M2 + QT
    RING = 4
    V1 = 32
    QB = S // 4
    scratch = [nc.dram_tensor(f"l0_{n}_parts", (3, B * P, S), BF16, kind="Internal").ap() for n in ("query", "key")]
    with ExitStack() as st:
        c = Core(nc, st, "l0a")
        v_tok, at_tok = c.sb("v_tok", [P, N]), c.sb("at_tok", [P, N])

        with ExitStack() as st2:
            c2 = Core(nc, st2, "l0r")
            cos, sin = c2.sb("cos", [P, QT, D // 2]), c2.sb("sin", [P, QT, D // 2])
            prod = c2.sb("prod", [P, 2, N // 2])
            loaded, halves, joined = c2.sem("loaded"), c2.sem("halves"), c2.sem("joined")
            with nc.Block() as block:

                @block.sync
                def _(sp):
                    sp.dma_start(cos[:].rearrange("p t d -> p (t d)"), a["rope_cos"]).then_inc(loaded, 16)
                    sp.dma_start(sin[:].rearrange("p t d -> p (t d)"), a["rope_sin"]).then_inc(loaded, 16)

                x4 = keep.x_tok[:].rearrange("p (b t d) -> p b t d", b=B, d=D)
                r4 = at_tok[:].rearrange("p (b t d) -> p b t d", b=B, d=D)
                h = D // 2
                wide = lambda m: m[:].unsqueeze(1).to_broadcast([P, B, QT, h])
                p4 = lambda n: prod[:, n].rearrange("p (b t d) -> p b t d", b=B, d=h)

                @block.vector
                def _(dve):
                    dve.wait_ge(loaded, 32)
                    for n, (m1, m2, op, o) in enumerate(((cos, sin, ALU.subtract, 0), (sin, cos, ALU.add, h))):
                        nc.vector.tensor_tensor(r4[:, :, :, o:o + h], x4[:, :, :, 0:h], wide(m1), ALU.mult)
                        nc.vector.tensor_tensor(p4(n), x4[:, :, :, h:D], wide(m2), ALU.mult).then_inc(halves, 1)
                        dve.wait_ge(halves, n + 1)
                        nc.vector.tensor_tensor(r4[:, :, :, o:o + h], r4[:, :, :, o:o + h], p4(n), op).then_inc(joined, 1)
                    dve.wait_ge(joined, 2)

        rT = keep.x_T
        flip_tokens(nc, keep, "l0a", at_tok, rT)
        project_tokens(nc, keep, "l0v", rT, a["L0_attn_WvT"], v_tok, bias_dram=a["L0_attn_bv"])

        with ExitStack() as st2:
            c2 = Core(nc, st2, "l0p")
            w = c2.sb("w", [P, 2, P])
            bias = c2.sb("bias", [P, 2])
            full = c2.sb("full", [P, 2, GW])
            rest, rest2 = c2.sb("rest", [P, 2, GW]), c2.sb("rest2", [P, 2, GW])
            parts = c2.sb("parts", [P, 2, 2, 3, GW], BF16)
            acc = c2.ps("acc", [P, 2, GW])
            loaded, acc_ready, full_done = c2.sem("loaded"), c2.sem("acc_ready"), c2.sem("full_done")
            cut, stored, chained = c2.sem("cut"), [[c2.sem(f"stored{half}{m}") for m in range(2)] for half in range(2)], c2.sem("chained")
            with nc.Block() as block:

                @block.sync
                def _(sp):
                    for m, n in enumerate(("q", "k")):
                        sp.dma_start(w[:, m], a[f"L0_attn_W{n}T"]).then_inc(loaded, 16)
                    sp.dma_start(bias[:], a["L0_attn_bqk_cols"]).then_inc(loaded, 16)
                    with sp.Fori(0, B) as b:
                        for half in range(2):
                            for m in range(2):
                                sp.wait_ge(cut, (b * 2 + half) * 4 + (2 * m + 2))
                                sp.dma_start(scratch[m][:, ds(b * P, P), half * GW:(half + 1) * GW].rearrange("i p s -> p i s"),
                                             parts[:, half, m]).then_inc(stored[half][m], 16)
                    for half in range(2):
                        for m in range(2):
                            sp.wait_ge(stored[half][m], 16 * B + 16)

                @block.tensor
                def _(pe):
                    pe.sem_inc(full_done, 2)
                    pe.wait_ge(loaded, 48)
                    with pe.Fori(0, NG) as g:
                        for m in range(2):
                            pe.wait_ge(full_done, g * 2 + (m + 1))
                            nc.tensor.matmul(acc[:, m], w[:, m], rT[:, ds(g * GW, GW)], start=True, stop=True).then_inc(acc_ready, 1)

                @block.scalar
                def _(act):
                    with act.Fori(0, B) as b:
                        for half in range(2):
                            g = b * 2 + half
                            for m in range(2):
                                act.wait_ge(acc_ready, g * 2 + (m + 1))
                                act.wait_ge(chained, g * 4 + (2 * m + 1))
                                nc.scalar.activation(full[:, m], acc[:, m], ACT.Identity, bias=bias[:, m:m + 1])
                                act.wait_ge(stored[half][m], b * 16 + 16)
                                nc.scalar.activation(parts[:, half, m, 0], acc[:, m], ACT.Identity,
                                                     bias=bias[:, m:m + 1]).then_inc(full_done, 1)

                @block.vector
                def _(dve):
                    dve.sem_inc(chained, 4)
                    for half in range(2):
                        for m in range(2):
                            dve.sem_inc(stored[half][m], 16)
                    with dve.Fori(0, B) as b:
                        for half in range(2):
                            g = b * 2 + half
                            for m in range(2):
                                part = parts[:, half, m]
                                dve.wait_ge(full_done, g * 2 + (m + 3))
                                nc.vector.tensor_tensor(rest[:, m], full[:, m], part[:, 0], ALU.subtract).then_inc(chained, 1)
                                dve.wait_ge(chained, g * 4 + (2 * m + 5))
                                nc.vector.tensor_copy(part[:, 1], rest[:, m]).then_inc(cut, 1)
                                dve.wait_ge(cut, g * 4 + (2 * m + 1))
                                nc.vector.tensor_tensor(rest2[:, m], rest[:, m], part[:, 1], ALU.subtract).then_inc(chained, 1)
                                dve.wait_ge(chained, g * 4 + (2 * m + 6))
                                nc.vector.tensor_copy(part[:, 2], rest2[:, m]).then_inc(cut, 1)

        with ExitStack() as st2:
            c2 = Core(nc, st2, "l0h")
            qs, ks = c2.sb("qs", [P, RING, S], BF16), c2.sb("ks", [P, RING, S], BF16)
            negmax = c2.sb("negmax", [P, 2, QT])
            first_part = c2.sb("first_part", [P, P], BF16)
            mcut = c2.sb("mcut", [P, P], BF16)
            diag = c2.sb("diag", [P, QT, P], BF16)
            vs = c2.sb("vs", [P, 2, QT, V1])
            TR = 4
            pT = c2.sb("pT", [P, TR, S])
            outT = c2.sb("outT", [P, QB])
            share = c2.sb("share", [P, QT])
            s1 = c2.ps("s1", [P, 2, S])
            s2 = c2.ps("s2", [P, 2, GW])
            mix = c2.ps("mix", [P, 2, GW])
            loaded = [c2.sem(f"loaded{r}") for r in range(RING)]
            s1_ready, max_done = c2.sem("s1_ready"), c2.sem("max_done")
            s2_ready, exp_done = c2.sem("s2_ready"), c2.sem("exp_done")
            pv_done, v_ready = c2.sem("pv_done"), c2.sem("v_ready")
            out_copied, flip_ready = c2.sem("out_copied"), c2.sem("flip_ready")
            m_cut, m_spread, prepared, hi_done = c2.sem("m_cut"), c2.sem("m_spread"), c2.sem("prepared"), c2.sem("hi_done")
            shared = c2.sem("shared")
            INV = 1.0 / math.sqrt(HD)
            v3 = v_tok[:].rearrange("p (t d) -> p t d", d=D)
            at3 = at_tok[:].rearrange("p (t d) -> p t d", d=D)
            LOADS = 6

            def over_heads(engine, head):
                for r in range(RING):
                    head(0, r, r == 0)
                with engine.Fori(1, HEADS // RING) as g:
                    for r in range(RING):
                        head(g, r, False)

            with nc.Block() as block:

                @block.sync
                def _(sp):
                    def load(n, r):
                        rows = ds(n % HEADS * HD, HD)
                        for i, j0, js in ((0, 0, 3), (1, 0, 3), (2, 0, 2)):
                            at = PARTS.index((i, j0)) * HD
                            sp.dma_start(ks[at:at + js * HD, r], scratch[1][0:js, rows]).then_inc(loaded[r], 16)
                            sp.dma_start(qs[at:at + js * HD, r],
                                         scratch[0][i:i + 1, rows].to_broadcast([js, HD, S])).then_inc(loaded[r], 16)

                    sp.wait_ge(prepared, 2)
                    for r in range(RING - 1):
                        load(r, r)

                    def head(g, r, first):
                        n = g * RING + r
                        if not first:
                            sp.wait_ge(s2_ready, n * (2 * QT))
                        load(n + (RING - 1), (r + RING - 1) % RING)

                    over_heads(sp, head)
                    for r in range(RING):
                        sp.wait_ge(loaded[r], 16 * LOADS * (HEADS // RING + (r < RING - 1)))

                @block.gpsimd
                def _(pool):
                    ch = Chain(pool, prepared)
                    ch.step(nc.gpsimd.memset(ks[ROWS:P], 1.0))
                    ch.step(nc.gpsimd.memset(qs[ROWS:P], 0.0))
                    ch.step(nc.gpsimd.memset(mcut[:], 0.0))
                    ch.step(nc.gpsimd.memset(vs[:], 0.0))
                    ch.step(nc.gpsimd.memset(vs[:, :, :, HD:HD + 1], 1.0))
                    ch.step(nc.gpsimd.memset(diag[:], 0.0))
                    for o in (M1, M2):
                        ch.step(nc.gpsimd.memset(diag[o:o + QT], 1.0))
                    for o in (M1, M2):
                        d = diag[o:o + QT]
                        ch.step(nc.gpsimd.affine_select(out=d, in_=d, compare_op=ALU.is_equal, fill=0.0, base=0,
                                                        pattern=[[-1, QT], [0, P]], channel_multiplier=1))

                    def values(n, q):
                        nc.gpsimd.tensor_copy(vs[:, q, :, 0:HD], v3[:, ds(n // H * QT, QT), ds(n % H * HD, HD)]).then_inc(v_ready, 1)

                    def spread(n, r):
                        pool.wait_ge(m_cut, (n + 1))
                        nc.gpsimd.tensor_tensor(qs[M1:FULL, r].rearrange("p (t q) -> p t q", q=P), diag[M1:FULL],
                                                mcut[M1:FULL].unsqueeze(1).to_broadcast([FULL - M1, QT, P]), ALU.mult).then_inc(m_spread, 1)
                        pool.wait_ge(m_spread, n + 1)

                    values(0, 0)
                    pool.wait_ge(v_ready, 1)
                    spread(0, 0)

                    def head(g, r, first):
                        n = g * RING + r
                        spread(n + 1, (r + 1) % RING)
                        pool.wait_ge(pv_done, n * QT + TR)
                        values((n + 1) % HEADS, (r + 1) % 2)
                        pool.wait_ge(v_ready, n + 2)

                    over_heads(pool, head)

                @block.tensor
                def _(pe):
                    pe.sem_inc(max_done, 2)
                    pe.sem_inc(exp_done, 2)
                    pe.sem_inc(pv_done, TR)

                    def first_product(n, r, t):
                        pe.wait_ge(max_done, n * QT + (t + 1))
                        for o in range(S // GW):
                            ins = nc.tensor.matmul(s1[:, t % 2, o * GW:(o + 1) * GW], qs[0:ROWS, r, t * P:(t + 1) * P],
                                                   ks[0:ROWS, r, o * GW:(o + 1) * GW], start=True, stop=True)
                        ins.then_inc(s1_ready, 1)

                    def second_product(n, r, t):
                        for o in range(S // GW):
                            pe.wait_ge(exp_done, (n * QT + t) * 2 + (o + 1))
                            nc.tensor.matmul(s2[:, o], ks[0:FULL, r, t * P:(t + 1) * P], qs[0:FULL, r, o * GW:(o + 1) * GW],
                                             start=True, stop=True).then_inc(s2_ready, 1)

                    def attend(n, q, t):
                        pe.wait_ge(exp_done, (n * QT + t) * 2 + 4)
                        if t == 0:
                            pe.wait_ge(v_ready, n + 1)
                            pe.wait_ge(m_cut, n + 1)
                        for k in range(4):
                            ins = nc.tensor.matmul(mix[k * V1:(k + 1) * V1, q, 0:QB], vs[:, q, t], pT[:, t % TR, k * QB:(k + 1) * QB],
                                                   start=(t == 0), stop=(t == QT - 1))
                        ins.then_inc(pv_done, 1)

                    def turn(n, q, result):
                        if result:
                            pe.wait_ge(out_copied, n)
                            for f in range(2):
                                nc.tensor.transpose(mix[:, q, (2 + f) * P:(3 + f) * P], outT[:, f * P:(f + 1) * P], keep.ident[:])
                        pe.wait_ge(max_done, (n + 2) * QT + 2)
                        nc.tensor.transpose(mix[0:QT, q, 0:P], negmax[:, q], keep.ident[:]).then_inc(flip_ready, 1)

                    for r in range(2):
                        pe.wait_ge(loaded[r], 16 * LOADS)
                        for t in range(QT):
                            first_product(r, r, t)
                        if r == 0:
                            turn(-1, 0, False)

                    def head(g, r, first):
                        n, q, r2 = g * RING + r, r % 2, (r + 2) % RING
                        pe.wait_ge(m_spread, n + 1)
                        pe.wait_ge(loaded[r2], (g + (1 if r < 2 else 2)) * (16 * LOADS))
                        for t in range(QT):
                            second_product(n, r, t)
                            first_product(n + 2, r2, t)
                            if t >= 2:
                                attend(n, q, t - 2)
                            elif not first:
                                attend(n - 1, 1 - q, QT - 2 + t)
                            if t == 2:
                                turn(n, 1 - q, not first)

                    over_heads(pe, head)
                    for t in range(QT - 2, QT):
                        attend(HEADS - 1, 1, t)
                    pe.wait_ge(out_copied, HEADS)
                    for f in range(2):
                        ins = nc.tensor.transpose(mix[:, 1, (2 + f) * P:(3 + f) * P], outT[:, f * P:(f + 1) * P], keep.ident[:])
                    ins.then_inc(flip_ready, 1)

                @block.scalar
                def _(act):
                    def copy_out(n, q):
                        act.wait_ge(pv_done, n * QT + (QT + TR))
                        nc.scalar.copy(outT[:], mix[:, q, 0:QB]).then_inc(out_copied, 1)

                    def head(g, r, first):
                        n = g * RING + r
                        for t in range(QT):
                            act.wait_ge(pv_done, n * QT + (t + 1))
                            for o in range(S // GW):
                                act.wait_ge(s2_ready, (n * QT + t) * 2 + (o + 1))
                                nc.scalar.activation(pT[:, t % TR, o * GW:(o + 1) * GW], s2[:, o], ACT.Exp, scale=INV).then_inc(exp_done, 1)
                            if t == 1 and not first:
                                copy_out(n - 1, (r + 1) % 2)

                    over_heads(act, head)
                    copy_out(HEADS - 1, 1)

                @block.vector
                def _(dve):
                    def maxima(n, q, t):
                        dve.wait_ge(s1_ready, n * QT + (t + 1))
                        nc.vector.tensor_reduce(negmax[:, q, t:t + 1], s1[:, t % 2], AX.X, ALU.max, negate=True).then_inc(max_done, 1)

                    def cut_maxima(n, q, count):
                        dve.wait_ge(flip_ready, count)
                        dve.wait_ge(m_spread, n)
                        src = mix[0:QT, q, 0:P]
                        nc.vector.tensor_copy(first_part[M2:M2 + QT], src).then_inc(hi_done, 1)
                        nc.vector.tensor_copy(mcut[M1:M1 + QT], src)
                        dve.wait_ge(hi_done, count)
                        nc.vector.tensor_tensor(mcut[M2:M2 + QT], src, first_part[M2:M2 + QT], ALU.subtract).then_inc(m_cut, 1)

                    def settle(n, q, count):
                        dve.wait_ge(flip_ready, count)
                        flat = mix[:, q, 2 * P:4 * P].rearrange("p (f k v) -> p f k v", f=2, v=V1)
                        nc.vector.reciprocal(share[:].rearrange("p (f k) -> p f k", f=2), flat[:, :, :, HD]).then_inc(shared, 1)
                        dve.wait_ge(shared, (n + 1))
                        dst = at3[:, ds(n // H * QT, QT), ds(n % H * HD, HD)].rearrange("p (k f) d -> p f k d", f=2)
                        nc.vector.tensor_tensor(dst, flat[:, :, :, 0:HD],
                                                share[:].rearrange("p (f k) -> p f k", f=2).unsqueeze(3).to_broadcast([P, 2, 4, HD]),
                                                ALU.mult)

                    for r in range(2):
                        for t in range(QT):
                            maxima(r, r, t)
                        if r == 0:
                            dve.wait_ge(prepared, 3)
                            cut_maxima(0, 0, 1)

                    def head(g, r, first):
                        n, q = g * RING + r, r % 2
                        for t in range(QT):
                            maxima(n + 2, q, t)
                            if t == 2:
                                cut_maxima(n + 1, 1 - q, n + 2)
                                if not first:
                                    settle(n - 1, 1 - q, n + 2)

                    over_heads(dve, head)
                    settle(HEADS - 1, 1, HEADS + 2)

        flip_tokens(nc, keep, "l0o", at_tok, rT)
        project_tokens(nc, keep, "l0o", rT, a["L0_attn_WoT"], keep.x_tok, bias_dram=a["L0_attn_bo"], add=True)


def layer0_ffn(nc, keep, a):
    E, F = 8, 256
    with ExitStack() as st:
        c = Core(nc, st, "l0f")
        w1, w2 = c.sb("w1", [P, E, F]), c.sb("w2", [P, E, 2, D])
        logits, probs, comb = c.sb("logits", [P, NT * 8]), c.sb("probs", [P, NT * 8]), c.sb("comb", [P, NT * 8])
        weights_in = c.sem("weights_in")
        router(nc, keep, "l0f", logits, a["L0_ffn_Wg"], None,
               [(w1[:], a["L0_ffn_W1"].rearrange("e d f -> d e f")),
                (w2[:], a["L0_ffn_W2"].rearrange("e (k p) d -> p e k d", p=P))], weights_in)
        softmax8(nc, keep, "l0f", logits, probs)
        pick_top(nc, keep, "l0f", probs, comb, 2)
        experts(nc, keep, "l0f", comb, weights_in, 2, E, [P, P], lambda u, f: w1[:, u, f * P:(f + 1) * P],
                lambda u, f: w2[:, u, f], 1, ACT.Relu)


def layer1_attn(nc, keep, a):
    DI, H, HD, DS, K = 256, 4, 64, 64, 4
    NC_ = S // P
    F2 = DI // P
    O_SSM, O_DT, O_B, O_C = DI, 2 * DI, 2 * DI + H, 2 * DI + H + DS
    PW = O_C + DS
    TM = H + DS
    PAD = K - 1
    with ExitStack() as st:
        c = Core(nc, st, "l1a")
        w_in, w_out = c.sb("w_in", [P, PW]), c.sb("w_out", [P, F2, D])
        scale = c.sb("scale", [P, 1])
        conv_w, conv_b = c.sb("conv_w", [P, F2, K]), c.sb("conv_b", [P, F2])
        a_log, dt_bias = c.sb("a_log", [P, H]), c.sb("dt_bias", [P, H])
        gate = c.sb("gate", [P, F2, N])
        tok = c.sb("tok", [P, NT, TM])
        bT, cT = c.sb("bT", [DS, N]), c.sb("cT", [DS, N])
        dt, adt = c.sb("dt", [P, NT, H]), c.sb("adt", [P, NT, H])
        hT = c.sb("hT", [P, F2, N])

        with ExitStack() as st2:
            c2 = Core(nc, st2, "l1p")
            ssm = c2.sb("ssm", [P, F2, B * (S + PAD)])
            s_b = S + PAD
            with ExitStack() as st3:
                c3 = Core(nc, st3, "l1q")
                xn = c3.sb("xn", [P, N])
                layernorm(nc, keep, "l1a", rms_T=xn, scratch=hT[:, 0])
                staged = c3.sb("staged", [P, 2, GW])
                spare = c3.sb("spare", [1, 1])
                acc = c3.ps("acc", [P, 5, GW])
                acc_t = c3.ps("acc_t", [P, 2, GW])
                loaded, scaled, staged_ready = c3.sem("loaded"), c3.sem("scaled"), c3.sem("staged_ready")
                acc_ready, acc_done = c3.sem("acc_ready"), c3.sem("acc_done")
                tok_ready, tok_done, padded = c3.sem("tok_ready"), c3.sem("tok_done"), c3.sem("padded")
                JOBS = [("gate", 0), ("gate", 1), ("ssm", 0), ("ssm", 1), ("bc", 0)]
                J = len(JOBS)
                with nc.Block() as block:

                    @block.sync
                    def _(sp):
                        for dst, src in [(w_in[:], a["L1_attn_w_in"]), (scale[:], a["L1_attn_norm_scale_col"]),
                                         (w_out[:], a["L1_attn_w_out"].rearrange("(k p) d -> p k d", p=P)),
                                         (conv_w[:].rearrange("p f k -> p (f k)"), a["L1_attn_conv_w_cols"]),
                                         (conv_b[:], a["L1_attn_conv_b_cols"]),
                                         (a_log[:], a["L1_attn_A_log"].rearrange("(o h) -> o h", o=1).broadcast_to([P, H])),
                                         (dt_bias[:], a["L1_attn_dt_bias"].rearrange("(o h) -> o h", o=1).broadcast_to([P, H]))]:
                            sp.dma_start(dst, src).then_inc(loaded, 16)
                        sp.wait_ge(loaded, 16 * 7)

                    @block.gpsimd
                    def _(pool):
                        nc.gpsimd.memset(ssm[:, :, :].rearrange("p f (b s) -> p (f b) s", b=B)[:, :, 0:PAD], 0.0).then_inc(padded, 1)
                        pool.wait_ge(padded, 1)

                    @block.tensor
                    def _(pe):
                        pe.sem_inc(acc_done, 5)
                        pe.sem_inc(tok_ready, 2)
                        pe.sem_inc(tok_done, 2)
                        pe.wait_ge(scaled, 1)
                        cols = {"gate": 0, "ssm": O_SSM, "bc": O_B}
                        with pe.Fori(0, B) as b:
                            for k in range(2):
                                for i, (kind, f) in enumerate(JOBS):
                                    n = k * J + i
                                    pe.wait_ge(acc_done, b * (2 * J) + (n + 1))
                                    o = cols[kind] + f * P
                                    nc.tensor.matmul(acc[:, n % 5], w_in[:, o:o + P],
                                                     xn[:, ds((b * 2 + k) * GW, GW)], start=True, stop=True).then_inc(acc_ready, 1)
                                pe.wait_ge(staged_ready, b * 2 + (k + 1))
                                pe.wait_ge(tok_done, b * 2 + (k + 1))
                                for j in range(TG):
                                    ins = nc.tensor.matmul(acc_t[:, k, j * TM:(j + 1) * TM], staged[:, k, j * P:(j + 1) * P],
                                                           w_in[:, O_DT:O_DT + TM], start=True, stop=True)
                                ins.then_inc(tok_ready, 1)

                    @block.scalar
                    def _(act):
                        bring_table(nc, keep, spare, ACT.Silu)
                        with act.Fori(0, B) as b:
                            for k in range(2):
                                for i, (kind, f) in enumerate(JOBS):
                                    n = k * J + i
                                    act.wait_ge(acc_ready, b * (2 * J) + (n + 1))
                                    here = ds((b * 2 + k) * GW, GW)
                                    src = acc[:, n % 5]
                                    if kind == "gate":
                                        ins = nc.scalar.activation(gate[:, f, here], src, ACT.Silu)
                                    elif kind == "ssm":
                                        ins = nc.scalar.copy(ssm[:, f, ds(b * s_b + (PAD + k * GW), GW)], src)
                                    else:
                                        nc.scalar.copy(bT[:, here], src[0:DS])
                                        ins = nc.scalar.copy(cT[:, here], src[DS:2 * DS])
                                    ins.then_inc(acc_done, 1)

                    @block.vector
                    def _(dve):
                        dve.wait_ge(loaded, 16 * 7)
                        nc.vector.tensor_scalar(w_in[:], w_in[:], scale[:], None, ALU.mult).then_inc(scaled, 1)
                        with dve.Fori(0, B) as b:
                            for k in range(2):
                                nc.vector.tensor_copy(staged[:, k], xn[:, ds((b * 2 + k) * GW, GW)]).then_inc(staged_ready, 1)
                                dve.wait_ge(tok_ready, b * 2 + (k + 3))
                                nc.vector.tensor_copy(tok[:].rearrange("p t m -> p (t m)")[:, ds((b * 2 + k) * TG * TM, TG * TM)],
                                                      acc_t[:, k, 0:TG * TM]).then_inc(tok_done, 1)

            with ExitStack() as st3:
                c3 = Core(nc, st3, "l1d")
                low, soft = c3.sb("low", [P, NT, H]), c3.sb("soft", [P, NT, H])
                conv = c3.sb("conv", [P, 2, F2, S])
                spare = c3.sb("spare", [1, 1])
                chain_sem, low_ready, a_ready = c3.sem("chain"), c3.sem("low_ready"), c3.sem("a_ready")
                begun = c3.sem("begun")
                soft_ready, act_chain, conv_ready, h_ready = c3.sem("soft_ready"), c3.sem("act_chain"), c3.sem("conv_ready"), c3.sem("h_ready")
                with nc.Block() as block:

                    @block.vector
                    def _(dve):
                        ch = Chain(dve, chain_sem)
                        ch.step(nc.vector.tensor_tensor(dt[:], tok[:, :, 0:H], dt_bias[:].unsqueeze(1).to_broadcast([P, NT, H]), ALU.add))
                        nc.vector.scalar_tensor_tensor(out=low[:], in0=dt[:], scalar=-1.0, in1=dt[:],
                                                       op0=ALU.mult, op1=ALU.min).then_inc(low_ready, 1)
                        dve.wait_ge(soft_ready, 1)
                        ch.step(nc.vector.scalar_tensor_tensor(out=dt[:], in0=dt[:], scalar=0.0, in1=soft[:],
                                                               op0=ALU.max, op1=ALU.add))
                        dve.wait_ge(a_ready, 1)
                        ch.step(nc.vector.scalar_tensor_tensor(out=adt[:], in0=dt[:], scalar=-1.0,
                                                               in1=a_log[:].unsqueeze(1).to_broadcast([P, NT, H]),
                                                               op0=ALU.mult, op1=ALU.mult))
                        base = ch.count
                        with dve.Fori(0, B // 2) as pair:
                            for q in range(2):
                                b = pair * 2 + q
                                for n in range(1, K):
                                    for f in range(F2):
                                        if n == 1:
                                            dve.wait_ge(begun, b * F2 + (f + 1))
                                        else:
                                            dve.wait_ge(chain_sem, b * (F2 * (K - 2)) + (base + (n - 2) * F2 + f + 1))
                                        ins = nc.vector.scalar_tensor_tensor(out=conv[:, q, f], in0=ssm[:, f, ds(b * s_b + (K - 1 - n), S)],
                                                                             scalar=conv_w[:, f, K - 1 - n:K - n], in1=conv[:, q, f],
                                                                             op0=ALU.mult, op1=ALU.add)
                                        ins.then_inc(conv_ready if n == K - 1 else chain_sem, 1)

                    @block.scalar
                    def _(act):
                        act.wait_ge(low_ready, 1)
                        nc.scalar.activation(low[:], low[:], ACT.Exp).then_inc(act_chain, 1)
                        act.wait_ge(act_chain, 1)
                        nc.scalar.activation(soft[:], low[:], ACT.Ln, bias=keep.ones[:, 0:1]).then_inc(soft_ready, 1)
                        nc.scalar.activation(a_log[:], a_log[:], ACT.Exp).then_inc(a_ready, 1)
                        bring_table(nc, keep, spare, ACT.Silu)

                        def begin(b, q):
                            for f in range(F2):
                                act.wait_ge(h_ready, b * F2 + (f + 1))
                                nc.scalar.activation(conv[:, q, f], ssm[:, f, ds(b * s_b + (K - 1), S)], ACT.Copy,
                                                     scale=conv_w[:, f, K - 1:K]).then_inc(begun, 1)

                        def batch(b, q, last):
                            if not last:
                                begin(b + 1, 1 - q)
                            for f in range(F2):
                                act.wait_ge(conv_ready, b * F2 + (f + 1))
                                nc.scalar.activation(hT[:, f, ds(b * S, S)], conv[:, q, f], ACT.Silu,
                                                     bias=conv_b[:, f:f + 1]).then_inc(h_ready, 1)

                        act.sem_inc(h_ready, 2 * F2)
                        begin(0, 0)
                        with act.Fori(0, B // 2 - 1) as pair:
                            for q in range(2):
                                batch(pair * 2 + q, q, False)
                        for q in range(2):
                            batch(B - 2 + q, q, q == 1)

        with ExitStack() as st2:
            c2 = Core(nc, st2, "l1s")
            hs, bs, ts = c2.sb("hs", [P, B, F2, P]), c2.sb("bs", [DS, B, P]), c2.sb("ts", [P, B, DS])
            acol = c2.sb("acol", [P, B, H])
            gap, decay = c2.sb("gap", [P, 2, H, P]), c2.sb("decay", [P, 2, H, P])
            into = c2.sb("into", [DS, 2, H, P])
            wgap, wcol = c2.sb("wgap", [P, 2, H]), c2.sb("wcol", [P, 2, H])
            gm, mix = c2.sb("gm", [P, 2, P]), c2.sb("mix", [P, 2, H, P])
            hd, hw = c2.sb("hd", [P, 2, DI]), c2.sb("hw", [P, 2, DI])
            cs = c2.sb("cs", [DS, 2, H, P])
            state = c2.sb("state", [DS, B, DI])
            ys = c2.sb("ys", [P, 2, F2, P])
            run = c2.ps("run", [P, 2, H, P])
            mid = c2.ps("mid", [P, 2, GW])
            res = c2.ps("res", [P, 2, GW])
            fin = c2.ps("fin", [P, 2, GW])
            col = lambda q: mid[:, q, 0:H]
            htok = lambda q: mid[:, q, P:P + DI]
            gram = lambda q: mid[:, q, P + DI:P + DI + P]
            yT = lambda q, f: res[:, q, f * P:(f + 1) * P]
            delta = lambda q: res[0:DS, q, DI:2 * DI]
            staged, sums, gaps = c2.sem("staged"), c2.sem("sums"), c2.sem("gaps")
            raised, mixed, pool_mixed = c2.sem("raised"), c2.sem("mixed"), c2.sem("pool_mixed")
            y_ready, gated, out_ready, added = c2.sem("y_ready"), c2.sem("gated"), c2.sem("out_ready"), c2.sem("added")
            hd_sem, state_sem, zeroed = c2.sem("hd_sem"), c2.sem("state_sem"), c2.sem("zeroed")
            NS = 4

            def over_chunks(engine, part):
                part(0, True, False)
                with engine.Fori(1, NC_ - 1) as ck:
                    part(ck, False, False)
                part(NC_ - 1, False, True)

            def back(ck, j, steps):
                return (ck, j - steps) if j >= steps else (ck - 1, j - steps + B)

            with nc.Block() as block:

                @block.gpsimd
                def _(pool):
                    def stage(ck, j):
                        pool.wait_ge(y_ready, ck * B + (j + 1))
                        at = ck * P + j * S
                        nc.gpsimd.tensor_copy(acol[:, j], adt[:].rearrange("p t h -> p (t h)")[:, ds(ck * H + j * NC_ * H, H)]).then_inc(staged, 1)
                        nc.gpsimd.tensor_copy(hs[:, j], hT[:, :, ds(at, P)]).then_inc(staged, 1)
                        nc.gpsimd.tensor_copy(bs[:, j], bT[:, ds(at, P)]).then_inc(staged, 1)
                        nc.gpsimd.tensor_copy(ts[:, j], tok[:].rearrange("p t m -> p (t m)")[:, ds(ck * TM + (j * NC_ * TM + H), DS)]).then_inc(staged, 1)

                    def chunk(ck, first, last):
                        for j in range(B):
                            if not (last and j == B - 1):
                                stage(ck if j < B - 1 else ck + 1, (j + 1) % B)
                            pool.wait_ge(raised, (ck * B + j) * 3 + 3)
                            pool.wait_ge(y_ready, ck * B + (j + 3))
                            nc.gpsimd.tensor_tensor(cs[:, j % 2], into[:, j % 2],
                                                    cT[:, ds(ck * P + j * S, P)].unsqueeze(1).to_broadcast([DS, H, P]),
                                                    ALU.mult).then_inc(pool_mixed, 1)

                    stage(0, 0)
                    over_chunks(pool, chunk)

                @block.tensor
                def _(pe):
                    pe.sem_inc(y_ready, B)
                    pe.sem_inc(mixed, 2)
                    pe.sem_inc(added, 2)
                    pe.sem_inc(gated, 2)
                    pe.wait_ge(zeroed, 1)

                    def project(ck, j):
                        pe.wait_ge(gated, ck * B + (j + 3))
                        pe.wait_ge(added, ck * B + (j + 1))
                        for f in range(F2):
                            ins = nc.tensor.matmul(fin[:, j % 2, 0:D], ys[:, j % 2, f], w_out[:, f], start=(f == 0), stop=(f == F2 - 1))
                        ins.then_inc(out_ready, 1)

                    def prepare(ck, j):
                        q = j % 2
                        pe.wait_ge(staged, (ck * B + j) * NS + NS)
                        pe.wait_ge(mixed, ck * B + (j + 1))
                        for h in range(H):
                            nc.tensor.matmul(run[:, q, h], acol[:, j, h:h + 1].to_broadcast([P, P]), keep.upto[:], start=True, stop=True)
                        nc.tensor.matmul(col(q), keep.upto[:], acol[:, j], start=True, stop=True)
                        for f in range(F2):
                            nc.tensor.transpose(htok(q)[:, f * P:(f + 1) * P], hs[:, j, f], keep.ident[:])
                        nc.tensor.matmul(gram(q), bs[:, j], cT[:, ds(ck * P + j * S, P)], start=True, stop=True).then_inc(sums, 1)

                    def chunk(ck, first, last):
                        for j in range(B):
                            q = j % 2
                            if not (last and j == B - 1):
                                prepare(ck if j < B - 1 else ck + 1, (j + 1) % B)
                            pe.wait_ge(mixed, ck * B + (j + 3))
                            pe.wait_ge(pool_mixed, ck * B + (j + 1))
                            pe.wait_ge(gated, ck * B + (j + 1))
                            for h in range(H):
                                f, o = divmod(h * HD, P)
                                out = yT(q, f)[o:o + HD]
                                nc.tensor.matmul(out, hd[:, q, h * HD:(h + 1) * HD], mix[:, q, h], start=True, stop=False)
                                nc.tensor.matmul(out, state[:, j, h * HD:(h + 1) * HD], cs[:, q, h], start=False, stop=True)
                            nc.tensor.matmul(delta(q), ts[:, j], hw[:, q], start=True, stop=True).then_inc(y_ready, 1)
                            if not (first and j == 0):
                                project(*back(ck, j, 1))

                    prepare(0, 0)
                    over_chunks(pe, chunk)
                    project(NC_ - 1, B - 1)

                @block.scalar
                def _(act):
                    def chunk(ck, first, last):
                        for j in range(B):
                            q = j % 2
                            act.wait_ge(gaps, ck * B + (j + 1))
                            act.wait_ge(gated, ck * B + (j + 1))
                            act.wait_ge(y_ready, ck * B + (j + 3))
                            nc.scalar.activation(decay[:, q], gap[:, q], ACT.Exp).then_inc(raised, 1)
                            nc.scalar.activation(wcol[:, q], wgap[:, q], ACT.Exp).then_inc(raised, 1)
                            nc.scalar.activation(into[:, q], run[0:DS, q], ACT.Exp).then_inc(raised, 1)

                    over_chunks(act, chunk)

                @block.vector
                def _(dve):
                    nc.vector.memset(state[:], 0.0).then_inc(zeroed, 1)

                    def finish(ck, j):
                        q = j % 2
                        dve.wait_ge(y_ready, ck * B + (j + 1 + B))
                        last = into[:, q, :, P - 1:P].to_broadcast([DS, H, HD])
                        st_ = state[:, j].rearrange("n (h p) -> n h p", h=H)
                        nc.vector.tensor_tensor(st_, st_, last, ALU.mult).then_inc(state_sem, 1)
                        nc.vector.tensor_tensor(ys[:, q], res[:, q, 0:DI].rearrange("p (f t) -> p f t", f=F2),
                                                gate[:, :, ds(ck * P + j * S, P)], ALU.mult)
                        dve.wait_ge(state_sem, ck * B + (j + 1))
                        nc.vector.tensor_tensor(state[:, j], delta(q), state[:, j], ALU.add).then_inc(gated, 1)

                    def add(ck, j):
                        dve.wait_ge(out_ready, ck * B + (j + 1))
                        x = keep.x_tok[:, ds(ck * P + j * S, D)]
                        nc.vector.scalar_tensor_tensor(out=x, in0=x, scalar=2.0, in1=fin[:, j % 2, 0:D],
                                                       op0=ALU.mult, op1=ALU.add).then_inc(added, 1)

                    def chunk(ck, first, last):
                        for j in range(B):
                            q = j % 2
                            dve.wait_ge(sums, ck * B + (j + 1))
                            for h in range(H):
                                nc.vector.tensor_scalar(gap[:, q, h], run[:, q, h], col(q)[:, h:h + 1], 0.0, ALU.subtract, ALU.min)
                            nc.vector.tensor_copy(wcol[:, q], col(q)).then_inc(hd_sem, 1)
                            dve.wait_ge(hd_sem, (ck * B + j) * 2 + 1)
                            nc.vector.tensor_tensor(wgap[:, q], run[:, q, :, P - 1], wcol[:, q], ALU.subtract).then_inc(gaps, 1)
                            if not (first and j < 2):
                                finish(*back(ck, j, 2))
                            nc.vector.tensor_tensor(gm[:, q], gram(q), keep.upto[:], ALU.mult)
                            d = dt[:].rearrange("p t h -> p (t h)")[:, ds(ck * H + j * NC_ * H, H)]
                            nc.vector.tensor_tensor(hd[:, q].rearrange("p (h d) -> p h d", h=H), htok(q).rearrange("p (h d) -> p h d", h=H),
                                                    d.unsqueeze(2).to_broadcast([P, H, HD]), ALU.mult).then_inc(hd_sem, 1)
                            dve.wait_ge(raised, (ck * B + j) * 3 + 3)
                            dve.wait_ge(hd_sem, (ck * B + j) * 2 + 2)
                            nc.vector.tensor_tensor(hw[:, q].rearrange("p (h d) -> p h d", h=H), hd[:, q].rearrange("p (h d) -> p h d", h=H),
                                                    wcol[:, q].unsqueeze(2).to_broadcast([P, H, HD]), ALU.mult)
                            nc.vector.tensor_tensor(mix[:, q], decay[:, q], gm[:, q].unsqueeze(1).to_broadcast([P, H, P]),
                                                    ALU.mult).then_inc(mixed, 1)
                            if not (first and j < 3):
                                add(*back(ck, j, 3))

                    over_chunks(dve, chunk)
                    for j in range(B - 2, B):
                        finish(NC_ - 1, j)
                    for j in range(B - 3, B):
                        add(NC_ - 1, j)


def layer1_ffn(nc, keep, a):
    H, HD, SLOTS, F = 16, 8, 16, 512
    NF = F // P
    CT = 32
    ROUNDS = SLOTS * CT // P
    BS = B * SLOTS
    HQ = H * SLOTS
    INV = 1.0 / math.sqrt(HD)
    with ExitStack() as st:
        c = Core(nc, st, "l1f")
        w1, wg = c.sb("w1", [P, SLOTS, F]), c.sb("wg", [P, SLOTS, F])
        w2 = c.sb("w2", [P, SLOTS, NF, D])
        small = c.sb("small", [P, 8, D])
        cols = c.sb("cols", [P, 8])
        slot_T = c.sb("slot_T", [P, SLOTS])
        ln_g, ln_b = c.sb("ln_g", [BS, D]), c.sb("ln_b", [BS, D])
        b2T = c.sb("b2T", [P, SLOTS])
        c_bo = c.sb("c_bo", [P, D])
        head_mask = c.sb("head_mask", [P, H])
        own = c.sb("own", [P, 2, D])
        fold = c.sb("fold", [P, SLOTS])
        qblk = c.sb("qblk", [P, H, SLOTS])
        attT = c.sb("attT", [P, BS])
        o_T, o2T = c.sb("o_T", [P, BS]), c.sb("o2T", [P, BS])
        kblk, vblk = c.sb("kblk", [P, B, H, SLOTS]), c.sb("vblk", [P, B, H, SLOTS])
        vw = c.sb("vw", [P, B, 2, D])
        big_loaded = c.sem("big_loaded")
        wide3 = lambda x, shape: x.to_broadcast(shape)

        with ExitStack() as st2:
            c2 = Core(nc, st2, "l1g")
            qT = c2.sb("qT", [P, SLOTS])
            acc = c2.ps("acc", [P, 512])
            loaded, masks, acc_ready, chain_sem = c2.sem("loaded"), c2.sem("masks"), c2.sem("acc_ready"), c2.sem("chain")
            with nc.Block() as block:

                @block.sync
                def _(sp):
                    for n, name in enumerate(("d_Wq", "d_Wk", "d_Wo", "c_Wq", "c_Wk", "c_Wv", "c_Wo")):
                        sp.dma_start(small[:, n], a["L1_ffn_" + name]).then_inc(loaded, 16)
                    for dst, src in ((cols[:], "L1_ffn_bias_cols"), (slot_T[:], "L1_ffn_slot_T"), (b2T[:], "L1_ffn_b2_T")):
                        sp.dma_start(dst, a[src]).then_inc(loaded, 16)
                    for b in range(B):
                        sp.dma_start(ln_g[b * SLOTS:(b + 1) * SLOTS], a["L1_ffn_e_ln_g"]).then_inc(loaded, 16)
                        sp.dma_start(ln_b[b * SLOTS:(b + 1) * SLOTS], a["L1_ffn_e_ln_b"]).then_inc(loaded, 16)
                    sp.dma_start(c_bo[:], a["L1_ffn_c_bo"].rearrange("(o d) -> o d", o=1).broadcast_to([P, D])).then_inc(loaded, 16)
                    sp.wait_ge(loaded, 16 * (7 + 3 + 2 * B + 1))

                @block.gpsimd
                def _(pool):
                    ch = Chain(pool, masks)
                    sel = lambda ap, base, pattern, cm: ch.step(nc.gpsimd.affine_select(
                        out=ap, in_=ap, compare_op=ALU.is_ge, fill=0.0, base=base, pattern=pattern, channel_multiplier=cm))
                    ch.step(nc.gpsimd.memset(head_mask[:], 1.0))
                    sel(head_mask[:], 0, [[-HD, H]], 1)
                    sel(head_mask[:], HD - 1, [[HD, H]], -1)
                    ch.step(nc.gpsimd.memset(own[:], 1.0))
                    for f in range(2):
                        m = own[:, f].rearrange("p (h d) -> p h d", d=HD)
                        sel(m, P * f, [[-SLOTS, H], [0, HD]], 1)
                        sel(m, SLOTS - 1 - P * f, [[SLOTS, H], [0, HD]], -1)

                @block.tensor
                def _(pe):
                    pe.wait_ge(loaded, 16 * (7 + 3 + 2 * B + 1))
                    nc.tensor.matmul(acc[:, 0:SLOTS], small[:, 0], slot_T[:], start=True, stop=True).then_inc(acc_ready, 1)

                @block.vector
                def _(dve):
                    ch = Chain(dve, chain_sem)
                    ch.step(nc.vector.tensor_reduce(fold[:], keep.ident[:].rearrange("p (h q) -> p q h", q=SLOTS), AX.X, ALU.add))
                    dve.wait_ge(acc_ready, 1)
                    ch.step(nc.vector.tensor_scalar(qT[:], acc[:, 0:SLOTS], cols[:, 0:1], None, ALU.add))
                    dve.wait_ge(masks, 8)
                    ch.step(nc.vector.tensor_tensor(qblk[:], qT[:].unsqueeze(1).to_broadcast([P, H, SLOTS]),
                                                    head_mask[:].unsqueeze(2).to_broadcast([P, H, SLOTS]), ALU.mult))

        with ExitStack() as st2:
            c2 = Core(nc, st2, "l1h")
            kT = c2.sb("kT", [P, N])
            v_tok = c2.sb("v_tok", [P, N])
            project_tokens(nc, keep, "l1v", keep.x_T, a["L1_ffn_d_Wv"], v_tok, bias_dram=a["L1_ffn_d_bv"],
                           later=[(w1[:], a["L1_ffn_e_W1"].rearrange("e d f -> d e f")),
                                  (wg[:], a["L1_ffn_e_Wg"].rearrange("e d f -> d e f")),
                                  (w2[:], a["L1_ffn_e_W2"].rearrange("e (k p) d -> p e k d", p=P))], later_in=big_loaded)
            with ExitStack() as st3:
                c3 = Core(nc, st3, "l1k")
                acc = c3.ps("acc", [P, 2, GW])
                acc_ready, acc_done = c3.sem("acc_ready"), c3.sem("acc_done")
                with nc.Block() as block:

                    @block.tensor
                    def _(pe):
                        pe.sem_inc(acc_done, 2)
                        with pe.Fori(0, NG // 2) as pair:
                            for k in range(2):
                                pe.wait_ge(acc_done, pair * 2 + (k + 1))
                                nc.tensor.matmul(acc[:, k], small[:, 1], keep.x_T[:, ds((pair * 2 + k) * GW, GW)], start=True, stop=True)\
                                    .then_inc(acc_ready, 1)

                    @block.scalar
                    def _(act):
                        with act.Fori(0, NG // 2) as pair:
                            for k in range(2):
                                act.wait_ge(acc_ready, pair * 2 + (k + 1))
                                nc.scalar.activation(kT[:, ds((pair * 2 + k) * GW, GW)], acc[:, k], ACT.Identity, bias=cols[:, 1:2]).then_inc(acc_done, 1)

            with ExitStack() as st3:
                c3 = Core(nc, st3, "l1m")
                prob = c3.sb("prob", [P, 2, S])
                probT = c3.sb("probT", [P, 2, S])
                negmax, total, share = c3.sb("negmax", [P, 2]), c3.sb("total", [P, 2]), c3.sb("share", [P, 2])
                inverse = c3.sb("inverse", [P, 2])
                res = c3.sb("res", [P, 2, D])
                sc = c3.ps("sc", [P, 2, S])
                out = c3.ps("out", [P, 2, GW])
                fin = c3.ps("fin", [P, 2, GW])
                sc_ready, max_done, p_ready = c3.sem("sc_ready"), c3.sem("max_done"), c3.sem("p_ready")
                t_ready, t_done, out_ready, share_done = c3.sem("t_ready"), c3.sem("t_done"), c3.sem("out_ready"), c3.sem("share_done")
                res_ready, fin_ready, fin_done, scaled = c3.sem("res_ready"), c3.sem("fin_ready"), c3.sem("fin_done"), c3.sem("scaled")
                query_rows = qblk[:].rearrange("p h q -> p (h q)")

                def over_batches(engine, part):
                    part(0, True, False)
                    with engine.Fori(1, B - 1) as b:
                        part(b, False, False)
                    part(B - 1, False, True)

                with nc.Block() as block:

                    @block.tensor
                    def _(pe):
                        pe.sem_inc(fin_done, 1)
                        pe.sem_inc(t_ready, 2)
                        pe.sem_inc(out_ready, 2)
                        pe.sem_inc(res_ready, 2)
                        pe.sem_inc(fin_ready, 1)

                        def scores(b, f):
                            for o in range(2):
                                ins = nc.tensor.matmul(sc[:, f, o * GW:(o + 1) * GW], query_rows[:, f * P:(f + 1) * P],
                                                       kT[:, ds(b * S + o * GW, GW)], start=True, stop=True)
                            ins.then_inc(sc_ready, 1)

                        def batch(b, first, last):
                            for f in range(2):
                                pe.wait_ge(p_ready, b * 2 + (f + 1))
                                for t in range(S // P):
                                    ins = nc.tensor.transpose(sc[:, f, t * P:(t + 1) * P], prob[:, f, t * P:(t + 1) * P], keep.ident[:])
                                ins.then_inc(t_ready, 1)
                            for f in range(2):
                                pe.wait_ge(t_done, b * 2 + (f + 1))
                                if not last:
                                    scores(b + 1, f)
                            for f in range(2):
                                pe.wait_ge(res_ready, b * 2 + (f + 1))
                                for t in range(S // P):
                                    ins = nc.tensor.matmul(out[:, f, 0:D], probT[:, f, t * P:(t + 1) * P], v_tok[:, ds(b * S + t * P, D)],
                                                           start=(t == 0), stop=(t == S // P - 1))
                                ins.then_inc(out_ready, 1)
                            pe.wait_ge(res_ready, b * 2 + 4)
                            pe.wait_ge(fin_done, b + 1)
                            for f in range(2):
                                ins = nc.tensor.matmul(fin[:, 0, 0:SLOTS], res[:, f], fold[:], start=(f == 0), stop=(f == 1))
                            ins.then_inc(fin_ready, 1)

                        for f in range(2):
                            scores(0, f)
                        over_batches(pe, batch)

                    @block.scalar
                    def _(act):
                        def raise_(b, f):
                            act.wait_ge(scaled, b * 2 + (f + 1))
                            act.wait_ge(share_done, b * 2 + (f + 1))
                            act.wait_ge(t_ready, b * 2 + (f + 1))
                            nc.scalar.activation(prob[:, f], sc[:, f], ACT.Exp, bias=share[:, f:f + 1], scale=INV,
                                                 accum_out=total[:, f:f + 1]).then_inc(p_ready, 1)

                        def batch(b, first, last):
                            for f in range(2):
                                act.wait_ge(t_ready, b * 2 + (f + 3))
                                act.wait_ge(out_ready, b * 2 + (f + 1))
                                nc.scalar.copy(probT[:, f], sc[:, f]).then_inc(t_done, 1)
                            if not last:
                                for f in range(2):
                                    raise_(b + 1, f)

                        for f in range(2):
                            raise_(0, f)
                        over_batches(act, batch)

                    @block.vector
                    def _(dve):
                        dve.sem_inc(share_done, 2)

                        def maxima(b, f):
                            dve.wait_ge(sc_ready, b * 2 + (f + 1))
                            nc.vector.tensor_reduce(negmax[:, f:f + 1], sc[:, f], AX.X, ALU.max, negate=True).then_inc(max_done, 1)
                            dve.wait_ge(max_done, b * 2 + (f + 1))
                            nc.vector.tensor_scalar(share[:, f:f + 1], negmax[:, f:f + 1], INV, None, ALU.mult).then_inc(scaled, 1)

                        def batch(b, first, last):
                            for f in range(2):
                                dve.wait_ge(p_ready, b * 2 + (f + 1))
                                nc.vector.reciprocal(inverse[:, f:f + 1], total[:, f:f + 1]).then_inc(share_done, 1)
                            if not last:
                                for f in range(2):
                                    maxima(b + 1, f)
                            for f in range(2):
                                dve.wait_ge(out_ready, b * 2 + (f + 3))
                                dve.wait_ge(share_done, b * 2 + (f + 3))
                                dve.wait_ge(fin_ready, b + 1)
                                nc.vector.scalar_tensor_tensor(out=res[:, f], in0=out[:, f, 0:D], scalar=inverse[:, f:f + 1], in1=own[:, f],
                                                               op0=ALU.mult, op1=ALU.mult).then_inc(res_ready, 1)
                            dve.wait_ge(fin_ready, b + 2)
                            nc.vector.tensor_copy(attT[:, ds(b * SLOTS, SLOTS)], fin[:, 0, 0:SLOTS]).then_inc(fin_done, 1)

                        for f in range(2):
                            maxima(0, f)
                        over_batches(dve, batch)

        with ExitStack() as st2:
            c2 = Core(nc, st2, "l1e")
            o_tok, h_tok = c2.sb("o_tok", [BS, D]), c2.sb("h_tok", [BS, D])
            stat, mv = c2.sb("stat", [BS, 6]), c2.sb("mv", [BS, 2])
            std = c2.sb("std", [BS, 1])
            hT = c2.sb("hT", [P, SLOTS, CT])
            b1, bg = c2.sb("b1", [P, ROUNDS, F]), c2.sb("bg", [P, ROUNDS, F])
            uu, gg = c2.sb("uu", [P, ROUNDS, F]), c2.sb("gg", [P, ROUNDS, F])
            loaded = c2.sem("loaded")
            hidT = c2.sb("hidT", [P, ROUNDS, NF, P])
            fell = c2.sb("fell", [P, ROUNDS, D])
            kvT = c2.sb("kvT", [P, 2, BS])
            bank = c2.ps("bank", [P, 2 * ROUNDS, GW])
            dve_sem, pe_sem, act_sem, padded = c2.sem("dve"), c2.sem("pe"), c2.sem("act"), c2.sem("padded")
            raw_ready, biased, lit, joined = c2.sem("raw_ready"), c2.sem("biased"), c2.sem("lit"), c2.sem("joined")
            turned, copied, down_ready, down_copied = c2.sem("turned"), c2.sem("copied"), c2.sem("down_ready"), c2.sem("down_copied")
            by_batch = lambda x: x.rearrange("p (b e) -> p b e", b=B)
            with nc.Block() as block:

                @block.sync
                def _(sp):
                    sp.dma_start(b1[:].rearrange("p r f -> p (r f)"), a["L1_ffn_b1_rows"]).then_inc(loaded, 16)
                    sp.dma_start(bg[:].rearrange("p r f -> p (r f)"), a["L1_ffn_bg_rows"]).then_inc(loaded, 16)

                @block.gpsimd
                def _(pool):
                    nc.gpsimd.memset(hT[:], 0.0).then_inc(padded, 1)

                @block.tensor
                def _(pe):
                    def down(r):
                        pe.wait_ge(copied, r + 1)
                        for q in range(4):
                            for f in range(NF):
                                ins = nc.tensor.matmul(bank[q * CT:(q + 1) * CT, ROUNDS + r, 0:D], hidT[:, r, f, q * CT:(q + 1) * CT],
                                                       w2[:, r * 4 + q, f], start=(f == 0), stop=(f == NF - 1))
                        ins.then_inc(down_ready, 1)

                    nc.tensor.matmul(bank[:, 0, 0:BS], small[:, 2], attT[:], start=True, stop=True).then_inc(pe_sem, 1)
                    pe.wait_ge(dve_sem, 2)
                    nc.tensor.transpose(bank[0:BS, 1, 0:D], o_T[:], keep.ident[:]).then_inc(pe_sem, 1)
                    pe.wait_ge(dve_sem, 8)
                    nc.tensor.transpose(bank[:, 2, 0:BS], h_tok[:], keep.ident[0:BS, 0:BS]).then_inc(pe_sem, 1)
                    pe.wait_ge(dve_sem, 9)
                    pe.wait_ge(big_loaded, 48)
                    for r in range(ROUNDS):
                        for place, w in ((r, w1), (ROUNDS + r, wg)):
                            for q in range(4):
                                e = r * 4 + q
                                ins = nc.tensor.matmul(bank[q * CT:(q + 1) * CT, place], hT[:, e], w[:, e], start=True, stop=True)
                        ins.then_inc(raw_ready, 1)
                    for r in range(ROUNDS):
                        pe.wait_ge(joined, r + 1)
                        for f in range(NF):
                            ins = nc.tensor.transpose(bank[:, r, f * P:(f + 1) * P], uu[:, r, f * P:(f + 1) * P], keep.ident[:])
                        ins.then_inc(turned, 1)
                        if r:
                            down(r - 1)
                    down(ROUNDS - 1)
                    for r in range(ROUNDS):
                        pe.wait_ge(down_copied, r + 1)
                        ins = nc.tensor.transpose(bank[:, 0, r * P:(r + 1) * P], fell[:, r], keep.ident[:])
                    ins.then_inc(pe_sem, 1)
                    pe.wait_ge(dve_sem, 11)
                    nc.tensor.matmul(bank[:, 1, 0:BS], small[:, 4], o2T[:], start=True, stop=True)
                    nc.tensor.matmul(bank[:, 1, BS:2 * BS], small[:, 5], o2T[:], start=True, stop=True).then_inc(pe_sem, 1)
                    pe.wait_ge(dve_sem, 13 + 2 * B)
                    for b in range(B):
                        for f in range(2):
                            ins = nc.tensor.matmul(bank[:, 2 + f, b * D:(b + 1) * D],
                                                   vblk[:, b].rearrange("p h k -> p (h k)")[:, f * P:(f + 1) * P], small[:, 6], start=True, stop=True)
                    ins.then_inc(pe_sem, 1)

                @block.scalar
                def _(act):
                    act.wait_ge(dve_sem, 4)
                    nc.scalar.activation(std[:], mv[:, 1:2], ACT.Sqrt, bias=keep.eps[0:BS]).then_inc(act_sem, 1)
                    for r in range(ROUNDS):
                        act.wait_ge(biased, r + 1)
                        nc.scalar.activation(uu[:, r], uu[:, r], ACT.Silu)
                        nc.scalar.activation(gg[:, r], gg[:, r], ACT.Silu).then_inc(lit, 1)
                    for r in range(ROUNDS):
                        act.wait_ge(turned, r + 1)
                        nc.scalar.copy(hidT[:, r].rearrange("p f c -> p (f c)"), bank[:, r]).then_inc(copied, 1)

                @block.vector
                def _(dve):
                    ch = Chain(dve, dve_sem)
                    dve.wait_ge(pe_sem, 1)
                    ch.step(nc.vector.tensor_scalar(o_T[:], bank[:, 0, 0:BS], cols[:, 2:3], None, ALU.add))
                    ch.step(nc.vector.tensor_tensor(by_batch(o_T[:]), by_batch(o_T[:]), slot_T[:].unsqueeze(1).to_broadcast([P, B, SLOTS]), ALU.add))
                    dve.wait_ge(pe_sem, 2)
                    ch.step(nc.vector.bn_stats(stat[:], bank[0:BS, 1, 0:D]))
                    ch.step(nc.vector.bn_aggr(mv[:], stat[:]))
                    dve.wait_ge(act_sem, 1)
                    ch.step(nc.vector.reciprocal(std[:], std[:]))
                    ch.step(nc.vector.tensor_scalar(h_tok[:], bank[0:BS, 1, 0:D], mv[:, 0:1], std[:], ALU.subtract, ALU.mult))
                    ch.step(nc.vector.tensor_tensor(h_tok[:], h_tok[:], ln_g[:], ALU.mult))
                    ch.step(nc.vector.tensor_tensor(h_tok[:], h_tok[:], ln_b[:], ALU.add))
                    dve.wait_ge(pe_sem, 3)
                    dve.wait_ge(padded, 1)
                    ch.step(nc.vector.tensor_copy(hT[:, :, 0:B].rearrange("p e b -> p b e"), by_batch(bank[:, 2, 0:BS])))

                    def join(r):
                        dve.wait_ge(lit, r + 1)
                        nc.vector.tensor_tensor(uu[:, r], uu[:, r], gg[:, r], ALU.mult).then_inc(joined, 1)

                    dve.wait_ge(loaded, 32)
                    for r in range(ROUNDS):
                        dve.wait_ge(raw_ready, r + 1)
                        nc.vector.tensor_tensor(uu[:, r], bank[:, r], b1[:, r], ALU.add)
                        nc.vector.tensor_tensor(gg[:, r], bank[:, ROUNDS + r], bg[:, r], ALU.add).then_inc(biased, 1)
                        if r:
                            join(r - 1)
                    join(ROUNDS - 1)
                    for r in range(ROUNDS):
                        dve.wait_ge(down_ready, r + 1)
                        nc.vector.tensor_copy(fell[:, r], bank[:, ROUNDS + r, 0:D]).then_inc(down_copied, 1)
                    dve.wait_ge(pe_sem, 4)
                    e_out = bank[:, 0].rearrange("p (r q z) -> p z r q", r=ROUNDS, z=CT)[:, 0:B]
                    four = lambda x: x.rearrange("p (b r q) -> p b r q", b=B, q=4)
                    ch.step(nc.vector.tensor_tensor(four(o2T[:]), e_out, four(o_T[:]), ALU.add))
                    ch.step(nc.vector.tensor_tensor(by_batch(o2T[:]), by_batch(o2T[:]), b2T[:].unsqueeze(1).to_broadcast([P, B, SLOTS]), ALU.add))
                    dve.wait_ge(pe_sem, 5)
                    for m in range(2):
                        ch.step(nc.vector.tensor_scalar(kvT[:, m], bank[:, 1, m * BS:(m + 1) * BS], cols[:, 4 + m:5 + m], None, ALU.add))
                    for b in range(B):
                        for m, dst in enumerate((kblk, vblk)):
                            ch.step(nc.vector.tensor_tensor(dst[:, b], kvT[:, m, b * SLOTS:(b + 1) * SLOTS].unsqueeze(1).to_broadcast([P, H, SLOTS]),
                                                            head_mask[:].unsqueeze(2).to_broadcast([P, H, SLOTS]), ALU.mult))
                    dve.wait_ge(pe_sem, 6)
                    for f in range(2):
                        ch.step(nc.vector.tensor_copy(vw[:, :, f], bank[:, 2 + f].rearrange("p (b d) -> p b d", b=B)))

        with ExitStack() as st2:
            c2 = Core(nc, st2, "l1c")
            PB = S // (2 * P)
            qT = c2.sb("qT", [P, 2, GW])
            z, e = c2.sb("z", [P, 2, GW]), c2.sb("e", [P, 2, GW])
            top, total = c2.sb("top", [P, 2, 2 * H]), c2.sb("total", [P, 2, 2 * H])
            pT = c2.sb("pT", [P, 2, GW])
            sums = c2.sb("sums", [P, 2, 2 * D])
            qp = c2.ps("qp", [P, GW])
            sc = c2.ps("sc", [P, 2, GW])
            tp = c2.ps("tp", [P, 2, GW])
            out = c2.ps("out", [P, 2, GW])
            q_ready, q_done = c2.sem("q_ready"), c2.sem("q_done")
            sc_ready, sc_done, top_done, raised = c2.sem("sc_ready"), c2.sem("sc_done"), c2.sem("top_done"), c2.sem("raised")
            normed, t_ready, t_done, out_ready = c2.sem("normed"), c2.sem("t_ready"), c2.sem("t_done"), c2.sem("out_ready")
            out_done, added, sum_done = c2.sem("out_done"), c2.sem("added"), c2.sem("sum_done")
            k3 = kblk[:].rearrange("p b h k -> p (b h k)")
            vw3 = vw[:].rearrange("p b f d -> p (b f d)")
            heads = lambda x: x.rearrange("p (g k) -> p g k", k=SLOTS)
            wide = lambda x: x.unsqueeze(2).to_broadcast([P, 2 * H, SLOTS])

            def over_batches(engine, part):
                part(0, True, False)
                with engine.Fori(1, B - 1) as b:
                    part(b, False, False)
                part(B - 1, False, True)

            def shifted(b, i, steps):
                return b + (i + steps) // PB, (i + steps) % PB

            with nc.Block() as block:

                @block.tensor
                def _(pe):
                    pe.sem_inc(sc_done, 2)
                    pe.sem_inc(t_done, 2)
                    pe.sem_inc(t_ready, 2)
                    pe.sem_inc(out_done, 2)
                    pe.sem_inc(out_ready, 2)

                    def queries(b, half):
                        pe.wait_ge(q_done, b * 2 + half)
                        nc.tensor.matmul(qp[:], small[:, 3], keep.x_T[:, ds((b * 2 + half) * GW, GW)], start=True, stop=True).then_inc(q_ready, 1)

                    def scores(b, i):
                        k = i % 2
                        pe.wait_ge(q_done, b * 2 + (i // 2 + 1))
                        pe.wait_ge(sc_done, b * PB + (i + 1))
                        for t in range(2):
                            ins = nc.tensor.matmul(sc[:, k, t * HQ:(t + 1) * HQ], qT[:, i // 2, (k * 2 + t) * P:(k * 2 + t + 1) * P],
                                                   k3[:, ds(b * HQ, HQ)], start=True, stop=True)
                        ins.then_inc(sc_ready, 1)

                    def turn(b, i):
                        k = i % 2
                        pe.wait_ge(normed, b * PB + (i + 1))
                        pe.wait_ge(t_done, b * PB + (i + 1))
                        for t in range(4):
                            ins = nc.tensor.transpose(tp[:, k, t * P:(t + 1) * P], e[:, k, t * P:(t + 1) * P], keep.ident[:])
                        ins.then_inc(t_ready, 1)

                    def finish(b, i):
                        k = i % 2
                        pe.wait_ge(t_done, b * PB + (i + 3))
                        pe.wait_ge(out_done, b * PB + (i + 1))
                        for t in range(2):
                            for f in range(2):
                                ins = nc.tensor.matmul(out[:, k, t * D:(t + 1) * D], pT[:, k, (t * 2 + f) * P:(t * 2 + f + 1) * P],
                                                       vw3[:, ds(b * (2 * D) + f * D, D)], start=(f == 0), stop=(f == 1))
                        ins.then_inc(out_ready, 1)

                    def batch(b, first, last):
                        for i in range(PB):
                            k = i % 2
                            if not (last and i == PB - 1):
                                scores(*shifted(b, i, 1))
                            if k == 0 and not (last and i == 2):
                                queries(b + i // 2, 1 - i // 2)
                            if not (first and i == 0):
                                turn(*shifted(b, i, -1))
                            if not (first and i < 2):
                                finish(*shifted(b, i, -2))

                    queries(0, 0)
                    scores(0, 0)
                    over_batches(pe, batch)
                    turn(B - 1, PB - 1)
                    finish(B - 1, PB - 2)
                    finish(B - 1, PB - 1)

                @block.scalar
                def _(act):
                    def queries(b, half):
                        act.wait_ge(q_ready, b * 2 + (half + 1))
                        nc.scalar.activation(qT[:, half], qp[:], ACT.Identity, bias=cols[:, 3:4]).then_inc(q_done, 1)

                    def take(b, i):
                        act.wait_ge(t_ready, b * PB + (i + 3))
                        act.wait_ge(out_ready, b * PB + (i + 1))
                        nc.scalar.copy(pT[:, i % 2], tp[:, i % 2]).then_inc(t_done, 1)

                    def raise_(b, i):
                        act.wait_ge(sc_done, b * PB + (i + 3))
                        nc.scalar.activation(z[:, i % 2], z[:, i % 2], ACT.Exp, scale=INV).then_inc(raised, 1)

                    def batch(b, first, last):
                        for i in range(PB):
                            k = i % 2
                            if not (last and i == PB - 1):
                                raise_(*shifted(b, i, 1))
                            if k == 0 and not (last and i == 2):
                                queries(b + i // 2, 1 - i // 2)
                            if not (first and i == 0):
                                take(*shifted(b, i, -1))

                    queries(0, 0)
                    raise_(0, 0)
                    over_batches(act, batch)
                    take(B - 1, PB - 1)

                @block.vector
                def _(dve):
                    def shift(b, i):
                        k, n = i % 2, b * PB + i
                        dve.wait_ge(sc_ready, n + 1)
                        nc.vector.tensor_reduce(top[:, k], heads(sc[:, k]), AX.X, ALU.max).then_inc(top_done, 1)
                        dve.wait_ge(top_done, n + 1)
                        nc.vector.tensor_tensor(heads(z[:, k]), heads(sc[:, k]), wide(top[:, k]), ALU.subtract).then_inc(sc_done, 1)

                    def add(b, i):
                        k, n = i % 2, b * PB + i
                        dve.wait_ge(out_ready, n + 3)
                        nc.vector.tensor_tensor(sums[:, k].rearrange("p (t d) -> p t d", d=D), out[:, k, 0:2 * D].rearrange("p (t d) -> p t d", d=D),
                                                c_bo[:].unsqueeze(1).to_broadcast([P, 2, D]), ALU.add).then_inc(out_done, 1)
                        dve.wait_ge(out_done, n + 3)
                        x = keep.x_tok[:, ds(b * S + i * (2 * D), 2 * D)]
                        nc.vector.tensor_tensor(x, x, sums[:, k], ALU.add).then_inc(added, 1)

                    def batch(b, first, last):
                        for i in range(PB):
                            k, n = i % 2, b * PB + i
                            if not (last and i == PB - 1):
                                shift(*shifted(b, i, 1))
                            if not (first and i < 3):
                                add(*shifted(b, i, -3))
                            dve.wait_ge(raised, n + 1)
                            nc.vector.tensor_reduce(total[:, k], heads(z[:, k]), AX.X, ALU.add).then_inc(sum_done, 1)
                            dve.wait_ge(sum_done, n * 2 + 1)
                            nc.vector.reciprocal(total[:, k], total[:, k]).then_inc(sum_done, 1)
                            dve.wait_ge(sum_done, n * 2 + 2)
                            dve.wait_ge(t_ready, n + 1)
                            nc.vector.tensor_tensor(heads(e[:, k]), heads(z[:, k]), wide(total[:, k]), ALU.mult).then_inc(normed, 1)

                    shift(0, 0)
                    over_batches(dve, batch)
                    for i in range(PB - 3, PB):
                        add(B - 1, i)


def project_tokens(nc, keep, tag, src_T, w_dram, out, scaled=(), loads=(), bias_dram=None, add=False, later=(), later_in=None):
    with ExitStack() as st:
        c = Core(nc, st, tag + "pt")
        w = c.sb("w", [P, D])
        bias = c.sb("bias", [P, D]) if bias_dram is not None else None
        acc = c.ps("acc", [P, NG, GW])
        sums = c.sb("sums", [P, 2, GW]) if add else None
        biased = c.sem("biased")
        loaded, w_loaded = c.sem("loaded"), c.sem("w_loaded")
        acc_ready, acc_done, scale_done = c.sem("acc_ready"), c.sem("acc_done"), c.sem("scale_done")
        with nc.Block() as block:

            @block.sync
            def _(sp):
                sp.dma_start(w[:], w_dram).then_inc(w_loaded, 16)
                if bias_dram is not None:
                    sp.dma_start(bias[:], bias_dram.rearrange("(o d) -> o d", o=1).broadcast_to([P, D])).then_inc(w_loaded, 16)
                for dst, src in loads:
                    sp.dma_start(dst, src).then_inc(loaded, 16)
                for dst, src in later:
                    sp.dma_start(dst, src).then_inc(later_in, 16)
                if loads:
                    sp.wait_ge(loaded, 16 * len(loads))

            @block.tensor
            def _(pe):
                pe.wait_ge(w_loaded, 16 if bias_dram is None else 32)
                for g in range(NG):
                    for j in range(TG):
                        t = g * TG + j
                        ins = nc.tensor.matmul(acc[:, g, j * D:(j + 1) * D], src_T[:, t * P:(t + 1) * P], w[:], start=True, stop=True)
                    ins.then_inc(acc_ready, 1)

            @block.vector
            def _(dve):
                wide = lambda x: x.rearrange("p (t d) -> p t d", d=D)
                for g in range(NG):
                    dve.wait_ge(acc_ready, g + 1)
                    dst = out[:, g * GW:(g + 1) * GW]
                    if bias is None:
                        nc.vector.tensor_copy(dst, acc[:, g]).then_inc(acc_done, 1)
                        continue
                    to = sums[:, g % 2] if add else dst
                    nc.vector.tensor_tensor(wide(to), wide(acc[:, g]), bias[:].unsqueeze(1).to_broadcast([P, TG, D]),
                                            ALU.add).then_inc(acc_done, 1)
                    if add:
                        dve.wait_ge(acc_done, g + 1)
                        nc.vector.tensor_tensor(dst, dst, sums[:, g % 2], ALU.add).then_inc(biased, 1)
                if add:
                    dve.wait_ge(biased, NG)
                if loads:
                    dve.wait_ge(loaded, 16 * len(loads))
                for tile, factor in scaled:
                    nc.vector.tensor_scalar(tile, tile, factor, None, ALU.mult).then_inc(scale_done, 1)


def layer2_attn(nc, keep, a):
    SL, KS, VD = 8, 64, 16
    VP = 32
    HEADS = B * S // P
    Q = SL * P
    with ExitStack() as st:
        c = Core(nc, st, "l2a")
        mq, mk = c.sb("mq", [P, SL * KS]), c.sb("mk", [P, SL * KS])
        xv = c.sb("xv", [P, NT * D])
        project_tokens(nc, keep, "l2a", keep.x_T, a["L2_attn_Mv"], xv, scaled=[(mq[:], 1.0 / math.sqrt(KS))],
                       loads=[(mq[:], a["L2_attn_Mq"]), (mk[:], a["L2_attn_Mk"])])
        kT, qT = c.sb("kT", [KS, 2, Q]), c.sb("qT", [KS, 2, Q])
        RING = 4
        pT = c.sb("pT", [P, RING, Q])
        vs = c.sb("vs", [P, RING, SL, VP])
        negmax, total, share = c.sb("negmax", [P, 2]), c.sb("total", [P, RING]), c.sb("share", [P, RING])
        outT = c.sb("outT", [P, 2, 2 * P])
        xv3 = xv[:].rearrange("p (t d) -> p t d", d=D)
        sc = c.ps("sc", [P, 2, Q])
        pj = c.ps("pj", [P, 2, GW])
        out = c.ps("out", [P, 2, GW])
        qk_ready, max_done, p_ready = c.sem("qk_ready"), c.sem("max_done"), c.sem("p_ready")
        share_done, v_ready, pv_done = c.sem("share_done"), c.sem("v_ready"), c.sem("pv_done")
        pj_ready, pj_done, out_done = c.sem("pj_ready"), c.sem("pj_done"), c.sem("out_done")
        outT_ready, fin_ready, padded = c.sem("outT_ready"), c.sem("fin_ready"), c.sem("padded")

        def over_heads(engine, part):
            part(0, 0, True, False)
            part(1, 1, False, False)
            with engine.Fori(1, HEADS // 2 - 1) as pair:
                for q in range(2):
                    part(pair * 2 + q, q, False, False)
            part(HEADS - 2, 0, False, False)
            part(HEADS - 1, 1, False, True)

        with nc.Block() as block:

            @block.gpsimd
            def _(pool):
                nc.gpsimd.memset(vs[:].rearrange("p r j v -> p (r j) v")[:, :, VD:VP], 0.0).then_inc(padded, 1)
                pool.wait_ge(padded, 1)

            @block.tensor
            def _(pe):
                pe.sem_inc(p_ready, 2)
                pe.sem_inc(pv_done, RING)
                pe.sem_inc(out_done, 2)
                pe.wait_ge(padded, 1)

                def project(n):
                    pe.wait_ge(pj_done, n * 4)
                    for m, w in enumerate((mk, mq)):
                        for jj in range(SL // 2):
                            ins = nc.tensor.matmul(pj[:, m, jj * P:(jj + 1) * P], w[:, jj * P:(jj + 1) * P],
                                                   keep.x_T[:, ds(n * P, P)], start=True, stop=True)
                    ins.then_inc(pj_ready, 1)

                def values(n, q, kt):
                    pe.wait_ge(v_ready, n * SL + (kt + 1))
                    if kt == 0:
                        pe.wait_ge(out_done, n + 1)
                    for j in range(SL):
                        g, half = j % 4, j // 4
                        ins = nc.tensor.matmul(out[g * VP:(g + 1) * VP, q, half * P:(half + 1) * P], vs[:, kt % RING, j],
                                               pT[:, kt % RING, j * P:(j + 1) * P], start=(kt == 0 and half == 0),
                                               stop=(kt == SL - 1), skip_group_check=True)
                    ins.then_inc(pv_done, 1)

                def turn(n, q):
                    pe.wait_ge(outT_ready, n + 1)
                    for half in range(2):
                        ins = nc.tensor.transpose(out[:, q, (2 + half) * P:(3 + half) * P], outT[:, q, half * P:(half + 1) * P],
                                                  keep.ident[:])
                    ins.then_inc(fin_ready, 1)

                def head(n, q, first, last):
                    pe.wait_ge(pj_done, n * 4 + 4)
                    for kt in range(SL):
                        pe.wait_ge(p_ready, n * SL + (kt + 1))
                        for o in range(Q // GW):
                            ins = nc.tensor.matmul(sc[:, kt % 2, o * GW:(o + 1) * GW], kT[:, q, kt * P:(kt + 1) * P],
                                                   qT[:, q, o * GW:(o + 1) * GW], start=True, stop=True)
                        ins.then_inc(qk_ready, 1)
                        if kt >= 2:
                            values(n, q, kt - 2)
                        elif not first:
                            values(n - 1, 1 - q, SL - 2 + kt)
                        if kt == 2 and not last:
                            project(n + 1)
                        if kt == 3 and not first:
                            turn(n - 1, 1 - q)

                project(0)
                over_heads(pe, head)
                values(HEADS - 1, 1, SL - 2)
                values(HEADS - 1, 1, SL - 1)
                turn(HEADS - 1, 1)

            @block.scalar
            def _(act):
                def evacuate(n, q):
                    act.wait_ge(pj_ready, n + 1)
                    for m, dst in enumerate((kT, qT)):
                        d4 = dst[:, q].rearrange("k (j two r) -> k j two r", two=2, r=P)
                        for par in range(2):
                            nc.scalar.copy(d4[:, :, par], pj[par * KS:(par + 1) * KS, m].rearrange("k (j r) -> k j r", r=P))\
                                .then_inc(pj_done, 1)

                def result(n, q):
                    act.wait_ge(pv_done, n * SL + (SL + RING))
                    nc.scalar.copy(outT[:, q], out[:, q, 0:2 * P]).then_inc(outT_ready, 1)

                def head(n, q, first, last):
                    for kt in range(SL):
                        i = n * SL + kt
                        act.wait_ge(max_done, i + 1)
                        act.wait_ge(pv_done, i + 1)
                        nc.scalar.activation(pT[:, kt % RING], sc[:, kt % 2], ACT.Exp, bias=negmax[:, kt % 2:kt % 2 + 1],
                                             accum_out=total[:, kt % RING:kt % RING + 1]).then_inc(p_ready, 1)
                        if kt == 2 and not first:
                            result(n - 1, 1 - q)
                        if kt == 4 and not last:
                            evacuate(n + 1, 1 - q)

                evacuate(0, 0)
                over_heads(act, head)
                result(HEADS - 1, 1)

            @block.vector
            def _(dve):
                def head(n, q, first, last):
                    for kt in range(SL):
                        dve.wait_ge(qk_ready, n * SL + (kt + 1))
                        nc.vector.tensor_reduce(negmax[:, kt % 2:kt % 2 + 1], sc[:, kt % 2], AX.X, ALU.max,
                                                negate=True).then_inc(max_done, 1)
                        if kt:
                            apply(n, kt - 1)
                        elif not first:
                            apply(n - 1, SL - 1)
                        if kt == 4 and not first:
                            take(n - 1, 1 - q)

                def apply(n, kt):
                    r = kt % RING
                    dve.wait_ge(p_ready, n * SL + (kt + 3))
                    nc.vector.reciprocal(share[:, r:r + 1], total[:, r:r + 1]).then_inc(share_done, 1)
                    dve.wait_ge(share_done, n * SL + (kt + 1))
                    v = xv3[:, ds(n // SL * SL, SL), kt * VD:(kt + 1) * VD]
                    nc.vector.tensor_scalar(vs[:, r, :, 0:VD], v, share[:, r:r + 1], None, ALU.mult).then_inc(v_ready, 1)

                def take(n, q):
                    dve.wait_ge(fin_ready, n + 1)
                    x = keep.x_tok[:, ds(n * D, D)].rearrange("p (j d) -> p j d", d=VD)
                    res = out[:, q, 2 * P:4 * P].rearrange("p (j d) -> p j d", d=VP)[:, :, 0:VD]
                    nc.vector.tensor_tensor(x, res, x, ALU.add).then_inc(out_done, 1)

                over_heads(dve, head)
                apply(HEADS - 1, SL - 1)
                take(HEADS - 1, 1)


def sorted_places(nc, keep, tag, comb, tiles, weight, place, owner, cleared, gathered, x_sorted):
    with ExitStack() as st:
        c = Core(nc, st, tag + "sp")
        three = lambda x: x[:].rearrange("p (t e) -> p t e", e=8)
        hot, rows = c.sb("hot", [P, NT * 8]), c.sb("rows", [P, NT * 8])
        some = c.sb("some", [P, NT])
        tot, cum, zeros = c.sb("tot", [P, 8, NT]), c.sb("cum", [P, 8, NT]), c.sb("zeros", [P, 8 * NT])
        count, up_to, end = c.sb("count", [P, 8]), c.sb("up_to", [P, 8]), c.sb("end", [P, 8])
        whole = c.sb("whole", [P, 8], mybir.dt.int32)
        first_row = c.sb("first_row", [P, tiles])
        past = c.sb("past", [P, tiles, 6])
        ids = c.sb("ids", [P, tiles])
        sums = c.ps("sums", [P, 2, GW])
        chain_sem, hot_ready, sums_ready, numbered = c.sem("chain"), c.sem("hot_ready"), c.sem("sums_ready"), c.sem("numbered")
        zeroed = c.sem("zeroed")
        with nc.Block() as block:

            @block.gpsimd
            def _(pool):
                nc.gpsimd.memset(gathered[:], 0.0).then_inc(zeroed, 1)
                nc.gpsimd.iota(first_row[:], pattern=[[P, tiles]], base=0, channel_multiplier=0,
                               allow_small_or_imprecise_dtypes=True).then_inc(numbered, 1)

            @block.sync
            def _(sp):
                sp.wait_ge(zeroed, 1)
                for t in range(0, tiles, NT):
                    n = min(NT, tiles - t)
                    sp.dma_start(x_sorted[t * P:(t + n) * P].rearrange("(t p) d -> p t d", p=P),
                                 gathered[:, 0:n * D].rearrange("p (t d) -> p t d", d=D)).then_inc(cleared, 16)

            @block.tensor
            def _(pe):
                pe.wait_ge(hot_ready, 1)
                nc.tensor.matmul(sums[:, 0, 0:NT * 8], keep.upto[:], hot[:], start=True, stop=True)
                nc.tensor.matmul(sums[:, 1, 0:NT * 8], keep.ones[:, 0:P], hot[:], start=True, stop=True).then_inc(sums_ready, 1)

            @block.vector
            def _(dve):
                ch = Chain(dve, chain_sem)
                ch.step(nc.vector.memset(zeros[:], 0.0))
                ch.step(nc.vector.tensor_scalar(hot[:], comb[:], 0.0, None, ALU.is_gt))
                ch.step(nc.vector.tensor_reduce(weight[:], three(comb)[:, :, 0:7], AX.X, ALU.add))
                ch.step(nc.vector.tensor_reduce(some[:], three(hot)[:, :, 0:7], AX.X, ALU.add))
                nc.vector.tensor_scalar(three(hot)[:, :, 7], some[:], -1.0, 1.0, ALU.mult, ALU.add).then_inc(hot_ready, 1)
                dve.wait_ge(sums_ready, 1)
                ch.step(nc.vector.tensor_copy(tot[:], sums[:, 1, 0:NT * 8].rearrange("p (t e) -> p e t", e=8)))
                ch.step(nc.vector.tensor_tensor_scan(cum[:].rearrange("p e t -> p (e t)"), tot[:].rearrange("p e t -> p (e t)"),
                                                     zeros[:], zeros[:, 0:1], ALU.add, ALU.add))
                ch.step(nc.vector.tensor_reduce(count[:], tot[:], AX.X, ALU.add))
                ch.step(nc.vector.tensor_scalar(whole[:], count[:], float(P - 1), None, ALU.add))
                ch.step(nc.vector.tensor_scalar(whole[:], whole[:], 7, None, ALU.logical_shift_right))
                ch.step(nc.vector.tensor_scalar(whole[:], whole[:], 7, None, ALU.logical_shift_left))
                ch.step(nc.vector.tensor_copy(up_to[:], whole[:]))
                ch.step(nc.vector.tensor_tensor_scan(end[:], up_to[:], zeros[:, 0:8], zeros[:, 0:1], ALU.add, ALU.add))
                ch.step(nc.vector.tensor_tensor(up_to[:], end[:], up_to[:], ALU.subtract))
                ch.step(nc.vector.tensor_tensor(up_to[:], up_to[:], cum[:, :, NT - 1], ALU.subtract))
                ch.step(nc.vector.tensor_tensor(up_to[:], up_to[:], count[:], ALU.add))
                ch.step(nc.vector.tensor_tensor(cum[:], cum[:], tot[:], ALU.subtract))
                ch.step(nc.vector.tensor_tensor(cum[:], cum[:], up_to[:].unsqueeze(2).to_broadcast([P, 8, NT]), ALU.add))
                ch.step(nc.vector.tensor_tensor(three(rows), sums[:, 0, 0:NT * 8].rearrange("p (t e) -> p t e", e=8),
                                                cum[:].rearrange("p e t -> p t e"), ALU.add))
                ch.step(nc.vector.tensor_tensor(rows[:], rows[:], hot[:], ALU.mult))
                ch.step(nc.vector.tensor_reduce(some[:], three(rows), AX.X, ALU.add))
                ch.step(nc.vector.tensor_scalar(place[:], some[:], -1.0, None, ALU.add))
                dve.wait_ge(numbered, 1)
                ch.step(nc.vector.tensor_tensor(past[:], first_row[:].unsqueeze(2).to_broadcast([P, tiles, 6]),
                                                end[:, 0:6].unsqueeze(1).to_broadcast([P, tiles, 6]), ALU.is_ge))
                ch.step(nc.vector.tensor_reduce(ids[:], past[:], AX.X, ALU.add))
                ch.step(nc.vector.tensor_copy(owner[:], ids[0:1]))


def sorted_experts(nc, keep, tag, tiles, owner, up, gate, down, F, x_sorted, y_sorted, weights_in, stored):
    nf = F // P
    with ExitStack() as st:
        c = Core(nc, st, tag + "se")
        xs, xT = c.sb("xs", [P, 2, D]), c.sb("xT", [P, 2, P])
        lit_sb, hid, hidT = c.sb("lit_sb", [P, 2, F]), c.sb("hid", [P, 2, F]), c.sb("hidT", [P, 2, F])
        ys = c.sb("ys", [P, 2, D])
        raw = c.ps("raw", [P, 2, 2, GW])
        turned = c.ps("turned", [P, 2, GW])
        mix = c.ps("mix", [P, 2, GW])
        x_in = [c.sem("x_in0"), c.sem("x_in1")]
        xT_ready, xT_copied, raw_ready, lit = c.sem("xT_ready"), c.sem("xT_copied"), c.sem("raw_ready"), c.sem("lit")
        joined, turn_ready, turn_copied = c.sem("joined"), c.sem("turn_ready"), c.sem("turn_copied")
        out_ready, out_copied = c.sem("out_ready"), c.sem("out_copied")
        flat = lambda w: w[:].rearrange("p e f -> p (e f)")
        down_flat = down[:].rearrange("p e k d -> p (e k d)")
        by_tile = lambda x: x.rearrange("(t p) d -> t p d", p=P)

        def over_tiles(engine, part):
            for k in range(2):
                part(k, k, True, False)
            with engine.Fori(1, tiles // 2 - 1) as pair:
                for k in range(2):
                    part(pair * 2 + k, k, False, False)
            for k in range(2):
                part(tiles - 2 + k, k, False, True)

        with nc.Block() as block:

            @block.sync
            def _(sp):
                def load(n, k):
                    sp.dma_start(xs[:, k], x_sorted[ds(n * P, P)]).then_inc(x_in[k], 16)

                def store(n, k):
                    sp.wait_ge(out_copied, n + 3)
                    sp.dma_start(y_sorted[ds(n * P, P)], ys[:, k]).then_inc(stored[k], 16)

                def tile(n, k, first, last):
                    if not last:
                        sp.wait_ge(xT_ready, n + 1)
                        load(n + 2, k)
                    if not first:
                        store(n - 2, k)

                for k in range(2):
                    load(k, k)
                over_tiles(sp, tile)
                for k in range(2):
                    store(tiles - 2 + k, k)
                for k in range(2):
                    sp.wait_ge(stored[k], 16 * (tiles // 2) + 16)

            @block.tensor
            def _(pe):
                pe.sem_inc(joined, 2)
                pe.sem_inc(turn_ready, 2)
                pe.sem_inc(turn_copied, 2)
                pe.sem_inc(out_ready, 2)
                pe.sem_inc(out_copied, 2)
                pe.sem_inc(raw_ready, 2)

                def turn_x(n, k, visit, reused):
                    pe.wait_ge(x_in[k], 16 * (visit + 1))
                    if reused:
                        pe.wait_ge(out_copied, n - 1)
                    nc.tensor.transpose(mix[:, k, 0:P], xs[:, k], keep.ident[:]).then_inc(xT_ready, 1)

                def owner_of(n):
                    return pe.value_load(owner[0:1, ds(n, 1)], min_val=0, max_val=6)

                def rise(n, k):
                    expert = owner_of(n)
                    pe.wait_ge(xT_copied, n + 1)
                    pe.wait_ge(joined, n + 1)
                    nc.tensor.matmul(raw[:, k, 1, 0:F], xT[:, k], flat(gate)[:, ds(expert * F, F)], start=True, stop=True)
                    nc.tensor.matmul(raw[:, k, 0, 0:F], xT[:, k], flat(up)[:, ds(expert * F, F)], start=True, stop=True).then_inc(raw_ready, 1)

                def turn_hidden(n, k):
                    pe.wait_ge(joined, n + 3)
                    pe.wait_ge(turn_copied, n + 1)
                    for f in range(nf):
                        ins = nc.tensor.transpose(turned[:, k, f * P:(f + 1) * P], hid[:, k, f * P:(f + 1) * P], keep.ident[:])
                    ins.then_inc(turn_ready, 1)

                def fall(n, k):
                    expert = owner_of(n)
                    pe.wait_ge(turn_copied, n + 3)
                    pe.wait_ge(out_copied, n + 1)
                    for f in range(nf):
                        ins = nc.tensor.matmul(mix[:, k, P:P + D], hidT[:, k, f * P:(f + 1) * P],
                                               down_flat[:, ds(expert * (nf * D) + f * D, D)], start=(f == 0), stop=(f == nf - 1))
                    ins.then_inc(out_ready, 1)

                def tile(n, k, first, last):
                    rise(n, k)
                    if not (last and k == 1):
                        visit = (0 if k == 0 else 1) if first else (n // 2 if k == 0 else (n + 1) // 2)
                        turn_x(n + 1, 1 - k, visit, not (first and k == 0))
                    if not (first and k == 0):
                        turn_hidden(n - 1, 1 - k)
                    if not first:
                        fall(n - 2, k)

                turn_x(0, 0, 0, False)
                pe.wait_ge(weights_in, 16 * 3)
                over_tiles(pe, tile)
                turn_hidden(tiles - 1, 1)
                for k in range(2):
                    fall(tiles - 2 + k, k)

            @block.scalar
            def _(act):
                def copy_turned(n, k):
                    act.wait_ge(turn_ready, n + 3)
                    act.wait_ge(out_ready, n + 1)
                    nc.scalar.copy(hidT[:, k], turned[:, k, 0:F]).then_inc(turn_copied, 1)

                def tile(n, k, first, last):
                    act.wait_ge(raw_ready, n + 3)
                    act.wait_ge(joined, n + 1)
                    nc.scalar.activation(lit_sb[:, k], raw[:, k, 1, 0:F], ACT.Silu).then_inc(lit, 1)
                    if not (first and k == 0):
                        copy_turned(n - 1, 1 - k)

                over_tiles(act, tile)
                copy_turned(tiles - 1, 1)

            @block.vector
            def _(dve):
                for k in range(2):
                    dve.sem_inc(stored[k], 16)

                def copy_x(n, k):
                    dve.wait_ge(xT_ready, n + 1)
                    dve.wait_ge(raw_ready, n + 1)
                    nc.vector.tensor_copy(xT[:, k], mix[:, k, 0:P]).then_inc(xT_copied, 1)

                def copy_out(n, k, visit):
                    dve.wait_ge(out_ready, n + 3)
                    dve.wait_ge(stored[k], 16 * visit + 16)
                    nc.vector.tensor_copy(ys[:, k], mix[:, k, P:P + D]).then_inc(out_copied, 1)

                def tile(n, k, first, last):
                    if not (last and k == 1):
                        copy_x(n + 1, 1 - k)
                    dve.wait_ge(lit, n + 1)
                    dve.wait_ge(turn_ready, n + 1)
                    nc.vector.tensor_tensor(hid[:, k], raw[:, k, 0, 0:F], lit_sb[:, k], ALU.mult).then_inc(joined, 1)
                    if not first:
                        copy_out(n - 2, k, (n - 2 - k) // 2)

                copy_x(0, 0)
                over_tiles(dve, tile)
                for k in range(2):
                    copy_out(tiles - 2 + k, k, tiles // 2 - 1)


def layer2_ffn(nc, keep, a):
    E, F = 8, 512
    nf = F // P
    TILES = 2 * math.ceil((N + (E - 1) * (P - 1)) / (2 * P))
    x_sorted, y_sorted = (nc.dram_tensor(f"l2_{n}_sorted", (TILES * P, D), F32, kind="Internal").ap() for n in "xy")
    with ExitStack() as st:
        c = Core(nc, st, "l2f")
        up, gate = c.sb("up", [P, E, F]), c.sb("gate", [P, E, F])
        down = c.sb("down", [P, E, nf, D])
        logits, probs, comb = c.sb("logits", [P, NT * 8]), c.sb("probs", [P, NT * 8]), c.sb("comb", [P, NT * 8])
        weight = c.sb("weight", [P, NT])
        place = c.sb("place", [P, NT], mybir.dt.int32)
        owner = c.sb("owner", [1, TILES], mybir.dt.int32)
        gathered = c.sb("gathered", [P, N])
        weights_in, shared_in, cleared = c.sem("weights_in"), c.sem("shared_in"), c.sem("cleared")
        x_copied, scattered, back = c.sem("x_copied"), c.sem("scattered"), c.sem("back")
        stored = [c.sem("stored0"), c.sem("stored1")]
        router(nc, keep, "l2f", logits, a["L2_ffn_router_w"], None,
               [(up[:, E - 1], a["L2_ffn_shared_up_w"], shared_in),
                (gate[:, E - 1], a["L2_ffn_shared_gate_w"], shared_in),
                (down[:, E - 1], a["L2_ffn_shared_down_w"].rearrange("(k p) d -> p k d", p=P), shared_in),
                (up[:, 0:E - 1], a["L2_ffn_up_w"].rearrange("e d f -> d e f")),
                (gate[:, 0:E - 1], a["L2_ffn_gate_w"].rearrange("e d f -> d e f")),
                (down[:, 0:E - 1], a["L2_ffn_down_w"].rearrange("e (k p) d -> p e k d", p=P))], weights_in)
        softmax8(nc, keep, "l2f", logits, probs)
        pick_top(nc, keep, "l2f", probs, comb, 1, scale_top=2.0)
        sorted_places(nc, keep, "l2f", comb, TILES, weight, place, owner, cleared, gathered, x_sorted)

        def copy_x(dve):
            dve.wait_ge(cleared, 16 * math.ceil(TILES / NT))
            nc.vector.tensor_copy(gathered[:], keep.x_tok[:]).then_inc(x_copied, 1)

        def scatter(pool):
            pool.wait_ge(x_copied, 1)
            for t in range(NT):
                nc.gpsimd.indirect_dma_start(out=x_sorted, out_offset=bass.IndirectOffsetOnAxis(ap=place[:, t:t + 1], axis=0),
                                             in_=gathered[:, t * D:(t + 1) * D], in_offset=None).then_inc(scattered, 16)
            pool.wait_ge(scattered, 16 * NT)

        def gather(pool):
            for t in range(NT):
                nc.gpsimd.indirect_dma_start(out=gathered[:, t * D:(t + 1) * D], out_offset=None, in_=y_sorted,
                                             in_offset=bass.IndirectOffsetOnAxis(ap=place[:, t:t + 1], axis=0)).then_inc(back, 16)

        def shared_expert(first_group, **meanwhile):
            experts(nc, keep, f"l2f{first_group}", comb, shared_in, 3, 1, [P] * nf, lambda u, f: up[:, E - 1, f * P:(f + 1) * P],
                    lambda u, f: down[:, E - 1, f], 1, ACT.Silu, gate=lambda u, f: gate[:, E - 1, f * P:(f + 1) * P],
                    first_column=E - 1, groups=NG // 2, first_group=first_group, **meanwhile)

        shared_expert(0, beside=scatter, ahead=copy_x)
        sorted_experts(nc, keep, "l2f", TILES, owner, up, gate, down, F, x_sorted, y_sorted, weights_in, stored)

        shared_expert(NG // 2, beside=gather)
        with nc.Block() as block:

            @block.vector
            def _(dve):
                dve.wait_ge(back, 16 * NT)
                with dve.Fori(0, NT // 8) as t8:
                    for j in range(8):
                        t = t8 * 8 + j
                        x = keep.x_tok[:, ds(t * D, D)]
                        nc.vector.scalar_tensor_tensor(out=x, in0=gathered[:, ds(t * D, D)], scalar=weight[:, ds(t, 1)],
                                                       in1=x, op0=ALU.mult, op1=ALU.add)


def layer3_attn(nc, keep, a):
    H2 = P // 2
    LV = int(math.log2(S))
    two_pi = 2 * math.pi
    C1 = float(np.float32(6.28125))
    C2 = float(np.float32(1.93500518798828125e-3))
    C3 = two_pi - C1 - C2
    MAGIC = 1.5 * 2 ** 23
    with ExitStack() as st:
        c = Core(nc, st, "l3a")
        par = c.sb("par", [P, 3])
        b_ri = c.sb("b_ri", [P, 2, D])
        c_ri = c.sb("c_ri", [P, 2, D])
        dvec = c.sb("dvec", [P, D])
        cosT, sinT = c.sb("cosT", [P, S]), c.sb("sinT", [P, S])
        w12 = c.sb("w12", [P, 2, D])
        v12 = c.sb("v12", [P, 2, D])
        mag = c.sb("mag", [P, 1])
        with ExitStack() as st2:
            c2 = Core(nc, st2, "l3b")
            col = {}
            for name in ("step x y t q em1 g2 re im den gr gi al1 be1 al2 be2 u1 u2 sgn").split():
                col[name] = c2.sb("v_" + name, [P, 1])
            pw, ang, kk = c2.sb("pw", [P, LV]), c2.sb("ang", [P, LV]), c2.sb("kk", [P, LV])
            half, habs = c2.sb("half", [P, LV]), c2.sb("habs", [P, LV])
            sh, chh = c2.sb("sh", [P, LV]), c2.sb("chh", [P, LV])
            cs_, sn_ = c2.sb("cs_", [P, LV]), c2.sb("sn_", [P, LV])
            tmp = c2.sb("tmp", [P, S // 2])
            wrow = c2.sb("wrow", [P, 2, D])
            half_pi = c2.sb("half_pi", [P, 1])
            wT = c2.ps("wT", [P, 2, 512])
            loaded, chain_sem, to_act, from_act = c2.sem("loaded"), c2.sem("chain"), c2.sem("to_act"), c2.sem("from_act")
            rows_ready, turned = c2.sem("rows_ready"), c2.sem("turned")
            v = {k: t[:] for k, t in col.items()}
            with nc.Block() as block:

                @block.sync
                def _(sp):
                    for dst, src in [(par[:], a["L3_attn_par"]), (b_ri[:], a["L3_attn_B_ri"]), (c_ri[:], a["L3_attn_C_ri"]),
                                     (dvec[:], a["L3_attn_D"].rearrange("(o d) -> o d", o=1).broadcast_to([P, D]))]:
                        sp.dma_start(dst, src).then_inc(loaded, 16)
                    sp.wait_ge(loaded, 64)

                @block.scalar
                def _(act):
                    act.wait_ge(loaded, 64)
                    nc.scalar.activation(v["step"], par[:, 2:3], ACT.Exp).then_inc(from_act, 1)
                    act.wait_ge(to_act, 1)
                    nc.scalar.activation(v["t"], v["x"], ACT.Tanh, scale=0.5).then_inc(from_act, 1)
                    act.wait_ge(to_act, 2)
                    nc.scalar.activation(sh[:], half[:], ACT.Sin).then_inc(from_act, 1)
                    nc.scalar.activation(chh[:], habs[:], ACT.Sin).then_inc(from_act, 1)

                @block.tensor
                def _(pe):
                    pe.wait_ge(rows_ready, 1)
                    nc.tensor.transpose(wT[:, 0, 0:D], wrow[:, 0], keep.ident[:])
                    nc.tensor.transpose(wT[:, 1, 0:D], wrow[:, 1], keep.ident[:]).then_inc(turned, 1)

                @block.vector
                def _(dve):
                    ch = Chain(dve, chain_sem)
                    tt = lambda o, x, y_, op: ch.step(nc.vector.tensor_tensor(o, x, y_, op))
                    t1 = lambda o, x, s1, op, s2=None, op1=ALU.bypass: ch.step(nc.vector.tensor_scalar(o, x, s1, s2, op, op1))
                    M, A_, S_ = ALU.mult, ALU.add, ALU.subtract
                    for k in range(LV):
                        ch.step(nc.vector.memset(pw[:, k:k + 1], float(2 ** k)))
                    ch.step(nc.vector.memset(v["sgn"][0:H2], 1.0))
                    ch.step(nc.vector.memset(v["sgn"][H2:P], -1.0))
                    dve.wait_ge(from_act, 1)
                    t1(v["q"], par[:, 0:1], -1e-4, ALU.min)
                    tt(v["y"], par[:, 1:2], v["step"], M)
                    nc.vector.tensor_tensor(v["x"], v["q"], v["step"], M).then_inc(to_act, 1)
                    t1(ang[:], pw[:], v["y"], M)
                    t1(kk[:], ang[:], 1.0 / two_pi, M, MAGIC, A_)
                    t1(kk[:], kk[:], MAGIC, S_)
                    for part in (C1, C2, C3):
                        ch.step(nc.vector.scalar_tensor_tensor(out=ang[:], in0=kk[:], scalar=-part, in1=ang[:], op0=M, op1=A_))
                    t1(half[:], ang[:], 0.5, M, math.pi / 2, ALU.min)
                    t1(half[:], half[:], -math.pi / 2, ALU.max)
                    ch.step(nc.vector.scalar_tensor_tensor(out=habs[:], in0=half[:], scalar=-1.0, in1=half[:], op0=M, op1=ALU.min))
                    nc.vector.tensor_scalar(habs[:], habs[:], math.pi / 2, None, A_).then_inc(to_act, 1)
                    dve.wait_ge(from_act, 2)
                    t1(v["em1"], v["t"], -1.0, M, 1.0, A_)
                    ch.step(nc.vector.reciprocal(v["em1"], v["em1"]))
                    tt(v["em1"], v["em1"], v["t"], M)
                    t1(v["em1"], v["em1"], 2.0, M)
                    t1(mag[:], v["em1"], 1.0, A_)
                    dve.wait_ge(from_act, 4)
                    tt(kk[:], sh[:], sh[:], M)
                    t1(cs_[:], kk[:], -2.0, M, 1.0, A_)
                    ch.step(nc.vector.scalar_tensor_tensor(out=sn_[:], in0=sh[:], scalar=2.0, in1=chh[:], op0=M, op1=M))
                    tt(v["re"], v["em1"], cs_[:, 0:1], M)
                    ch.step(nc.vector.scalar_tensor_tensor(out=v["re"], in0=kk[:, 0:1], scalar=-2.0, in1=v["re"], op0=M, op1=A_))
                    tt(v["im"], mag[:], sn_[:, 0:1], M)
                    lre, lim = v["q"], par[:, 1:2]
                    tt(v["den"], lre, lre, M)
                    ch.step(nc.vector.scalar_tensor_tensor(out=v["den"], in0=lim, scalar=lim, in1=v["den"], op0=M, op1=A_))
                    ch.step(nc.vector.reciprocal(v["den"], v["den"]))
                    tt(v["u1"], v["im"], lim, M)
                    ch.step(nc.vector.scalar_tensor_tensor(out=v["gr"], in0=v["re"], scalar=lre, in1=v["u1"], op0=M, op1=A_))
                    tt(v["gr"], v["gr"], v["den"], M)
                    tt(v["u2"], v["re"], lim, M)
                    ch.step(nc.vector.scalar_tensor_tensor(out=v["gi"], in0=v["im"], scalar=lre, in1=v["u2"], op0=M, op1=S_))
                    tt(v["gi"], v["gi"], v["den"], M)
                    lo, hi = slice(0, H2), slice(H2, P)
                    for dst, half_, src, sign in (("al1", lo, "gr", 1.0), ("be1", lo, "gi", -1.0), ("al1", hi, "gi", 1.0), ("be1", hi, "gr", 1.0),
                                                  ("al2", lo, "gi", 1.0), ("be2", lo, "gr", 1.0), ("al2", hi, "gr", -1.0), ("be2", hi, "gi", 1.0)):
                        t1(v[dst][half_], v[src][half_], sign, M)
                    for n, (al, be) in enumerate((("al1", "be1"), ("al2", "be2"))):
                        t1(wrow[:, n], b_ri[:, 0], v[al], M)
                        ins = nc.vector.scalar_tensor_tensor(out=wrow[:, n], in0=b_ri[:, 1], scalar=v[be], in1=wrow[:, n], op0=M, op1=A_)
                        ch.step(ins)
                    dve.sem_inc(rows_ready, 1)
                    t1(v12[:, 0], c_ri[:, 0], v["sgn"], M)
                    t1(v12[:, 1], c_ri[:, 1], -1.0, M)
                    t1(dvec[:], dvec[:], 1.0, A_)
                    ch.step(nc.vector.memset(cosT[:, 0:1], 1.0))
                    ch.step(nc.vector.memset(sinT[:, 0:1], 0.0))
                    for k in range(LV):
                        w = 2 ** k
                        ck_, sk_ = cs_[:, k:k + 1], sn_[:, k:k + 1]
                        t1(tmp[:, 0:w], sinT[:, 0:w], sk_, M)
                        ch.step(nc.vector.scalar_tensor_tensor(out=cosT[:, w:2 * w], in0=cosT[:, 0:w], scalar=ck_, in1=tmp[:, 0:w], op0=M, op1=S_))
                        t1(tmp[:, 0:w], cosT[:, 0:w], sk_, M)
                        ch.step(nc.vector.scalar_tensor_tensor(out=sinT[:, w:2 * w], in0=sinT[:, 0:w], scalar=ck_, in1=tmp[:, 0:w], op0=M, op1=A_))
                    dve.wait_ge(turned, 1)
                    ch.step(nc.vector.tensor_copy(w12[:], wT[:, :, 0:D]))

        with ExitStack() as st2:
            c2 = Core(nc, st2, "l3c")
            uc, us = c2.sb("uc", [P, 2, GW]), c2.sb("us", [P, 2, GW])
            z, z1, z2 = c2.sb("z", [P, 2, GW]), c2.sb("z1", [P, 2, GW]), c2.sb("z2", [P, 2, GW])
            u = c2.ps("u", [P, 2, 2, GW])
            y = c2.ps("y", [P, 2, GW])
            u_ready, u_turned, summed = c2.sem("u_ready"), c2.sem("u_turned"), c2.sem("summed")
            scanned, back1, back2 = c2.sem("scanned"), c2.sem("back1"), c2.sem("back2")
            y_ready, added, skipped = c2.sem("y_ready"), c2.sem("added"), c2.sem("skipped")
            K2 = range(2)

            def over_batches(engine, part):
                part(0, True, False)
                with engine.Fori(1, B - 1) as b:
                    part(b, False, False)
                part(B - 1, False, True)

            with nc.Block() as block:

                @block.tensor
                def _(pe):
                    pe.sem_inc(u_turned, 2)
                    pe.sem_inc(added, 2)
                    pe.sem_inc(y_ready, 2)
                    pe.sem_inc(back2, 2)

                    def inputs(b):
                        for k in K2:
                            pe.wait_ge(u_turned, b * 2 + (k + 1))
                            x = keep.x_T[:, ds((b * 2 + k) * GW, GW)]
                            nc.tensor.matmul(u[:, k, 0], w12[:, 0], x, start=True, stop=True)
                            nc.tensor.matmul(u[:, k, 1], w12[:, 1], x, start=True, stop=True).then_inc(u_ready, 1)

                    def batch(b, first, last):
                        if not last:
                            inputs(b + 1)
                        for k in K2:
                            pe.wait_ge(back1, b * 2 + (k + 1))
                            pe.wait_ge(back2, b * 2 + (k + 3))
                            pe.wait_ge(added, b * 2 + (k + 1))
                            for j in range(TG):
                                o = slice(j * P, (j + 1) * P)
                                nc.tensor.matmul(y[:, k, o], z1[:, k, o], v12[:, 0], start=True, stop=False)
                                ins = nc.tensor.matmul(y[:, k, o], z2[:, k, o], v12[:, 1], start=False, stop=True)
                            ins.then_inc(y_ready, 1)

                    inputs(0)
                    over_batches(pe, batch)

                @block.gpsimd
                def _(pool):
                    with pool.Fori(0, B) as b:
                        for k in K2:
                            x3 = keep.x_tok[:, ds((b * 2 + k) * GW, GW)].rearrange("p (t d) -> p t d", d=D)
                            nc.gpsimd.tensor_tensor(x3, x3, dvec[:].unsqueeze(1).to_broadcast([P, TG, D]), ALU.mult).then_inc(skipped, 1)
                        for k in K2:
                            pool.wait_ge(scanned, b * 2 + (k + 1))
                            pool.wait_ge(y_ready, b * 2 + (k + 1))
                            nc.gpsimd.tensor_tensor(z2[:, k], z[:, k], sinT[:, k * GW:(k + 1) * GW], ALU.mult).then_inc(back2, 1)

                @block.vector
                def _(dve):
                    def add(b):
                        for k in K2:
                            x = keep.x_tok[:, ds((b * 2 + k) * GW, GW)]
                            dve.wait_ge(y_ready, b * 2 + (k + 3))
                            dve.wait_ge(skipped, b * 2 + (k + 1))
                            nc.vector.tensor_tensor(x, y[:, k], x, ALU.add).then_inc(added, 1)

                    def batch(b, first, last):
                        for k in K2:
                            o = slice(k * GW, (k + 1) * GW)
                            dve.wait_ge(u_ready, b * 2 + (k + 1))
                            nc.vector.tensor_tensor(uc[:, k], u[:, k, 0], cosT[:, o], ALU.mult)
                            nc.vector.tensor_tensor(us[:, k], u[:, k, 1], sinT[:, o], ALU.mult).then_inc(u_turned, 1)
                        for k in K2:
                            dve.wait_ge(u_turned, b * 2 + (k + 3))
                            nc.vector.tensor_tensor(uc[:, k], uc[:, k], us[:, k], ALU.add).then_inc(summed, 1)
                        for k in K2:
                            dve.wait_ge(summed, b * 2 + (k + 1))
                            dve.wait_ge(back2, b * 2 + (k + 1))
                            if k:
                                dve.wait_ge(scanned, b * 2 + k)
                            nc.vector.tensor_tensor_scan(z[:, k], mag[:].to_broadcast([P, GW]), uc[:, k],
                                                         z[:, 0, GW - 1:GW] if k else 0.0, ALU.mult, ALU.add).then_inc(scanned, 1)
                        if not first:
                            add(b - 1)
                        for k in K2:
                            dve.wait_ge(scanned, b * 2 + (k + 1))
                            dve.wait_ge(y_ready, b * 2 + (k + 1))
                            nc.vector.tensor_tensor(z1[:, k], z[:, k], cosT[:, k * GW:(k + 1) * GW], ALU.mult).then_inc(back1, 1)

                    over_batches(dve, batch)
                    add(B - 1)


def top_tokens(nc, keep, tag, probs, comb, count):
    Q = 16
    W = N // Q
    TP = NT // Q
    BITS = 30
    with ExitStack() as st:
        c = Core(nc, st, tag + "tt")
        val = c.sb("val", [P, W])
        ge, eq, before = c.sb("ge", [P, W]), c.sb("eq", [P, W]), c.sb("before", [P, W])
        cnt, carry = c.sb("cnt", [P, 2]), c.sb("carry", [P, 2])
        cut, trial = c.sb("cut", [P, 1], mybir.dt.int32), c.sb("trial", [P, 1], mybir.dt.int32)
        keepbit, room = c.sb("keepbit", [P, 1], mybir.dt.int32), c.sb("room", [P, 1])
        same, prior = c.sb("same", [P, P]), c.sb("prior", [P, P])
        tmp = c.sb("tmp", [P, P])
        zeros = c.sb("zeros", [P, W])
        spread = c.sb("spread", [P, 8, NT])
        turned = c.ps("turned", [P, 8, 512])
        sums = turned[:, 6]
        chain_sem, pool_sem, masks = c.sem("chain"), c.sem("pool_sem"), c.sem("masks")
        flips, counted, moved = c.sem("flips"), c.sem("counted"), c.sem("moved")
        asked, cast = c.sem("asked"), c.sem("cast")
        with nc.Block() as block:

            @block.gpsimd
            def _(pool):
                ch = Chain(pool, pool_sem)
                ch.step(nc.gpsimd.memset(same[:], 1.0))
                s3 = same[:].rearrange("p (e q) -> p e q", q=Q)
                ch.step(nc.gpsimd.affine_select(out=s3, in_=s3, compare_op=ALU.is_ge, fill=0.0, base=0,
                                                pattern=[[-Q, 8], [0, Q]], channel_multiplier=1))
                ch.step(nc.gpsimd.affine_select(out=s3, in_=s3, compare_op=ALU.is_ge, fill=0.0, base=Q - 1,
                                                pattern=[[Q, 8], [0, Q]], channel_multiplier=-1))
                ch.step(nc.gpsimd.affine_select(out=prior[:], in_=same[:], compare_op=ALU.is_gt, fill=0.0, base=0,
                                                pattern=[[1, P]], channel_multiplier=-1))
                nc.gpsimd.memset(zeros[:], 0.0).then_inc(masks, 1)
                pool.wait_ge(masks, 1)

            p3 = probs[:].rearrange("p (t e) -> p t e", e=8)
            @block.vector
            def _(dve):
                ch = Chain(dve, chain_sem)
                s4 = spread[:].rearrange("p e (q r) -> p r e q", r=TP)
                for r in range(TP):
                    ch.step(nc.vector.tensor_copy(spread[:].rearrange("p (r a) t -> p r (a t)", r=TP)[:, r].rearrange(
                        "p (e q) -> p e q", q=Q), p3.rearrange("p (q r) e -> p r e q", r=TP)[:, r]))
                nc.vector.memset(cut[:], 0).then_inc(asked, 1)
                dve.wait_ge(flips, 1)
                for r in range(TP):
                    ins = nc.vector.tensor_copy(val[:, r * P:(r + 1) * P], turned[:, r, 0:P])
                ch.step(ins)
                dve.wait_ge(masks, 1)
                n = [0]

                def count_from(bits, op, out_tile):
                    nc.vector.tensor_scalar(out_tile[:], val[:], bits.bitcast(F32), None, op, ALU.add,
                                            accum_out=cnt[:, 0:1]).then_inc(asked, 1)
                    n[0] += 1
                    dve.wait_ge(counted, n[0])

                for bit in reversed(range(BITS)):
                    ch.step(nc.vector.tensor_scalar(trial[:], cut[:], 1 << bit, None, ALU.bitwise_or))
                    count_from(trial[:], ALU.is_ge, ge)
                    ch.step(nc.vector.tensor_scalar(keepbit[:], sums[:, 0:1], float(count), float(1 << bit), ALU.is_ge, ALU.mult))
                    ch.step(nc.vector.tensor_tensor(cut[:], cut[:], keepbit[:], ALU.bitwise_or))
                count_from(cut[:], ALU.is_gt, ge)
                ch.step(nc.vector.tensor_scalar(room[:], sums[:, 0:1], -1.0, float(count), ALU.mult, ALU.add))
                nc.vector.tensor_scalar(eq[:], val[:], cut[:].bitcast(F32), None, ALU.is_equal, ALU.add,
                                        accum_out=cnt[:, 0:1]).then_inc(asked, 1)
                n[0] += 1
                dve.wait_ge(counted, n[0])
                ch.step(nc.vector.tensor_copy(carry[:, 0:1], sums[:, 1:2]))
                ch.step(nc.vector.tensor_tensor_scan(before[:], eq[:], zeros[:], carry[:, 0:1], ALU.add, ALU.add))
                ch.step(nc.vector.tensor_scalar(before[:], before[:], room[:], None, ALU.is_le))
                ch.step(nc.vector.tensor_tensor(eq[:], eq[:], before[:], ALU.mult))
                ch.step(nc.vector.tensor_tensor(ge[:], ge[:], eq[:], ALU.add))
                nc.vector.tensor_tensor(val[:], val[:], ge[:], ALU.mult).then_inc(moved, 1)
                dve.wait_ge(flips, 2)
                for r in range(TP):
                    ch.step(nc.vector.tensor_copy(
                        comb[:].rearrange("p (q r e) -> p r e q", r=TP, e=8)[:, r],
                        turned[:, 2 + r, 0:P].rearrange("p (e q) -> p e q", q=Q)))

            @block.tensor
            def _(pe):
                pe.wait_ge(asked, 1)
                pe.wait_ge(chain_sem, TP)
                for r in range(TP):
                    ins = nc.tensor.transpose(turned[:, r, 0:P], spread[:].rearrange("p (r a) t -> p r (a t)", r=TP)[:, r],
                                              keep.ident[:])
                ins.then_inc(flips, 1)
                pe.wait_ge(masks, 1)
                for i in range(BITS + 2):
                    pe.wait_ge(asked, i + 2)
                    which, column = (same, 0) if i <= BITS else (prior, 1)
                    nc.tensor.matmul(sums[:, column:column + 1], which[:], cnt[:, 0:1], start=True, stop=True).then_inc(counted, 1)
                pe.wait_ge(moved, 1)
                for r in range(TP):
                    ins = nc.tensor.transpose(turned[:, 2 + r, 0:P], val[:, r * P:(r + 1) * P], keep.ident[:])
                ins.then_inc(flips, 1)


def layer3_ffn(nc, keep, a):
    E, F, pairs = 8, 341, 4
    rows = [P, P, F - 2 * P]
    with ExitStack() as st:
        c = Core(nc, st, "l3f")
        up = c.sb("up", [P, pairs, F])
        b_up = c.sb("b_up", [P, pairs, 3])
        down = c.sb("down", [P, pairs, 3, 2, D])
        logits, probs, comb = c.sb("logits", [P, NT * 8]), c.sb("probs", [P, NT * 8]), c.sb("comb", [P, NT * 8])
        wd = a["L3_ffn_W_down"]
        loads = [(up[:], a["L3_ffn_W_up"].rearrange("g h f -> h g f")),
                 (b_up[:].rearrange("p g k -> p (g k)"), a["L3_ffn_b_up_cols"])]
        for f, r in enumerate(rows):
            for g in range(pairs):
                loads.append((down[0:r, g, f], wd[2 * g:2 * g + 2, f * P:f * P + r, :].rearrange("e p h -> p e h")))
        for g in range(pairs):
            loads.append((down[rows[2]:rows[2] + 1, g, 2],
                          a["L3_ffn_b_down"][2 * g:2 * g + 2].rearrange("(o e) h -> o e h", o=1)))
        weights_in = c.sem("weights_in")
        router(nc, keep, "l3f", logits, a["L3_ffn_Wr"], a["L3_ffn_br"].rearrange("(o e) -> o e", o=1), loads, weights_in)
        softmax8(nc, keep, "l3f", logits, probs)
        top_tokens(nc, keep, "l3f", probs, comb, N // E)
        heights = [P, P, rows[2] + 1]
        experts(nc, keep, "l3f", comb, weights_in, len(loads), pairs, rows, lambda u, f: up[:, u, f * P:f * P + rows[f]],
                lambda u, f: down[0:heights[f], u, f], 2, ACT.Silu, bias=lambda u, f: b_up[0:rows[f], u, f:f + 1])


def laid_out(inputs):
    out = {k: np.ascontiguousarray(v) for k, v in inputs.items()}
    b_up = out.pop("L3_ffn_b_up")
    cols = np.zeros((b_up.shape[0], 3 * P), b_up.dtype)
    cols[:, :b_up.shape[1]] = b_up
    out["L3_ffn_b_up_cols"] = np.ascontiguousarray(cols.reshape(-1, P).T)
    out["L1_attn_norm_scale_col"] = out.pop("L1_attn_norm_scale").reshape(P, 1)
    conv_w = out.pop("L1_attn_conv_weight")
    out["L1_attn_conv_w_cols"] = np.ascontiguousarray(conv_w.reshape(-1, 2, P).transpose(2, 1, 0).reshape(P, -1))
    out["L1_attn_conv_b_cols"] = np.ascontiguousarray(out.pop("L1_attn_conv_bias").reshape(2, P).T)
    par = np.stack([out.pop("L3_attn_Lambda_re"), out.pop("L3_attn_Lambda_im"), out.pop("L3_attn_log_step")[:, 0]], 1)
    out["L3_attn_par"] = np.concatenate([par, par])
    b_ri = out.pop("L3_attn_B").transpose(0, 2, 1)
    out["L3_attn_B_ri"] = np.concatenate([b_ri, b_ri])
    c_ri = out.pop("L3_attn_C").transpose(1, 2, 0)
    out["L3_attn_C_ri"] = np.concatenate([c_ri, c_ri[:, ::-1]])
    for n in ("q", "k", "v", "o"):
        out[f"L0_attn_W{n}T"] = np.ascontiguousarray(out.pop(f"L0_attn_W{n}").T)
    out["L0_attn_bqk_cols"] = np.ascontiguousarray(np.stack([out.pop("L0_attn_bq"), out.pop("L0_attn_bk")], 1))
    freq = np.exp(np.arange(0, D, 2, dtype=np.float32) * np.float32(-np.log(10000.0) / D))
    angle = np.arange(S, dtype=np.float32)[:, None] * freq[None, :]
    for name, f in (("rope_cos", np.cos), ("rope_sin", np.sin)):
        table = f(angle).astype(np.float32).reshape(S // P, P, D // 2)
        out[name] = np.ascontiguousarray(table.transpose(1, 0, 2).reshape(P, -1))
    cols = [out.pop("L1_ffn_" + n) for n in ("d_bq", "d_bk", "d_bo", "c_bq", "c_bk", "c_bv")]
    out["L1_ffn_bias_cols"] = np.ascontiguousarray(np.stack(cols + [np.zeros_like(cols[0])] * 2, 1))
    out["L1_ffn_slot_T"] = np.ascontiguousarray(out.pop("L1_ffn_slot_query")[0].T)
    for n in ("b1", "bg"):
        b = out.pop("L1_ffn_e_" + n)
        rows = np.zeros((4, P // 4, b.shape[0] // 4, b.shape[1]), b.dtype)
        rows[:, :B] = b.reshape(-1, 4, b.shape[1]).transpose(1, 0, 2)[:, None]
        out[f"L1_ffn_{n}_rows"] = rows.reshape(P, -1)
    out["L1_ffn_b2_T"] = np.ascontiguousarray(out.pop("L1_ffn_e_b2").T)
    return out


class Keep:

    def __init__(self, nc, stack):
        sb = lambda name, shape: stack.enter_context(nc.sbuf_tensor(name, shape, F32))
        self.x_tok = sb("x_tok", [P, N])
        self.x_T = sb("x_T", [P, N])
        self.ident = sb("ident", [P, P])
        self.upto = sb("upto", [P, P])
        self.ones = sb("ones", [P, GW])
        self.eps, self.rms_eps = sb("eps", [P, 1]), sb("rms_eps", [P, 1])


def sequence_kernel(nc, a, out):
    with ExitStack() as st:
        keep = Keep(nc, st)
        moved = st.enter_context(nc.semaphore("moved"))
        tiles = lambda x: x.rearrange("(t p) d -> p t d", p=P)
        x3 = keep.x_tok[:].rearrange("p (t d) -> p t d", d=D)
        with nc.Block() as block:

            @block.sync
            def _(sp):
                sp.dma_start(x3, tiles(a["L0_attn_x"])).then_inc(moved, 16)
                sp.wait_ge(moved, 16)

        constants(nc, keep)
        layers = (layer0_attn, layer0_ffn, layer1_attn, layer1_ffn, layer2_attn, layer2_ffn, layer3_attn, layer3_ffn)
        for n, layer in enumerate(layers):
            with nc.cleanup_on_exit():
                layer(nc, keep, a)
                layernorm(nc, keep, f"n{n}", want_T=n < len(layers) - 1)
        with nc.Block() as block:

            @block.sync
            def _(sp):
                sp.dma_start(tiles(out), x3).then_inc(moved, 16)
                sp.wait_ge(moved, 32)


def kernel(**inputs):
    import concourse.bacc as bacc
    from concourse.bass_utils import run_bass_kernel_spmd

    arrays = laid_out({k: np.asarray(v) for k, v in inputs.items()})
    arrays["L0_attn_x"] = arrays["L0_attn_x"].reshape(N, D)
    nc = bacc.Bacc("TRN2", target_bir_lowering=False, num_devices=1)
    a = {k: nc.dram_tensor(f"in_{k}", v.shape, mybir.dt.from_np(v.dtype), kind="ExternalInput").ap() for k, v in arrays.items()}
    out = nc.dram_tensor("out", (N, D), F32, kind="ExternalOutput").ap()
    sequence_kernel(nc, a, out)
    result = run_bass_kernel_spmd(nc, [{f"in_{k}": v for k, v in arrays.items()}], core_ids=[0])
    return result.results[0]["out"].reshape(B, S, D)
```
